# Optimizing a Trainium2 kernel written in Bass

```python
import numpy as np
import jax
import jax.numpy as jnp

def _softmax(x, axis=-1):
    return jax.nn.softmax(x, axis=axis)

def _gelu(x):
    return jax.nn.gelu(x, approximate=True)

def _silu(x):
    return jax.nn.silu(x)

def _sigmoid(x):
    return jax.nn.sigmoid(x)

def _layernorm(x, axis=-1, eps=1e-05):
    m = jnp.mean(x, axis=axis, keepdims=True)
    v = jnp.var(x, axis=axis, keepdims=True)
    return (x - m) / jnp.sqrt(v + eps)

def _scatter_add(tgt, idx, src, axis=0):
    return tgt.at[idx].add(src)

def _segment_sum(src, seg, n):
    return jax.ops.segment_sum(src, seg, n)
kernel_name = 'mk_sandwich_d4_jaxref_r4_fef1c5'

def setup_inputs(seed: int=0):
    np.random.seed(seed)
    _w = jnp.asarray

    def _L0_attn_setup():
        import jax, jax.numpy as jnp
        import numpy as np
        D = 256
        H = 16
        HD = D // H
        K = 4
        I = int(D * 2.7)
        B, T = (2, 512)
        EPS = 1e-06
        GATE_BIAS = 4.0

        def _rmsnorm(x, w):
            return x * jax.lax.rsqrt(jnp.mean(x * x, axis=-1, keepdims=True) + EPS) * w

        def _causal_depthwise_conv(x, conv_w, conv_b):
            xt = jnp.transpose(x, (0, 2, 1))
            y = jax.lax.conv_general_dilated(xt, conv_w[:, None, :], window_strides=(1,), padding=[(K - 1, 0)], feature_group_count=D, dimension_numbers=('NCH', 'OIH', 'NCH'))
            y = jnp.transpose(y, (0, 2, 1)) + conv_b
            return jax.nn.silu(y)

        def _l2norm(x):
            return x * jax.lax.rsqrt(jnp.sum(x * x, axis=-1, keepdims=True) + EPS)

        def _gated_delta_rule(xc, wq, wk, wv, wb, wa):
            b, t = (xc.shape[0], xc.shape[1])
            q = _l2norm((xc @ wq).reshape(b, t, H, HD))
            k = _l2norm((xc @ wk).reshape(b, t, H, HD))
            v = (xc @ wv).reshape(b, t, H, HD)
            beta = jax.nn.sigmoid(xc @ wb)
            alpha = jax.nn.sigmoid(xc @ wa + GATE_BIAS)
            qt = jnp.moveaxis(q, 1, 0)
            kt = jnp.moveaxis(k, 1, 0)
            vt = jnp.moveaxis(v, 1, 0)
            bt = jnp.moveaxis(beta, 1, 0)
            at = jnp.moveaxis(alpha, 1, 0)
            S0 = jnp.zeros((b, H, HD, HD), xc.dtype)

            def step(S, inp):
                q_, k_, v_, b_, a_ = inp
                S = a_[..., None, None] * S
                pred = jnp.einsum('bhkv,bhk->bhv', S, k_)
                S = S + k_[..., :, None] * (b_[..., None] * (v_ - pred))[..., None, :]
                o = jnp.einsum('bhkv,bhk->bhv', S, q_)
                return (S, o)
            _, o = jax.lax.scan(step, S0, (qt, kt, vt, bt, at))
            return jnp.moveaxis(o, 1, 0).reshape(b, t, D)
        key = jax.random.key(seed)
        ks = jax.random.split(key, 16)
        s = D ** (-0.5)
        return {'x': jax.random.normal(ks[0], (B, T, D), jnp.float32), 'norm1_w': jnp.ones((D,), jnp.float32), 'norm2_w': jnp.ones((D,), jnp.float32), 'conv_w': jax.random.normal(ks[1], (D, K), jnp.float32) * 0.2, 'conv_b': jnp.zeros((D,), jnp.float32), 'wq': jax.random.normal(ks[2], (D, D), jnp.float32) * s, 'wk': jax.random.normal(ks[3], (D, D), jnp.float32) * s, 'wv': jax.random.normal(ks[4], (D, D), jnp.float32) * s, 'wb': jax.random.normal(ks[5], (D, H), jnp.float32) * s, 'wa': jax.random.normal(ks[6], (D, H), jnp.float32) * s, 'wo': jax.random.normal(ks[7], (D, D), jnp.float32) * s, 'wg': jax.random.normal(ks[8], (D, I), jnp.float32) * s, 'wu': jax.random.normal(ks[9], (D, I), jnp.float32) * s, 'wd': jax.random.normal(ks[10], (I, D), jnp.float32) * I ** (-0.5)}
    _L0_attn_in = _L0_attn_setup()

    def _L0_ffn_setup():
        import jax, jax.numpy as jnp
        import numpy as np
        HIDDEN = 256
        N_ROUTED = 16
        N_SHARED = 2
        TOP_K = 2
        MID_R = HIDDEN // 4
        MID_S = HIDDEN // 2
        key = jax.random.key(seed)
        ks = jax.random.split(key, 8)
        s = 0.02
        return {'x': jax.random.normal(ks[0], (2, 256, HIDDEN), dtype=jnp.float32), 'router_w': jax.random.normal(ks[1], (HIDDEN, N_ROUTED), dtype=jnp.float32) * s, 'wg_r': jax.random.normal(ks[2], (N_ROUTED, HIDDEN, MID_R), dtype=jnp.float32) * s, 'wu_r': jax.random.normal(ks[3], (N_ROUTED, HIDDEN, MID_R), dtype=jnp.float32) * s, 'wd_r': jax.random.normal(ks[4], (N_ROUTED, MID_R, HIDDEN), dtype=jnp.float32) * s, 'wg_s': jax.random.normal(ks[5], (N_SHARED, HIDDEN, MID_S), dtype=jnp.float32) * s, 'wu_s': jax.random.normal(ks[6], (N_SHARED, HIDDEN, MID_S), dtype=jnp.float32) * s, 'wd_s': jax.random.normal(ks[7], (N_SHARED, MID_S, HIDDEN), dtype=jnp.float32) * s}
    _L0_ffn_in = _L0_ffn_setup()

    def _L1_attn_setup():
        import jax, jax.numpy as jnp
        from jax import lax
        import numpy as np
        D_MODEL = 256
        D_STATE = 16
        D_CONV = 4
        EXPAND = 2
        D_INNER = EXPAND * D_MODEL
        DT_RANK = D_MODEL // 16
        B, L = (1, 256)

        def _mamba(x, in_w, conv_w, conv_b, xproj_w, dt_w, dt_b, Alog, Dp, out_w):
            xz = x @ in_w.T
            xi, z = jnp.split(xz, 2, axis=-1)
            xc = lax.conv_general_dilated(jnp.swapaxes(xi, 1, 2), conv_w, (1,), [(D_CONV - 1, 0)], feature_group_count=D_INNER)
            u = jnp.swapaxes(jax.nn.silu(xc + conv_b[None, :, None]), 1, 2)
            x_dbl = u @ xproj_w.T
            dt = x_dbl[..., :DT_RANK]
            Bm = x_dbl[..., DT_RANK:DT_RANK + D_STATE]
            Cm = x_dbl[..., DT_RANK + D_STATE:]
            delta = jax.nn.softplus(dt @ dt_w.T + dt_b)
            A = -jnp.exp(Alog)
            dA = jnp.exp(jnp.einsum('bld,dn->bldn', delta, A))
            dBu = jnp.einsum('bld,bln,bld->bldn', delta, Bm, u)

            def step(h, inputs):
                a, b, c = inputs
                h = a * h + b
                return (h, jnp.einsum('bdn,bn->bd', h, c))
            h0 = jnp.zeros((x.shape[0], D_INNER, D_STATE), x.dtype)
            _, ys = lax.scan(step, h0, (jnp.moveaxis(dA, 1, 0), jnp.moveaxis(dBu, 1, 0), jnp.moveaxis(Cm, 1, 0)))
            y = jnp.moveaxis(ys, 0, 1) + u * Dp
            return y * jax.nn.silu(z) @ out_w.T

        def _block(x, fw_in_w, fw_conv_w, fw_conv_b, fw_xproj_w, fw_dt_w, fw_dt_b, fw_Alog, fw_Dp, fw_out_w, bw_in_w, bw_conv_w, bw_conv_b, bw_xproj_w, bw_dt_w, bw_dt_b, bw_Alog, bw_Dp, bw_out_w, proj_w, proj_b, ln_w, ln_b):
            out_fw = _mamba(x, fw_in_w, fw_conv_w, fw_conv_b, fw_xproj_w, fw_dt_w, fw_dt_b, fw_Alog, fw_Dp, fw_out_w) + x
            xb = jnp.flip(x, axis=1)
            out_bw = jnp.flip(_mamba(xb, bw_in_w, bw_conv_w, bw_conv_b, bw_xproj_w, bw_dt_w, bw_dt_b, bw_Alog, bw_Dp, bw_out_w) + xb, axis=1)
            out = jnp.concatenate([out_fw, out_bw], axis=-1) @ proj_w.T + proj_b
            mu = out.mean(-1, keepdims=True)
            var = out.var(-1, keepdims=True)
            return (out - mu) / jnp.sqrt(var + 1e-05) * ln_w + ln_b
        key = jax.random.key(seed)
        ks = jax.random.split(key, 8)

        def nrm(k, shape, s=0.02):
            return jax.random.normal(k, shape, jnp.float32) * s

        def mamba_params(kbase):
            k = jax.random.split(kbase, 7)
            return {'in_w': nrm(k[0], (2 * D_INNER, D_MODEL)), 'conv_w': nrm(k[1], (D_INNER, 1, D_CONV), 0.1), 'conv_b': nrm(k[2], (D_INNER,), 0.1), 'xproj_w': nrm(k[3], (DT_RANK + 2 * D_STATE, D_INNER)), 'dt_w': nrm(k[4], (D_INNER, DT_RANK), 0.1), 'dt_b': nrm(k[5], (D_INNER,), 0.1), 'Alog': jnp.log(jnp.broadcast_to(jnp.arange(1.0, D_STATE + 1, dtype=jnp.float32), (D_INNER, D_STATE))), 'Dp': jnp.ones((D_INNER,), jnp.float32), 'out_w': nrm(k[6], (D_MODEL, D_INNER))}
        fw = mamba_params(ks[0])
        bw = mamba_params(ks[1])
        inp = {'x': jax.random.normal(ks[2], (B, L, D_MODEL), jnp.float32)}
        for n, p in fw.items():
            inp['fw_' + n] = p
        for n, p in bw.items():
            inp['bw_' + n] = p
        inp['proj_w'] = nrm(ks[3], (D_MODEL, 2 * D_MODEL))
        inp['proj_b'] = jnp.zeros((D_MODEL,), jnp.float32)
        inp['ln_w'] = jnp.ones((D_MODEL,), jnp.float32)
        inp['ln_b'] = jnp.zeros((D_MODEL,), jnp.float32)
        return inp
    _L1_attn_in = _L1_attn_setup()

    def _L1_ffn_setup():
        import jax, jax.numpy as jnp
        import numpy as np
        B, S, H, E, K = (4, 512, 256, 8, 2)
        key = jax.random.key(seed)
        k0, k1, k2, k3 = jax.random.split(key, 4)
        x = jax.random.normal(k0, (B, S, H), dtype=jnp.float32)
        router_w = jax.random.normal(k1, (E, H), dtype=jnp.float32) * np.float32(1.0 / np.sqrt(H))
        xav1 = np.float32(np.sqrt(2.0 / (2 * H + H)))
        w1 = jax.random.normal(k2, (E, 2 * H, H), dtype=jnp.float32) * xav1
        w2 = jax.random.normal(k3, (E, H, 2 * H), dtype=jnp.float32) * xav1
        return {'x': x, 'router_w': router_w, 'w1': w1, 'w2': w2}
    _L1_ffn_in = _L1_ffn_setup()

    def _L2_attn_setup():
        import jax, jax.numpy as jnp
        import numpy as np
        N_HEADS = 8
        BUCKET = 64
        EPS = 0.0001
        key = jax.random.key(seed)
        ks = jax.random.split(key, 8)
        B, S, D = (4, 2048, 256)
        s = 1.0 / np.sqrt(D).astype(np.float32)
        x = jax.random.normal(ks[0], (B, S, D), dtype=jnp.float32)
        W_hash = jax.random.normal(ks[1], (D, 2 * N_HEADS), dtype=jnp.float32) * s
        W_q = jax.random.normal(ks[2], (D, D), dtype=jnp.float32) * s
        b_q = jax.random.normal(ks[3], (D,), dtype=jnp.float32) * 0.01
        W_v = jax.random.normal(ks[4], (D, D), dtype=jnp.float32) * s
        b_v = jax.random.normal(ks[5], (D,), dtype=jnp.float32) * 0.01
        W_o = jax.random.normal(ks[6], (D, D), dtype=jnp.float32) * s
        b_o = jax.random.normal(ks[7], (D,), dtype=jnp.float32) * 0.01
        return {'x': x, 'W_hash': W_hash, 'W_q': W_q, 'b_q': b_q, 'W_v': W_v, 'b_v': b_v, 'W_o': W_o, 'b_o': b_o}
    _L2_attn_in = _L2_attn_setup()

    def _L2_ffn_setup():
        import jax, jax.numpy as jnp
        import numpy as np
        B, S, K, N = (8, 2048, 256, 256)
        key = jax.random.key(seed)
        k1, k2, k3, k4 = jax.random.split(key, 4)
        x = jax.random.normal(k1, (B, S, K), dtype=jnp.float32)
        CB = jnp.clip(jnp.round(jax.random.normal(k2, (N, K), dtype=jnp.float32) * 42.0), -127.0, 127.0)
        SCB = jax.random.uniform(k3, (N,), dtype=jnp.float32, minval=0.5, maxval=2.0)
        bias = jax.random.normal(k4, (N,), dtype=jnp.float32) * 0.02
        return {'x': x, 'CB': CB, 'SCB': SCB, 'bias': bias}
    _L2_ffn_in = _L2_ffn_setup()

    def _L3_attn_setup():
        import jax, jax.numpy as jnp
        import numpy as np
        N_HEAD = 16
        NEG_INF = jnp.finfo(jnp.float32).min
        key = jax.random.key(seed)
        k1, k2, k3, k4 = jax.random.split(key, 4)
        B, T, C = (4, 512, 256)
        x = jax.random.normal(k1, (B, T, C), dtype=jnp.float32)
        w_attn = jax.random.normal(k2, (C, 3 * C), dtype=jnp.float32) * C ** (-0.5)
        w_proj = jax.random.normal(k3, (C, C), dtype=jnp.float32) * C ** (-0.5)
        decay_raw = jax.random.normal(k4, (N_HEAD,), dtype=jnp.float32)
        return {'x': x, 'w_attn': w_attn, 'w_proj': w_proj, 'decay_raw': decay_raw}
    _L3_attn_in = _L3_attn_setup()

    def _L3_ffn_setup():
        import jax, jax.numpy as jnp
        import numpy as np
        B, N, D = (4, 512, 256)
        SPARSITY = 0.01
        key = jax.random.key(seed)
        k1, k2, k3 = jax.random.split(key, 3)
        x = jax.random.normal(k1, (B, N, D), dtype=jnp.float32)
        spatial = jax.random.normal(k2, (D, D), dtype=jnp.float32) * 0.02
        freq = jnp.fft.fft(spatial, axis=-1)
        k = int(D * SPARSITY)
        mag = jnp.abs(freq)
        kth = jax.lax.top_k(mag, k)[0][:, -1:]
        w_sparse = jnp.where(mag >= kth, freq, 0.0 + 0j)
        bias = jax.random.normal(k3, (D,), dtype=jnp.float32) * 0.01
        return {'x': x, 'w_freq_real': jnp.real(w_sparse).astype(jnp.float32), 'w_freq_imag': jnp.imag(w_sparse).astype(jnp.float32), 'bias': bias}
    _L3_ffn_in = _L3_ffn_setup()
    _d = {'L0_attn_x': _L0_attn_in['x'], 'L0_attn_norm1_w': _L0_attn_in['norm1_w'], 'L0_attn_norm2_w': _L0_attn_in['norm2_w'], 'L0_attn_conv_w': _L0_attn_in['conv_w'], 'L0_attn_conv_b': _L0_attn_in['conv_b'], 'L0_attn_wq': _L0_attn_in['wq'], 'L0_attn_wk': _L0_attn_in['wk'], 'L0_attn_wv': _L0_attn_in['wv'], 'L0_attn_wb': _L0_attn_in['wb'], 'L0_attn_wa': _L0_attn_in['wa'], 'L0_attn_wo': _L0_attn_in['wo'], 'L0_attn_wg': _L0_attn_in['wg'], 'L0_attn_wu': _L0_attn_in['wu'], 'L0_attn_wd': _L0_attn_in['wd'], 'L0_ffn_router_w': _L0_ffn_in['router_w'], 'L0_ffn_wg_r': _L0_ffn_in['wg_r'], 'L0_ffn_wu_r': _L0_ffn_in['wu_r'], 'L0_ffn_wd_r': _L0_ffn_in['wd_r'], 'L0_ffn_wg_s': _L0_ffn_in['wg_s'], 'L0_ffn_wu_s': _L0_ffn_in['wu_s'], 'L0_ffn_wd_s': _L0_ffn_in['wd_s'], 'L1_attn_fw_in_w': _L1_attn_in['fw_in_w'], 'L1_attn_fw_conv_w': _L1_attn_in['fw_conv_w'], 'L1_attn_fw_conv_b': _L1_attn_in['fw_conv_b'], 'L1_attn_fw_xproj_w': _L1_attn_in['fw_xproj_w'], 'L1_attn_fw_dt_w': _L1_attn_in['fw_dt_w'], 'L1_attn_fw_dt_b': _L1_attn_in['fw_dt_b'], 'L1_attn_fw_Alog': _L1_attn_in['fw_Alog'], 'L1_attn_fw_Dp': _L1_attn_in['fw_Dp'], 'L1_attn_fw_out_w': _L1_attn_in['fw_out_w'], 'L1_attn_bw_in_w': _L1_attn_in['bw_in_w'], 'L1_attn_bw_conv_w': _L1_attn_in['bw_conv_w'], 'L1_attn_bw_conv_b': _L1_attn_in['bw_conv_b'], 'L1_attn_bw_xproj_w': _L1_attn_in['bw_xproj_w'], 'L1_attn_bw_dt_w': _L1_attn_in['bw_dt_w'], 'L1_attn_bw_dt_b': _L1_attn_in['bw_dt_b'], 'L1_attn_bw_Alog': _L1_attn_in['bw_Alog'], 'L1_attn_bw_Dp': _L1_attn_in['bw_Dp'], 'L1_attn_bw_out_w': _L1_attn_in['bw_out_w'], 'L1_attn_proj_w': _L1_attn_in['proj_w'], 'L1_attn_proj_b': _L1_attn_in['proj_b'], 'L1_attn_ln_w': _L1_attn_in['ln_w'], 'L1_attn_ln_b': _L1_attn_in['ln_b'], 'L1_ffn_router_w': _L1_ffn_in['router_w'], 'L1_ffn_w1': _L1_ffn_in['w1'], 'L1_ffn_w2': _L1_ffn_in['w2'], 'L2_attn_W_hash': _L2_attn_in['W_hash'], 'L2_attn_W_q': _L2_attn_in['W_q'], 'L2_attn_b_q': _L2_attn_in['b_q'], 'L2_attn_W_v': _L2_attn_in['W_v'], 'L2_attn_b_v': _L2_attn_in['b_v'], 'L2_attn_W_o': _L2_attn_in['W_o'], 'L2_attn_b_o': _L2_attn_in['b_o'], 'L2_ffn_CB': _L2_ffn_in['CB'], 'L2_ffn_SCB': _L2_ffn_in['SCB'], 'L2_ffn_bias': _L2_ffn_in['bias'], 'L3_attn_w_attn': _L3_attn_in['w_attn'], 'L3_attn_w_proj': _L3_attn_in['w_proj'], 'L3_attn_decay_raw': _L3_attn_in['decay_raw'], 'L3_ffn_w_freq_real': _L3_ffn_in['w_freq_real'], 'L3_ffn_w_freq_imag': _L3_ffn_in['w_freq_imag'], 'L3_ffn_bias': _L3_ffn_in['bias']}
    _x0 = _d['L0_attn_x']
    _d['L0_attn_x'] = jax.random.normal(jax.random.fold_in(jax.random.key(seed), 1), (8, 512, 256), dtype=_x0.dtype)
    del _x0
    return _d

def reference(L0_attn_x, L0_attn_norm1_w, L0_attn_norm2_w, L0_attn_conv_w, L0_attn_conv_b, L0_attn_wq, L0_attn_wk, L0_attn_wv, L0_attn_wb, L0_attn_wa, L0_attn_wo, L0_attn_wg, L0_attn_wu, L0_attn_wd, L0_ffn_router_w, L0_ffn_wg_r, L0_ffn_wu_r, L0_ffn_wd_r, L0_ffn_wg_s, L0_ffn_wu_s, L0_ffn_wd_s, L1_attn_fw_in_w, L1_attn_fw_conv_w, L1_attn_fw_conv_b, L1_attn_fw_xproj_w, L1_attn_fw_dt_w, L1_attn_fw_dt_b, L1_attn_fw_Alog, L1_attn_fw_Dp, L1_attn_fw_out_w, L1_attn_bw_in_w, L1_attn_bw_conv_w, L1_attn_bw_conv_b, L1_attn_bw_xproj_w, L1_attn_bw_dt_w, L1_attn_bw_dt_b, L1_attn_bw_Alog, L1_attn_bw_Dp, L1_attn_bw_out_w, L1_attn_proj_w, L1_attn_proj_b, L1_attn_ln_w, L1_attn_ln_b, L1_ffn_router_w, L1_ffn_w1, L1_ffn_w2, L2_attn_W_hash, L2_attn_W_q, L2_attn_b_q, L2_attn_W_v, L2_attn_b_v, L2_attn_W_o, L2_attn_b_o, L2_ffn_CB, L2_ffn_SCB, L2_ffn_bias, L3_attn_w_attn, L3_attn_w_proj, L3_attn_decay_raw, L3_ffn_w_freq_real, L3_ffn_w_freq_imag, L3_ffn_bias):

    def _L0_attn_ref(x, norm1_w, norm2_w, conv_w, conv_b, wq, wk, wv, wb, wa, wo, wg, wu, wd):
        import jax, jax.numpy as jnp
        import numpy as np
        D = 256
        H = 16
        HD = D // H
        K = 4
        I = int(D * 2.7)
        B, T = (2, 512)
        EPS = 1e-06
        GATE_BIAS = 4.0

        def _rmsnorm(x, w):
            return x * jax.lax.rsqrt(jnp.mean(x * x, axis=-1, keepdims=True) + EPS) * w

        def _causal_depthwise_conv(x, conv_w, conv_b):
            xt = jnp.transpose(x, (0, 2, 1))
            y = jax.lax.conv_general_dilated(xt, conv_w[:, None, :], window_strides=(1,), padding=[(K - 1, 0)], feature_group_count=D, dimension_numbers=('NCH', 'OIH', 'NCH'))
            y = jnp.transpose(y, (0, 2, 1)) + conv_b
            return jax.nn.silu(y)

        def _l2norm(x):
            return x * jax.lax.rsqrt(jnp.sum(x * x, axis=-1, keepdims=True) + EPS)

        def _gated_delta_rule(xc, wq, wk, wv, wb, wa):
            b, t = (xc.shape[0], xc.shape[1])
            q = _l2norm((xc @ wq).reshape(b, t, H, HD))
            k = _l2norm((xc @ wk).reshape(b, t, H, HD))
            v = (xc @ wv).reshape(b, t, H, HD)
            beta = jax.nn.sigmoid(xc @ wb)
            alpha = jax.nn.sigmoid(xc @ wa + GATE_BIAS)
            qt = jnp.moveaxis(q, 1, 0)
            kt = jnp.moveaxis(k, 1, 0)
            vt = jnp.moveaxis(v, 1, 0)
            bt = jnp.moveaxis(beta, 1, 0)
            at = jnp.moveaxis(alpha, 1, 0)
            S0 = jnp.zeros((b, H, HD, HD), xc.dtype)

            def step(S, inp):
                q_, k_, v_, b_, a_ = inp
                S = a_[..., None, None] * S
                pred = jnp.einsum('bhkv,bhk->bhv', S, k_)
                S = S + k_[..., :, None] * (b_[..., None] * (v_ - pred))[..., None, :]
                o = jnp.einsum('bhkv,bhk->bhv', S, q_)
                return (S, o)
            _, o = jax.lax.scan(step, S0, (qt, kt, vt, bt, at))
            return jnp.moveaxis(o, 1, 0).reshape(b, t, D)
        residual = x
        xn = _rmsnorm(x, norm1_w)
        xc = _causal_depthwise_conv(xn, conv_w, conv_b)
        mixer_out = _gated_delta_rule(xc, wq, wk, wv, wb, wa) @ wo
        h = residual + mixer_out
        hn = _rmsnorm(h, norm2_w)
        ffn = jax.nn.silu(hn @ wg) * (hn @ wu) @ wd
        return h + ffn

    def _L0_ffn_ref(x, router_w, wg_r, wu_r, wd_r, wg_s, wu_s, wd_s):
        import jax, jax.numpy as jnp
        import numpy as np
        HIDDEN = 256
        N_ROUTED = 16
        N_SHARED = 2
        TOP_K = 2
        MID_R = HIDDEN // 4
        MID_S = HIDDEN // 2
        orig_shape = x.shape
        flat = x.reshape(-1, orig_shape[-1])
        gs = jnp.einsum('td,ndm->tnm', flat, wg_s)
        us = jnp.einsum('td,ndm->tnm', flat, wu_s)
        out = jnp.einsum('tnm,nmd->td', jax.nn.silu(gs) * us, wd_s)
        logits = (flat @ router_w).astype(jnp.float32)
        probs = jax.nn.softmax(logits, axis=-1)
        weights, indices = jax.lax.top_k(probs, TOP_K)
        weights = weights / (weights.sum(axis=-1, keepdims=True) + 1e-09)
        weights = weights.astype(x.dtype)
        comb = jnp.sum(jax.nn.one_hot(indices, N_ROUTED, dtype=x.dtype) * weights[..., None], axis=1)
        g = jnp.einsum('td,edm->tem', flat, wg_r)
        u = jnp.einsum('td,edm->tem', flat, wu_r)
        h = jax.nn.silu(g) * u
        h = h * comb[:, :, None]
        out = out + jnp.einsum('tem,emd->td', h, wd_r)
        return out.reshape(orig_shape)

    def _L1_attn_ref(x, fw_in_w, fw_conv_w, fw_conv_b, fw_xproj_w, fw_dt_w, fw_dt_b, fw_Alog, fw_Dp, fw_out_w, bw_in_w, bw_conv_w, bw_conv_b, bw_xproj_w, bw_dt_w, bw_dt_b, bw_Alog, bw_Dp, bw_out_w, proj_w, proj_b, ln_w, ln_b):
        import jax, jax.numpy as jnp
        from jax import lax
        import numpy as np
        D_MODEL = 256
        D_STATE = 16
        D_CONV = 4
        EXPAND = 2
        D_INNER = EXPAND * D_MODEL
        DT_RANK = D_MODEL // 16
        B, L = (1, 256)

        def _mamba(x, in_w, conv_w, conv_b, xproj_w, dt_w, dt_b, Alog, Dp, out_w):
            xz = x @ in_w.T
            xi, z = jnp.split(xz, 2, axis=-1)
            xc = lax.conv_general_dilated(jnp.swapaxes(xi, 1, 2), conv_w, (1,), [(D_CONV - 1, 0)], feature_group_count=D_INNER)
            u = jnp.swapaxes(jax.nn.silu(xc + conv_b[None, :, None]), 1, 2)
            x_dbl = u @ xproj_w.T
            dt = x_dbl[..., :DT_RANK]
            Bm = x_dbl[..., DT_RANK:DT_RANK + D_STATE]
            Cm = x_dbl[..., DT_RANK + D_STATE:]
            delta = jax.nn.softplus(dt @ dt_w.T + dt_b)
            A = -jnp.exp(Alog)
            dA = jnp.exp(jnp.einsum('bld,dn->bldn', delta, A))
            dBu = jnp.einsum('bld,bln,bld->bldn', delta, Bm, u)

            def step(h, inputs):
                a, b, c = inputs
                h = a * h + b
                return (h, jnp.einsum('bdn,bn->bd', h, c))
            h0 = jnp.zeros((x.shape[0], D_INNER, D_STATE), x.dtype)
            _, ys = lax.scan(step, h0, (jnp.moveaxis(dA, 1, 0), jnp.moveaxis(dBu, 1, 0), jnp.moveaxis(Cm, 1, 0)))
            y = jnp.moveaxis(ys, 0, 1) + u * Dp
            return y * jax.nn.silu(z) @ out_w.T

        def _block(x, fw_in_w, fw_conv_w, fw_conv_b, fw_xproj_w, fw_dt_w, fw_dt_b, fw_Alog, fw_Dp, fw_out_w, bw_in_w, bw_conv_w, bw_conv_b, bw_xproj_w, bw_dt_w, bw_dt_b, bw_Alog, bw_Dp, bw_out_w, proj_w, proj_b, ln_w, ln_b):
            out_fw = _mamba(x, fw_in_w, fw_conv_w, fw_conv_b, fw_xproj_w, fw_dt_w, fw_dt_b, fw_Alog, fw_Dp, fw_out_w) + x
            xb = jnp.flip(x, axis=1)
            out_bw = jnp.flip(_mamba(xb, bw_in_w, bw_conv_w, bw_conv_b, bw_xproj_w, bw_dt_w, bw_dt_b, bw_Alog, bw_Dp, bw_out_w) + xb, axis=1)
            out = jnp.concatenate([out_fw, out_bw], axis=-1) @ proj_w.T + proj_b
            mu = out.mean(-1, keepdims=True)
            var = out.var(-1, keepdims=True)
            return (out - mu) / jnp.sqrt(var + 1e-05) * ln_w + ln_b
        return _block(x, fw_in_w, fw_conv_w, fw_conv_b, fw_xproj_w, fw_dt_w, fw_dt_b, fw_Alog, fw_Dp, fw_out_w, bw_in_w, bw_conv_w, bw_conv_b, bw_xproj_w, bw_dt_w, bw_dt_b, bw_Alog, bw_Dp, bw_out_w, proj_w, proj_b, ln_w, ln_b)

    def _L1_ffn_ref(x, router_w, w1, w2):
        import jax, jax.numpy as jnp
        import numpy as np
        B, S, H, E, K = (4, 512, 256, 8, 2)
        bsz, seq, hidden = x.shape
        n_experts = w1.shape[0]
        tokens = x.reshape(-1, hidden)
        T = tokens.shape[0]
        logits = tokens @ router_w.T
        topv, topi = jax.lax.top_k(logits, K)
        w = jax.nn.softmax(topv, axis=-1).astype(tokens.dtype)
        gate = jnp.zeros((T, n_experts), tokens.dtype).at[jnp.arange(T)[:, None], topi].add(w)
        out = jnp.zeros_like(tokens)
        for e in range(n_experts):
            h = jax.nn.gelu(tokens @ w1[e].T, approximate=False)
            y = h @ w2[e].T
            out = out + gate[:, e:e + 1] * y
        return out.reshape(bsz, seq, hidden)

    def _L2_attn_ref(x, W_hash, W_q, b_q, W_v, b_v, W_o, b_o):
        import jax, jax.numpy as jnp
        import numpy as np
        N_HEADS = 8
        BUCKET = 64
        EPS = 0.0001
        B, S, D = x.shape
        H, dh = (N_HEADS, D // N_HEADS)
        nb = S // BUCKET
        h = (x @ W_hash).reshape(B, S, H, 2)
        angles = h[..., 0] / (h[..., 1] + EPS)
        idx = jnp.argsort(angles.transpose(0, 2, 1), axis=2)
        q = x @ W_q + b_q
        k = q
        v = x @ W_v + b_v

        def to_heads(t):
            return t.reshape(B, S, H, dh).transpose(0, 2, 1, 3)
        qh, kh, vh = (to_heads(q), to_heads(k), to_heads(v))
        gather = lambda t: jnp.take_along_axis(t, idx[..., None], axis=2)
        qs = gather(qh).reshape(B, H, nb, BUCKET, dh)
        ks = gather(kh).reshape(B, H, nb, BUCKET, dh)
        vs = gather(vh).reshape(B, H, nb, BUCKET, dh)
        scale = 1.0 / np.sqrt(dh).astype(np.float32)
        scores = jnp.einsum('bhnid,bhnjd->bhnij', qs, ks) * scale
        attn = jax.nn.softmax(scores, axis=-1)
        o = jnp.einsum('bhnij,bhnjd->bhnid', attn, vs).reshape(B, H, S, dh)
        inv = jnp.argsort(idx, axis=2)
        o = jnp.take_along_axis(o, inv[..., None], axis=2)
        o = o.transpose(0, 2, 1, 3).reshape(B, S, D)
        return o @ W_o + b_o

    def _L2_ffn_ref(x, CB, SCB, bias):
        import jax, jax.numpy as jnp
        import numpy as np
        B, S, K, N = (8, 2048, 256, 256)
        out = jnp.einsum('bsk,nk->bsn', x, CB)
        out = out * (SCB * (1.0 / 127.0)) + bias
        return out

    def _L3_attn_ref(x, w_attn, w_proj, decay_raw):
        import jax, jax.numpy as jnp
        import numpy as np
        N_HEAD = 16
        NEG_INF = jnp.finfo(jnp.float32).min
        B, T, C = x.shape
        H = N_HEAD
        D = C // H
        qkv = x @ w_attn
        q, k, v = jnp.split(qkv, 3, axis=-1)
        q = q.reshape(B, T, H, D).transpose(0, 2, 1, 3)
        k = k.reshape(B, T, H, D).transpose(0, 2, 1, 3)
        v = v.reshape(B, T, H, D).transpose(0, 2, 1, 3)
        idx = jnp.arange(T)
        causal = jnp.where(idx[None, :] > idx[:, None], NEG_INF, 0.0).astype(jnp.float32)
        decay = jax.nn.softplus(decay_raw)
        dist = jnp.maximum(idx[:, None] - idx[None, :], 0).astype(jnp.float32)
        log1p_dist = jnp.log1p(dist)
        logw = -jnp.log1p(decay[:, None, None] * log1p_dist)
        attn_mask = causal[None, :, :] + logw
        scores = jnp.einsum('bhqd,bhkd->bhqk', q, k) * (1.0 / jnp.sqrt(jnp.float32(D)))
        scores = scores + attn_mask[None]
        att = jax.nn.softmax(scores, axis=-1)
        y = jnp.einsum('bhqk,bhkd->bhqd', att, v)
        y = y.transpose(0, 2, 1, 3).reshape(B, T, C)
        return y @ w_proj

    def _L3_ffn_ref(x, w_freq_real, w_freq_imag, bias):
        import jax, jax.numpy as jnp
        import numpy as np
        B, N, D = (4, 512, 256)
        SPARSITY = 0.01
        w = jax.lax.complex(w_freq_real, w_freq_imag)
        x_freq = jnp.fft.fft(x, axis=-1)
        y_freq = jnp.einsum('bnd,do->bno', x_freq, w)
        y = jnp.real(jnp.fft.ifft(y_freq, axis=-1))
        return y + bias
    x = L0_attn_x
    x = x + _layernorm(_L0_attn_ref(_layernorm(x, axis=-1), L0_attn_norm1_w, L0_attn_norm2_w, L0_attn_conv_w, L0_attn_conv_b, L0_attn_wq, L0_attn_wk, L0_attn_wv, L0_attn_wb, L0_attn_wa, L0_attn_wo, L0_attn_wg, L0_attn_wu, L0_attn_wd), axis=-1)
    x = x + _layernorm(_L0_ffn_ref(_layernorm(x, axis=-1), L0_ffn_router_w, L0_ffn_wg_r, L0_ffn_wu_r, L0_ffn_wd_r, L0_ffn_wg_s, L0_ffn_wu_s, L0_ffn_wd_s), axis=-1)
    x = x + _layernorm(_L1_attn_ref(_layernorm(x, axis=-1), L1_attn_fw_in_w, L1_attn_fw_conv_w, L1_attn_fw_conv_b, L1_attn_fw_xproj_w, L1_attn_fw_dt_w, L1_attn_fw_dt_b, L1_attn_fw_Alog, L1_attn_fw_Dp, L1_attn_fw_out_w, L1_attn_bw_in_w, L1_attn_bw_conv_w, L1_attn_bw_conv_b, L1_attn_bw_xproj_w, L1_attn_bw_dt_w, L1_attn_bw_dt_b, L1_attn_bw_Alog, L1_attn_bw_Dp, L1_attn_bw_out_w, L1_attn_proj_w, L1_attn_proj_b, L1_attn_ln_w, L1_attn_ln_b), axis=-1)
    x = x + _layernorm(_L1_ffn_ref(_layernorm(x, axis=-1), L1_ffn_router_w, L1_ffn_w1, L1_ffn_w2), axis=-1)
    x = x + _layernorm(_L2_attn_ref(_layernorm(x, axis=-1), L2_attn_W_hash, L2_attn_W_q, L2_attn_b_q, L2_attn_W_v, L2_attn_b_v, L2_attn_W_o, L2_attn_b_o), axis=-1)
    x = x + _layernorm(_L2_ffn_ref(_layernorm(x, axis=-1), L2_ffn_CB, L2_ffn_SCB, L2_ffn_bias), axis=-1)
    x = x + _layernorm(_L3_attn_ref(_layernorm(x, axis=-1), L3_attn_w_attn, L3_attn_w_proj, L3_attn_decay_raw), axis=-1)
    x = x + _layernorm(_L3_ffn_ref(_layernorm(x, axis=-1), L3_ffn_w_freq_real, L3_ffn_w_freq_imag, L3_ffn_bias), axis=-1)
    return x

_drawn_inputs = setup_inputs


def setup_inputs(seed=0):
    import zlib

    import numpy as np

    out = dict(_drawn_inputs(seed))
    spreads = {'L0_attn_norm1_w': (1.0, 0.2),
     'L0_attn_norm2_w': (1.0, 0.2),
     'L0_attn_conv_b': (0.0, 0.1),
     'L1_attn_fw_Dp': (1.0, 0.6),
     'L1_attn_bw_Dp': (1.0, 0.6),
     'L1_attn_proj_b': (0.0, 0.8),
     'L1_attn_ln_w': (1.0, 0.2),
     'L1_attn_ln_b': (0.0, 0.1)}
    factors = {'L0_attn_wa': 3.369,
     'L1_attn_fw_in_w': 4.044,
     'L1_attn_fw_conv_w': 7.498,
     'L1_attn_fw_conv_b': 5.183,
     'L1_attn_fw_xproj_w': 8.0,
     'L1_attn_fw_dt_w': 8.0,
     'L1_attn_fw_dt_b': 8.0,
     'L1_attn_fw_Alog': 8.0,
     'L1_attn_fw_out_w': 4.346,
     'L1_attn_bw_in_w': 5.061,
     'L1_attn_bw_conv_w': 5.946,
     'L1_attn_bw_conv_b': 5.13,
     'L1_attn_bw_xproj_w': 8.0,
     'L1_attn_bw_dt_w': 8.0,
     'L1_attn_bw_dt_b': 8.0,
     'L1_attn_bw_Alog': 8.0,
     'L1_attn_bw_out_w': 4.836,
     'L2_attn_b_q': 64.0,
     'L2_attn_b_v': 6.071,
     'L2_attn_b_o': 5.804,
     'L2_ffn_bias': 31.318,
     'L3_ffn_bias': 8.0}
    for name, (base, spread) in spreads.items():
        noise = np.random.default_rng([zlib.crc32(name.encode()), seed]).standard_normal(out[name].shape)
        drawn = base * np.exp(spread * noise) if base else spread * noise
        out[name] = jnp.asarray(drawn.astype(out[name].dtype))
    for name, factor in factors.items():
        out[name] = (out[name] * factor).astype(out[name].dtype)
    return out
```

```python
from contextlib import ExitStack

import numpy as np

import concourse.bass as bass
from concourse import mybir

F32 = mybir.dt.float32
BF16 = mybir.dt.bfloat16
I32 = mybir.dt.int32
U32 = mybir.dt.uint32
ALU = mybir.AluOpType
ACT = mybir.ActivationFunctionType
AX = mybir.AxisListType

P = 128
BATCH, SEQ, DIM = 8, 512, 256
TPB = SEQ // P
NT = BATCH * TPB
KC = DIM // P
LN_EPS = 1e-5
RSQRT_MAGIC = 0x5F3759DF


class Chain:

    def __init__(self, eng, sem):
        self.eng, self.sem, self.n = eng, sem, 0

    def mark(self, ins):
        self.n += 1
        return ins.then_inc(self.sem, 1)

    def wait(self):
        self.eng.wait_ge(self.sem, self.n)

    def link(self, ins):
        self.mark(ins)
        self.wait()

    def restart(self):
        self.wait()
        self.eng.sem_clear(self.sem)
        self.n = 0


class Signals:

    def __init__(self, nc, ctx, layer):
        self.nc, self.ctx, self.layer, self.taken = nc, ctx, layer, []

    def __call__(self, name):
        self.taken.append(self.ctx.enter_context(self.nc.semaphore(f"{self.layer}_{name}")))
        return self.taken[-1]

    def block(self):
        self.ctx.callback(self.clear)
        return self.ctx.enter_context(self.nc.Block())

    def clear(self):
        with self.nc.Block() as block:
            @block.sync
            def _(sp):
                for sem in self.taken:
                    sp.sem_clear(sem)


class Core:

    def __init__(self, nc, ctx):
        self.nc = nc
        sb = lambda name, shape, dt=F32: ctx.enter_context(nc.sbuf_tensor(name, shape, dt))
        self.X = sb("X", [P, NT, DIM])
        self.ident = sb("ident", [P, P])
        self.ident_bf = sb("ident_bf", [P, P], BF16)
        self.stats = sb("stats", [P, TPB, 6])
        self.mv = sb("mv", [P, TPB, 2])
        self.rs = sb("rs", [P, 4, TPB])
        self.tmp = sb("tmp", [P, TPB, DIM])


def rsqrt(dve, chain, y, v, half, t):
    chain.mark(dve.tensor_scalar(half, v, 0.5, None, ALU.mult))
    chain.link(dve.tensor_scalar(y.bitcast(I32), v.bitcast(I32), -0.5, float(RSQRT_MAGIC), ALU.mult, ALU.add))
    for _ in range(3):
        chain.link(dve.tensor_tensor(t, y, y, ALU.mult))
        chain.link(dve.tensor_tensor(t, t, half, ALU.mult))
        chain.link(dve.scalar_tensor_tensor(out=y, in0=t, scalar=1.5, in1=y, op0=ALU.subtract, op1=ALU.mult))
    chain.link(dve.tensor_scalar(y, y, -1.0, None, ALU.mult))


def norm_stats(dve, chain, core, tiles, eps=LN_EPS):
    for j, tile in enumerate(tiles):
        chain.mark(dve.bn_stats(core.stats[:, j, :], tile))
    chain.wait()
    for j in range(TPB):
        chain.mark(dve.bn_aggr(core.mv[:, j, :], core.stats[:, j, :]))
    chain.wait()
    chain.link(dve.tensor_scalar(core.rs[:, 1, :], core.mv[:, :, 1], eps, None, ALU.add))
    rsqrt(dve, chain, core.rs[:, 0, :], core.rs[:, 1, :], core.rs[:, 2, :], core.rs[:, 3, :])




def front(dve, chain, core, b, xn, xn_ready):
    norm_stats(dve, chain, core, [core.X[:, TPB * b + j, :] for j in range(TPB)])
    for j in range(TPB):
        last = dve.tensor_scalar(xn[:, j, :], core.X[:, TPB * b + j, :], core.mv[:, j, 0:1], core.rs[:, 0, j:j + 1],
                                 ALU.subtract, ALU.mult)
    last.then_inc(xn_ready, 1)


def back(dve, chain, core, b, y, y_read=None):
    norm_stats(dve, chain, core, [y[:, j, :] for j in range(TPB)])
    for j in range(TPB):
        last = dve.tensor_scalar(core.tmp[:, j, :], y[:, j, :], core.mv[:, j, 0:1], core.rs[:, 0, j:j + 1],
                                 ALU.subtract, ALU.mult)
        if y_read is None or j < TPB - 1:
            chain.mark(last)
    chain.wait()
    if y_read is not None:
        last.then_inc(y_read, 1)
        dve.wait_ge(y_read, b + 1)
    xb = core.X[:, bass.ds(TPB * b, TPB), :]
    chain.mark(dve.tensor_tensor(xb, xb, core.tmp[:, :, :], ALU.add))


def transposes(pe, core, xn, pt, sent):
    for j in range(TPB):
        for k in range(KC):
            last = pe.transpose(pt[:, k, j * P:(j + 1) * P], xn[:, j, k * P:(k + 1) * P], core.ident[:, :])
    last.then_inc(sent, 1)


def row_of(ap):
    return ap.rearrange("(a n) -> a n", a=1)


def prologue(core, ctx, x_dram):
    nc = core.nc
    x_loaded = ctx.enter_context(nc.semaphore("x_loaded"))
    blank = ctx.enter_context(nc.semaphore("ident_steps"))
    with nc.Block() as block:
        @block.sync
        def _(sp):
            sp.dma_start(core.X[:, :, :], x_dram.rearrange("b (j p) d -> p (b j) d", p=P)).then_inc(x_loaded, 16)
            sp.wait_ge(x_loaded, 16)

        @block.gpsimd
        def _(pool):
            pool.memset(core.ident[:, :], 0.0).then_inc(blank, 1)
            pool.wait_ge(blank, 1)
            pool.affine_select(out=core.ident[:, :], in_=core.ident[:, :], compare_op=ALU.not_equal, fill=1.0,
                               base=0, pattern=[[-1, P]], channel_multiplier=1).then_inc(blank, 1)
            pool.wait_ge(blank, 2)
            pool.tensor_copy(core.ident_bf[:, :], core.ident[:, :]).then_inc(blank, 1)
            pool.wait_ge(blank, 3)


def epilogue(core, out_dram):
    nc = core.nc
    with nc.semaphore("x_stored") as x_stored, nc.Block() as block:
        @block.sync
        def _(sp):
            sp.dma_start(out_dram.rearrange("b (j p) d -> p (b j) d", p=P), core.X[:, :, :]).then_inc(x_stored, 16)
            sp.wait_ge(x_stored, 16)


def delta_project(core, ctx0, qkv, gates, x_scale, conv_w_dram, conv_b_dram, norm_w_dram, w_dram):
    nc = core.nc
    name = "proj"
    K = conv_w_dram.shape[1]
    HEADS, HD = 16, 16
    QK = 2 * DIM
    with ExitStack() as ctx:
        sb = lambda n, shape, dt=F32: ctx.enter_context(nc.sbuf_tensor(f"{name}_{n}", shape, dt))
        ps = lambda n, shape: ctx.enter_context(nc.psum_tensor(f"{name}_{n}", shape, F32))
        sem = Signals(nc, ctx, name)
        xn = sb("xn", [P, TPB, DIM])
        xs = sb("xs", [P, KC, K - 1 + SEQ])
        conv = sb("conv", [P, KC, SEQ])
        xc = sb("xc", [P, KC, SEQ])
        cw, cb, nw = sb("cw", [P, KC, K]), sb("cb", [P, KC]), sb("nw", [P, KC])
        w = sb("w", [P, KC, 3 * DIM + 2 * HEADS])
        sq = sb("sq", [P, TPB, 2 * HD, HEADS])
        norm = sb("norm", [P, 5, TPB * QK // HD])
        gate_bias = sb("gate_bias", [P, 2])
        pt = ps("pt", [P, KC, SEQ])
        pq = ps("pq", [P, 2, 2, SEQ])
        loaded, consts = sem("loaded"), sem("consts")
        xn_ready, turned, xs_ready, conv_ready, xc_ready = (sem(n) for n in ("xn_ready", "turned", "xs_ready", "conv_ready", "xc_ready"))
        tile_ready, tile_read, qk_ready, sq_ready, qk_done = (sem(n) for n in ("tile_ready", "tile_read", "qk_ready", "sq_ready", "qk_done"))
        chain_dve = sem("chain_dve")
        block = sem.block()

        @block.sync
        def _(sp):
            sp.dma_start(cw[:, :, :], conv_w_dram.rearrange("(k p) n -> p k n", p=P)).then_inc(loaded, 16)
            with nc.allow_non_contiguous_dma(reason="two short vectors"):
                sp.dma_start(cb[:, :], conv_b_dram.rearrange("(k p) -> p k", p=P)).then_inc(loaded, 16)
                sp.dma_start(nw[:, :], norm_w_dram.rearrange("(k p) -> p k", p=P)).then_inc(loaded, 16)
            sp.dma_start(w[:, :, :], w_dram.rearrange("(k p) n -> p k n", p=P)).then_inc(loaded, 16)

        @block.tensor
        def _(pe):
            pe.wait_ge(loaded, 16 * 4)

            def row(b):
                pe.wait_ge(xn_ready, b + 1)
                transposes(pe, core, xn, pt, turned)
                pe.wait_ge(xc_ready, b + 1)
                for j in range(TPB):
                    wait_from(pe, tile_read, 3 * (TPB * b + j - 1))
                    for half, (lo, hi) in enumerate(((0, QK), (QK, 3 * DIM + 2 * HEADS))):
                        for k in range(KC):
                            last = pe.matmul(pq[:, j % 2, half, 0:hi - lo], xc[:, k, j * P:(j + 1) * P], w[:, k, lo:hi],
                                             start=k == 0, stop=k == KC - 1)
                    last.then_inc(tile_ready, 1)

            row(0)
            with pe.Fori(1, BATCH) as b:
                row(b)

        @block.scalar
        def _(act):
            act.wait_ge(loaded, 16 * 4)
            act.wait_ge(consts, 2)

            def row(b):
                act.wait_ge(turned, b + 1)
                wait_from(act, conv_ready, KC * b)
                for k in range(KC):
                    last = act.activation(xs[:, k, K - 1:], pt[:, k, :], ACT.Copy, scale=nw[:, k:k + 1])
                last.then_inc(xs_ready, 1)
                wait_from(act, tile_ready, TPB * b)
                for k in range(KC):
                    act.wait_ge(conv_ready, KC * b + k + 1)
                    last = act.activation(xc[:, k, :], conv[:, k, :], ACT.Silu)
                last.then_inc(xc_ready, 1)
                for j in range(TPB):
                    act.wait_ge(tile_ready, TPB * b + j + 1)
                    heads = bass.ds(HEADS * b, HEADS)
                    for c in range(3):
                        src = pq[:, j % 2, c // 2, c % 2 * DIM:c % 2 * DIM + DIM].rearrange("p (h e) -> p e h", e=HD)
                        act.activation(qkv[:, j, c * HD:(c + 1) * HD, heads], src, ACT.Copy).then_inc(qk_ready if c == 1 else tile_read, 1)
                    for c in range(2):
                        at = DIM + c * HEADS
                        last = act.activation(gates[:, j, c, heads], pq[:, j % 2, 1, at:at + HEADS], ACT.Sigmoid,
                                              bias=gate_bias[:, c:c + 1])
                    last.then_inc(tile_read, 1)

            row(0)
            with act.Fori(1, BATCH) as b:
                row(b)

        @block.gpsimd
        def _(pool):
            pool.memset(xs[:, :, 0:K - 1], 0.0).then_inc(consts, 1)
            pool.memset(gate_bias[:, 0:1], 0.0)
            pool.memset(gate_bias[:, 1:2], 4.0).then_inc(consts, 1)

            def row(b):
                pool.wait_ge(qk_ready, TPB * (b + 1))
                wait_from(pool, qk_done, b)
                own = qkv[:, :, 0:2 * HD, bass.ds(HEADS * b, HEADS)]
                pool.tensor_tensor(sq[:, :, :, :], own, own, ALU.mult).then_inc(sq_ready, 1)
            row(0)
            with pool.Fori(1, BATCH) as b:
                row(b)

        @block.vector
        def _(dve):
            chain = Chain(dve, chain_dve)
            dve.wait_ge(loaded, 16 * 4)

            def front_rms(b):
                tiles = [core.X[:, TPB * b + j, :] for j in range(TPB)]
                norm_stats(dve, chain, core, tiles)
                rs, var = core.rs, core.mv[:, :, 1]
                chain.link(dve.tensor_copy(x_scale[:, 0, :], rs[:, 0, :]))
                chain.link(dve.tensor_tensor(x_scale[:, 1, :], rs[:, 0, :], rs[:, 0, :], ALU.mult))
                chain.link(dve.tensor_tensor(x_scale[:, 1, :], x_scale[:, 1, :], var, ALU.mult))
                chain.link(dve.tensor_scalar(x_scale[:, 1, :], x_scale[:, 1, :], 1e-6, None, ALU.add))
                rsqrt(dve, chain, rs[:, 0, :], x_scale[:, 1, :], rs[:, 2, :], rs[:, 3, :])
                chain.link(dve.tensor_tensor(x_scale[:, 0, :], x_scale[:, 0, :], rs[:, 0, :], ALU.mult))
                for j in range(TPB):
                    last = dve.tensor_scalar(xn[:, j, :], tiles[j], core.mv[:, j, 0:1], x_scale[:, 0, j:j + 1],
                                             ALU.subtract, ALU.mult)
                last.then_inc(xn_ready, 1)

            def convolve(b):
                dve.wait_ge(xs_ready, b + 1)
                for k in range(KC):
                    chain.mark(dve.tensor_scalar(conv[:, k, :], xs[:, k, K - 1:], cw[:, k, K - 1:K], cb[:, k:k + 1], ALU.mult, ALU.add))
                chain.wait()
                for tap in range(K - 1):
                    for k in range(KC):
                        ins = dve.scalar_tensor_tensor(out=conv[:, k, :], in0=xs[:, k, tap:tap + SEQ], scalar=cw[:, k, tap:tap + 1],
                                                       in1=conv[:, k, :], op0=ALU.mult, op1=ALU.add)
                        if tap == K - 2:
                            ins.then_inc(conv_ready, 1)
                        else:
                            chain.mark(ins)
                    if tap < K - 2:
                        chain.wait()

            def lengths(b):
                dve.wait_ge(sq_ready, b + 1)
                chain.link(dve.tensor_reduce(norm[:, 1, :].rearrange("p (g h) -> p g h", h=HEADS), sq[:, :, :, :].rearrange("p j (c e) h -> p (j c) h e", e=HD), AX.X, ALU.add))
                chain.link(dve.tensor_scalar(norm[:, 2, :], norm[:, 1, :], 1e-6, None, ALU.add))
                rsqrt(dve, chain, norm[:, 0, :], norm[:, 2, :], norm[:, 3, :], norm[:, 4, :])
                for c in range(2):
                    part = qkv[:, :, c * HD:(c + 1) * HD, bass.ds(HEADS * b, HEADS)]
                    scale = norm[:, 0, :].rearrange("p (j c h) -> p j c h", j=TPB, c=2)[:, :, c, :]
                    last = dve.tensor_tensor(part, part, scale.unsqueeze(2).broadcast_to([P, TPB, HD, HEADS]), ALU.mult)
                last.then_inc(qk_done, 1)

            front_rms(0)
            chain.restart()

            def row(b, last):
                wait_from(dve, xc_ready, b)
                convolve(b)
                if not last:
                    dve.wait_ge(turned, b + 1)
                    front_rms(b + 1)
                lengths(b)
                chain.restart()

            row(0, False)
            with dve.Fori(1, BATCH - 1) as b:
                row(b, False)
            row(BATCH - 1, True)


def delta_recurrence(core, qkv, gates):
    nc = core.nc
    name = "scan"
    HEADS, HD = 16, 16
    SPANS = SEQ // P
    GROUPS = 3 * HD // 4
    with ExitStack() as ctx:
        sb = lambda n, shape, dt=F32: ctx.enter_context(nc.sbuf_tensor(f"{name}_{n}", shape, dt))
        ps = lambda n, shape: ctx.enter_context(nc.psum_tensor(f"{name}_{n}", shape, F32))
        sem = Signals(nc, ctx, name)
        kqv = sb("kqv", [P, P, 3, HD])
        ba = sb("ba", [P, 4, P])
        seen = sb("seen", [P, P, 2, HD])
        d = sb("d", [P, P, HD])
        S = sb("S", [P, HD, HD])
        prod = sb("prod", [P, 2, HD, HD])
        outer = sb("outer", [P, HD, HD])
        big = sb("big", [P, P, HD])
        pk = ps("pk", [P, 4, 4, P])
        po = ps("po", [P, 4, 4, P])
        sent, taken, o_ready, o_sent, o_taken = (sem(n) for n in ("sent", "taken", "o_ready", "o_sent", "o_taken"))
        chain_dve = sem("chain_dve")
        block = sem.block()

        PER = GROUPS + 1

        @block.tensor
        def _(pe):
            for s in range(SPANS):
                for g in range(PER):
                    n = PER * s + g
                    wait_from(pe, taken, n - 3)
                    for i in range(4):
                        if g < GROUPS:
                            src = qkv[:, s, g * 4 + i, :]
                        elif i < 2:
                            src = gates[:, s, i, :]
                        else:
                            continue
                        last = pe.transpose(pk[:, n % 4, i, :], src, core.ident[:, :])
                    last.then_inc(sent, 1)
                for g in range(HD // 4):
                    pe.wait_ge(o_ready, s + 1)
                    wait_from(pe, o_taken, 4 * (s - 1) + g + 1)
                    for i in range(4):
                        last = pe.transpose(po[:, g, i, :], seen[:, :, 1, 4 * g + i], core.ident[:, :])
                    last.then_inc(o_sent, 1)

        @block.scalar
        def _(act):
            for s in range(SPANS):
                wait_from(act, o_ready, s)
                for g in range(PER):
                    n = PER * s + g
                    act.wait_ge(sent, n + 1)
                    if g < GROUPS:
                        part, at = g // 4, g % 4 * 4
                        part = (1, 0, 2)[part]
                        act.activation(kqv[:, :, part, at:at + 4].rearrange("p t i -> p i t"), pk[:, n % 4, :, :],
                                       ACT.Copy).then_inc(taken, 1)
                    else:
                        act.activation(ba[:, 0:2, :], pk[:, n % 4, 0:2, :], ACT.Copy).then_inc(taken, 1)
                for g in range(4):
                    act.wait_ge(o_sent, 4 * s + g + 1)
                    last = act.activation(qkv[:, s, 4 * g:4 * g + 4, :], po[:, g, :, :], ACT.Copy)
                    last.then_inc(o_taken, 1)

        @block.vector
        def _(dve):
            chain = Chain(dve, chain_dve)
            chain.mark(dve.memset(S[:, :, :], 0.0))
            chain.restart()
            with dve.Fori(0, SPANS) as s:
                dve.wait_ge(taken, PER * (s + 1))
                beta, alpha = ba[:, 0, :], ba[:, 1, :]
                chain.mark(dve.scalar_tensor_tensor(out=ba[:, 2, :], in0=beta, scalar=-1.0, in1=alpha, op0=ALU.mult, op1=ALU.mult))
                chain.mark(dve.tensor_tensor(big[:, :, :], kqv[:, :, 0, :], kqv[:, :, 1, :], ALU.mult))
                chain.mark(dve.tensor_tensor(kqv[:, :, 2, :], kqv[:, :, 2, :], beta.unsqueeze(2).broadcast_to([P, P, HD]), ALU.mult))
                chain.wait()
                chain.mark(dve.tensor_reduce(ba[:, 3, :], big[:, :, :], AX.X, ALU.add))
                chain.restart()
                for t in range(P):
                    kq4 = kqv[:, t, 0:2, :].unsqueeze(2).broadcast_to([P, 2, HD, HD])
                    chain.link(dve.tensor_tensor(prod[:, :, :, :], S[:, :, :].unsqueeze(1).broadcast_to([P, 2, HD, HD]), kq4, ALU.mult))
                    chain.link(dve.tensor_reduce(seen[:, t, :, :], prod[:, :, :, :], AX.X, ALU.add))
                    chain.link(dve.scalar_tensor_tensor(out=d[:, t, :], in0=seen[:, t, 0, :], scalar=ba[:, 2, t:t + 1],
                                                    in1=kqv[:, t, 2, :], op0=ALU.mult, op1=ALU.add))
                    chain.link(dve.tensor_tensor(outer[:, :, :], d[:, t, :].unsqueeze(2).broadcast_to([P, HD, HD]),
                                             kqv[:, t, 0, :].unsqueeze(1).broadcast_to([P, HD, HD]), ALU.mult))
                    chain.link(dve.scalar_tensor_tensor(out=S[:, :, :], in0=S[:, :, :], scalar=ba[:, 1, t:t + 1], in1=outer[:, :, :],
                                                    op0=ALU.mult, op1=ALU.add))
                chain.mark(dve.tensor_tensor(seen[:, :, 1, :], seen[:, :, 1, :], ba[:, 1, :].unsqueeze(2).broadcast_to([P, P, HD]), ALU.mult))
                chain.link(dve.tensor_tensor(big[:, :, :], d[:, :, :], ba[:, 3, :].unsqueeze(2).broadcast_to([P, P, HD]), ALU.mult))
                dve.tensor_tensor(seen[:, :, 1, :], seen[:, :, 1, :], big[:, :, :], ALU.add).then_inc(o_ready, 1)
                chain.restart()


def delta_finish(core, o, wo_dram, norm_w_dram, wg_dram, wu_dram, wd_dram):
    nc = core.nc
    name = "fin"
    HEADS, HD = 16, 16
    I = wg_dram.shape[1]
    NB = -(-I // P)
    sizes = [min(P, I - P * m) for m in range(NB)]
    with ExitStack() as ctx:
        sb = lambda n, shape, dt=F32: ctx.enter_context(nc.sbuf_tensor(f"{name}_{n}", shape, dt))
        ps = lambda n, shape: ctx.enter_context(nc.psum_tensor(f"{name}_{n}", shape, F32))
        sem = Signals(nc, ctx, name)
        xn = sb("xn", [P, TPB, DIM])
        os = sb("os", [P, TPB, DIM])
        oT = sb("oT", [P, KC, SEQ])
        h, hn = sb("h", [P, TPB, DIM]), sb("hn", [P, TPB, DIM])
        hnT = sb("hnT", [P, KC, SEQ])
        y = sb("y", [P, TPB, DIM])
        act_g, mid = sb("act_g", [P, 2, SEQ]), sb("mid", [P, 2, SEQ])
        wo, wg, wu = sb("wo", [P, KC, DIM]), sb("wg", [P, KC, I]), sb("wu", [P, KC, I])
        wd, nw = sb("wd", [P, NB, DIM]), sb("nw", [P, KC])
        sq = sb("sq", [P, TPB])
        pt = ps("pt", [P, KC, SEQ])
        pgu = ps("pgu", [P, 2, 2, SEQ])
        py = ps("py", [P, TPB, DIM])
        loaded = sem("loaded")
        os_ready, o_sent, oT_ready, mix_ready, hn_ready, hn_sent, hnT_ready = (
            sem(n) for n in ("os_ready", "o_sent", "oT_ready", "mix_ready", "hn_ready", "hn_sent", "hnT_ready"))
        gu_ready, silu_ready, mid_ready, y_ready, y_read, chain_dve = (
            sem(n) for n in ("gu_ready", "silu_ready", "mid_ready", "y_ready", "y_read", "chain_dve"))
        block = sem.block()

        @block.sync
        def _(sp):
            sp.dma_start(wo[:, :, :], wo_dram.rearrange("(k p) n -> p k n", p=P)).then_inc(loaded, 16)
            sp.dma_start(wg[:, :, :], wg_dram.rearrange("(k p) n -> p k n", p=P)).then_inc(loaded, 16)
            sp.dma_start(wu[:, :, :], wu_dram.rearrange("(k p) n -> p k n", p=P)).then_inc(loaded, 16)
            for m in range(NB):
                sp.dma_start(wd[0:sizes[m], m, :], wd_dram[P * m:P * m + sizes[m], :]).then_inc(loaded, 16)
            with nc.allow_non_contiguous_dma(reason="a short vector"):
                sp.dma_start(nw[:, :], norm_w_dram.rearrange("(k p) -> p k", p=P)).then_inc(loaded, 16)

        LOADS = 16 * (4 + NB)

        @block.gpsimd
        def _(pool):
            def row(b):
                wait_from(pool, o_sent, b)
                pool.tensor_copy(os[:, :, :].rearrange("p j (h e) -> p j h e", e=HD),
                                 o[:, :, :, bass.ds(HEADS * b, HEADS)].rearrange("p j e h -> p j h e")).then_inc(os_ready, 1)
            row(0)
            with pool.Fori(1, BATCH) as b:
                row(b)

        @block.tensor
        def _(pe):
            pe.wait_ge(loaded, LOADS)

            def row(b):
                def up(m):
                    wait_from(pe, mid_ready, NB * b + m - 1)
                    for i, w in enumerate((wg, wu)):
                        for k in range(KC):
                            last = pe.matmul(pgu[0:sizes[m], m % 2, i, :], w[:, k, m * P:m * P + sizes[m]], hnT[:, k, :],
                                             start=k == 0, stop=k == KC - 1)
                    last.then_inc(gu_ready, 1)

                def down(m):
                    pe.wait_ge(mid_ready, NB * b + m + 1)
                    for j in range(TPB):
                        last = pe.matmul(py[:, j, :], mid[0:sizes[m], m % 2, j * P:(j + 1) * P], wd[0:sizes[m], m, :],
                                         start=m == 0 and j % 2 == 0, stop=m == NB - 1, skip_group_check=True)
                    return last

                pe.wait_ge(os_ready, b + 1)
                wait_from(pe, hnT_ready, b)
                transposes(pe, core, os, pt, o_sent)
                pe.wait_ge(oT_ready, b + 1)
                wait_from(pe, y_read, b)
                for j in range(TPB):
                    for k in range(KC):
                        last = pe.matmul(py[:, j, :], oT[:, k, j * P:(j + 1) * P], wo[:, k, :], start=k == 0, stop=k == KC - 1)
                last.then_inc(mix_ready, 1)
                pe.wait_ge(hn_ready, b + 1)
                transposes(pe, core, hn, pt, hn_sent)
                pe.wait_ge(hnT_ready, b + 1)
                up(0)
                for m in range(1, NB):
                    up(m)
                    down(m - 1)
                down(NB - 1).then_inc(y_ready, 1)

            row(0)
            with pe.Fori(1, BATCH) as b:
                row(b)

        @block.scalar
        def _(act):
            act.wait_ge(loaded, LOADS)

            def row(b):
                act.wait_ge(o_sent, b + 1)
                wait_from(act, mix_ready, b)
                act.activation(oT[:, :, :], pt[:, :, :], ACT.Copy).then_inc(oT_ready, 1)
                act.wait_ge(hn_sent, b + 1)
                for k in range(KC):
                    last = act.activation(hnT[:, k, :], pt[:, k, :], ACT.Copy, scale=nw[:, k:k + 1])
                last.then_inc(hnT_ready, 1)
                for m in range(NB):
                    act.wait_ge(gu_ready, NB * b + m + 1)
                    wait_from(act, mid_ready, NB * b + m - 1)
                    act.activation(act_g[0:sizes[m], m % 2, :], pgu[0:sizes[m], m % 2, 0, :], ACT.Silu).then_inc(silu_ready, 1)

            row(0)
            with act.Fori(1, BATCH) as b:
                row(b)

        @block.vector
        def _(dve):
            chain = Chain(dve, chain_dve)

            def residual(b):
                tiles = [core.X[:, TPB * b + j, :] for j in range(TPB)]
                norm_stats(dve, chain, core, tiles)
                for j in range(TPB):
                    chain.mark(dve.tensor_scalar(xn[:, j, :], tiles[j], core.mv[:, j, 0:1], core.rs[:, 0, j:j + 1],
                                                 ALU.subtract, ALU.mult))
                chain.wait()

            residual(0)
            chain.restart()

            def row(b, last):
                dve.wait_ge(mix_ready, b + 1)
                chain.link(dve.tensor_tensor(h[:, :, :], xn[:, :, :], py[:, :, :], ALU.add))
                for j in range(TPB):
                    chain.mark(dve.bn_stats(core.stats[:, j, :], h[:, j, :]))
                chain.wait()
                for j in range(TPB):
                    chain.mark(dve.bn_aggr(core.mv[:, j, :], core.stats[:, j, :]))
                chain.wait()
                chain.link(dve.tensor_tensor(sq[:, :], core.mv[:, :, 0], core.mv[:, :, 0], ALU.mult))
                chain.link(dve.scalar_tensor_tensor(out=core.rs[:, 1, :], in0=sq[:, :], scalar=1e-6, in1=core.mv[:, :, 1],
                                                    op0=ALU.add, op1=ALU.add))
                rsqrt(dve, chain, core.rs[:, 0, :], core.rs[:, 1, :], core.rs[:, 2, :], core.rs[:, 3, :])
                for j in range(TPB):
                    ins = dve.tensor_scalar(hn[:, j, :], h[:, j, :], core.rs[:, 0, j:j + 1], None, ALU.mult)
                ins.then_inc(hn_ready, 1)
                if not last:
                    residual(b + 1)
                for m in range(NB):
                    dve.wait_ge(silu_ready, NB * b + m + 1)
                    if m < 2:
                        wait_from(dve, y_ready, b)
                    dve.tensor_tensor(mid[0:sizes[m], m % 2, :], act_g[0:sizes[m], m % 2, :], pgu[0:sizes[m], m % 2, 1, :],
                                      ALU.mult).then_inc(mid_ready, 1)
                dve.wait_ge(y_ready, b + 1)
                dve.tensor_tensor(y[:, :, :], h[:, :, :], py[:, :, :], ALU.add).then_inc(y_read, 1)
                dve.wait_ge(y_read, b + 1)
                back(dve, chain, core, b, y)
                chain.restart()

            row(0, False)
            with dve.Fori(1, BATCH - 1) as b:
                row(b, False)
            row(BATCH - 1, True)


def delta_layer(core, conv_w, conv_b, norm1_w, norm2_w, wqkvba, wo, wg, wu, wd):
    nc = core.nc
    with ExitStack() as ctx:
        qkv = ctx.enter_context(nc.sbuf_tensor("qkv", [P, TPB, 48, P], F32))
        gates = ctx.enter_context(nc.sbuf_tensor("gates", [P, TPB, 2, P], F32))
        with nc.sbuf_tensor("x_scale", [P, 2, TPB], F32) as x_scale:
            delta_project(core, ctx, qkv, gates, x_scale, conv_w, conv_b, norm1_w, wqkvba)
        delta_recurrence(core, qkv, gates)
        delta_finish(core, qkv[:, :, 0:16, :], wo, norm2_w, wg, wu, wd)


def wait_from(eng, sem, value):
    if not isinstance(value, int) or value > 0:
        eng.wait_ge(sem, value)


def fused_moe_layer(core, router_dram, wg_dram, wu_dram, wd_dram, spread_dram):
    nc = core.nc
    E = router_dram.shape[1]
    NB = wg_dram.shape[1] // P
    ROWS = spread_dram.shape[0]
    name = "moe0"
    with ExitStack() as ctx:
        sb = lambda n, shape, dt=F32: ctx.enter_context(nc.sbuf_tensor(f"{name}_{n}", shape, dt))
        ps = lambda n, shape: ctx.enter_context(nc.psum_tensor(f"{name}_{n}", shape, F32))
        sem = Signals(nc, ctx, name)
        xn = sb("xn", [P, TPB, DIM])
        xT = sb("xT", [P, KC, SEQ])
        wr = sb("wr", [P, KC, E])
        wg, wu = sb("wg", [P, KC, NB * P]), sb("wu", [P, KC, NB * P])
        wd = sb("wd", [P, NB, DIM])
        spread = sb("spread", [ROWS, NB, P])
        logit = sb("logit", [P, TPB, E])
        prob = sb("prob", [P, TPB, E])
        total = sb("total", [P, 4, TPB])
        best = sb("best", [P, TPB, 8])
        at = sb("at", [P, TPB, 8], U32)
        atf = sb("atf", [P, TPB, 8])
        share = sb("share", [P, 4, TPB])
        number = sb("number", [P, E])
        comb = sb("comb", [P, TPB, 2, ROWS])
        combT = sb("combT", [ROWS, SEQ])
        act_g = sb("act_g", [P, 2, SEQ])
        hT = sb("hT", [P, 2, SEQ])
        pt = ps("pt", [P, KC, SEQ])
        pgu = ps("pgu", [P, 2, SEQ])
        pr = ps("pr", [P, 2, SEQ])
        py = ps("py", [P, TPB, DIM])
        loaded, consts = sem("loaded"), sem("consts")
        xn_ready, turned, xT_ready = sem("xn_ready"), sem("turned"), sem("xT_ready")
        logits_ready, shifted, exps_ready, comb_ready = sem("logits_ready"), sem("shifted"), sem("exps_ready"), sem("comb_ready")
        combT_sent, combT_ready = sem("combT_sent"), sem("combT_ready")
        gu_ready, silu_ready, h_ready = sem("gu_ready"), sem("silu_ready"), sem("h_ready")
        y_ready, y_read, chain_dve = sem("y_ready"), sem("y_read"), sem("chain_dve")
        block = sem.block()

        @block.sync
        def _(sp):
            sp.dma_start(wr[:, :, :], router_dram.rearrange("(k p) n -> p k n", p=P)).then_inc(loaded, 16)
            sp.dma_start(spread[:, :, :], spread_dram).then_inc(loaded, 16)
            sp.dma_start(wg[:, :, :], wg_dram.rearrange("(k p) n -> p k n", p=P)).then_inc(loaded, 16)
            sp.dma_start(wu[:, :, :], wu_dram.rearrange("(k p) n -> p k n", p=P)).then_inc(loaded, 16)
            sp.dma_start(wd[:, :, :], wd_dram.rearrange("(m p) n -> p m n", p=P)).then_inc(loaded, 16)

        @block.gpsimd
        def _(pool):
            pool.iota(number[:, :], pattern=[[1, E]], base=0, channel_multiplier=0,
                      allow_small_or_imprecise_dtypes=True).then_inc(consts, 1)
            pool.memset(comb[:, :, :, :], 0.0).then_inc(consts, 1)
            pool.wait_ge(consts, 2)
            pool.memset(comb[:, :, 0, E:E + 1], 1.0).then_inc(consts, 1)

        @block.tensor
        def _(pe):
            pe.wait_ge(loaded, 16 * 5)

            def row(b):
                def up(m):
                    wait_from(pe, h_ready, NB * b + m - 1)
                    dst = pgu if m % 2 == 0 else pt
                    for i, w in enumerate((wg, wu)):
                        for k in range(KC):
                            last = pe.matmul(dst[:, i, :], w[:, k, m * P:(m + 1) * P], xT[:, k, :],
                                             start=k == 0, stop=k == KC - 1)
                    if m == 0:
                        pe.wait_ge(combT_ready, b + 1)
                    last = pe.matmul(pr[:, m % 2, :], spread[:, m, :], combT[:, :], start=True, stop=True)
                    last.then_inc(gu_ready, 1)

                def down(m):
                    pe.wait_ge(h_ready, NB * b + m + 1)
                    if m == 0:
                        wait_from(pe, y_read, b)
                    for j in range(TPB):
                        last = pe.matmul(py[:, j, :], hT[:, m % 2, j * P:(j + 1) * P], wd[:, m, :],
                                         start=m == 0 and j % 2 == 0, stop=m == NB - 1, skip_group_check=True)
                    return last

                pe.wait_ge(xn_ready, b + 1)
                wait_from(pe, h_ready, NB * b)
                transposes(pe, core, xn, pt, turned)
                pe.wait_ge(xT_ready, b + 1)
                for j in range(TPB):
                    for k in range(KC):
                        last = pe.matmul(pgu[:, 0, j * E:(j + 1) * E], xT[:, k, j * P:(j + 1) * P],
                                         wr[:, k, :], start=k == 0, stop=k == KC - 1)
                last.then_inc(logits_ready, 1)
                pe.wait_ge(comb_ready, b + 1)
                for j in range(TPB):
                    last = pe.transpose(pr[0:ROWS, 1, j * P:(j + 1) * P], comb[:, j, 0, :], core.ident[:, :])
                last.then_inc(combT_sent, 1)
                up(0)
                for m in range(1, NB):
                    up(m)
                    down(m - 1)
                down(NB - 1).then_inc(y_ready, 1)

            row(0)
            with pe.Fori(1, BATCH) as b:
                row(b)

        @block.scalar
        def _(act):
            def row(b):
                act.wait_ge(turned, b + 1)
                wait_from(act, y_ready, b)
                act.activation(xT[:, :, :], pt[:, :, :], ACT.Copy).then_inc(xT_ready, 1)
                act.wait_ge(shifted, b + 1)
                act.activation(prob[:, :, :], logit[:, :, :], ACT.Exp).then_inc(exps_ready, 1)
                act.wait_ge(combT_sent, b + 1)
                act.activation(combT[:, :], pr[0:ROWS, 1, :], ACT.Copy).then_inc(combT_ready, 1)
                for m in range(NB):
                    act.wait_ge(gu_ready, NB * b + m + 1)
                    wait_from(act, h_ready, NB * b + m - 1)
                    act.activation(act_g[:, m % 2, :], (pgu if m % 2 == 0 else pt)[:, 0, :], ACT.Silu).then_inc(silu_ready, 1)

            row(0)
            with act.Fori(1, BATCH) as b:
                row(b)

        @block.vector
        def _(dve):
            chain = Chain(dve, chain_dve)
            dve.wait_ge(consts, 3)
            front(dve, chain, core, 0, xn, xn_ready)
            chain.restart()

            def weigh(b):
                dve.wait_ge(logits_ready, b + 1)
                pl = pgu[:, 0, 0:TPB * E].rearrange("p (j e) -> p j e", e=E)
                chain.link(dve.tensor_reduce(total[:, 0, :], pl, AX.X, ALU.max))
                dve.tensor_tensor(logit[:, :, :], pl, total[:, 0, :].unsqueeze(2).broadcast_to([P, TPB, E]),
                                  ALU.subtract).then_inc(shifted, 1)
                dve.wait_ge(exps_ready, b + 1)
                chain.mark(dve.tensor_reduce(total[:, 1, :], prob[:, :, :], AX.X, ALU.add))
                for j in range(TPB):
                    chain.mark(dve.max(best[:, j, :], prob[:, j, :]))
                chain.wait()
                for j in range(TPB):
                    chain.mark(dve.max_index(at[:, j, :], best[:, j, :], prob[:, j, :]))
                chain.link(dve.reciprocal(total[:, 2, :], total[:, 1, :]))
                chain.mark(dve.tensor_copy(atf[:, :, 0:2], at[:, :, 0:2]))
                for i in range(2):
                    chain.mark(dve.tensor_tensor(share[:, i, :], best[:, :, i], total[:, 2, :], ALU.mult))
                chain.wait()
                chain.link(dve.scalar_tensor_tensor(out=share[:, 2, :], in0=share[:, 0, :], scalar=1e-9, in1=share[:, 1, :],
                                                    op0=ALU.add, op1=ALU.add))
                chain.link(dve.reciprocal(share[:, 3, :], share[:, 2, :]))
                for i in range(2):
                    chain.mark(dve.tensor_tensor(share[:, i, :], share[:, i, :], share[:, 3, :], ALU.mult))
                chain.wait()
                for j in range(TPB):
                    for i in range(2):
                        chain.mark(dve.tensor_scalar(comb[:, j, i, 0:E], number[:, :], atf[:, j, i:i + 1], share[:, i, j:j + 1],
                                                     ALU.is_equal, ALU.mult))
                chain.wait()
                dve.tensor_tensor(comb[:, :, 0, 0:E], comb[:, :, 0, 0:E], comb[:, :, 1, 0:E], ALU.add).then_inc(comb_ready, 1)

            def row(b, last):
                weigh(b)
                for m in range(NB):
                    dve.wait_ge(silu_ready, NB * b + m + 1)
                    if m < 2:
                        wait_from(dve, y_ready, b)
                    src = pgu if m % 2 == 0 else pt
                    chain.link(dve.tensor_tensor(act_g[:, m % 2, :], act_g[:, m % 2, :], src[:, 1, :], ALU.mult))
                    dve.tensor_tensor(hT[:, m % 2, :], act_g[:, m % 2, :], pr[:, m % 2, :], ALU.mult).then_inc(h_ready, 1)
                    if m == 4 and not last:
                        dve.wait_ge(turned, b + 1)
                        front(dve, chain, core, b + 1, xn, xn_ready)
                dve.wait_ge(y_ready, b + 1)
                back(dve, chain, core, b, py, y_read)
                chain.restart()

            row(0, False)
            with dve.Fori(1, BATCH - 1) as b:
                row(b, False)
            row(BATCH - 1, True)


def mamba_direction(core, name, flipped, bc_dram, part_dram, w, proj_dram, post=None):
    nc = core.nc
    CI = w["Alog"].shape[0] // P
    N = w["Alog"].shape[1]
    R = w["dt_w"].shape[0]
    K = w["conv_w"].shape[1]
    XD = w["xproj_w"].shape[1]
    Q = 2
    STEPS = N // Q * CI
    with ExitStack() as ctx:
        sb = lambda n, shape, dt=F32: ctx.enter_context(nc.sbuf_tensor(f"{name}_{n}", shape, dt))
        ps = lambda n, shape: ctx.enter_context(nc.psum_tensor(f"{name}_{n}", shape, F32))
        sem = Signals(nc, ctx, name)
        in_w, xproj_w, dt_w = sb("in_w", [P, KC, 2 * CI * P]), sb("xproj_w", [P, CI, XD]), sb("dt_w", [R, CI * P])
        out_w, proj = sb("out_w", [P, CI, DIM]), sb("proj", [P, KC, DIM])
        cw, vec = sb("cw", [P, CI, K]), sb("vec", [P, 3, CI])
        alog, A = sb("alog", [P, CI, N]), sb("A", [P, CI, N])
        xn, xT = sb("xn", [P, TPB, DIM]), sb("xT", [P, KC, SEQ])
        conv = sb("conv", [P, 2, SEQ])
        u, sz = sb("u", [P, CI, SEQ]), sb("sz", [P, CI, SEQ])
        xd = sb("xd", [XD, SEQ])
        pre, ln1p = sb("pre", [P, CI, SEQ]), sb("ln1p", [P, CI, SEQ])
        delta, du = sb("delta", [P, CI, SEQ]), sb("du", [P, CI, SEQ])
        Bs, Cs = sb("Bs", [P, 2, Q, SEQ]), sb("Cs", [P, 2, Q, SEQ])
        dA = sb("dA", [P, 2, Q, SEQ])
        G = sb("G", [P, 4, Q, SEQ])
        yz = sb("yz", [P, CI, SEQ])
        cat = sb("cat", [P, KC, SEQ])
        y = sb("y", [P, TPB, DIM])
        if post:
            part = sb("part", [P, TPB, DIM])
            rows = sb("rows", [P, 3, DIM])
        pt = ps("pt", [P, KC, SEQ])
        pw = ps("pw", [P, 2, SEQ])
        py = ps("py", [P, CI, SEQ])
        loaded, consts = sem("loaded"), sem("consts")
        names = ("xn_ready turned xT_ready xi_ready conv_ready u_ready z_ready z_read xd_ready xd_copied dt_ready dt_read "
                 "ln_ready delta_ready du_ready bc_stored dA_ready g_ready scanned hc_ready summed y_ready yz_ready "
                 "out_ready cat_ready proj_ready proj_read stored chain_dve chain_act").split()
        S = {n: sem(n) for n in names}
        (xn_ready, turned, xT_ready, xi_ready, conv_ready, u_ready, z_ready, z_read, xd_ready, xd_copied, dt_ready, dt_read,
         ln_ready, delta_ready, du_ready, bc_stored, dA_ready, g_ready, scanned, hc_ready, summed, y_ready, yz_ready,
         out_ready, cat_ready, proj_ready, proj_read, stored, chain_dve, chain_act) = (S[n] for n in names)
        b_loaded, c_loaded = ([sem(f"{n}_loaded{i}") for i in range(2)] for n in "bc")
        block = sem.block()
        LOADS = 16 * (10 + (3 if post else 0))
        REUSE = 4

        def time(ap):
            return ap[:, ::-1] if flipped else ap

        @block.sync
        def _(sp):
            for dst, src in ((in_w, w["in_w"]), (xproj_w, w["xproj_w"]), (out_w, w["out_w"]), (proj, proj_dram),
                             (cw, w["conv_w"]), (alog, w["Alog"])):
                sp.dma_start(dst[:, :, :], src.rearrange("(k p) n -> p k n", p=P)).then_inc(loaded, 16)
            sp.dma_start(dt_w[:, :], w["dt_w"]).then_inc(loaded, 16)
            with nc.allow_non_contiguous_dma(reason="short vectors"):
                for i, n in enumerate(("conv_b", "dt_b", "Dp")):
                    sp.dma_start(vec[:, i, :], w[n].rearrange("(k p) -> p k", p=P)).then_inc(loaded, 16)
            if post:
                for i, v in enumerate(post):
                    sp.dma_start(rows[:, i, :], row_of(v).broadcast_to([P, DIM])).then_inc(loaded, 16)

            def row(b):
                if post:
                    wait_from(sp, proj_read, b)
                    sp.dma_start(part[:, :, :], part_dram[:, bass.ds(TPB * b, TPB), :]).then_inc(stored, 16)
                sp.wait_ge(xd_copied, b + 1)
                for i in range(2):
                    sp.dma_start(bc_dram[i], xd[32 * (i + 1):32 * (i + 1) + N, :]).then_inc(bc_stored, 16)
                sp.wait_ge(bc_stored, 32 * b + 32)
                for q in range(N // Q):
                    wait_from(sp, g_ready, STEPS * b + CI * (q - 1))
                    sp.dma_start(Bs[:, q % 2, :, :], bc_dram[0, Q * q:Q * q + Q, :].rearrange("(a n) t -> a (n t)", a=1)
                                 .broadcast_to([P, Q * SEQ])).then_inc(b_loaded[q % 2], 16)
                    wait_from(sp, hc_ready, STEPS * b + CI * (q - 1))
                    sp.dma_start(Cs[:, q % 2, :, :], bc_dram[1, Q * q:Q * q + Q, :].rearrange("(a n) t -> a (n t)", a=1)
                                 .broadcast_to([P, Q * SEQ])).then_inc(c_loaded[q % 2], 16)
                if not post:
                    sp.wait_ge(proj_read, b + 1)
                    sp.dma_start(part_dram[:, bass.ds(TPB * b, TPB), :], y[:, :, :]).then_inc(stored, 16)

            for b in range(BATCH):
                row(b)
            sp.wait_ge(stored, 16 * BATCH)

        @block.tensor
        def _(pe):
            pe.wait_ge(loaded, LOADS)

            def row(b):
                pe.wait_ge(xn_ready, b + 1)
                wait_from(pe, cat_ready, b)
                transposes(pe, core, xn, pt, turned)
                pe.wait_ge(xT_ready, b + 1)
                for c in range(2 * CI):
                    if c < 2:
                        wait_from(pe, proj_read, b)
                    elif c < CI + 2:
                        pe.wait_ge(conv_ready, CI * b + c - 1)
                    else:
                        pe.wait_ge(z_read, CI * b + c - CI - 1)
                    for k in range(KC):
                        last = pe.matmul(pw[:, c % 2, :], in_w[:, k, c * P:(c + 1) * P], xT[:, k, :], start=k == 0, stop=k == KC - 1)
                    last.then_inc(xi_ready if c < CI else z_ready, 1)
                for c in range(CI):
                    pe.wait_ge(u_ready, CI * b + c + 1)
                    last = pe.matmul(pt[0:XD, 0, :], xproj_w[:, c, :], u[:, c, :], start=c == 0, stop=c == CI - 1)
                last.then_inc(xd_ready, 1)
                pe.wait_ge(xd_copied, b + 1)
                for c in range(CI):
                    if c < 2:
                        pe.wait_ge(z_read, CI * b + CI + c - 1)
                    else:
                        pe.wait_ge(dt_read, CI * b + c - 1)
                    pe.matmul(pw[:, c % 2, :], dt_w[:, c * P:(c + 1) * P], xd[0:R, :], start=True, stop=True).then_inc(dt_ready, 1)
                for s in range(STEPS):
                    q, c = s // CI, s % CI
                    pe.wait_ge(hc_ready, STEPS * b + s + 1)
                    if q == 0:
                        wait_from(pe, y_ready, CI * (b - 1) + c + 1)
                    for i in range(Q):
                        last = pe.matmul(py[:, c, :], core.ident[:, :], G[:, s % REUSE, i, :],
                                         start=q == 0 and i == 0, stop=q == N // Q - 1 and i == Q - 1)
                    last.then_inc(summed, 1)
                pe.wait_ge(yz_ready, CI * b + CI)
                for m in range(KC):
                    for c in range(CI):
                        last = pe.matmul(pt[:, m, :], out_w[:, c, m * P:(m + 1) * P], yz[:, c, :], start=c == 0, stop=c == CI - 1)
                last.then_inc(out_ready, 1)
                pe.wait_ge(cat_ready, b + 1)
                pe.wait_ge(dt_read, CI * b + CI)
                for j in range(TPB):
                    for k in range(KC):
                        last = pe.matmul(pw[:, j // 2, j % 2 * DIM:(j % 2 + 1) * DIM], cat[:, k, j * P:(j + 1) * P], proj[:, k, :],
                                         start=k == 0, stop=k == KC - 1)
                last.then_inc(proj_ready, 1)

            row(0)
            with pe.Fori(1, BATCH) as b:
                row(b)

        @block.scalar
        def _(act):
            chain = Chain(act, chain_act)
            act.wait_ge(loaded, LOADS)
            chain.link(act.activation(A[:, :, :], alog[:, :, :], ACT.Exp))
            chain.link(act.activation(A[:, :, :], A[:, :, :], ACT.Copy, scale=-1.0))
            act.wait_ge(consts, 1)
            chain.restart()

            def row(b):
                act.wait_ge(turned, b + 1)
                wait_from(act, cat_ready, b)
                for k in range(KC):
                    last = act.activation(time(xT[:, k, :]), pt[:, k, :], ACT.Copy)
                last.then_inc(xT_ready, 1)
                wait_from(act, yz_ready, CI * b)
                for c in range(CI):
                    act.wait_ge(conv_ready, CI * b + c + 1)
                    act.activation(u[:, c, :], conv[:, c % 2, :], ACT.Silu).then_inc(u_ready, 1)
                for c in range(CI):
                    act.wait_ge(z_ready, CI * b + c + 1)
                    act.activation(sz[:, c, :], pw[:, c % 2, :], ACT.Silu).then_inc(z_read, 1)
                act.wait_ge(xd_ready, b + 1)
                wait_from(act, bc_stored, 32 * b)
                act.activation(xd[:, :], pt[0:XD, 0, :], ACT.Copy).then_inc(xd_copied, 1)
                wait_from(act, delta_ready, b)
                for c in range(CI):
                    act.wait_ge(dt_ready, CI * b + c + 1)
                    act.activation(pre[:, c, :], pw[:, c % 2, :], ACT.Identity, bias=vec[:, 1, c:c + 1]).then_inc(dt_read, 1)
                act.wait_ge(dt_read, CI * b + CI)
                chain.link(act.activation(ln1p[:, :, :], pre[:, :, :], ACT.Abs))
                wait_from(act, g_ready, STEPS * b)
                chain.link(act.activation(du[:, :, :], ln1p[:, :, :], ACT.Exp, scale=-1.0))
                chain.link(act.activation(ln1p[:, :, :], du[:, :, :], ACT.Identity, bias=1.0))
                act.activation(delta[:, :, :], ln1p[:, :, :], ACT.Ln).then_inc(ln_ready, 1)
                act.wait_ge(delta_ready, b + 1)
                for s in range(STEPS):
                    q, c = s // CI, s % CI
                    wait_from(act, scanned, STEPS * b + s - 1)
                    for i in range(Q):
                        last = act.activation(dA[:, s % 2, i, 1:], delta[:, c, 1:], ACT.Exp, scale=A[:, c, Q * q + i:Q * q + i + 1])
                    last.then_inc(dA_ready, 1)
                chain.restart()

            row(0)
            with act.Fori(1, BATCH) as b:
                row(b)

        @block.gpsimd
        def _(pool):
            pool.memset(dA[:, :, :, 0:1], 0.0).then_inc(consts, 1)

            def row(b):
                pool.wait_ge(delta_ready, b + 1)
                pool.wait_ge(u_ready, CI * b + CI)
                wait_from(pool, g_ready, STEPS * b)
                for c in range(CI):
                    pool.tensor_tensor(du[:, c, :], delta[:, c, :], u[:, c, :], ALU.mult).then_inc(du_ready, 1)
                for s in range(STEPS):
                    q, c = s // CI, s % CI
                    pool.wait_ge(scanned, STEPS * b + s + 1)
                    if c == 0:
                        pool.wait_ge(c_loaded[q % 2], 16 * (N // Q // 2) * b + 16 * (q // 2 + 1))
                    pool.tensor_tensor(G[:, s % REUSE, :, :], G[:, s % REUSE, :, :], Cs[:, q % 2, :, :], ALU.mult).then_inc(hc_ready, 1)
                pool.wait_ge(z_read, CI * b + CI)
                for c in range(CI):
                    pool.wait_ge(y_ready, CI * b + c + 1)
                    pool.tensor_tensor(yz[:, c, :], yz[:, c, :], sz[:, c, :], ALU.mult).then_inc(yz_ready, 1)

            row(0)
            with pool.Fori(1, BATCH) as b:
                row(b)

        @block.vector
        def _(dve):
            chain = Chain(dve, chain_dve)
            dve.wait_ge(loaded, LOADS)

            def convolve(b):
                for c in range(CI):
                    dve.wait_ge(xi_ready, CI * b + c + 1)
                    wait_from(dve, u_ready, CI * b + c - 1)
                    src, dst = pw[:, c % 2, :], conv[:, c % 2, :]
                    chain.link(dve.tensor_scalar(dst, src, cw[:, c, K - 1:K], vec[:, 0, c:c + 1], ALU.mult, ALU.add))
                    for back_by in range(1, K):
                        ins = dve.scalar_tensor_tensor(out=dst[:, back_by:], in0=src[:, 0:SEQ - back_by],
                                                       scalar=cw[:, c, K - 1 - back_by:K - back_by], in1=dst[:, back_by:],
                                                       op0=ALU.mult, op1=ALU.add)
                        if back_by < K - 1:
                            chain.link(ins)
                        else:
                            ins.then_inc(conv_ready, 1)

            front(dve, chain, core, 0, xn, xn_ready)
            chain.restart()

            def row(b, last):
                convolve(b)
                dve.wait_ge(ln_ready, b + 1)
                chain.link(dve.scalar_tensor_tensor(out=ln1p[:, :, :], in0=ln1p[:, :, :], scalar=1.0, in1=du[:, :, :],
                                                    op0=ALU.subtract, op1=ALU.subtract))
                chain.link(dve.tensor_tensor(delta[:, :, :], delta[:, :, :], ln1p[:, :, :], ALU.subtract))
                dve.scalar_tensor_tensor(out=delta[:, :, :], in0=pre[:, :, :], scalar=0.0, in1=delta[:, :, :],
                                         op0=ALU.max, op1=ALU.add).then_inc(delta_ready, 1)
                if not last:
                    dve.wait_ge(turned, b + 1)
                    front(dve, chain, core, b + 1, xn, xn_ready)

                def scan(s):
                    dve.wait_ge(g_ready, STEPS * b + s + 1)
                    dve.wait_ge(dA_ready, STEPS * b + s + 1)
                    g = G[:, s % REUSE, :, :].rearrange("p n t -> p (n t)")
                    dve.tensor_tensor_scan(g, dA[:, s % 2, :, :].rearrange("p n t -> p (n t)"), g, 0.0, ALU.mult, ALU.add
                                           ).then_inc(scanned, 1)

                for s in range(STEPS):
                    q, c = s // CI, s % CI
                    if q == 0:
                        dve.wait_ge(du_ready, CI * b + c + 1)
                    if c == 0:
                        dve.wait_ge(b_loaded[q % 2], 16 * (N // Q // 2) * b + 16 * (q // 2 + 1))
                    if s < REUSE:
                        wait_from(dve, summed, STEPS * b)
                    else:
                        dve.wait_ge(summed, STEPS * b + s - REUSE + 1)
                    dve.tensor_tensor(G[:, s % REUSE, :, :], Bs[:, q % 2, :, :], du[:, c, :].unsqueeze(1).broadcast_to([P, Q, SEQ]),
                                      ALU.mult).then_inc(g_ready, 1)
                    if s > 0:
                        scan(s - 1)
                scan(STEPS - 1)
                dve.wait_ge(summed, STEPS * b + STEPS)
                wait_from(dve, out_ready, b)
                for c in range(CI):
                    dve.scalar_tensor_tensor(out=yz[:, c, :], in0=u[:, c, :], scalar=vec[:, 2, c:c + 1], in1=py[:, c, :],
                                             op0=ALU.mult, op1=ALU.add).then_inc(y_ready, 1)
                dve.wait_ge(out_ready, b + 1)
                wait_from(dve, proj_ready, b)
                for k in range(KC):
                    ins = dve.tensor_tensor(time(cat[:, k, :]), pt[:, k, :], xT[:, k, :], ALU.add)
                    if k == KC - 1:
                        ins.then_inc(cat_ready, 1)
                dve.wait_ge(proj_ready, b + 1)
                pp = pw[:, :, :].rearrange("p a (j n) -> p (a j) n", n=DIM)
                if not post:
                    wait_from(dve, stored, 16 * b)
                    dve.tensor_copy(y[:, :, :], pp).then_inc(proj_read, 1)
                else:
                    wide = lambda i: rows[:, i, :].unsqueeze(1).broadcast_to([P, TPB, DIM])
                    dve.wait_ge(stored, 16 * b + 16)
                    dve.tensor_tensor(y[:, :, :], pp, part[:, :, :], ALU.add).then_inc(proj_read, 1)
                    dve.wait_ge(proj_read, b + 1)
                    chain.link(dve.tensor_tensor(y[:, :, :], y[:, :, :], wide(0), ALU.add))
                    norm_stats(dve, chain, core, [y[:, j, :] for j in range(TPB)])
                    for j in range(TPB):
                        chain.mark(dve.tensor_scalar(y[:, j, :], y[:, j, :], core.mv[:, j, 0:1], core.rs[:, 0, j:j + 1],
                                                     ALU.subtract, ALU.mult))
                    chain.wait()
                    chain.link(dve.tensor_tensor(y[:, :, :], y[:, :, :], wide(1), ALU.mult))
                    chain.link(dve.tensor_tensor(y[:, :, :], y[:, :, :], wide(2), ALU.add))
                    back(dve, chain, core, b, y)
                chain.restart()

            row(0, False)
            with dve.Fori(1, BATCH - 1) as b:
                row(b, False)
            row(BATCH - 1, True)


def mamba_layer(core, fw, bw, proj_w, proj_b, ln_w, ln_b):
    nc = core.nc
    SCAN_N = fw["Alog"].shape[1]
    bc = nc.dram_tensor("b_and_c", (2, 2, SCAN_N, SEQ), F32, kind="Internal").ap()
    part = nc.dram_tensor("part", (P, NT, DIM), F32, kind="Internal").ap()
    mamba_direction(core, "fw", False, bc[0], part, fw, proj_w[0:DIM, :])
    mamba_direction(core, "bw", True, bc[1], part, bw, proj_w[DIM:2 * DIM, :], (proj_b, ln_w, ln_b))


def expert_mlp_layer(core, router_dram, w1_dram, w2_dram):
    nc = core.nc
    E, _, H = w1_dram.shape
    HC = H // P
    UP = E * HC
    name = "moe1"
    with ExitStack() as ctx:
        sb = lambda n, shape, dt=F32: ctx.enter_context(nc.sbuf_tensor(f"{name}_{n}", shape, dt))
        ps = lambda n, shape: ctx.enter_context(nc.psum_tensor(f"{name}_{n}", shape, F32))
        sem = Signals(nc, ctx, name)
        xn = sb("xn", [P, TPB, DIM])
        xT = sb("xT", [P, KC, SEQ])
        wr = sb("wr", [P, KC, E])
        w1 = sb("w1", [P, E, KC, H])
        w2 = sb("w2", [P, E, HC, DIM])
        logit = sb("logit", [P, TPB, E])
        best = sb("best", [P, TPB, 8])
        at = sb("at", [P, TPB, 8], U32)
        atf = sb("atf", [P, TPB, 8])
        gap = sb("gap", [P, 4, TPB])
        share = sb("share", [P, 2, TPB])
        number = sb("number", [P, E])
        gate = sb("gate", [P, 2, TPB, E])
        hT = sb("hT", [P, 2, HC, SEQ])
        acc = sb("acc", [P, TPB, DIM])
        pt = ps("pt", [P, KC, SEQ])
        ph = ps("ph", [P, 2, SEQ])
        py = ps("py", [P, 2, TPB, DIM])
        loaded, consts = sem("loaded"), sem("consts")
        w_loaded = [sem(f"w_loaded{e}") for e in range(2)]
        xn_ready, turned, xT_ready = sem("xn_ready"), sem("turned"), sem("xT_ready")
        logits_ready, gap_ready, exps_ready = sem("logits_ready"), sem("gap_ready"), sem("exps_ready")
        up_ready, h_ready, y_ready, y_read, chain_dve = sem("up_ready"), sem("h_ready"), sem("y_ready"), sem("y_read"), sem("chain_dve")
        block = sem.block()

        @block.sync
        def _(sp):
            sp.dma_start(wr[:, :, :], router_dram.rearrange("(k p) n -> p k n", p=P)).then_inc(loaded, 16)
            for i in range(2):
                part = slice(i * E // 2, (i + 1) * E // 2)
                for k in range(KC):
                    sp.dma_start(w1[:, part, k, :], w1_dram[part, k * P:(k + 1) * P, :].rearrange("e p h -> p e h")).then_inc(w_loaded[i], 16)
                for c in range(HC):
                    sp.dma_start(w2[:, part, c, :], w2_dram[part, c * P:(c + 1) * P, :].rearrange("e p h -> p e h")).then_inc(w_loaded[i], 16)

        @block.gpsimd
        def _(pool):
            pool.iota(number[:, :], pattern=[[1, E]], base=0, channel_multiplier=0,
                      allow_small_or_imprecise_dtypes=True).then_inc(consts, 1)

        @block.tensor
        def _(pe):
            pe.wait_ge(loaded, 16)

            def row(b, first=False):
                def up(e):
                    for c in range(HC):
                        n = UP * b + HC * e + c
                        wait_from(pe, h_ready, n - 1)
                        for k in range(KC):
                            last = pe.matmul(ph[:, c % 2, :], w1[:, e, k, c * P:(c + 1) * P], xT[:, k, :],
                                             start=k == 0, stop=k == KC - 1)
                        last.then_inc(up_ready, 1)

                def down(e):
                    pe.wait_ge(h_ready, UP * b + HC * (e + 1))
                    wait_from(pe, y_read, E * b + e - 1)
                    for j in range(TPB):
                        for c in range(HC):
                            last = pe.matmul(py[:, e % 2, j, :], hT[:, e % 2, c, j * P:(j + 1) * P], w2[:, e, c, :],
                                             start=c == 0, stop=c == HC - 1)
                    last.then_inc(y_ready, 1)

                pe.wait_ge(xn_ready, b + 1)
                wait_from(pe, gap_ready, b)
                transposes(pe, core, xn, pt, turned)
                pe.wait_ge(xT_ready, b + 1)
                for j in range(TPB):
                    for k in range(KC):
                        last = pe.matmul(pt[:, 0, j * E:(j + 1) * E], xT[:, k, j * P:(j + 1) * P], wr[:, k, :],
                                         start=k == 0, stop=k == KC - 1)
                last.then_inc(logits_ready, 1)
                if first:
                    pe.wait_ge(w_loaded[0], 16 * (KC + HC))
                up(0)
                for e in range(1, E):
                    if first and e == E // 2:
                        pe.wait_ge(w_loaded[1], 16 * (KC + HC))
                    up(e)
                    down(e - 1)
                down(E - 1)

            row(0, True)
            with pe.Fori(1, BATCH) as b:
                row(b)

        @block.scalar
        def _(act):
            def row(b):
                act.wait_ge(turned, b + 1)
                wait_from(act, y_ready, E * b)
                act.activation(xT[:, :, :], pt[:, :, :], ACT.Copy).then_inc(xT_ready, 1)
                act.wait_ge(gap_ready, b + 1)
                act.activation(gap[:, 1, :], gap[:, 0, :], ACT.Exp).then_inc(exps_ready, 1)
                for e in range(E):
                    wait_from(act, y_ready, E * b + e - 1)
                    for c in range(HC):
                        act.wait_ge(up_ready, UP * b + HC * e + c + 1)
                        act.activation(hT[:, e % 2, c, :], ph[:, c % 2, :], ACT.Gelu).then_inc(h_ready, 1)

            row(0)
            with act.Fori(1, BATCH) as b:
                row(b)

        @block.vector
        def _(dve):
            chain = Chain(dve, chain_dve)
            dve.wait_ge(consts, 1)
            front(dve, chain, core, 0, xn, xn_ready)
            chain.restart()

            def weigh(b):
                dve.wait_ge(logits_ready, b + 1)
                chain.link(dve.tensor_copy(logit[:, :, :], pt[:, 0, 0:TPB * E].rearrange("p (j e) -> p j e", e=E)))
                for j in range(TPB):
                    chain.mark(dve.max(best[:, j, :], logit[:, j, :]))
                chain.wait()
                dve.tensor_tensor(gap[:, 0, :], best[:, :, 1], best[:, :, 0], ALU.subtract).then_inc(gap_ready, 1)
                for j in range(TPB):
                    chain.mark(dve.max_index(at[:, j, :], best[:, j, :], logit[:, j, :]))
                chain.wait()
                chain.mark(dve.tensor_copy(atf[:, :, 0:2], at[:, :, 0:2]))
                dve.wait_ge(exps_ready, b + 1)
                chain.link(dve.tensor_scalar(gap[:, 2, :], gap[:, 1, :], 1.0, None, ALU.add))
                chain.link(dve.reciprocal(share[:, 0, :], gap[:, 2, :]))
                chain.link(dve.tensor_tensor(share[:, 1, :], gap[:, 1, :], share[:, 0, :], ALU.mult))
                for i in range(2):
                    for j in range(TPB):
                        chain.mark(dve.tensor_scalar(gate[:, i, j, :], number[:, :], atf[:, j, i:i + 1], share[:, i, j:j + 1],
                                                     ALU.is_equal, ALU.mult))
                chain.wait()
                chain.link(dve.tensor_tensor(gate[:, 0, :, :], gate[:, 0, :, :], gate[:, 1, :, :], ALU.add))

            def row(b, last):
                weigh(b)
                for e in range(E):
                    dve.wait_ge(y_ready, E * b + e + 1)
                    for j in range(TPB):
                        g = gate[:, 0, j, e:e + 1]
                        if e == 0:
                            ins = dve.tensor_scalar(acc[:, j, :], py[:, 0, j, :], g, None, ALU.mult)
                        else:
                            ins = dve.scalar_tensor_tensor(out=acc[:, j, :], in0=py[:, e % 2, j, :], scalar=g, in1=acc[:, j, :],
                                                           op0=ALU.mult, op1=ALU.add)
                    ins.then_inc(y_read, 1)
                    dve.wait_ge(y_read, E * b + e + 1)
                    if e == E // 2 and not last:
                        dve.wait_ge(turned, b + 1)
                        front(dve, chain, core, b + 1, xn, xn_ready)
                back(dve, chain, core, b, acc)
                chain.restart()

            row(0, False)
            with dve.Fori(1, BATCH - 1) as b:
                row(b, False)
            row(BATCH - 1, True)


def bucket_attention_layer(core, hash_dram, wq_dram, bq_dram, wv_dram, bv_dram, wo_dram, bo_dram, limits_dram):
    nc = core.nc
    name = "lsh"
    HEADS, HD = 8, 32
    BIG = 1e30
    SCALE = float(np.float32(1.0) / np.sqrt(HD).astype(np.float32))
    UNITS = HEADS * TPB
    with ExitStack() as ctx:
        sb = lambda n, shape, dt=F32: ctx.enter_context(nc.sbuf_tensor(f"{name}_{n}", shape, dt))
        ps = lambda n, shape: ctx.enter_context(nc.psum_tensor(f"{name}_{n}", shape, F32))
        wh, wq, wv, wo = sb("wh", [P, KC, 2 * HEADS]), sb("wq", [P, KC, DIM]), sb("wv", [P, KC, DIM]), sb("wo", [P, KC, DIM])
        bq = sb("bq", [P, KC])
        rows = sb("rows", [P, 2, DIM])
        limits = sb("limits", [P, 2])
        xn, xT = sb("xn", [P, TPB, DIM]), sb("xT", [P, KC, SEQ])
        qT = sb("qT", [P, KC, SEQ])
        v = sb("v", [P, TPB, DIM])
        below = sb("below", [P, TPB, HEADS])
        angle = sb("angle", [P, TPB, HEADS])
        angleT = sb("angleT", [HEADS, SEQ])
        others = sb("others", [P, HEADS, SEQ])
        later = sb("later", [P, P])
        before = sb("before", [P, 2, SEQ], BF16)
        tied = sb("tied", [P, 2, P], BF16)
        mine = sb("mine", [P, HEADS, P], BF16)
        least = sb("least", [P, KC, SEQ])
        hot = sb("hot", [P, KC, SEQ], BF16)
        cold = sb("cold", [P, KC, SEQ], BF16)
        top = sb("top", [P, 4, 2])
        prob = sb("prob", [P, 2, SEQ])
        probT = sb("probT", [P, 2, TPB, P])
        total = sb("total", [P, 2, TPB, HEADS])
        o, oT = sb("o", [P, TPB, DIM]), sb("oT", [P, KC, SEQ])
        y = sb("y", [P, TPB, DIM])
        pt, pscore = ps("pt", [P, KC, SEQ]), ps("pscore", [P, 2, SEQ])
        pturn, pout = ps("pturn", [P, 2, TPB, P]), ps("pout", [P, TPB, DIM])
        names = ("loaded consts xn_ready turned xT_ready q_ready qT_ready v_ready v_taken hash_ready angle_ready angleT_sent angleT_ready "
                 "angle_stored others_ready compared counted hot_ready score_ready top_ready exp_ready turned_p copied pv_ready o_ready "
                 "o_sent oT_ready y_ready y_read chain_dve").split()
        sem = Signals(nc, ctx, name)
        s = type("Semaphores", (), {n: sem(n) for n in names})
        angle_dram = nc.dram_tensor("lsh_angles", (HEADS, SEQ), F32, kind="Internal").ap()
        LOADS = 16 * 8
        block = sem.block()

        @block.sync
        def _(sp):
            for dst, src in ((wh, hash_dram), (wq, wq_dram), (wv, wv_dram), (wo, wo_dram)):
                sp.dma_start(dst[:, :, :], src.rearrange("(k p) n -> p k n", p=P)).then_inc(s.loaded, 16)
            with nc.allow_non_contiguous_dma(reason="a short vector"):
                sp.dma_start(bq[:, :], bq_dram.rearrange("(k p) -> p k", p=P)).then_inc(s.loaded, 16)
            for i, vec in enumerate((bv_dram, bo_dram)):
                sp.dma_start(rows[:, i, :], row_of(vec).broadcast_to([P, DIM])).then_inc(s.loaded, 16)
            sp.dma_start(limits[:, :], limits_dram).then_inc(s.loaded, 16)
            for b in range(BATCH):
                sp.wait_ge(s.angleT_ready, b + 1)
                sp.dma_start(angle_dram, angleT[:, :]).then_inc(s.angle_stored, 16)
                sp.wait_ge(s.angle_stored, 16 * (b + 1))
                wait_from(sp, s.compared, UNITS * b)
                sp.dma_start(others[:, :, :], angle_dram.rearrange("(a h) t -> a (h t)", a=1).broadcast_to([P, HEADS * SEQ])
                             ).then_inc(s.others_ready, 16)

        @block.gpsimd
        def _(pool):
            pool.memset(later[:, :], 0.0).then_inc(s.consts, 1)
            pool.memset(mine[:, :, :], 0.0).then_inc(s.consts, 1)
            pool.wait_ge(s.consts, 2)
            pool.affine_select(out=later[:, :], in_=later[:, :], compare_op=ALU.is_ge, fill=1.0, base=0,
                               pattern=[[-1, P]], channel_multiplier=1).then_inc(s.consts, 1)
            for h in range(HEADS):
                pool.memset(mine[:, h, h % 4 * HD:h % 4 * HD + SEQ // 64], 1.0).then_inc(s.consts, 1)

        CONSTS = 3 + HEADS

        @block.tensor
        def _(pe):
            pe.wait_ge(s.loaded, LOADS)
            pe.wait_ge(s.consts, CONSTS)

            def row(b):
                pe.wait_ge(s.xn_ready, b + 1)
                wait_from(pe, s.oT_ready, b)
                transposes(pe, core, xn, pt, s.turned)
                pe.wait_ge(s.xT_ready, b + 1)
                for j in range(TPB):
                    for k in range(KC):
                        last = pe.matmul(pt[:, 0, j * 2 * HEADS:(j + 1) * 2 * HEADS], xT[:, k, j * P:(j + 1) * P], wh[:, k, :],
                                         start=k == 0, stop=k == KC - 1)
                last.then_inc(s.hash_ready, 1)
                for m in range(KC):
                    for k in range(KC):
                        last = pe.matmul(pscore[:, m, :], wq[:, k, m * P:(m + 1) * P], xT[:, k, :], start=k == 0, stop=k == KC - 1)
                last.then_inc(s.q_ready, 1)
                wait_from(pe, s.y_read, b)
                for j in range(TPB):
                    for k in range(KC):
                        last = pe.matmul(pout[:, j, :], xT[:, k, j * P:(j + 1) * P], wv[:, k, :], start=k == 0, stop=k == KC - 1)
                last.then_inc(s.v_ready, 1)
                pe.wait_ge(s.angle_ready, b + 1)
                for j in range(TPB):
                    last = pe.transpose(pt[0:HEADS, 1, j * P:(j + 1) * P], angle[:, j, :], core.ident[:, :])
                last.then_inc(s.angleT_sent, 1)
                pe.wait_ge(s.angleT_ready, b + 1)
                for n in range(UNITS):
                    h, j = n // TPB, n % TPB
                    pe.wait_ge(s.compared, UNITS * b + n + 1)
                    pe.matmul(pt[:, h // 4, :], mine[:, h, :], before[:, n % 2, :], start=h % 4 == 0 and j == 0, stop=False,
                              skip_group_check=True)
                    pe.matmul(pt[:, h // 4, j * P:(j + 1) * P], mine[:, h, :], tied[:, n % 2, :], start=False,
                              stop=h % 4 == 3 and j == TPB - 1, skip_group_check=True).then_inc(s.counted, 1)

                def scores(n):
                    h, i = n // TPB, n % TPB
                    at, c = slice(h % 4 * HD, h % 4 * HD + HD), h // 4
                    if n >= 2:
                        pe.wait_ge(s.exp_ready, UNITS * b + n - 1)
                    pe.matmul(pscore[:, n % 2, :], qT[at, c, i * P:(i + 1) * P], qT[at, c, :], start=True, stop=False)
                    pe.matmul(pscore[:, n % 2, :], hot[at, c, i * P:(i + 1) * P], cold[at, c, :], start=False, stop=True
                              ).then_inc(s.score_ready, 1)

                def turn(n):
                    pe.wait_ge(s.exp_ready, UNITS * b + n + 1)
                    wait_from(pe, s.copied, UNITS * b + n - 1)
                    for j in range(TPB):
                        last = pe.transpose(pturn[:, n % 2, j, :], prob[:, n % 2, j * P:(j + 1) * P], core.ident[:, :])
                    last.then_inc(s.turned_p, 1)

                def weigh(n):
                    h, i = n // TPB, n % TPB
                    pe.wait_ge(s.copied, UNITS * b + n + 1)
                    for j in range(TPB):
                        last = pe.matmul(pout[:, i, h * HD:(h + 1) * HD], probT[:, n % 2, j, :], v[:, j, h * HD:(h + 1) * HD],
                                         start=j == 0, stop=j == TPB - 1)
                    last.then_inc(s.pv_ready, 1)

                pe.wait_ge(s.qT_ready, b + 1)
                pe.wait_ge(s.hot_ready, b + 1)
                pe.wait_ge(s.v_taken, b + 1)
                for n in range(UNITS + 2):
                    if n < UNITS:
                        scores(n)
                    if 1 <= n <= UNITS:
                        turn(n - 1)
                    if n >= 2:
                        weigh(n - 2)
                pe.wait_ge(s.o_ready, b + 1)
                transposes(pe, core, o, pt, s.o_sent)
                pe.wait_ge(s.oT_ready, b + 1)
                for j in range(TPB):
                    for k in range(KC):
                        last = pe.matmul(pout[:, j, :], oT[:, k, j * P:(j + 1) * P], wo[:, k, :], start=k == 0, stop=k == KC - 1)
                last.then_inc(s.y_ready, 1)

            row(0)
            with pe.Fori(1, BATCH) as b:
                row(b)

        @block.scalar
        def _(act):
            act.wait_ge(s.loaded, LOADS)

            def row(b):
                act.wait_ge(s.turned, b + 1)
                act.activation(xT[:, :, :], pt[:, :, :], ACT.Copy).then_inc(s.xT_ready, 1)
                act.wait_ge(s.q_ready, b + 1)
                for k in range(KC):
                    last = act.activation(qT[:, k, :], pscore[:, k, :], ACT.Identity, bias=bq[:, k:k + 1])
                last.then_inc(s.qT_ready, 1)
                act.wait_ge(s.angleT_sent, b + 1)
                act.activation(angleT[:, :], pt[0:HEADS, 1, :], ACT.Copy).then_inc(s.angleT_ready, 1)
                for n in range(UNITS):
                    h, i = n // TPB, n % TPB
                    act.wait_ge(s.top_ready, UNITS * b + n + 1)
                    wait_from(act, s.turned_p, UNITS * b + n - 1)
                    if n == 0:
                        wait_from(act, s.o_ready, b)
                    act.activation(prob[:, n % 2, :], pscore[:, n % 2, :], ACT.Exp, bias=top[:, n % 4, 1:2], scale=SCALE,
                                   accum_out=total[:, 0, i, h:h + 1]).then_inc(s.exp_ready, 1)
                act.wait_ge(s.o_sent, b + 1)
                act.activation(oT[:, :, :], pt[:, :, :], ACT.Copy).then_inc(s.oT_ready, 1)

            row(0)
            with act.Fori(1, BATCH) as b:
                row(b)

        @block.vector
        def _(dve):
            chain = Chain(dve, s.chain_dve)
            dve.wait_ge(s.loaded, LOADS)
            dve.wait_ge(s.consts, CONSTS)
            front(dve, chain, core, 0, xn, s.xn_ready)
            chain.restart()
            wide = lambda i: rows[:, i, :].unsqueeze(1).broadcast_to([P, TPB, DIM])

            def row(b, last):
                dve.wait_ge(s.hash_ready, b + 1)
                pairs = pt[:, 0, 0:TPB * 2 * HEADS].rearrange("p (j h two) -> p j h two", h=HEADS, two=2)
                chain.link(dve.tensor_scalar(below[:, :, :], pairs[:, :, :, 1], 1e-4, None, ALU.add))
                chain.link(dve.reciprocal(below[:, :, :], below[:, :, :]))
                dve.tensor_tensor(angle[:, :, :], pairs[:, :, :, 0], below[:, :, :], ALU.mult).then_inc(s.angle_ready, 1)
                dve.wait_ge(s.v_ready, b + 1)
                dve.tensor_tensor(v[:, :, :], pout[:, :, :], wide(0), ALU.add).then_inc(s.v_taken, 1)
                if not last:
                    front(dve, chain, core, b + 1, xn, s.xn_ready)
                dve.wait_ge(s.angle_ready, b + 1)
                dve.wait_ge(s.others_ready, 16 * (b + 1))
                for n in range(UNITS):
                    h, j = n // TPB, n % TPB
                    own, edge = angle[:, j, h:h + 1], (j + 1) * P
                    if n >= 2:
                        dve.wait_ge(s.counted, UNITS * b + n - 1)
                    dve.tensor_scalar(before[:, n % 2, 0:edge], others[:, h, 0:edge], own, None, ALU.is_gt)
                    if edge < SEQ:
                        dve.tensor_scalar(before[:, n % 2, edge:], others[:, h, edge:], own, None, ALU.is_ge)
                    dve.scalar_tensor_tensor(out=tied[:, n % 2, :], in0=others[:, h, j * P:edge], scalar=own, in1=later[:, :],
                                             op0=ALU.is_equal, op1=ALU.mult).then_inc(s.compared, 1)
                dve.wait_ge(s.counted, UNITS * b + UNITS)
                chain.link(dve.tensor_scalar(least[:, :, :], pt[:, :, :], limits[:, 0:1], None, ALU.is_ge))
                chain.link(dve.scalar_tensor_tensor(out=hot[:, :, :], in0=pt[:, :, :], scalar=limits[:, 1:2], in1=least[:, :, :],
                                                    op0=ALU.is_lt, op1=ALU.mult))
                dve.tensor_scalar(cold[:, :, :], hot[:, :, :], 1.0, BIG, ALU.subtract, ALU.mult).then_inc(s.hot_ready, 1)
                for n in range(UNITS + 1):
                    if n < UNITS:
                        dve.wait_ge(s.score_ready, UNITS * b + n + 1)
                        chain.link(dve.reduce_max(top[:, n % 4, 0:1], pscore[:, n % 2, :], AX.X))
                        dve.tensor_scalar(top[:, n % 4, 1:2], top[:, n % 4, 0:1], -SCALE, None, ALU.mult).then_inc(s.top_ready, 1)
                    if n >= 1:
                        m = n - 1
                        dve.wait_ge(s.turned_p, UNITS * b + m + 1)
                        wait_from(dve, s.pv_ready, UNITS * b + m - 1)
                        dve.tensor_copy(probT[:, m % 2, :, :], pturn[:, m % 2, :, :]).then_inc(s.copied, 1)
                dve.wait_ge(s.pv_ready, UNITS * b + UNITS)
                chain.link(dve.reciprocal(total[:, 1, :, :], total[:, 0, :, :]))
                dve.tensor_tensor(o[:, :, :].rearrange("p j (h e) -> p j h e", e=HD), pout[:, :, :].rearrange("p j (h e) -> p j h e", e=HD),
                                  total[:, 1, :, :].unsqueeze(3).broadcast_to([P, TPB, HEADS, HD]), ALU.mult).then_inc(s.o_ready, 1)
                dve.wait_ge(s.y_ready, b + 1)
                dve.tensor_tensor(y[:, :, :], pout[:, :, :], wide(1), ALU.add).then_inc(s.y_read, 1)
                dve.wait_ge(s.y_read, b + 1)
                back(dve, chain, core, b, y)
                chain.restart()

            row(0, False)
            with dve.Fori(1, BATCH - 1) as b:
                row(b, False)
            row(BATCH - 1, True)


def decay_attention_layer(core, wqk_dram, wv_dram, wo_dram, decay_dram, log_dist_dram):
    nc = core.nc
    name = "causal"
    HEADS, HD, ROOM = 16, 16, 32
    QC = HEADS * ROOM // P
    BIG = 1e30
    SCALE = 0.25
    UNITS = HEADS * TPB
    with ExitStack() as ctx:
        sb = lambda n, shape, dt=F32: ctx.enter_context(nc.sbuf_tensor(f"{name}_{n}", shape, dt))
        ps = lambda n, shape: ctx.enter_context(nc.psum_tensor(f"{name}_{n}", shape, F32))
        wqk, wv, wo = sb("wqk", [P, KC, 2 * QC * P]), sb("wv", [P, KC, DIM]), sb("wo", [P, KC, DIM])
        log_dist = sb("log_dist", [P, SEQ])
        soft = sb("soft", [P, 5, HEADS])
        far = sb("far", [P, HEADS, SEQ])
        after = sb("after", [P, P])
        after_bf = sb("after_bf", [P, P], BF16)
        xn, xT = sb("xn", [P, TPB, DIM]), sb("xT", [P, KC, SEQ])
        qk = sb("qk", [P, 2 * QC, SEQ])
        v = sb("v", [P, TPB, DIM])
        top = sb("top", [P, 4, 2])
        prob = sb("prob", [P, 3, SEQ])
        probT = sb("probT", [P, 2, TPB, P])
        total = sb("total", [P, 2, TPB, HEADS])
        o, oT = sb("o", [P, TPB, DIM]), sb("oT", [P, KC, SEQ])
        pt, pscore = ps("pt", [P, KC, SEQ]), ps("pscore", [P, 2, SEQ])
        pturn, pout = ps("pturn", [P, 2, TPB, P]), ps("pout", [P, TPB, DIM])
        names = ("loaded consts far_ready xn_ready turned xT_ready qk_ready qk_taken v_ready v_taken score_ready top_ready exp_ready "
                 "prob_ready turned_p copied pv_ready o_ready o_sent oT_ready y_ready y_read chain_dve chain_act").split()
        sem = Signals(nc, ctx, name)
        s = type("Semaphores", (), {n: sem(n) for n in names})
        LOADS = 16 * 5
        block = sem.block()

        @block.sync
        def _(sp):
            for dst, src in ((wqk, wqk_dram), (wv, wv_dram), (wo, wo_dram)):
                sp.dma_start(dst[:, :, :], src.rearrange("(k p) n -> p k n", p=P)).then_inc(s.loaded, 16)
            sp.dma_start(log_dist[:, :], log_dist_dram).then_inc(s.loaded, 16)
            sp.dma_start(soft[:, 0, :], row_of(decay_dram).broadcast_to([P, HEADS])).then_inc(s.loaded, 16)

        @block.gpsimd
        def _(pool):
            pool.memset(after[:, :], 0.0).then_inc(s.consts, 1)
            pool.wait_ge(s.consts, 1)
            pool.affine_select(out=after[:, :], in_=after[:, :], compare_op=ALU.is_ge, fill=-BIG, base=0,
                               pattern=[[-1, P]], channel_multiplier=1).then_inc(s.consts, 1)
            pool.wait_ge(s.consts, 2)
            pool.tensor_copy(after_bf[:, :], after[:, :]).then_inc(s.consts, 1)

        @block.tensor
        def _(pe):
            pe.wait_ge(s.loaded, LOADS)
            pe.wait_ge(s.consts, 3)

            def row(b):
                pe.wait_ge(s.xn_ready, b + 1)
                wait_from(pe, s.oT_ready, b)
                transposes(pe, core, xn, pt, s.turned)
                pe.wait_ge(s.xT_ready, b + 1)
                for m in range(2 * QC):
                    if m >= 2:
                        pe.wait_ge(s.qk_taken, 2 * QC * b + m - 1)
                    for k in range(KC):
                        last = pe.matmul(pscore[:, m % 2, :], wqk[:, k, m * P:(m + 1) * P], xT[:, k, :], start=k == 0, stop=k == KC - 1)
                    last.then_inc(s.qk_ready, 1)
                wait_from(pe, s.y_read, b)
                for j in range(TPB):
                    for k in range(KC):
                        last = pe.matmul(pout[:, j, :], xT[:, k, j * P:(j + 1) * P], wv[:, k, :], start=k == 0, stop=k == KC - 1)
                last.then_inc(s.v_ready, 1)

                def scores(n):
                    h, i = n // TPB, n % TPB
                    at, c, width = slice(h % 4 * ROOM, h % 4 * ROOM + ROOM), h // 4, (i + 1) * P
                    if n >= 2:
                        pe.wait_ge(s.exp_ready, UNITS * b + n - 1)
                    pe.matmul(pscore[:, n % 2, 0:width], qk[at, c, i * P:width], qk[at, QC + c, 0:width], start=True, stop=True)
                    pe.matmul(pscore[:, n % 2, i * P:width], core.ident_bf[:, :], after_bf[:, :], start=False, stop=True,
                              skip_group_check=True).then_inc(s.score_ready, 1)

                def turn(n):
                    pe.wait_ge(s.prob_ready, UNITS * b + n + 1)
                    wait_from(pe, s.copied, UNITS * b + n - 1)
                    for j in range(n % TPB + 1):
                        last = pe.transpose(pturn[:, n % 2, j, :], prob[:, n % 3, j * P:(j + 1) * P], core.ident[:, :])
                    last.then_inc(s.turned_p, 1)

                def weigh(n):
                    h, i = n // TPB, n % TPB
                    pe.wait_ge(s.copied, UNITS * b + n + 1)
                    for j in range(i + 1):
                        last = pe.matmul(pout[:, i, h * HD:(h + 1) * HD], probT[:, n % 2, j, :], v[:, j, h * HD:(h + 1) * HD],
                                         start=j == 0, stop=j == i)
                    last.then_inc(s.pv_ready, 1)

                pe.wait_ge(s.qk_taken, 2 * QC * (b + 1))
                pe.wait_ge(s.v_taken, b + 1)
                for n in range(UNITS + 3):
                    if n < UNITS:
                        scores(n)
                    if 2 <= n < UNITS + 2:
                        turn(n - 2)
                    if n >= 3:
                        weigh(n - 3)
                pe.wait_ge(s.o_ready, b + 1)
                transposes(pe, core, o, pt, s.o_sent)
                pe.wait_ge(s.oT_ready, b + 1)
                for j in range(TPB):
                    for k in range(KC):
                        last = pe.matmul(pout[:, j, :], oT[:, k, j * P:(j + 1) * P], wo[:, k, :], start=k == 0, stop=k == KC - 1)
                last.then_inc(s.y_ready, 1)

            row(0)
            with pe.Fori(1, BATCH) as b:
                row(b)

        @block.scalar
        def _(act):
            chain = Chain(act, s.chain_act)
            act.wait_ge(s.loaded, LOADS)
            chain.link(act.activation(soft[:, 1, :], soft[:, 0, :], ACT.Abs))
            chain.link(act.activation(soft[:, 2, :], soft[:, 1, :], ACT.Exp, scale=-1.0))
            chain.link(act.activation(soft[:, 3, :], soft[:, 2, :], ACT.Identity, bias=1.0))
            act.activation(soft[:, 4, :], soft[:, 3, :], ACT.Ln).then_inc(s.far_ready, 1)

            def row(b):
                act.wait_ge(s.turned, b + 1)
                act.activation(xT[:, :, :], pt[:, :, :], ACT.Copy).then_inc(s.xT_ready, 1)
                for m in range(2 * QC):
                    act.wait_ge(s.qk_ready, 2 * QC * b + m + 1)
                    act.activation(qk[:, m, :], pscore[:, m % 2, :], ACT.Copy).then_inc(s.qk_taken, 1)
                for n in range(UNITS + 2):
                    if n < UNITS:
                        h, i = n // TPB, n % TPB
                        act.wait_ge(s.top_ready, UNITS * b + n + 1)
                        wait_from(act, s.turned_p, UNITS * b + n - 2)
                        act.activation(prob[:, n % 3, 0:(i + 1) * P], pscore[:, n % 2, 0:(i + 1) * P], ACT.Exp,
                                       bias=top[:, n % 4, 1:2], scale=SCALE).then_inc(s.exp_ready, 1)
                    if n >= 2:
                        m = n - 2
                        act.wait_ge(s.turned_p, UNITS * b + m + 1)
                        wait_from(act, s.pv_ready, UNITS * b + m - 1)
                        act.activation(probT[:, m % 2, 0:m % TPB + 1, :], pturn[:, m % 2, 0:m % TPB + 1, :], ACT.Copy).then_inc(s.copied, 1)
                act.wait_ge(s.o_sent, b + 1)
                act.activation(oT[:, :, :], pt[:, :, :], ACT.Copy).then_inc(s.oT_ready, 1)

            row(0)
            with act.Fori(1, BATCH) as b:
                row(b)

        @block.vector
        def _(dve):
            chain = Chain(dve, s.chain_dve)
            front(dve, chain, core, 0, xn, s.xn_ready)
            dve.wait_ge(s.loaded, LOADS)
            dve.wait_ge(s.far_ready, 1)
            chain.link(dve.scalar_tensor_tensor(out=soft[:, 3, :], in0=soft[:, 3, :], scalar=1.0, in1=soft[:, 2, :],
                                                op0=ALU.subtract, op1=ALU.subtract))
            chain.link(dve.tensor_tensor(soft[:, 4, :], soft[:, 4, :], soft[:, 3, :], ALU.subtract))
            chain.link(dve.scalar_tensor_tensor(out=soft[:, 0, :], in0=soft[:, 0, :], scalar=0.0, in1=soft[:, 4, :],
                                                op0=ALU.max, op1=ALU.add))
            for h in range(HEADS):
                chain.mark(dve.tensor_scalar(far[:, h, :], log_dist[:, :], soft[:, 0, h:h + 1], 1.0, ALU.mult, ALU.add))
            chain.wait()
            chain.link(dve.reciprocal(far[:, :, :], far[:, :, :]))
            chain.restart()

            def row(b, last):
                dve.wait_ge(s.v_ready, b + 1)
                dve.tensor_copy(v[:, :, :], pout[:, :, :]).then_inc(s.v_taken, 1)
                if not last:
                    front(dve, chain, core, b + 1, xn, s.xn_ready)
                for n in range(UNITS + 1):
                    if n < UNITS:
                        width = (n % TPB + 1) * P
                        dve.wait_ge(s.score_ready, UNITS * b + n + 1)
                        chain.link(dve.reduce_max(top[:, n % 4, 0:1], pscore[:, n % 2, 0:width], AX.X))
                        dve.tensor_scalar(top[:, n % 4, 1:2], top[:, n % 4, 0:1], -SCALE, None, ALU.mult).then_inc(s.top_ready, 1)
                    if n >= 1:
                        m = n - 1
                        h, i = m // TPB, m % TPB
                        dve.wait_ge(s.exp_ready, UNITS * b + m + 1)
                        part = prob[:, m % 3, 0:(i + 1) * P]
                        dve.scalar_tensor_tensor(out=part, in0=part, scalar=1.0, in1=far[:, h, (TPB - 1 - i) * P:],
                                                 op0=ALU.mult, op1=ALU.mult, accum_out=total[:, 0, i, h:h + 1]).then_inc(s.prob_ready, 1)
                dve.wait_ge(s.pv_ready, UNITS * b + UNITS)
                dve.wait_ge(s.prob_ready, UNITS * b + UNITS)
                chain.link(dve.reciprocal(total[:, 1, :, :], total[:, 0, :, :]))
                dve.tensor_tensor(o[:, :, :].rearrange("p j (h e) -> p j h e", e=HD), pout[:, :, :].rearrange("p j (h e) -> p j h e", e=HD),
                                  total[:, 1, :, :].unsqueeze(3).broadcast_to([P, TPB, HEADS, HD]), ALU.mult).then_inc(s.o_ready, 1)
                dve.wait_ge(s.y_ready, b + 1)
                back(dve, chain, core, b, pout, s.y_read)
                chain.restart()

            row(0, False)
            with dve.Fori(1, BATCH - 1) as b:
                row(b, False)
            row(BATCH - 1, True)
def linear_layer(core, name, w_dram, scale_dram, bias_dram, dft=None):
    nc = core.nc
    with ExitStack() as ctx:
        sb = lambda n, shape, dt=F32: ctx.enter_context(nc.sbuf_tensor(f"{name}_{n}", shape, dt))
        sem = Signals(nc, ctx, name)
        xn = sb("xn", [P, TPB, DIM])
        xT = sb("xT", [P, KC, SEQ])
        w = sb("w", [P, KC, DIM])
        bias = sb("bias", [P, DIM])
        scale = sb("scale", [P, DIM])
        y = sb("y", [P, TPB, DIM])
        if dft:
            wf = sb("wf", [P, 2, KC, DIM])
            cs = sb("cs", [P, 3, KC, DIM])
            fw = sb("fw", [P, 2, KC, DIM])
        pt = ctx.enter_context(nc.psum_tensor(f"{name}_pt", [P, KC, SEQ], F32))
        py = ctx.enter_context(nc.psum_tensor(f"{name}_py", [P, TPB, DIM], F32))
        loaded, w_ready, w_acc = sem("loaded"), sem("w_ready"), sem("w_acc")
        xn_ready, turned, xT_ready, y_ready, y_read = (sem(n) for n in ("xn_ready", "turned", "xT_ready", "y_ready", "y_read"))
        _, chain_dve = None, sem("chain_dve")
        loads = 16 * (5 if dft else 3)
        block = sem.block()

        @block.sync
        def _(sp):
            sp.dma_start(bias[:, :], row_of(bias_dram).broadcast_to([P, DIM])).then_inc(loaded, 16)
            if dft:
                for i in range(2):
                    sp.dma_start(wf[:, i, :, :], w_dram[i].rearrange("(k p) n -> p k n", p=P)).then_inc(loaded, 16)
                    sp.dma_start(cs[:, i, :, :], dft[i].rearrange("(k p) n -> p k n", p=P)).then_inc(loaded, 16)
            else:
                sp.dma_start(w[:, :, :], w_dram.rearrange("(k p) n -> p k n", p=P)).then_inc(loaded, 16)
                sp.dma_start(scale[:, :], row_of(scale_dram).broadcast_to([P, DIM])).then_inc(loaded, 16)

        @block.tensor
        def _(pe):
            pe.wait_ge(loaded, loads)
            if dft:
                pe.wait_ge(w_ready, 1)
                for part, terms in enumerate([((0, 0), (1, 1)), ((1, 0), (0, 2))]):
                    for m in range(KC):
                        n = 0
                        for wi, ci in terms:
                            for k in range(KC):
                                last = pe.matmul(pt[:, part, m * DIM:(m + 1) * DIM], wf[:, wi, k, m * P:(m + 1) * P],
                                                 cs[:, ci, k, :], start=n == 0, stop=n == 2 * KC - 1)
                                n += 1
                last.then_inc(w_acc, 1)
                pe.wait_ge(w_ready, 2)
                for m in range(KC):
                    n = 0
                    for part, ci in ((0, 0), (1, 2)):
                        for k in range(KC):
                            last = pe.matmul(py[:, m, :], fw[:, part, k, m * P:(m + 1) * P], cs[:, ci, k, :],
                                             start=n == 0, stop=n == 2 * KC - 1)
                            n += 1
                last.then_inc(w_acc, 1)
                pe.wait_ge(w_ready, 3)

            def row(b):
                pe.wait_ge(xn_ready, b + 1)
                transposes(pe, core, xn, pt, turned)
                pe.wait_ge(xT_ready, b + 1)
                if not (isinstance(b, int) and b == 0):
                    pe.wait_ge(y_read, b)
                for j in range(TPB):
                    for k in range(KC):
                        last = pe.matmul(py[:, j, :], xT[:, k, j * P:(j + 1) * P], w[:, k, :], start=k == 0, stop=k == KC - 1)
                last.then_inc(y_ready, 1)

            row(0)
            with pe.Fori(1, BATCH) as b:
                row(b)

        @block.scalar
        def _(act):
            def copy_xT(b):
                act.wait_ge(turned, b + 1)
                act.activation(xT[:, :, :], pt[:, :, :], ACT.Copy).then_inc(xT_ready, 1)
            copy_xT(0)
            with act.Fori(1, BATCH) as b:
                act.wait_ge(y_ready, b)
                copy_xT(b)

        @block.vector
        def _(dve):
            chain = Chain(dve, chain_dve)
            if dft:
                dve.wait_ge(loaded, loads)
                dve.tensor_scalar(cs[:, 2, :, :], cs[:, 1, :, :], -1.0, None, ALU.mult).then_inc(w_ready, 1)
                dve.wait_ge(w_acc, 1)
                dve.tensor_copy(fw[:, :, :, :], pt[:, :, :].rearrange("p a (m n) -> p a m n", m=KC)).then_inc(w_ready, 1)
                dve.wait_ge(w_acc, 2)
                dve.tensor_scalar(w[:, :, :], py[:, 0:KC, :], 1.0 / DIM, None, ALU.mult).then_inc(w_ready, 1)
            front(dve, chain, core, 0, xn, xn_ready)
            chain.restart()

            def row(b, last):
                if not last:
                    dve.wait_ge(turned, b + 1)
                    front(dve, chain, core, b + 1, xn, xn_ready)
                dve.wait_ge(y_ready, b + 1)
                if not dft:
                    chain.link(dve.scalar_tensor_tensor(out=y[:, :, :], in0=py[:, :, :], scalar=1.0 / 127.0,
                                                        in1=scale[:, :].unsqueeze(1).broadcast_to([P, TPB, DIM]),
                                                        op0=ALU.mult, op1=ALU.mult))
                src = py if dft else y
                dve.tensor_tensor(y[:, :, :], src[:, :, :], bias[:, :].unsqueeze(1).broadcast_to([P, TPB, DIM]),
                                  ALU.add).then_inc(y_read, 1)
                if last: dve.wait_ge(y_read, BATCH)
                else: dve.wait_ge(y_read, b + 1)
                back(dve, chain, core, b, y)
                chain.restart()

            with dve.Fori(0, BATCH - 1) as b:
                row(b, False)
            row(BATCH - 1, True)


def whole_network(nc, a, out):
    with ExitStack() as ctx:
        core = Core(nc, ctx)
        prologue(core, ctx, a["x"])
        delta_layer(core, a["l0a_conv_w"], a["l0a_conv_b"], a["l0a_norm1_w"], a["l0a_norm2_w"], a["l0a_wqkvba"], a["l0a_wo"],
                    a["l0a_wg"], a["l0a_wu"], a["l0a_wd"])
        fused_moe_layer(core, a["l0f_router"], a["l0f_wg"], a["l0f_wu"], a["l0f_wd"], a["l0f_spread"])
        side = lambda d: {n: a[f"{d}_{n}"] for n in MAMBA_WEIGHTS}
        mamba_layer(core, side("fw"), side("bw"), a["l1a_proj"], a["l1a_proj_b"], a["l1a_ln_w"], a["l1a_ln_b"])
        expert_mlp_layer(core, a["l1f_router"], a["l1f_w1"], a["l1f_w2"])
        bucket_attention_layer(core, a["l2a_hash"], a["l2a_wq"], a["l2a_bq"], a["l2a_wv"], a["l2a_bv"], a["l2a_wo"], a["l2a_bo"],
                               a["l2a_limits"])
        linear_layer(core, "l2f", a["l2f_w"], a["l2f_scale"], a["l2f_bias"])
        decay_attention_layer(core, a["l3a_wqk"], a["l3a_wv"], a["l3a_wo"], a["l3a_decay"], a["l3a_log_dist"])
        linear_layer(core, "l3f", (a["l3f_real"], a["l3f_imag"]), None, a["l3f_bias"], (a["l3f_cos"], a["l3f_sin"]))
        epilogue(core, out)


MAMBA_WEIGHTS = ("in_w", "conv_w", "conv_b", "xproj_w", "dt_w", "dt_b", "Alog", "Dp", "out_w")


def side_by_side(routed, shared):
    flat = [np.moveaxis(w, 0, 1).reshape(w.shape[1], -1) for w in (routed, shared)]
    return np.concatenate(flat, axis=1)


def shape_constants():
    spread = np.zeros((32, 10, P), np.float32)
    for m in range(8):
        spread[2 * m, m, 0:64] = 1
        spread[2 * m + 1, m, 64:128] = 1
    spread[16, 8:] = 1
    limits = np.full((P, 2), 1e9, np.float32)
    for p in range(P):
        if p % 32 < 8:
            limits[p] = 64 * (p % 32), 64 * (p % 32) + 64
    distance = np.arange(P)[:, None] + (SEQ - P) - np.arange(SEQ)[None, :]
    n = np.arange(DIM)
    turn = 2 * np.pi * (np.outer(n, n) % DIM) / DIM
    return {"l0f_spread": spread, "l2a_limits": limits,
            "l3a_log_dist": np.log1p(np.maximum(distance, 0)).astype(np.float32),
            "l3f_cos": np.cos(turn).astype(np.float32), "l3f_sin": np.sin(turn).astype(np.float32)}


def laid_out(v):
    a = {"x": v["L0_attn_x"]}
    for n in ("conv_w", "conv_b", "norm1_w", "norm2_w", "wo", "wg", "wu", "wd"):
        a["l0a_" + n] = v["L0_attn_" + n]
    a["l0a_wqkvba"] = np.concatenate([v["L0_attn_" + n] for n in ("wq", "wk", "wv", "wb", "wa")], axis=1)
    a["l0f_router"] = v["L0_ffn_router_w"]
    a["l0f_wg"] = side_by_side(v["L0_ffn_wg_r"], v["L0_ffn_wg_s"])
    a["l0f_wu"] = side_by_side(v["L0_ffn_wu_r"], v["L0_ffn_wu_s"])
    a["l0f_wd"] = np.concatenate([v["L0_ffn_wd_r"].reshape(-1, DIM), v["L0_ffn_wd_s"].reshape(-1, DIM)], axis=0)
    for d in ("fw", "bw"):
        w = {n: v[f"L1_attn_{d}_{n}"] for n in MAMBA_WEIGHTS}
        for n in ("in_w", "dt_w", "out_w"):
            w[n] = w[n].T
        w["conv_w"] = w["conv_w"][:, 0, :]
        xproj = np.zeros((w["xproj_w"].shape[1], 80), np.float32)
        for i in range(3):
            xproj[:, 32 * i:32 * i + 16] = w["xproj_w"].T[:, 16 * i:16 * i + 16]
        w["xproj_w"] = xproj
        for n in MAMBA_WEIGHTS:
            a[f"{d}_{n}"] = w[n]
    a["l1a_proj"], a["l1a_proj_b"] = v["L1_attn_proj_w"].T, v["L1_attn_proj_b"]
    a["l1a_ln_w"], a["l1a_ln_b"] = v["L1_attn_ln_w"], v["L1_attn_ln_b"]
    a["l1f_router"] = v["L1_ffn_router_w"].T
    a["l1f_w1"], a["l1f_w2"] = np.swapaxes(v["L1_ffn_w1"], 1, 2), np.swapaxes(v["L1_ffn_w2"], 1, 2)
    for to, n in (("hash", "W_hash"), ("wq", "W_q"), ("bq", "b_q"), ("wv", "W_v"), ("bv", "b_v"), ("wo", "W_o"), ("bo", "b_o")):
        a["l2a_" + to] = v["L2_attn_" + n]
    a["l2f_w"], a["l2f_scale"], a["l2f_bias"] = v["L2_ffn_CB"].T, v["L2_ffn_SCB"], v["L2_ffn_bias"]
    qkv = v["L3_attn_w_attn"]
    wqk = np.zeros((DIM, 2, 16, 32), np.float32)
    wqk[:, :, :, 0:16] = qkv[:, 0:2 * DIM].reshape(DIM, 2, 16, 16)
    a["l3a_wqk"], a["l3a_wv"] = wqk.reshape(DIM, 1024), qkv[:, 2 * DIM:]
    a["l3a_wo"], a["l3a_decay"] = v["L3_attn_w_proj"], v["L3_attn_decay_raw"]
    a["l3f_real"], a["l3f_imag"], a["l3f_bias"] = v["L3_ffn_w_freq_real"], v["L3_ffn_w_freq_imag"], v["L3_ffn_bias"]
    a.update(shape_constants())
    return a


def kernel(**inputs):
    import concourse.bacc as bacc
    from concourse.bass_utils import run_bass_kernel_spmd

    nc = bacc.Bacc("TRN2", target_bir_lowering=False, num_devices=1)
    arrays, aps = {}, {}
    for name, value in laid_out({k: np.asarray(v) for k, v in inputs.items()}).items():
        arrays["in_" + name] = np.ascontiguousarray(value)
        aps[name] = nc.dram_tensor("in_" + name, value.shape, mybir.dt.from_np(value.dtype), kind="ExternalInput").ap()
    out = nc.dram_tensor("out", (BATCH, SEQ, DIM), F32, kind="ExternalOutput").ap()
    whole_network(nc, aps, out)
    return run_bass_kernel_spmd(nc, [arrays], core_ids=[0]).results[0]["out"]
```

```python
from contextlib import ExitStack

import numpy as np

import concourse.bass as bass
from concourse import mybir

F32 = mybir.dt.float32
BF16 = mybir.dt.bfloat16
I32 = mybir.dt.int32
U32 = mybir.dt.uint32
ALU = mybir.AluOpType
ACT = mybir.ActivationFunctionType
AX = mybir.AxisListType

P = 128
BATCH, SEQ, DIM = 8, 512, 256
TPB = SEQ // P
NT = BATCH * TPB
KC = DIM // P
LN_EPS = 1e-5
RSQRT_MAGIC = 0x5F3759DF


class Chain:

    def __init__(self, eng, sem):
        self.eng, self.sem, self.n = eng, sem, 0

    def mark(self, ins):
        self.n += 1
        return ins.then_inc(self.sem, 1)

    def wait(self):
        self.eng.wait_ge(self.sem, self.n)

    def link(self, ins):
        self.mark(ins)
        self.wait()

    def restart(self):
        self.wait()
        self.eng.sem_clear(self.sem)
        self.n = 0


class Signals:

    def __init__(self, nc, ctx, layer):
        self.nc, self.ctx, self.layer, self.taken = nc, ctx, layer, []

    def __call__(self, name):
        self.taken.append(self.ctx.enter_context(self.nc.semaphore(f"{self.layer}_{name}")))
        return self.taken[-1]

    def block(self):
        self.ctx.callback(self.clear)
        return self.ctx.enter_context(self.nc.Block())

    def clear(self):
        with self.nc.Block() as block:
            @block.sync
            def _(sp):
                for sem in self.taken:
                    sp.sem_clear(sem)


class Core:

    def __init__(self, nc, ctx):
        self.nc = nc
        sb = lambda name, shape, dt=F32: ctx.enter_context(nc.sbuf_tensor(name, shape, dt))
        self.X = sb("X", [P, NT, DIM])
        self.ident = sb("ident", [P, P])
        self.ident_bf = sb("ident_bf", [P, P], BF16)
        self.stats = sb("stats", [P, TPB, 6])
        self.mv = sb("mv", [P, TPB, 2])
        self.rs = sb("rs", [P, 4, TPB])
        self.tmp = sb("tmp", [P, TPB, DIM])


def rsqrt_stage(dve, chain, y, v, half, t, stage):
    chain.wait()
    if stage == 0:
        chain.mark(dve.tensor_scalar(half, v, 0.5, None, ALU.mult))
        chain.mark(dve.tensor_scalar(y.bitcast(I32), v.bitcast(I32), -0.5, float(RSQRT_MAGIC), ALU.mult, ALU.add))
        return
    chain.link(dve.tensor_tensor(t, y, y, ALU.mult))
    chain.link(dve.tensor_tensor(t, t, half, ALU.mult))
    chain.mark(dve.scalar_tensor_tensor(out=y, in0=t, scalar=1.5, in1=y, op0=ALU.subtract, op1=ALU.mult))
    if stage == 3:
        chain.wait()
        chain.mark(dve.tensor_scalar(y, y, -1.0, None, ALU.mult))


def rsqrt(dve, chain, y, v, half, t):
    for stage in range(4):
        rsqrt_stage(dve, chain, y, v, half, t, stage)
    chain.wait()


NORM_STAGES = 7


def norm_stage(dve, chain, core, tiles, stage, eps=LN_EPS):
    if stage == 0:
        for j, tile in enumerate(tiles):
            chain.mark(dve.bn_stats(core.stats[:, j, :], tile))
    elif stage == 1:
        chain.wait()
        for j in range(TPB):
            chain.mark(dve.bn_aggr(core.mv[:, j, :], core.stats[:, j, :]))
        chain.wait()
        chain.mark(dve.tensor_scalar(core.rs[:, 1, :], core.mv[:, :, 1], eps, None, ALU.add))
    else:
        rsqrt_stage(dve, chain, core.rs[:, 0, :], core.rs[:, 1, :], core.rs[:, 2, :], core.rs[:, 3, :], stage - 2)


def norm_stats(dve, chain, core, tiles):
    for stage in range(NORM_STAGES - 1):
        norm_stage(dve, chain, core, tiles, stage)
    chain.wait()


def front_stage(dve, chain, core, b, xn, xn_ready, stage):
    tiles = [core.X[:, TPB * b + j, :] for j in range(TPB)]
    if stage < NORM_STAGES - 1:
        norm_stage(dve, chain, core, tiles, stage)
        return
    chain.wait()
    for j in range(TPB):
        last = dve.tensor_scalar(xn[:, j, :], tiles[j], core.mv[:, j, 0:1], core.rs[:, 0, j:j + 1], ALU.subtract, ALU.mult)
    last.then_inc(xn_ready, 1)


def front(dve, chain, core, b, xn, xn_ready):
    for stage in range(NORM_STAGES):
        front_stage(dve, chain, core, b, xn, xn_ready, stage)


def back_stage(dve, chain, core, b, y, stage, y_read=None):
    if stage < NORM_STAGES - 1:
        norm_stage(dve, chain, core, [y[:, j, :] for j in range(TPB)], stage)
        return
    chain.wait()
    for j in range(TPB):
        last = dve.tensor_scalar(core.tmp[:, j, :], y[:, j, :], core.mv[:, j, 0:1], core.rs[:, 0, j:j + 1],
                                 ALU.subtract, ALU.mult)
        if y_read is None or j < TPB - 1:
            chain.mark(last)
    chain.wait()
    if y_read is not None:
        last.then_inc(y_read, 1)
        dve.wait_ge(y_read, b + 1)
    xb = core.X[:, bass.ds(TPB * b, TPB), :]
    chain.mark(dve.tensor_tensor(xb, xb, core.tmp[:, :, :], ALU.add))


def back(dve, chain, core, b, y, y_read=None):
    for stage in range(NORM_STAGES):
        back_stage(dve, chain, core, b, y, stage, y_read)


def transposes(pe, core, xn, pt, sent):
    for j in range(TPB):
        for k in range(KC):
            last = pe.transpose(pt[:, k, j * P:(j + 1) * P], xn[:, j, k * P:(k + 1) * P], core.ident[:, :])
    last.then_inc(sent, 1)


def row_of(ap):
    return ap.rearrange("(a n) -> a n", a=1)


def prologue(core, ctx, x_dram):
    nc = core.nc
    x_loaded = ctx.enter_context(nc.semaphore("x_loaded"))
    blank = ctx.enter_context(nc.semaphore("ident_steps"))
    with nc.Block() as block:
        @block.sync
        def _(sp):
            sp.dma_start(core.X[:, :, :], x_dram.rearrange("b (j p) d -> p (b j) d", p=P)).then_inc(x_loaded, 16)
            sp.wait_ge(x_loaded, 16)

        @block.gpsimd
        def _(pool):
            pool.memset(core.ident[:, :], 0.0).then_inc(blank, 1)
            pool.wait_ge(blank, 1)
            pool.affine_select(out=core.ident[:, :], in_=core.ident[:, :], compare_op=ALU.not_equal, fill=1.0,
                               base=0, pattern=[[-1, P]], channel_multiplier=1).then_inc(blank, 1)
            pool.wait_ge(blank, 2)
            pool.tensor_copy(core.ident_bf[:, :], core.ident[:, :]).then_inc(blank, 1)
            pool.wait_ge(blank, 3)


def epilogue(core, out_dram):
    nc = core.nc
    with nc.semaphore("x_stored") as x_stored, nc.Block() as block:
        @block.sync
        def _(sp):
            sp.dma_start(out_dram.rearrange("b (j p) d -> p (b j) d", p=P), core.X[:, :, :]).then_inc(x_stored, 16)
            sp.wait_ge(x_stored, 16)


def delta_project(core, ctx0, qkv, gates, x_scale, conv_w_dram, conv_b_dram, norm_w_dram, w_dram):
    nc = core.nc
    name = "proj"
    K = conv_w_dram.shape[1]
    HEADS, HD = 16, 16
    QK = 2 * DIM
    with ExitStack() as ctx:
        sb = lambda n, shape, dt=F32: ctx.enter_context(nc.sbuf_tensor(f"{name}_{n}", shape, dt))
        ps = lambda n, shape: ctx.enter_context(nc.psum_tensor(f"{name}_{n}", shape, F32))
        sem = Signals(nc, ctx, name)
        xn = sb("xn", [P, TPB, DIM])
        xs = sb("xs", [P, KC, K - 1 + SEQ])
        conv = sb("conv", [P, KC, SEQ])
        xc = sb("xc", [P, KC, SEQ])
        cw, cb, nw = sb("cw", [P, KC, K]), sb("cb", [P, KC]), sb("nw", [P, KC])
        w = sb("w", [P, KC, 3 * DIM + 2 * HEADS])
        sq = sb("sq", [P, TPB, 2 * HD, HEADS])
        norm = sb("norm", [P, 5, TPB * QK // HD])
        gate_bias = sb("gate_bias", [P, 2])
        pt = ps("pt", [P, KC, SEQ])
        pq = ps("pq", [P, 2, 2, SEQ])
        loaded, consts = sem("loaded"), sem("consts")
        xn_ready, turned, xs_ready, conv_ready, xc_ready = (sem(n) for n in ("xn_ready", "turned", "xs_ready", "conv_ready", "xc_ready"))
        tile_ready, tile_read, qk_ready, sq_ready, qk_done = (sem(n) for n in ("tile_ready", "tile_read", "qk_ready", "sq_ready", "qk_done"))
        chain_dve = sem("chain_dve")
        block = sem.block()

        @block.sync
        def _(sp):
            sp.dma_start(cw[:, :, :], conv_w_dram.rearrange("(k p) n -> p k n", p=P)).then_inc(loaded, 16)
            with nc.allow_non_contiguous_dma(reason="two short vectors"):
                sp.dma_start(cb[:, :], conv_b_dram.rearrange("(k p) -> p k", p=P)).then_inc(loaded, 16)
                sp.dma_start(nw[:, :], norm_w_dram.rearrange("(k p) -> p k", p=P)).then_inc(loaded, 16)
            sp.dma_start(w[:, :, :], w_dram.rearrange("(k p) n -> p k n", p=P)).then_inc(loaded, 16)

        @block.tensor
        def _(pe):
            pe.wait_ge(loaded, 16 * 4)

            def row(b):
                pe.wait_ge(xn_ready, b + 1)
                transposes(pe, core, xn, pt, turned)
                pe.wait_ge(xc_ready, b + 1)
                for j in range(TPB):
                    wait_from(pe, tile_read, 3 * (TPB * b + j - 1))
                    for half, (lo, hi) in enumerate(((0, QK), (QK, 3 * DIM + 2 * HEADS))):
                        for k in range(KC):
                            last = pe.matmul(pq[:, j % 2, half, 0:hi - lo], xc[:, k, j * P:(j + 1) * P], w[:, k, lo:hi],
                                             start=k == 0, stop=k == KC - 1)
                    last.then_inc(tile_ready, 1)

            row(0)
            with pe.Fori(1, BATCH) as b:
                row(b)

        @block.scalar
        def _(act):
            act.wait_ge(loaded, 16 * 4)
            act.wait_ge(consts, 2)

            def row(b):
                act.wait_ge(turned, b + 1)
                wait_from(act, conv_ready, KC * b)
                for k in range(KC):
                    last = act.activation(xs[:, k, K - 1:], pt[:, k, :], ACT.Copy, scale=nw[:, k:k + 1])
                last.then_inc(xs_ready, 1)
                wait_from(act, tile_ready, TPB * b)
                for k in range(KC):
                    act.wait_ge(conv_ready, KC * b + k + 1)
                    last = act.activation(xc[:, k, :], conv[:, k, :], ACT.Silu)
                last.then_inc(xc_ready, 1)
                for j in range(TPB):
                    act.wait_ge(tile_ready, TPB * b + j + 1)
                    heads = bass.ds(HEADS * b, HEADS)
                    for c in range(3):
                        src = pq[:, j % 2, c // 2, c % 2 * DIM:c % 2 * DIM + DIM].rearrange("p (h e) -> p e h", e=HD)
                        act.activation(qkv[:, j, c * HD:(c + 1) * HD, heads], src, ACT.Copy).then_inc(qk_ready if c == 1 else tile_read, 1)
                    for c in range(2):
                        at = DIM + c * HEADS
                        last = act.activation(gates[:, j, c, heads], pq[:, j % 2, 1, at:at + HEADS], ACT.Sigmoid,
                                              bias=gate_bias[:, c:c + 1])
                    last.then_inc(tile_read, 1)

            row(0)
            with act.Fori(1, BATCH) as b:
                row(b)

        @block.gpsimd
        def _(pool):
            pool.memset(xs[:, :, 0:K - 1], 0.0).then_inc(consts, 1)
            pool.memset(gate_bias[:, 0:1], 0.0)
            pool.memset(gate_bias[:, 1:2], 4.0).then_inc(consts, 1)

            def row(b):
                pool.wait_ge(qk_ready, TPB * (b + 1))
                wait_from(pool, qk_done, b)
                own = qkv[:, :, 0:2 * HD, bass.ds(HEADS * b, HEADS)]
                pool.tensor_tensor(sq[:, :, :, :], own, own, ALU.mult).then_inc(sq_ready, 1)
            row(0)
            with pool.Fori(1, BATCH) as b:
                row(b)

        @block.vector
        def _(dve):
            chain = Chain(dve, chain_dve)
            dve.wait_ge(loaded, 16 * 4)

            def front_rms(b):
                tiles = [core.X[:, TPB * b + j, :] for j in range(TPB)]
                norm_stats(dve, chain, core, tiles)
                rs, var = core.rs, core.mv[:, :, 1]
                chain.link(dve.tensor_copy(x_scale[:, 0, :], rs[:, 0, :]))
                chain.link(dve.tensor_tensor(x_scale[:, 1, :], rs[:, 0, :], rs[:, 0, :], ALU.mult))
                chain.link(dve.tensor_tensor(x_scale[:, 1, :], x_scale[:, 1, :], var, ALU.mult))
                chain.link(dve.tensor_scalar(x_scale[:, 1, :], x_scale[:, 1, :], 1e-6, None, ALU.add))
                rsqrt(dve, chain, rs[:, 0, :], x_scale[:, 1, :], rs[:, 2, :], rs[:, 3, :])
                chain.link(dve.tensor_tensor(x_scale[:, 0, :], x_scale[:, 0, :], rs[:, 0, :], ALU.mult))
                for j in range(TPB):
                    last = dve.tensor_scalar(xn[:, j, :], tiles[j], core.mv[:, j, 0:1], x_scale[:, 0, j:j + 1],
                                             ALU.subtract, ALU.mult)
                last.then_inc(xn_ready, 1)

            def convolve(b):
                dve.wait_ge(xs_ready, b + 1)
                for k in range(KC):
                    chain.mark(dve.tensor_scalar(conv[:, k, :], xs[:, k, K - 1:], cw[:, k, K - 1:K], cb[:, k:k + 1], ALU.mult, ALU.add))
                chain.wait()
                for tap in range(K - 1):
                    for k in range(KC):
                        ins = dve.scalar_tensor_tensor(out=conv[:, k, :], in0=xs[:, k, tap:tap + SEQ], scalar=cw[:, k, tap:tap + 1],
                                                       in1=conv[:, k, :], op0=ALU.mult, op1=ALU.add)
                        if tap == K - 2:
                            ins.then_inc(conv_ready, 1)
                        else:
                            chain.mark(ins)
                    if tap < K - 2:
                        chain.wait()

            def lengths(b):
                dve.wait_ge(sq_ready, b + 1)
                chain.link(dve.tensor_reduce(norm[:, 1, :].rearrange("p (g h) -> p g h", h=HEADS), sq[:, :, :, :].rearrange("p j (c e) h -> p (j c) h e", e=HD), AX.X, ALU.add))
                chain.link(dve.tensor_scalar(norm[:, 2, :], norm[:, 1, :], 1e-6, None, ALU.add))
                rsqrt(dve, chain, norm[:, 0, :], norm[:, 2, :], norm[:, 3, :], norm[:, 4, :])
                for c in range(2):
                    part = qkv[:, :, c * HD:(c + 1) * HD, bass.ds(HEADS * b, HEADS)]
                    scale = norm[:, 0, :].rearrange("p (j c h) -> p j c h", j=TPB, c=2)[:, :, c, :]
                    last = dve.tensor_tensor(part, part, scale.unsqueeze(2).broadcast_to([P, TPB, HD, HEADS]), ALU.mult)
                last.then_inc(qk_done, 1)

            front_rms(0)
            chain.restart()

            def row(b, last):
                wait_from(dve, xc_ready, b)
                convolve(b)
                if not last:
                    dve.wait_ge(turned, b + 1)
                    front_rms(b + 1)
                lengths(b)
                chain.restart()

            row(0, False)
            with dve.Fori(1, BATCH - 1) as b:
                row(b, False)
            row(BATCH - 1, True)


def delta_recurrence(core, qkv, gates):
    nc = core.nc
    name = "scan"
    HEADS, HD = 16, 16
    SPANS = SEQ // P
    GROUPS = 3 * HD // 4
    G = 4
    TURNS = P // G
    HALF = HD // 2
    with ExitStack() as ctx:
        sb = lambda n, shape, dt=F32: ctx.enter_context(nc.sbuf_tensor(f"{name}_{n}", shape, dt))
        ps = lambda n, shape: ctx.enter_context(nc.psum_tensor(f"{name}_{n}", shape, F32))
        sem = Signals(nc, ctx, name)
        kqv = sb("kqv", [P, P, 4, HD])
        ba = sb("ba", [P, 3, P])
        prod = sb("prod", [P, 2 * G, HD, HD + 1])
        d = sb("d", [P, 2, HD])
        outer = sb("outer", [P, HD, HD])
        states = sb("states", [P, 2 * G, HD, HD])
        times_q = sb("times_q", [P, G, HD, HD])
        o = sb("o", [P, P, HD])
        pk = ps("pk", [P, 4, 4, P])
        po = ps("po", [P, 4, 4, P])
        names = "sent taken scaled filled states_ready states_used o_sent o_taken chain_dve chain_pool".split()
        sent, taken, scaled, filled, states_ready, states_used, o_sent, o_taken, chain_dve, chain_pool = (sem(n) for n in names)
        block = sem.block()

        PER = GROUPS + 1

        @block.tensor
        def _(pe):
            for s in range(SPANS):
                for g in range(PER):
                    n = PER * s + g
                    wait_from(pe, taken, n - 3)
                    for i in range(4):
                        if g < GROUPS:
                            src = qkv[:, s, g * 4 + i, :]
                        elif i < 2:
                            src = gates[:, s, i, :]
                        else:
                            continue
                        last = pe.transpose(pk[:, n % 4, i, :], src, core.ident[:, :])
                    last.then_inc(sent, 1)
                for g in range(HD // 4):
                    pe.wait_ge(states_used, TURNS * (s + 1))
                    wait_from(pe, o_taken, 4 * (s - 1) + g + 1)
                    for i in range(4):
                        last = pe.transpose(po[:, g, i, :], o[:, :, 4 * g + i], core.ident[:, :])
                    last.then_inc(o_sent, 1)

        @block.scalar
        def _(act):
            for s in range(SPANS):
                wait_from(act, states_used, TURNS * s)
                for g in range(PER):
                    n = PER * s + g
                    act.wait_ge(sent, n + 1)
                    if g < GROUPS:
                        part, at = (1, 0, 2)[g // 4], g % 4 * 4
                        act.activation(kqv[:, :, part, at:at + 4].rearrange("p t i -> p i t"), pk[:, n % 4, :, :],
                                       ACT.Copy).then_inc(taken, 1)
                    else:
                        act.activation(ba[:, 0:2, :], pk[:, n % 4, 0:2, :], ACT.Copy).then_inc(taken, 1)
                act.wait_ge(scaled, s + 1)
                for g in range(TURNS):
                    wait_from(act, states_ready, TURNS * s + g - 1)
                    act.activation(prod[:, g % 2 * G:(g % 2 + 1) * G, :, HD], kqv[:, g * G:(g + 1) * G, 2, :], ACT.Copy).then_inc(filled, 1)
                for g in range(4):
                    act.wait_ge(o_sent, 4 * s + g + 1)
                    last = act.activation(qkv[:, s, 4 * g:4 * g + 4, :], po[:, g, :, :], ACT.Copy)
                    last.then_inc(o_taken, 1)

        @block.gpsimd
        def _(pool):
            chain = Chain(pool, chain_pool)

            def span(s):
                for g in range(TURNS):
                    pool.wait_ge(states_ready, TURNS * s + g + 1)
                    if g == 0:
                        wait_from(pool, o_sent, 4 * s)
                    tokens = slice(g * G, (g + 1) * G)
                    chain.link(pool.tensor_tensor(times_q[:, :, :, :], states[:, g % 2 * G:(g % 2 + 1) * G, :, :],
                                                  kqv[:, tokens, 1, :].unsqueeze(2).broadcast_to([P, G, HD, HD]), ALU.mult))
                    width = HD // 2
                    while width > 1:
                        chain.link(pool.tensor_tensor(times_q[:, :, :, 0:width], times_q[:, :, :, 0:width],
                                                      times_q[:, :, :, width:2 * width], ALU.add))
                        width //= 2
                    if g == TURNS - 1:
                        chain.restart()
                    pool.tensor_tensor(o[:, tokens, :], times_q[:, :, :, 0], times_q[:, :, :, 1], ALU.add).then_inc(states_used, 1)
                    pool.wait_ge(states_used, TURNS * s + g + 1)

            span(0)
            with pool.Fori(1, SPANS) as s:
                span(s)

        @block.vector
        def _(dve):
            chain = Chain(dve, chain_dve)
            chain.mark(dve.memset(states[:, 2 * G - 1, :, :], 0.0))

            def span(s):
                dve.wait_ge(taken, PER * (s + 1))
                beta, alpha = ba[:, 0, :], ba[:, 1, :]
                spread = lambda row: row.unsqueeze(2).broadcast_to([P, P, HD])
                chain.link(dve.scalar_tensor_tensor(out=ba[:, 2, :], in0=beta, scalar=-1.0, in1=alpha, op0=ALU.mult, op1=ALU.mult))
                chain.mark(dve.tensor_tensor(kqv[:, :, 3, :], kqv[:, :, 0, :], spread(ba[:, 2, :]), ALU.mult))
                dve.tensor_tensor(kqv[:, :, 2, :], kqv[:, :, 2, :], spread(beta), ALU.mult).then_inc(scaled, 1)
                chain.restart()
                for t in range(P):
                    g, now, old = t // G, t % (2 * G), (t - 1) % (2 * G)
                    if t % G == 0:
                        dve.wait_ge(filled, TURNS * s + g + 1)
                        wait_from(dve, states_used, TURNS * s + g - 1)
                    halves = [slice(i * HALF, (i + 1) * HALF) for i in range(2)]
                    key = lambda i: kqv[:, t, i, :].unsqueeze(1).broadcast_to([P, HALF, HD])
                    base = chain.n

                    def after(step):
                        dve.wait_ge(chain_dve, base + step)

                    for i, half in enumerate(halves):
                        if t % G > 0:
                            after(i - 1)
                        elif t > 0 and i == 0:
                            after(0)
                        elif t > 0:
                            dve.wait_ge(states_ready, TURNS * s + g)
                        chain.mark(dve.tensor_tensor(prod[:, now, half, 0:HD], states[:, old, half, :], key(3), ALU.mult))
                    for i, half in enumerate(halves):
                        after(1 + i)
                        chain.mark(dve.tensor_reduce(d[:, t % 2, half], prod[:, now, half, :], AX.X, ALU.add))
                    for i, half in enumerate(halves):
                        after(3 + i)
                        chain.mark(dve.tensor_tensor(outer[:, half, :], d[:, t % 2, half].unsqueeze(2).broadcast_to([P, HALF, HD]),
                                                     key(0), ALU.mult))
                    for i, half in enumerate(halves):
                        after(5 + i)
                        ins = dve.scalar_tensor_tensor(out=states[:, now, half, :], in0=states[:, old, half, :],
                                                       scalar=ba[:, 1, t:t + 1], in1=outer[:, half, :], op0=ALU.mult, op1=ALU.add)
                        if t % G == G - 1 and i == 1:
                            ins.then_inc(states_ready, 1)
                        else:
                            chain.mark(ins)
                chain.restart()

            span(0)
            with dve.Fori(1, SPANS) as s:
                span(s)


def delta_finish(core, o, wo_dram, norm_w_dram, wg_dram, wu_dram, wd_dram):
    nc = core.nc
    name = "fin"
    HEADS, HD = 16, 16
    I = wg_dram.shape[1]
    NB = -(-I // P)
    sizes = [min(P, I - P * m) for m in range(NB)]
    with ExitStack() as ctx:
        sb = lambda n, shape, dt=F32: ctx.enter_context(nc.sbuf_tensor(f"{name}_{n}", shape, dt))
        ps = lambda n, shape: ctx.enter_context(nc.psum_tensor(f"{name}_{n}", shape, F32))
        sem = Signals(nc, ctx, name)
        xn = sb("xn", [P, TPB, DIM])
        os = sb("os", [P, TPB, DIM])
        oT = sb("oT", [P, KC, SEQ])
        h, hn = sb("h", [P, TPB, DIM]), sb("hn", [P, TPB, DIM])
        hnT = sb("hnT", [P, KC, SEQ])
        y = sb("y", [P, TPB, DIM])
        act_g, mid = sb("act_g", [P, 2, SEQ]), sb("mid", [P, 2, SEQ])
        wo, wg, wu = sb("wo", [P, KC, DIM]), sb("wg", [P, KC, I]), sb("wu", [P, KC, I])
        wd, nw = sb("wd", [P, NB, DIM]), sb("nw", [P, KC])
        sq = sb("sq", [P, TPB])
        pt = ps("pt", [P, KC, SEQ])
        pgu = ps("pgu", [P, 2, 2, SEQ])
        py = ps("py", [P, TPB, DIM])
        loaded = sem("loaded")
        os_ready, o_sent, oT_ready, mix_ready, hn_ready, hn_sent, hnT_ready = (
            sem(n) for n in ("os_ready", "o_sent", "oT_ready", "mix_ready", "hn_ready", "hn_sent", "hnT_ready"))
        gu_ready, silu_ready, mid_ready, y_ready, y_read, chain_dve = (
            sem(n) for n in ("gu_ready", "silu_ready", "mid_ready", "y_ready", "y_read", "chain_dve"))
        block = sem.block()

        @block.sync
        def _(sp):
            sp.dma_start(wo[:, :, :], wo_dram.rearrange("(k p) n -> p k n", p=P)).then_inc(loaded, 16)
            sp.dma_start(wg[:, :, :], wg_dram.rearrange("(k p) n -> p k n", p=P)).then_inc(loaded, 16)
            sp.dma_start(wu[:, :, :], wu_dram.rearrange("(k p) n -> p k n", p=P)).then_inc(loaded, 16)
            for m in range(NB):
                sp.dma_start(wd[0:sizes[m], m, :], wd_dram[P * m:P * m + sizes[m], :]).then_inc(loaded, 16)
            with nc.allow_non_contiguous_dma(reason="a short vector"):
                sp.dma_start(nw[:, :], norm_w_dram.rearrange("(k p) -> p k", p=P)).then_inc(loaded, 16)

        LOADS = 16 * (4 + NB)

        @block.gpsimd
        def _(pool):
            def row(b):
                wait_from(pool, o_sent, b)
                pool.tensor_copy(os[:, :, :].rearrange("p j (h e) -> p j h e", e=HD),
                                 o[:, :, :, bass.ds(HEADS * b, HEADS)].rearrange("p j e h -> p j h e")).then_inc(os_ready, 1)
            row(0)
            with pool.Fori(1, BATCH) as b:
                row(b)

        @block.tensor
        def _(pe):
            pe.wait_ge(loaded, LOADS)

            def row(b):
                def up(m):
                    wait_from(pe, mid_ready, NB * b + m - 1)
                    for i, w in enumerate((wg, wu)):
                        for k in range(KC):
                            last = pe.matmul(pgu[0:sizes[m], m % 2, i, :], w[:, k, m * P:m * P + sizes[m]], hnT[:, k, :],
                                             start=k == 0, stop=k == KC - 1)
                    last.then_inc(gu_ready, 1)

                def down(m):
                    pe.wait_ge(mid_ready, NB * b + m + 1)
                    for j in range(TPB):
                        last = pe.matmul(py[:, j, :], mid[0:sizes[m], m % 2, j * P:(j + 1) * P], wd[0:sizes[m], m, :],
                                         start=m == 0 and j % 2 == 0, stop=m == NB - 1, skip_group_check=True)
                    return last

                pe.wait_ge(os_ready, b + 1)
                wait_from(pe, hnT_ready, b)
                transposes(pe, core, os, pt, o_sent)
                pe.wait_ge(oT_ready, b + 1)
                wait_from(pe, y_read, b)
                for j in range(TPB):
                    for k in range(KC):
                        last = pe.matmul(py[:, j, :], oT[:, k, j * P:(j + 1) * P], wo[:, k, :], start=k == 0, stop=k == KC - 1)
                last.then_inc(mix_ready, 1)
                pe.wait_ge(hn_ready, b + 1)
                transposes(pe, core, hn, pt, hn_sent)
                pe.wait_ge(hnT_ready, b + 1)
                up(0)
                for m in range(1, NB):
                    up(m)
                    down(m - 1)
                down(NB - 1).then_inc(y_ready, 1)

            row(0)
            with pe.Fori(1, BATCH) as b:
                row(b)

        @block.scalar
        def _(act):
            act.wait_ge(loaded, LOADS)

            def row(b):
                act.wait_ge(o_sent, b + 1)
                wait_from(act, mix_ready, b)
                act.activation(oT[:, :, :], pt[:, :, :], ACT.Copy).then_inc(oT_ready, 1)
                act.wait_ge(hn_sent, b + 1)
                for k in range(KC):
                    last = act.activation(hnT[:, k, :], pt[:, k, :], ACT.Copy, scale=nw[:, k:k + 1])
                last.then_inc(hnT_ready, 1)
                for m in range(NB):
                    act.wait_ge(gu_ready, NB * b + m + 1)
                    wait_from(act, mid_ready, NB * b + m - 1)
                    act.activation(act_g[0:sizes[m], m % 2, :], pgu[0:sizes[m], m % 2, 0, :], ACT.Silu).then_inc(silu_ready, 1)

            row(0)
            with act.Fori(1, BATCH) as b:
                row(b)

        @block.vector
        def _(dve):
            chain = Chain(dve, chain_dve)

            def residual(b):
                tiles = [core.X[:, TPB * b + j, :] for j in range(TPB)]
                norm_stats(dve, chain, core, tiles)
                for j in range(TPB):
                    chain.mark(dve.tensor_scalar(xn[:, j, :], tiles[j], core.mv[:, j, 0:1], core.rs[:, 0, j:j + 1],
                                                 ALU.subtract, ALU.mult))
                chain.wait()

            residual(0)
            chain.restart()

            def row(b, last):
                dve.wait_ge(mix_ready, b + 1)
                chain.link(dve.tensor_tensor(h[:, :, :], xn[:, :, :], py[:, :, :], ALU.add))
                for j in range(TPB):
                    chain.mark(dve.bn_stats(core.stats[:, j, :], h[:, j, :]))
                chain.wait()
                for j in range(TPB):
                    chain.mark(dve.bn_aggr(core.mv[:, j, :], core.stats[:, j, :]))
                chain.wait()
                chain.link(dve.tensor_tensor(sq[:, :], core.mv[:, :, 0], core.mv[:, :, 0], ALU.mult))
                chain.link(dve.scalar_tensor_tensor(out=core.rs[:, 1, :], in0=sq[:, :], scalar=1e-6, in1=core.mv[:, :, 1],
                                                    op0=ALU.add, op1=ALU.add))
                rsqrt(dve, chain, core.rs[:, 0, :], core.rs[:, 1, :], core.rs[:, 2, :], core.rs[:, 3, :])
                for j in range(TPB):
                    ins = dve.tensor_scalar(hn[:, j, :], h[:, j, :], core.rs[:, 0, j:j + 1], None, ALU.mult)
                ins.then_inc(hn_ready, 1)
                if not last:
                    residual(b + 1)
                for m in range(NB):
                    dve.wait_ge(silu_ready, NB * b + m + 1)
                    if m < 2:
                        wait_from(dve, y_ready, b)
                    dve.tensor_tensor(mid[0:sizes[m], m % 2, :], act_g[0:sizes[m], m % 2, :], pgu[0:sizes[m], m % 2, 1, :],
                                      ALU.mult).then_inc(mid_ready, 1)
                dve.wait_ge(y_ready, b + 1)
                dve.tensor_tensor(y[:, :, :], h[:, :, :], py[:, :, :], ALU.add).then_inc(y_read, 1)
                dve.wait_ge(y_read, b + 1)
                back(dve, chain, core, b, y)
                chain.restart()

            row(0, False)
            with dve.Fori(1, BATCH - 1) as b:
                row(b, False)
            row(BATCH - 1, True)


def delta_layer(core, conv_w, conv_b, norm1_w, norm2_w, wqkvba, wo, wg, wu, wd):
    nc = core.nc
    with ExitStack() as ctx:
        qkv = ctx.enter_context(nc.sbuf_tensor("qkv", [P, TPB, 48, P], F32))
        gates = ctx.enter_context(nc.sbuf_tensor("gates", [P, TPB, 2, P], F32))
        with nc.sbuf_tensor("x_scale", [P, 2, TPB], F32) as x_scale:
            delta_project(core, ctx, qkv, gates, x_scale, conv_w, conv_b, norm1_w, wqkvba)
        delta_recurrence(core, qkv, gates)
        delta_finish(core, qkv[:, :, 0:16, :], wo, norm2_w, wg, wu, wd)


def wait_from(eng, sem, value):
    if not isinstance(value, int) or value > 0:
        eng.wait_ge(sem, value)


def fused_moe_layer(core, router_dram, wg_dram, wu_dram, wd_dram, spread_dram):
    nc = core.nc
    E = router_dram.shape[1]
    NB = wg_dram.shape[1] // P
    ROWS = spread_dram.shape[0]
    name = "moe0"
    with ExitStack() as ctx:
        sb = lambda n, shape, dt=F32: ctx.enter_context(nc.sbuf_tensor(f"{name}_{n}", shape, dt))
        ps = lambda n, shape: ctx.enter_context(nc.psum_tensor(f"{name}_{n}", shape, F32))
        sem = Signals(nc, ctx, name)
        xn = sb("xn", [P, TPB, DIM])
        xT = sb("xT", [P, KC, SEQ])
        wr = sb("wr", [P, KC, E])
        wg, wu = sb("wg", [P, KC, NB * P]), sb("wu", [P, KC, NB * P])
        wd = sb("wd", [P, NB, DIM])
        spread = sb("spread", [ROWS, NB, P])
        logit = sb("logit", [P, TPB, E])
        prob = sb("prob", [P, TPB, E])
        total = sb("total", [P, 4, TPB])
        best = sb("best", [P, TPB, 8])
        at = sb("at", [P, TPB, 8], U32)
        atf = sb("atf", [P, TPB, 8])
        share = sb("share", [P, 4, TPB])
        number = sb("number", [P, E])
        comb = sb("comb", [P, TPB, 2, ROWS])
        combT = sb("combT", [ROWS, SEQ])
        act_g = sb("act_g", [P, 2, SEQ])
        hT = sb("hT", [P, 2, SEQ])
        pt = ps("pt", [P, KC, SEQ])
        pgu = ps("pgu", [P, 2, SEQ])
        pr = ps("pr", [P, 2, SEQ])
        py = ps("py", [P, TPB, DIM])
        loaded, consts = sem("loaded"), sem("consts")
        xn_ready, turned, xT_ready = sem("xn_ready"), sem("turned"), sem("xT_ready")
        logits_ready, shifted, exps_ready, comb_ready = sem("logits_ready"), sem("shifted"), sem("exps_ready"), sem("comb_ready")
        combT_sent, combT_ready = sem("combT_sent"), sem("combT_ready")
        gu_ready, silu_ready, h_ready = sem("gu_ready"), sem("silu_ready"), sem("h_ready")
        y_ready, y_read, chain_dve = sem("y_ready"), sem("y_read"), sem("chain_dve")
        block = sem.block()

        @block.sync
        def _(sp):
            sp.dma_start(wr[:, :, :], router_dram.rearrange("(k p) n -> p k n", p=P)).then_inc(loaded, 16)
            sp.dma_start(spread[:, :, :], spread_dram).then_inc(loaded, 16)
            sp.dma_start(wg[:, :, :], wg_dram.rearrange("(k p) n -> p k n", p=P)).then_inc(loaded, 16)
            sp.dma_start(wu[:, :, :], wu_dram.rearrange("(k p) n -> p k n", p=P)).then_inc(loaded, 16)
            sp.dma_start(wd[:, :, :], wd_dram.rearrange("(m p) n -> p m n", p=P)).then_inc(loaded, 16)

        @block.gpsimd
        def _(pool):
            pool.iota(number[:, :], pattern=[[1, E]], base=0, channel_multiplier=0,
                      allow_small_or_imprecise_dtypes=True).then_inc(consts, 1)
            pool.memset(comb[:, :, :, :], 0.0).then_inc(consts, 1)
            pool.wait_ge(consts, 2)
            pool.memset(comb[:, :, 0, E:E + 1], 1.0).then_inc(consts, 1)

        @block.tensor
        def _(pe):
            pe.wait_ge(loaded, 16 * 5)

            def row(b):
                def up(m):
                    wait_from(pe, h_ready, NB * b + m - 1)
                    dst = pgu if m % 2 == 0 else pt
                    for i, w in enumerate((wg, wu)):
                        for k in range(KC):
                            last = pe.matmul(dst[:, i, :], w[:, k, m * P:(m + 1) * P], xT[:, k, :],
                                             start=k == 0, stop=k == KC - 1)
                    if m == 0:
                        pe.wait_ge(combT_ready, b + 1)
                    last = pe.matmul(pr[:, m % 2, :], spread[:, m, :], combT[:, :], start=True, stop=True)
                    last.then_inc(gu_ready, 1)

                def down(m):
                    pe.wait_ge(h_ready, NB * b + m + 1)
                    if m == 0:
                        wait_from(pe, y_read, b)
                    for j in range(TPB):
                        last = pe.matmul(py[:, j, :], hT[:, m % 2, j * P:(j + 1) * P], wd[:, m, :],
                                         start=m == 0 and j % 2 == 0, stop=m == NB - 1, skip_group_check=True)
                    return last

                pe.wait_ge(xn_ready, b + 1)
                wait_from(pe, h_ready, NB * b)
                transposes(pe, core, xn, pt, turned)
                pe.wait_ge(xT_ready, b + 1)
                for j in range(TPB):
                    for k in range(KC):
                        last = pe.matmul(pgu[:, 0, j * E:(j + 1) * E], xT[:, k, j * P:(j + 1) * P],
                                         wr[:, k, :], start=k == 0, stop=k == KC - 1)
                last.then_inc(logits_ready, 1)
                pe.wait_ge(comb_ready, b + 1)
                for j in range(TPB):
                    last = pe.transpose(pr[0:ROWS, 1, j * P:(j + 1) * P], comb[:, j, 0, :], core.ident[:, :])
                last.then_inc(combT_sent, 1)
                up(0)
                for m in range(1, NB):
                    up(m)
                    down(m - 1)
                down(NB - 1).then_inc(y_ready, 1)

            row(0)
            with pe.Fori(1, BATCH) as b:
                row(b)

        @block.scalar
        def _(act):
            def row(b):
                act.wait_ge(turned, b + 1)
                wait_from(act, y_ready, b)
                act.activation(xT[:, :, :], pt[:, :, :], ACT.Copy).then_inc(xT_ready, 1)
                act.wait_ge(shifted, b + 1)
                act.activation(prob[:, :, :], logit[:, :, :], ACT.Exp).then_inc(exps_ready, 1)
                act.wait_ge(combT_sent, b + 1)
                act.activation(combT[:, :], pr[0:ROWS, 1, :], ACT.Copy).then_inc(combT_ready, 1)
                for m in range(NB):
                    act.wait_ge(gu_ready, NB * b + m + 1)
                    wait_from(act, h_ready, NB * b + m - 1)
                    act.activation(act_g[:, m % 2, :], (pgu if m % 2 == 0 else pt)[:, 0, :], ACT.Silu).then_inc(silu_ready, 1)

            row(0)
            with act.Fori(1, BATCH) as b:
                row(b)

        @block.vector
        def _(dve):
            chain = Chain(dve, chain_dve)
            dve.wait_ge(consts, 3)
            front(dve, chain, core, 0, xn, xn_ready)
            chain.restart()

            def weigh(b):
                dve.wait_ge(logits_ready, b + 1)
                pl = pgu[:, 0, 0:TPB * E].rearrange("p (j e) -> p j e", e=E)
                chain.link(dve.tensor_reduce(total[:, 0, :], pl, AX.X, ALU.max))
                dve.tensor_tensor(logit[:, :, :], pl, total[:, 0, :].unsqueeze(2).broadcast_to([P, TPB, E]),
                                  ALU.subtract).then_inc(shifted, 1)
                dve.wait_ge(exps_ready, b + 1)
                chain.mark(dve.tensor_reduce(total[:, 1, :], prob[:, :, :], AX.X, ALU.add))
                for j in range(TPB):
                    chain.mark(dve.max(best[:, j, :], prob[:, j, :]))
                chain.wait()
                for j in range(TPB):
                    chain.mark(dve.max_index(at[:, j, :], best[:, j, :], prob[:, j, :]))
                chain.link(dve.reciprocal(total[:, 2, :], total[:, 1, :]))
                chain.mark(dve.tensor_copy(atf[:, :, 0:2], at[:, :, 0:2]))
                for i in range(2):
                    chain.mark(dve.tensor_tensor(share[:, i, :], best[:, :, i], total[:, 2, :], ALU.mult))
                chain.wait()
                chain.link(dve.scalar_tensor_tensor(out=share[:, 2, :], in0=share[:, 0, :], scalar=1e-9, in1=share[:, 1, :],
                                                    op0=ALU.add, op1=ALU.add))
                chain.link(dve.reciprocal(share[:, 3, :], share[:, 2, :]))
                for i in range(2):
                    chain.mark(dve.tensor_tensor(share[:, i, :], share[:, i, :], share[:, 3, :], ALU.mult))
                chain.wait()
                for j in range(TPB):
                    for i in range(2):
                        chain.mark(dve.tensor_scalar(comb[:, j, i, 0:E], number[:, :], atf[:, j, i:i + 1], share[:, i, j:j + 1],
                                                     ALU.is_equal, ALU.mult))
                chain.wait()
                dve.tensor_tensor(comb[:, :, 0, 0:E], comb[:, :, 0, 0:E], comb[:, :, 1, 0:E], ALU.add).then_inc(comb_ready, 1)

            def row(b, last):
                weigh(b)
                for m in range(NB):
                    dve.wait_ge(silu_ready, NB * b + m + 1)
                    if m < 2:
                        wait_from(dve, y_ready, b)
                    src = pgu if m % 2 == 0 else pt
                    chain.link(dve.tensor_tensor(act_g[:, m % 2, :], act_g[:, m % 2, :], src[:, 1, :], ALU.mult))
                    dve.tensor_tensor(hT[:, m % 2, :], act_g[:, m % 2, :], pr[:, m % 2, :], ALU.mult).then_inc(h_ready, 1)
                    if m == 4 and not last:
                        dve.wait_ge(turned, b + 1)
                        front(dve, chain, core, b + 1, xn, xn_ready)
                dve.wait_ge(y_ready, b + 1)
                back(dve, chain, core, b, py, y_read)
                chain.restart()

            row(0, False)
            with dve.Fori(1, BATCH - 1) as b:
                row(b, False)
            row(BATCH - 1, True)


def mamba_direction(core, name, flipped, bc_dram, part_dram, w, proj_dram, post=None):
    nc = core.nc
    DVE_AT = {"y": 0, "conv": (6, 8, 10, 12), "cat": 14, "end": 24, "rest": 26, "delta": 29, "front": 31}
    PE_AT = {"turn": 0, "xi": (2, 4, 6, 8, 10, 11, 21, 22), "out": (3, 5, 7, 9), "xproj": 13, "dt": 17, "proj": (15, 16, 19, 20)}
    ACT_AT = {"cat": 3, "xT": 4, "silu": 14, "z": (15, 16, 26, 27), "silu_z": 30, "xd": 19, "dt": 22, "abs": 24, "exp": 25, "w": 26, "ln": 28}
    POOL_AT = {"yz": (0, 1, 3, 5), "du": 29}
    CI = w["Alog"].shape[0] // P
    N = w["Alog"].shape[1]
    R = w["dt_w"].shape[0]
    K = w["conv_w"].shape[1]
    XD = w["xproj_w"].shape[1]
    Q = 2
    STEPS = N // Q * CI
    REUSE = 8
    with ExitStack() as ctx:
        sb = lambda n, shape, dt=F32: ctx.enter_context(nc.sbuf_tensor(f"{name}_{n}", shape, dt))
        ps = lambda n, shape: ctx.enter_context(nc.psum_tensor(f"{name}_{n}", shape, F32))
        sem = Signals(nc, ctx, name)
        in_w, xproj_w, dt_w = sb("in_w", [P, KC, 2 * CI * P]), sb("xproj_w", [P, CI, XD]), sb("dt_w", [R, CI * P])
        out_w, proj = sb("out_w", [P, CI, DIM]), sb("proj", [P, KC, DIM])
        cw, vec = sb("cw", [P, CI, K]), sb("vec", [P, 3, CI])
        alog, A = sb("alog", [P, CI, N]), sb("A", [P, CI, N])
        xn, xT = sb("xn", [P, TPB, DIM]), sb("xT", [P, 2, KC, SEQ])
        u, sz = sb("u", [P, 2, CI, SEQ]), sb("sz", [P, 2, CI, SEQ])
        xd = sb("xd", [XD, SEQ])
        e = sb("e", [P, CI, SEQ])
        delta, du = sb("delta", [P, 2, CI, SEQ]), sb("du", [P, 2, CI, SEQ])
        Bs, Cs = sb("Bs", [P, 2, Q, SEQ]), sb("Cs", [P, 2, Q, SEQ])
        dA = sb("dA", [P, 2, Q, SEQ])
        G = sb("G", [P, REUSE, Q, SEQ])
        yz = sb("yz", [P, CI, SEQ])
        cat = xn.rearrange("p (k j) n -> p k (j n)", k=KC)
        y = core.tmp
        if post:
            rows = sb("rows", [P, 3, DIM])
        pt = ps("pt", [P, KC, SEQ])
        pw = ps("pw", [P, 2, SEQ])
        py = ps("py", [P, CI, SEQ])
        loaded, consts = sem("loaded"), sem("consts")
        names = ("xn_ready turned xT_ready x_ready xi_ready conv_ready u_ready z_ready z_read sz_ready xd_ready xd_copied dt_ready dt_read "
                 "w_ready rest_ready ln_ready delta_ready du_ready bc_stored dA_ready g_ready scanned hc_ready summed y_ready yz_ready "
                 "out_ready cat_ready proj_ready proj_read stored chain_dve chain_act").split()
        (xn_ready, turned, xT_ready, x_ready, xi_ready, conv_ready, u_ready, z_ready, z_read, sz_ready, xd_ready, xd_copied, dt_ready, dt_read,
         w_ready, rest_ready, ln_ready, delta_ready, du_ready, bc_stored, dA_ready, g_ready, scanned, hc_ready, summed, y_ready, yz_ready,
         out_ready, cat_ready, proj_ready, proj_read, stored, chain_dve, chain_act) = (sem(n) for n in names)
        b_loaded, c_loaded = ([sem(f"{n}_loaded{i}") for i in range(2)] for n in "bc")
        block = sem.block()
        LOADS = 16 * (10 + (3 if post else 0))

        def time(ap):
            return ap[:, ::-1] if flipped else ap

        @block.sync
        def _(sp):
            for dst, src in ((in_w, w["in_w"]), (xproj_w, w["xproj_w"]), (out_w, w["out_w"]), (proj, proj_dram),
                             (cw, w["conv_w"]), (alog, w["Alog"])):
                sp.dma_start(dst[:, :, :], src.rearrange("(k p) n -> p k n", p=P)).then_inc(loaded, 16)
            sp.dma_start(dt_w[:, :], w["dt_w"]).then_inc(loaded, 16)
            with nc.allow_non_contiguous_dma(reason="short vectors"):
                for i, n in enumerate(("conv_b", "dt_b", "Dp")):
                    sp.dma_start(vec[:, i, :], w[n].rearrange("(k p) -> p k", p=P)).then_inc(loaded, 16)
            if post:
                for i, v in enumerate(post):
                    sp.dma_start(rows[:, i, :], row_of(v).broadcast_to([P, DIM])).then_inc(loaded, 16)

            def store_bc(b):
                sp.wait_ge(xd_copied, b + 1)
                for i in range(2):
                    sp.dma_start(bc_dram[b % 2, i], xd[32 * (i + 1):32 * (i + 1) + N, :]).then_inc(bc_stored, 16)

            def row(b):
                sp.wait_ge(bc_stored, 32 * b + 32)
                for q in range(N // Q):
                    wait_from(sp, g_ready, STEPS * b + CI * (q - 1))
                    sp.dma_start(Bs[:, q % 2, :, :], bc_dram[b % 2, 0, Q * q:Q * q + Q, :].rearrange("(a n) t -> a (n t)", a=1)
                                 .broadcast_to([P, Q * SEQ])).then_inc(b_loaded[q % 2], 16)
                    wait_from(sp, hc_ready, STEPS * b + CI * (q - 1))
                    sp.dma_start(Cs[:, q % 2, :, :], bc_dram[b % 2, 1, Q * q:Q * q + Q, :].rearrange("(a n) t -> a (n t)", a=1)
                                 .broadcast_to([P, Q * SEQ])).then_inc(c_loaded[q % 2], 16)
                    if q == 5 and b + 1 < BATCH:
                        store_bc(b + 1)
                    if q == 2 and b > 0:
                        share(b - 1)

            def share(b):
                if post:
                    sp.dma_start(y[:, :, :], part_dram[:, TPB * b:TPB * (b + 1), :]).then_inc(stored, 16)
                elif b > 0:
                    store(b - 1)

            def store(b):
                sp.wait_ge(proj_read, b + 1)
                sp.dma_start(part_dram[:, TPB * b:TPB * (b + 1), :], y[:, :, :]).then_inc(stored, 16)

            store_bc(0)
            for b in range(BATCH):
                row(b)
            sp.wait_ge(scanned, STEPS * BATCH)
            share(BATCH - 1)
            if not post:
                store(BATCH - 1)
            sp.wait_ge(stored, 16 * BATCH)

        @block.tensor
        def _(pe):
            pe.wait_ge(loaded, LOADS)

            def turn_input(b):
                pe.wait_ge(xn_ready, b + 1)
                wait_from(pe, proj_read, b - 2)
                transposes(pe, core, xn, pt, turned)

            def inner(b, p, c):
                if c == 0:
                    pe.wait_ge(xT_ready, b + 1)
                    wait_from(pe, z_read, CI * b)
                elif 2 <= c < CI + 2:
                    pe.wait_ge(conv_ready, CI * b + c - 1)
                elif c >= CI + 2:
                    pe.wait_ge(dt_read, CI * b + CI)
                for k in range(KC):
                    last = pe.matmul(pw[:, c % 2, :], in_w[:, k, c * P:(c + 1) * P], xT[:, p, k, :], start=k == 0, stop=k == KC - 1)
                last.then_inc(xi_ready if c < CI else z_ready, 1)

            def xproj(b, p, c):
                pe.wait_ge(u_ready, b + 1)
                if c == 0:
                    pe.wait_ge(z_read, CI * b + 1)
                last = pe.matmul(pw[0:XD, 0, :], xproj_w[:, c, :], u[:, p, c, :], start=c == 0, stop=c == CI - 1)
                if c == CI - 1:
                    last.then_inc(xd_ready, 1)

            def dt(b, c):
                pe.wait_ge(xd_copied, b + 1)
                if c == 0:
                    pe.wait_ge(z_read, CI * b + 2)
                elif c >= 2:
                    pe.wait_ge(dt_read, CI * b + c - 1)
                pe.matmul(pw[:, (c + 1) % 2, :], dt_w[:, c * P:(c + 1) * P], xd[0:R, :], start=True, stop=True).then_inc(dt_ready, 1)

            def project_out(b, c, last):
                pe.wait_ge(yz_ready, CI * b + c + 1)
                if c == 0:
                    pe.wait_ge(xT_ready, b + 3 if not last else BATCH)
                for m in range(KC):
                    last = pe.matmul(pt[:, m, :], out_w[:, c, m * P:(m + 1) * P], yz[:, c, :], start=c == 0, stop=c == CI - 1)
                if c == CI - 1:
                    last.then_inc(out_ready, 1)

            def project(b, j):
                if j == 0:
                    pe.wait_ge(cat_ready, b + 1)
                for k in range(KC):
                    done = pe.matmul(pt[:, j // 2, j % 2 * DIM:(j % 2 + 1) * DIM], cat[:, k, j * P:(j + 1) * P], proj[:, k, :],
                                     start=k == 0, stop=k == KC - 1)
                if j == TPB - 1:
                    done.then_inc(proj_ready, 1)

            def head(b, p, s):
                if s == PE_AT["turn"]:
                    turn_input(b)
                if s in PE_AT["xi"]:
                    inner(b, p, PE_AT["xi"].index(s))
                at = s - PE_AT["xproj"]
                if 0 <= at < CI // 2:
                    xproj(b, p, 2 * at)
                    xproj(b, p, 2 * at + 1)
                at = s - PE_AT["dt"]
                if 0 <= at < CI // 2:
                    dt(b, 2 * at)
                    dt(b, 2 * at + 1)

            def tail(b, s, last=False):
                if s in PE_AT["out"]:
                    project_out(b, PE_AT["out"].index(s), last)
                if s in PE_AT["proj"]:
                    project(b, PE_AT["proj"].index(s))

            def row(b, p, first=False, last=False, more=True):
                for s in range(STEPS):
                    q, c = s // CI, s % CI
                    pe.wait_ge(hc_ready, STEPS * b + s + 1)
                    if q == 0:
                        wait_from(pe, y_ready, CI * (b - 1) + c + 1)
                    for i in range(Q):
                        done = pe.matmul(py[:, c, :], core.ident[:, :], G[:, s % REUSE, i, :],
                                         start=q == 0 and i == 0, stop=q == N // Q - 1 and i == Q - 1)
                    done.then_inc(summed, 1)
                    if not last:
                        head(b + 1, 1 - p, s)
                    if not first:
                        tail(b - 1, s, last)

            for s in range(STEPS):
                head(0, 0, s)
            rows_in_pairs(pe, row)
            for s in range(STEPS):
                tail(BATCH - 1, s, True)

        @block.scalar
        def _(act):
            chain = Chain(act, chain_act)
            act.wait_ge(loaded, LOADS)
            chain.link(act.activation(A[:, :, :], alog[:, :, :], ACT.Exp))
            chain.link(act.activation(A[:, :, :], A[:, :, :], ACT.Copy, scale=-1.0))
            act.wait_ge(consts, 1)
            chain.restart()

            def head(b, p, s):
                if s == ACT_AT["xT"]:
                    act.wait_ge(turned, b + 1)
                    wait_from(act, x_ready, b - 1)
                    for k in range(KC):
                        last = act.activation(time(xT[:, p, k, :]), pt[:, k, :], ACT.Copy)
                    last.then_inc(xT_ready, 1)
                if s == ACT_AT["silu"]:
                    act.wait_ge(conv_ready, CI * b + CI)
                    act.activation(u[:, p, :, :], u[:, p, :, :], ACT.Silu).then_inc(u_ready, 1)
                if s in ACT_AT["z"]:
                    c = ACT_AT["z"].index(s)
                    act.wait_ge(z_ready, CI * b + c + 1)
                    wait_from(act, yz_ready, CI * (b - 1))
                    act.activation(sz[:, p, c, :], pw[:, c % 2, :], ACT.Copy).then_inc(z_read, 1)
                if s == ACT_AT["silu_z"]:
                    act.wait_ge(z_read, CI * b + CI)
                    act.activation(sz[:, p, :, :], sz[:, p, :, :], ACT.Silu).then_inc(sz_ready, 1)
                if s == ACT_AT["xd"]:
                    act.wait_ge(xd_ready, b + 1)
                    wait_from(act, bc_stored, 32 * b)
                    act.activation(xd[:, :], pw[0:XD, 0, :], ACT.Copy).then_inc(xd_copied, 1)
                at = s - ACT_AT["dt"]
                if 0 <= at < CI // 2:
                    wait_from(act, g_ready, STEPS * (b - 1))
                    for c in (2 * at, 2 * at + 1):
                        act.wait_ge(dt_ready, CI * b + c + 1)
                        act.activation(du[:, p, c, :], pw[:, (c + 1) % 2, :], ACT.Identity, bias=vec[:, 1, c:c + 1]).then_inc(dt_read, 1)
                if s == ACT_AT["abs"]:
                    act.wait_ge(dt_read, CI * b + CI)
                    wait_from(act, delta_ready, b)
                    chain.mark(act.activation(e[:, :, :], du[:, p, :, :], ACT.Abs))
                if s == ACT_AT["exp"]:
                    chain.wait()
                    chain.mark(act.activation(e[:, :, :], e[:, :, :], ACT.Exp, scale=-1.0))
                if s == ACT_AT["w"]:
                    chain.wait()
                    act.activation(delta[:, p, :, :], e[:, :, :], ACT.Identity, bias=1.0).then_inc(w_ready, 1)
                if s == ACT_AT["ln"]:
                    act.wait_ge(rest_ready, b + 1)
                    act.activation(delta[:, p, :, :], delta[:, p, :, :], ACT.Ln).then_inc(ln_ready, 1)

            def tail(b, p, last_row=False):
                if not last_row:
                    act.wait_ge(turned, b + 3)
                else:
                    act.wait_ge(proj_ready, b)
                for k in range(KC):
                    last = act.activation(cat[:, k, :], time(xT[:, p, k, :]), ACT.Copy)
                last.then_inc(x_ready, 1)

            def row(b, p, first=False, last=False, more=True):
                for s in range(STEPS):
                    q, c = s // CI, s % CI
                    if s == 0:
                        act.wait_ge(delta_ready, b + 1)
                    wait_from(act, scanned, STEPS * b + s - 1)
                    for i in range(Q):
                        done = act.activation(dA[:, s % 2, i, 1:], delta[:, p, c, 1:], ACT.Exp, scale=A[:, c, Q * q + i:Q * q + i + 1])
                    done.then_inc(dA_ready, 1)
                    if s == ACT_AT["cat"] and not first:
                        tail(b - 1, 1 - p, last)
                    if not last:
                        head(b + 1, 1 - p, s)
                chain.restart()

            for s in range(STEPS):
                head(0, 0, s)
            chain.restart()
            rows_in_pairs(act, row)
            tail(BATCH - 1, (BATCH - 1) % 2, True)

        @block.gpsimd
        def _(pool):
            pool.memset(dA[:, :, :, 0:1], 0.0).then_inc(consts, 1)

            def head(b, p, c):
                pool.wait_ge(delta_ready, b + 1)
                pool.wait_ge(u_ready, b + 1)
                pool.tensor_tensor(du[:, p, c, :], delta[:, p, c, :], u[:, p, c, :], ALU.mult).then_inc(du_ready, 1)

            def tail(b, p, c):
                pool.wait_ge(sz_ready, b + 1)
                pool.wait_ge(y_ready, CI * b + c + 1)
                pool.tensor_tensor(yz[:, c, :], yz[:, c, :], sz[:, p, c, :], ALU.mult).then_inc(yz_ready, 1)

            def row(b, p, first=False, last=False, more=True):
                for s in range(STEPS):
                    q, c = s // CI, s % CI
                    if s >= POOL_AT["du"] and not last:
                        head(b + 1, 1 - p, s - POOL_AT["du"])
                    pool.wait_ge(scanned, STEPS * b + s + 1)
                    if c == 0:
                        pool.wait_ge(c_loaded[q % 2], 16 * (N // Q // 2) * b + 16 * (q // 2 + 1))
                    pool.tensor_tensor(G[:, s % REUSE, :, :], G[:, s % REUSE, :, :], Cs[:, q % 2, :, :], ALU.mult).then_inc(hc_ready, 1)
                    if not first and s in POOL_AT["yz"]:
                        tail(b - 1, 1 - p, POOL_AT["yz"].index(s))
                for c in range(STEPS - POOL_AT["du"], CI):
                    if not last:
                        head(b + 1, 1 - p, c)

            for c in range(CI):
                head(0, 0, c)
            rows_in_pairs(pool, row)
            for c in range(CI):
                tail(BATCH - 1, (BATCH - 1) % 2, c)

        @block.vector
        def _(dve):
            chain = Chain(dve, chain_dve)
            dve.wait_ge(loaded, LOADS)

            def convolve(b, p, c):
                dve.wait_ge(xi_ready, CI * b + c + 1)
                src, dst = pw[:, c % 2, :], u[:, p, c, :]
                chain.link(dve.tensor_scalar(dst, src, cw[:, c, K - 1:K], vec[:, 0, c:c + 1], ALU.mult, ALU.add))
                for back_by in range(1, K):
                    ins = dve.scalar_tensor_tensor(out=dst[:, back_by:], in0=src[:, 0:SEQ - back_by],
                                                   scalar=cw[:, c, K - 1 - back_by:K - back_by], in1=dst[:, back_by:],
                                                   op0=ALU.mult, op1=ALU.add)
                    if back_by < K - 1:
                        chain.link(ins)
                    else:
                        ins.then_inc(conv_ready, 1)

            def head(b, p, s):
                if s in DVE_AT["conv"]:
                    convolve(b, p, DVE_AT["conv"].index(s))
                if s == DVE_AT["rest"]:
                    dve.wait_ge(w_ready, b + 1)
                    dve.scalar_tensor_tensor(out=e[:, :, :], in0=delta[:, p, :, :], scalar=1.0, in1=e[:, :, :],
                                             op0=ALU.subtract, op1=ALU.subtract).then_inc(rest_ready, 1)
                if s == DVE_AT["delta"]:
                    dve.wait_ge(ln_ready, b + 1)
                    chain.link(dve.tensor_tensor(delta[:, p, :, :], delta[:, p, :, :], e[:, :, :], ALU.subtract))
                    dve.scalar_tensor_tensor(out=delta[:, p, :, :], in0=du[:, p, :, :], scalar=0.0, in1=delta[:, p, :, :],
                                             op0=ALU.max, op1=ALU.add).then_inc(delta_ready, 1)

            def normalise(b):
                wait_from(dve, turned, b)
                wait_from(dve, proj_ready, b - 2)
                front(dve, chain, core, b, xn, xn_ready)

            def wide(i):
                return rows[:, i, :].unsqueeze(1).broadcast_to([P, TPB, DIM])

            def inner_norm(stage):
                chain.wait()
                if stage < NORM_STAGES - 1:
                    norm_stage(dve, chain, core, [y[:, j, :] for j in range(TPB)], stage)
                    return
                for j in range(TPB):
                    chain.mark(dve.tensor_scalar(y[:, j, :], y[:, j, :], core.mv[:, j, 0:1], core.rs[:, 0, j:j + 1],
                                                 ALU.subtract, ALU.mult))
                chain.wait()
                chain.link(dve.tensor_tensor(y[:, :, :], y[:, :, :], wide(1), ALU.mult))
                chain.link(dve.tensor_tensor(y[:, :, :], y[:, :, :], wide(2), ALU.add))

            def tail(b, p, s):
                c = s - DVE_AT["y"]
                if 0 <= c < CI:
                    dve.wait_ge(summed, STEPS * b + STEPS - CI + c + 1)
                    wait_from(dve, out_ready, b)
                    dve.scalar_tensor_tensor(out=yz[:, c, :], in0=u[:, p, c, :], scalar=vec[:, 2, c:c + 1], in1=py[:, c, :],
                                             op0=ALU.mult, op1=ALU.add).then_inc(y_ready, 1)
                if s == DVE_AT["cat"]:
                    dve.wait_ge(out_ready, b + 1)
                    dve.wait_ge(x_ready, b + 1)
                    for k in range(KC):
                        ins = dve.tensor_tensor(time(cat[:, k, :]), pt[:, k, :], time(cat[:, k, :]), ALU.add)
                        if k == KC - 1:
                            ins.then_inc(cat_ready, 1)
                if s == DVE_AT["end"]:
                    dve.wait_ge(proj_ready, b + 1)
                    pp = pt[:, :, :].rearrange("p a (j n) -> p (a j) n", n=DIM)
                    if not post:
                        wait_from(dve, stored, 16 * b)
                        dve.tensor_copy(y[:, :, :], pp).then_inc(proj_read, 1)
                        return
                    dve.wait_ge(stored, 16 * b + 16)
                    dve.tensor_tensor(y[:, :, :], pp, y[:, :, :], ALU.add).then_inc(proj_read, 1)
                    dve.wait_ge(proj_read, b + 1)
                    chain.mark(dve.tensor_tensor(y[:, :, :], y[:, :, :], wide(0), ALU.add))
                if post and DVE_AT["end"] < s <= DVE_AT["end"] + NORM_STAGES:
                    for stage in (2 * (s - DVE_AT["end"] - 1), 2 * (s - DVE_AT["end"] - 1) + 1):
                        if stage < NORM_STAGES:
                            inner_norm(stage)
                        else:
                            back_stage(dve, chain, core, b, y, stage - NORM_STAGES)

            def scan(b, s):
                dve.wait_ge(g_ready, STEPS * b + s + 1)
                dve.wait_ge(dA_ready, STEPS * b + s + 1)
                g = G[:, s % REUSE, :, :].rearrange("p n t -> p (n t)")
                dve.tensor_tensor_scan(g, dA[:, s % 2, :, :].rearrange("p n t -> p (n t)"), g, 0.0, ALU.mult, ALU.add
                                       ).then_inc(scanned, 1)

            def row(b, p, first=False, last=False, more=True):
                for s in range(STEPS):
                    q, c = s // CI, s % CI
                    if q == 0:
                        dve.wait_ge(du_ready, CI * b + c + 1)
                    if c == 0:
                        dve.wait_ge(b_loaded[q % 2], 16 * (N // Q // 2) * b + 16 * (q // 2 + 1))
                    wait_from(dve, summed, STEPS * b + s - REUSE + 1)
                    dve.tensor_tensor(G[:, s % REUSE, :, :], Bs[:, q % 2, :, :], du[:, p, c, :].unsqueeze(1).broadcast_to([P, Q, SEQ]),
                                      ALU.mult).then_inc(g_ready, 1)
                    if s > 0:
                        scan(b, s - 1)
                    elif not first:
                        scan(b - 1, STEPS - 1)
                    if not first:
                        tail(b - 1, 1 - p, s)
                    if not last:
                        head(b + 1, 1 - p, s)
                    if s == DVE_AT["front"] and more:
                        normalise(b + 2)
                chain.restart()

            normalise(0)
            for s in range(STEPS):
                head(0, 0, s)
            normalise(1)
            chain.restart()
            rows_in_pairs(dve, row)
            scan(BATCH - 1, STEPS - 1)
            for s in range(STEPS):
                tail(BATCH - 1, (BATCH - 1) % 2, s)
            chain.wait()


def rows_in_pairs(eng, row):
    row(0, 0, first=True)
    with eng.Fori(0, (BATCH - 4) // 2) as pair:
        row(pair * 2 + 1, 1)
        row(pair * 2 + 2, 0)
    row(BATCH - 3, 1)
    row(BATCH - 2, 0, more=False)
    row(BATCH - 1, 1, last=True, more=False)


def mamba_layer(core, fw, bw, proj_w, proj_b, ln_w, ln_b):
    nc = core.nc
    SCAN_N = fw["Alog"].shape[1]
    bc = nc.dram_tensor("b_and_c", (2, 2, 2, SCAN_N, SEQ), F32, kind="Internal").ap()
    part = nc.dram_tensor("part", (P, NT, DIM), F32, kind="Internal").ap()
    mamba_direction(core, "fw", False, bc[0], part, fw, proj_w[0:DIM, :])
    mamba_direction(core, "bw", True, bc[1], part, bw, proj_w[DIM:2 * DIM, :], (proj_b, ln_w, ln_b))


def expert_mlp_layer(core, router_dram, w1_dram, w2_dram):
    nc = core.nc
    E, _, H = w1_dram.shape
    HC = H // P
    UP = E * HC
    name = "moe1"
    with ExitStack() as ctx:
        sb = lambda n, shape, dt=F32: ctx.enter_context(nc.sbuf_tensor(f"{name}_{n}", shape, dt))
        ps = lambda n, shape: ctx.enter_context(nc.psum_tensor(f"{name}_{n}", shape, F32))
        sem = Signals(nc, ctx, name)
        xn = sb("xn", [P, TPB, DIM])
        xT = sb("xT", [P, KC, SEQ])
        wr = sb("wr", [P, KC, E])
        w1 = sb("w1", [P, E, KC, H])
        w2 = sb("w2", [P, E, HC, DIM])
        logit = sb("logit", [P, TPB, E])
        best = sb("best", [P, TPB, 8])
        at = sb("at", [P, TPB, 8], U32)
        atf = sb("atf", [P, TPB, 8])
        gap = sb("gap", [P, 4, TPB])
        share = sb("share", [P, 2, TPB])
        number = sb("number", [P, E])
        gate = sb("gate", [P, 2, TPB, E])
        hT = sb("hT", [P, 2, HC, SEQ])
        acc = sb("acc", [P, TPB, DIM])
        pt = ps("pt", [P, KC, SEQ])
        ph = ps("ph", [P, 2, SEQ])
        py = ps("py", [P, 2, TPB, DIM])
        loaded, consts = sem("loaded"), sem("consts")
        w_loaded = [sem(f"w_loaded{e}") for e in range(2)]
        xn_ready, turned, xT_ready = sem("xn_ready"), sem("turned"), sem("xT_ready")
        logits_ready, gap_ready, exps_ready = sem("logits_ready"), sem("gap_ready"), sem("exps_ready")
        up_ready, h_ready, y_ready, y_read, chain_dve = sem("up_ready"), sem("h_ready"), sem("y_ready"), sem("y_read"), sem("chain_dve")
        block = sem.block()

        @block.sync
        def _(sp):
            sp.dma_start(wr[:, :, :], router_dram.rearrange("(k p) n -> p k n", p=P)).then_inc(loaded, 16)
            for i in range(2):
                part = slice(i * E // 2, (i + 1) * E // 2)
                for k in range(KC):
                    sp.dma_start(w1[:, part, k, :], w1_dram[part, k * P:(k + 1) * P, :].rearrange("e p h -> p e h")).then_inc(w_loaded[i], 16)
                for c in range(HC):
                    sp.dma_start(w2[:, part, c, :], w2_dram[part, c * P:(c + 1) * P, :].rearrange("e p h -> p e h")).then_inc(w_loaded[i], 16)

        @block.gpsimd
        def _(pool):
            pool.iota(number[:, :], pattern=[[1, E]], base=0, channel_multiplier=0,
                      allow_small_or_imprecise_dtypes=True).then_inc(consts, 1)

        @block.tensor
        def _(pe):
            pe.wait_ge(loaded, 16)

            def row(b, first=False):
                def up(e):
                    for c in range(HC):
                        n = UP * b + HC * e + c
                        wait_from(pe, h_ready, n - 1)
                        for k in range(KC):
                            last = pe.matmul(ph[:, c % 2, :], w1[:, e, k, c * P:(c + 1) * P], xT[:, k, :],
                                             start=k == 0, stop=k == KC - 1)
                        last.then_inc(up_ready, 1)

                def down(e):
                    pe.wait_ge(h_ready, UP * b + HC * (e + 1))
                    wait_from(pe, y_read, E * b + e - 1)
                    for j in range(TPB):
                        for c in range(HC):
                            last = pe.matmul(py[:, e % 2, j, :], hT[:, e % 2, c, j * P:(j + 1) * P], w2[:, e, c, :],
                                             start=c == 0, stop=c == HC - 1)
                    last.then_inc(y_ready, 1)

                pe.wait_ge(xn_ready, b + 1)
                wait_from(pe, gap_ready, b)
                transposes(pe, core, xn, pt, turned)
                pe.wait_ge(xT_ready, b + 1)
                for j in range(TPB):
                    for k in range(KC):
                        last = pe.matmul(pt[:, 0, j * E:(j + 1) * E], xT[:, k, j * P:(j + 1) * P], wr[:, k, :],
                                         start=k == 0, stop=k == KC - 1)
                last.then_inc(logits_ready, 1)
                if first:
                    pe.wait_ge(w_loaded[0], 16 * (KC + HC))
                up(0)
                for e in range(1, E):
                    if first and e == E // 2:
                        pe.wait_ge(w_loaded[1], 16 * (KC + HC))
                    up(e)
                    down(e - 1)
                down(E - 1)

            row(0, True)
            with pe.Fori(1, BATCH) as b:
                row(b)

        @block.scalar
        def _(act):
            def row(b):
                act.wait_ge(turned, b + 1)
                wait_from(act, y_ready, E * b)
                act.activation(xT[:, :, :], pt[:, :, :], ACT.Copy).then_inc(xT_ready, 1)
                act.wait_ge(gap_ready, b + 1)
                act.activation(gap[:, 1, :], gap[:, 0, :], ACT.Exp).then_inc(exps_ready, 1)
                for e in range(E):
                    wait_from(act, y_ready, E * b + e - 1)
                    for c in range(HC):
                        act.wait_ge(up_ready, UP * b + HC * e + c + 1)
                        act.activation(hT[:, e % 2, c, :], ph[:, c % 2, :], ACT.Gelu).then_inc(h_ready, 1)

            row(0)
            with act.Fori(1, BATCH) as b:
                row(b)

        @block.vector
        def _(dve):
            chain = Chain(dve, chain_dve)
            dve.wait_ge(consts, 1)
            front(dve, chain, core, 0, xn, xn_ready)
            chain.restart()

            def weigh(b):
                dve.wait_ge(logits_ready, b + 1)
                chain.link(dve.tensor_copy(logit[:, :, :], pt[:, 0, 0:TPB * E].rearrange("p (j e) -> p j e", e=E)))
                for j in range(TPB):
                    chain.mark(dve.max(best[:, j, :], logit[:, j, :]))
                chain.wait()
                dve.tensor_tensor(gap[:, 0, :], best[:, :, 1], best[:, :, 0], ALU.subtract).then_inc(gap_ready, 1)
                for j in range(TPB):
                    chain.mark(dve.max_index(at[:, j, :], best[:, j, :], logit[:, j, :]))
                chain.wait()
                chain.mark(dve.tensor_copy(atf[:, :, 0:2], at[:, :, 0:2]))
                dve.wait_ge(exps_ready, b + 1)
                chain.link(dve.tensor_scalar(gap[:, 2, :], gap[:, 1, :], 1.0, None, ALU.add))
                chain.link(dve.reciprocal(share[:, 0, :], gap[:, 2, :]))
                chain.link(dve.tensor_tensor(share[:, 1, :], gap[:, 1, :], share[:, 0, :], ALU.mult))
                for i in range(2):
                    for j in range(TPB):
                        chain.mark(dve.tensor_scalar(gate[:, i, j, :], number[:, :], atf[:, j, i:i + 1], share[:, i, j:j + 1],
                                                     ALU.is_equal, ALU.mult))
                chain.wait()
                chain.link(dve.tensor_tensor(gate[:, 0, :, :], gate[:, 0, :, :], gate[:, 1, :, :], ALU.add))

            def row(b, last):
                weigh(b)
                for e in range(E):
                    dve.wait_ge(y_ready, E * b + e + 1)
                    for j in range(TPB):
                        g = gate[:, 0, j, e:e + 1]
                        if e == 0:
                            ins = dve.tensor_scalar(acc[:, j, :], py[:, 0, j, :], g, None, ALU.mult)
                        else:
                            ins = dve.scalar_tensor_tensor(out=acc[:, j, :], in0=py[:, e % 2, j, :], scalar=g, in1=acc[:, j, :],
                                                           op0=ALU.mult, op1=ALU.add)
                    ins.then_inc(y_read, 1)
                    dve.wait_ge(y_read, E * b + e + 1)
                    if e == E // 2 and not last:
                        dve.wait_ge(turned, b + 1)
                        front(dve, chain, core, b + 1, xn, xn_ready)
                back(dve, chain, core, b, acc)
                chain.restart()

            row(0, False)
            with dve.Fori(1, BATCH - 1) as b:
                row(b, False)
            row(BATCH - 1, True)


def bucket_attention_layer(core, hash_dram, wq_dram, bq_dram, wv_dram, bv_dram, wo_dram, bo_dram, limits_dram):
    nc = core.nc
    name = "lsh"
    HEADS, HD = 8, 32
    SPAN = P // HEADS
    BIG = 1e30
    SCALE = float(np.float32(1.0) / np.sqrt(HD).astype(np.float32))
    UNITS = HEADS * TPB
    SIDES = (((0, 0, 1, 1), (0, 1, 0, 1)), ((0, 2, 1, 2), (2, 0, 2, 1)))
    ROUNDS = (("o", 0), ("o", 1), ("y", 0), ("y", 1), ("q", 0), ("q", 1), ("v", 0), ("v", 1),
              ("x", 0), ("x", 1), ("hash", 0), ("angle", 0))
    SLOT_OF_ROUND = (4, 6, 8, 9, 11, 13, 15, 17, 25, 26, 27, 29)
    AT_BACK, AT_FRONT, AT_HOT = 11, 18, UNITS - 1

    def compared_by(slot):
        return min(UNITS, slot + min(slot, 2))

    def round_number(b, r, first=False):
        n_y, n_v, n = 4, 8, len(ROUNDS)
        ahead = (n - n_y) + (n - n_v)
        if first:
            return ahead + r - n_y
        start = ahead + (n - n_y) + n * (b - 1)
        if isinstance(b, int) and b == BATCH - 1:
            start -= n - n_v
        if isinstance(b, int) and b == BATCH:
            start -= 2 * (n - n_v) + (n_v - n_y)
        return start + r

    def rounds_in(slot, b, p, first, last, more, tail):
        if slot not in SLOT_OF_ROUND:
            return []
        r = SLOT_OF_ROUND.index(slot)
        kind, part = ROUNDS[r]
        if kind in ("o", "y"):
            return [] if first else [(r, kind, part, b - 1, 1 - p)]
        if kind in ("q", "v"):
            return [] if last or tail else [(r, kind, part, b + 1, 1 - p)]
        return [(r, kind, part, b + 2, p)] if more and not tail else []

    def q_round(b, part):
        return 4 + part if b == 0 else round_number(b - 1, ROUNDS.index(("q", part)), b == 1)

    def angle_round(b):
        return (3, 11)[b] if b < 2 else round_number(b - 2, ROUNDS.index(("angle", 0)), b == 2)

    ROUNDS_AHEAD = ([(k, i, 0) for k, i in ROUNDS[8:]] + [(k, i, 0) for k, i in ROUNDS[4:8]] + [(k, i, 1) for k, i in ROUNDS[8:]])

    with ExitStack() as ctx:
        sb = lambda n, shape, dt=F32: ctx.enter_context(nc.sbuf_tensor(f"{name}_{n}", shape, dt))
        ps = lambda n, shape: ctx.enter_context(nc.psum_tensor(f"{name}_{n}", shape, F32))
        wh, wq, wv, wo = sb("wh", [P, KC, 2 * HEADS]), sb("wq", [P, KC, DIM]), sb("wv", [P, KC, DIM]), sb("wo", [P, KC, DIM])
        bq = sb("bq", [P, KC])
        rows = sb("rows", [P, 2, DIM])
        limits = sb("limits", [P, 4])
        xn, xT = sb("xn", [P, TPB, DIM]), sb("xT", [P, 2, KC, SEQ])
        q = sb("q", [P, KC, SEQ])
        rest = sb("rest", [P, SEQ])
        parts = sb("parts", [P, 3, KC, SEQ], BF16)
        stack = sb("stack", [P, 2, 2, HEADS, SEQ], BF16)
        v = sb("v", [P, 2, TPB, DIM])
        below = sb("below", [P, TPB, HEADS])
        angle = sb("angle", [P, 2, TPB, HEADS])
        angleT = sb("angleT", [HEADS, SEQ])
        others = sb("others", [P, HEADS, SEQ])
        later = sb("later", [P, P])
        before = sb("before", [P, 2, SEQ], BF16)
        tied = sb("tied", [P, 2, P], BF16)
        mine = sb("mine", [P, HEADS, P], BF16)
        least = sb("least", [P, SEQ])
        hot = sb("hot", [P, 2, SEQ], BF16)
        cold = sb("cold", [P, 2, 2, SEQ], BF16)
        top = sb("top", [P, 4, 2])
        prob = sb("prob", [P, 4, SEQ])
        probT = sb("probT", [P, 2, TPB, P])
        total, recip = sb("total", [P, 2, TPB, HEADS]), sb("recip", [P, TPB, HEADS])
        o, oT = sb("o", [P, TPB, DIM]), sb("oT", [P, KC, SEQ])
        y = sb("y", [P, TPB, DIM])
        ranks, spare = ps("ranks", [P, SEQ]), ps("spare", [P, SEQ])
        pscore = ps("pscore", [P, 2, SEQ])
        pturn, pout = ps("pturn", [P, 2, TPB, P]), ps("pout", [P, TPB, DIM])
        names = ("loaded consts xn_ready spare_sent spare_taken angles_stored compared counted hot_ready "
                 "high_ready rest_ready mid_ready parts_ready parts_stored early_loaded late_loaded "
                 "score_ready top_ready exp_ready turned_p copied pv_ready o_ready y_ready chain_dve").split()
        sem = Signals(nc, ctx, name)
        s = type("Semaphores", (), {n: sem(n) for n in names})
        others_ready = [sem(f"others_ready{h}") for h in range(HEADS)]
        angle_dram = nc.dram_tensor("lsh_angles", (2, HEADS, SEQ), F32, kind="Internal").ap()
        parts_dram = nc.dram_tensor("lsh_query_parts", (3, HEADS, HD, SEQ), BF16, kind="Internal").ap()
        LOADS = 16 * 8
        CONSTS = 3 + HEADS
        block = sem.block()

        @block.sync
        def _(sp):
            for dst, src in ((wh, hash_dram), (wq, wq_dram), (wv, wv_dram), (wo, wo_dram)):
                sp.dma_start(dst[:, :, :], src.rearrange("(k p) n -> p k n", p=P)).then_inc(s.loaded, 16)
            with nc.allow_non_contiguous_dma(reason="a short vector"):
                sp.dma_start(bq[:, :], bq_dram.rearrange("(k p) -> p k", p=P)).then_inc(s.loaded, 16)
            for i, vec in enumerate((bv_dram, bo_dram)):
                sp.dma_start(rows[:, i, :], row_of(vec).broadcast_to([P, DIM])).then_inc(s.loaded, 16)
            sp.dma_start(limits[:, :], limits_dram).then_inc(s.loaded, 16)

            def queries(b):
                sp.wait_ge(s.parts_ready, KC * (b + 1))
                wait_from(sp, s.late_loaded, 16 * 16 * b)
                for part in range(3):
                    sp.dma_start(parts_dram[part].rearrange("(c h) d t -> (h d) c t", c=KC), parts[:, part, :, :]).then_inc(s.parts_stored, 16)
                sp.wait_ge(s.parts_stored, 48 * (b + 1))

            def stacked(b, half):
                done = s.late_loaded if half else s.early_loaded
                wait_from(sp, s.score_ready, UNITS * b - (0 if half else UNITS // 2))
                heads = slice(half * HEADS // 2, (half + 1) * HEADS // 2)
                for turn in range(2):
                    for side in range(2):
                        for row, part in enumerate(SIDES[turn][side]):
                            sp.dma_start(stack[row * HD:(row + 1) * HD, turn, side, heads, :],
                                         parts_dram[part, heads].rearrange("h d t -> d h t")).then_inc(done, 16)

            def angles(b, heads):
                if 0 in heads:
                    sp.wait_ge(s.spare_taken, angle_round(b) + 1)
                    sp.dma_start(angle_dram[b % 2], angleT[:, :]).then_inc(s.angles_stored, 16)
                    sp.wait_ge(s.angles_stored, 16 * (b + 1))
                for h in heads:
                    wait_from(sp, s.compared, UNITS * (b - 1) + TPB * (h + 1))
                    sp.dma_start(others[:, h, :], angle_dram[b % 2, h:h + 1, :].broadcast_to([P, SEQ])).then_inc(others_ready[h], 16)

            angles(0, range(HEADS))
            queries(0)
            stacked(0, 0)
            stacked(0, 1)
            angles(1, range(HEADS))
            for b in range(BATCH):
                if b + 1 < BATCH:
                    queries(b + 1)
                    stacked(b + 1, 0)
                if b + 2 < BATCH:
                    angles(b + 2, range(HEADS))
                if b + 1 < BATCH:
                    stacked(b + 1, 1)

        @block.gpsimd
        def _(pool):
            pool.memset(later[:, :], 0.0).then_inc(s.consts, 1)
            pool.memset(mine[:, :, :], 0.0).then_inc(s.consts, 1)
            pool.wait_ge(s.consts, 2)
            pool.affine_select(out=later[:, :], in_=later[:, :], compare_op=ALU.is_ge, fill=1.0, base=0,
                               pattern=[[-1, P]], channel_multiplier=1).then_inc(s.consts, 1)
            for h in range(HEADS):
                pool.memset(mine[:, h, h * SPAN:h * SPAN + SEQ // 64], 1.0).then_inc(s.consts, 1)

            for b in range(BATCH):
                for m in range(KC):
                    n = KC * b + m + 1
                    pool.wait_ge(s.spare_taken, q_round(b, m) + 1)
                    wait_from(pool, s.parts_stored, 48 * b)
                    pool.tensor_copy(parts[:, 0, m, :], q[:, m, :]).then_inc(s.high_ready, 1)
                    pool.wait_ge(s.high_ready, n)
                    pool.tensor_tensor(rest[:, :], q[:, m, :], parts[:, 0, m, :], ALU.subtract).then_inc(s.rest_ready, 1)
                    pool.wait_ge(s.rest_ready, n)
                    pool.tensor_copy(parts[:, 1, m, :], rest[:, :]).then_inc(s.mid_ready, 1)
                    pool.wait_ge(s.mid_ready, n)
                    pool.tensor_tensor(parts[:, 2, m, :], rest[:, :], parts[:, 1, m, :], ALU.subtract).then_inc(s.parts_ready, 1)
                    pool.wait_ge(s.parts_ready, n)

        @block.tensor
        def _(pe):
            pe.wait_ge(s.loaded, LOADS)
            pe.wait_ge(s.consts, CONSTS)

            def use_spare(kind, part, b, p, number):
                wait_from(pe, s.spare_taken, number)
                if kind == "x":
                    pe.wait_ge(s.xn_ready, b + 1)
                    for j in range(TPB):
                        last = pe.transpose(spare[:, j * P:(j + 1) * P], xn[:, j, part * P:(part + 1) * P], core.ident[:, :])
                if kind == "hash":
                    for j in range(TPB):
                        for k in range(KC):
                            last = pe.matmul(spare[:, j * 2 * HEADS:(j + 1) * 2 * HEADS], xT[:, p, k, j * P:(j + 1) * P], wh[:, k, :],
                                             start=k == 0, stop=k == KC - 1)
                if kind == "angle":
                    for j in range(TPB):
                        last = pe.transpose(spare[0:HEADS, j * P:(j + 1) * P], angle[:, p, j, :], core.ident[:, :])
                if kind == "q":
                    for k in range(KC):
                        last = pe.matmul(spare[:, :], wq[:, k, part * P:(part + 1) * P], xT[:, p, k, :], start=k == 0, stop=k == KC - 1)
                if kind == "v":
                    for j in range(2):
                        for k in range(KC):
                            at = (2 * part + j) * P
                            last = pe.matmul(spare[:, j * DIM:(j + 1) * DIM], xT[:, p, k, at:at + P], wv[:, k, :],
                                             start=k == 0, stop=k == KC - 1)
                if kind == "o":
                    pe.wait_ge(s.o_ready, 2 * (b + 1))
                    for j in range(TPB):
                        last = pe.transpose(spare[:, j * P:(j + 1) * P], o[:, j, part * P:(part + 1) * P], core.ident[:, :])
                if kind == "y":
                    for j in range(2):
                        for k in range(KC):
                            at = (2 * part + j) * P
                            last = pe.matmul(spare[:, j * DIM:(j + 1) * DIM], oT[:, k, at:at + P], wo[:, k, :],
                                             start=k == 0, stop=k == KC - 1)
                last.then_inc(s.spare_sent, 1)

            def count(b, n):
                h, j = n // TPB, n % TPB
                pe.wait_ge(s.compared, UNITS * b + n + 1)
                if n == 0:
                    wait_from(pe, s.hot_ready, b)
                pe.matmul(ranks[:, :], mine[:, h, :], before[:, n % 2, :], start=n == 0, stop=False, skip_group_check=True)
                pe.matmul(ranks[:, j * P:(j + 1) * P], mine[:, h, :], tied[:, n % 2, :], start=False,
                          stop=n == UNITS - 1, skip_group_check=True).then_inc(s.counted, 1)

            def scores(b, p, n):
                h, i = n // TPB, n % TPB
                group = slice(h // 2 * 2 * SPAN, (h // 2 + 1) * 2 * SPAN)
                if n == 0:
                    pe.wait_ge(s.hot_ready, b + 1)
                    pe.wait_ge(s.early_loaded, 16 * 16 * (b + 1))
                if n == UNITS // 2:
                    pe.wait_ge(s.late_loaded, 16 * 16 * (b + 1))
                wait_from(pe, s.exp_ready, UNITS * b + n - 1)
                own = slice(i * P, (i + 1) * P)
                for turn in range(2):
                    pe.matmul(pscore[:, n % 2, :], stack[:, turn, 0, h, own], stack[:, turn, 1, h, :], start=turn == 0, stop=False)
                pe.matmul(pscore[:, n % 2, :], hot[group, p, own], cold[group, p, h % 2, :], start=False, stop=True).then_inc(s.score_ready, 1)

            def turn(b, n):
                pe.wait_ge(s.exp_ready, UNITS * b + n + 1)
                wait_from(pe, s.copied, UNITS * b + n - 1)
                for j in range(TPB):
                    last = pe.transpose(pturn[:, n % 2, j, :], prob[:, n % 4, j * P:(j + 1) * P], core.ident[:, :])
                last.then_inc(s.turned_p, 1)

            def weigh(b, p, n):
                h, i = n // TPB, n % TPB
                pe.wait_ge(s.copied, UNITS * b + n + 1)
                if n in (0, 2):
                    wait_from(pe, s.o_ready, 2 * (b - 1) + n // 2 + 1)
                for j in range(TPB):
                    last = pe.matmul(pout[:, i, h * HD:(h + 1) * HD], probT[:, n % 2, j, :], v[:, p, j, h * HD:(h + 1) * HD],
                                     start=j == 0, stop=j == TPB - 1)
                last.then_inc(s.pv_ready, 1)

            def row(b, p, first=False, last=False, more=True, tail=False):
                for n in range(UNITS if not tail else SLOT_OF_ROUND[3] + 1):
                    old = lambda lag: (b, p, n - lag) if n >= lag else (b - 1, 1 - p, n - lag + UNITS)
                    if not tail:
                        scores(b, p, n)
                    if (n >= 3 or not first) and not (tail and n >= 3):
                        at, _, unit = old(3)
                        turn(at, unit)
                    if not last and not tail:
                        for unit in range(compared_by(n - 1) if n > 0 else 0, compared_by(n)):
                            count(b + 1, unit)
                    if (n >= 4 or not first) and not (tail and n >= 4):
                        weigh(*old(4))
                    for r, kind, part, served, parity in rounds_in(n, b, p, first, last, more, tail):
                        use_spare(kind, part, served, parity, round_number(b, r, first))

            def ahead():
                for number, (kind, part, b) in enumerate(ROUNDS_AHEAD):
                    use_spare(kind, part, b, b, number)
                for n in range(UNITS):
                    count(0, n)

            ahead()
            rows_in_pairs(pe, row)
            row(BATCH, 0, tail=True)

        @block.scalar
        def _(act):
            act.wait_ge(s.loaded, LOADS)

            def take_spare(kind, part, b, p, number):
                if kind not in ("x", "q", "angle", "o"):
                    return
                act.wait_ge(s.spare_sent, number + 1)
                if kind == "x":
                    act.activation(xT[:, p, part, :], spare[:, :], ACT.Copy).then_inc(s.spare_taken, 1)
                if kind == "q":
                    wait_from(act, s.parts_ready, KC * b)
                    act.activation(q[:, part, :], spare[:, :], ACT.Identity, bias=bq[:, part:part + 1]).then_inc(s.spare_taken, 1)
                if kind == "angle":
                    wait_from(act, s.angles_stored, 16 * b)
                    act.activation(angleT[:, :], spare[0:HEADS, :], ACT.Copy).then_inc(s.spare_taken, 1)
                if kind == "o":
                    act.activation(oT[:, part, :], spare[:, :], ACT.Copy).then_inc(s.spare_taken, 1)

            def exps(b, p, n):
                h, i = n // TPB, n % TPB
                act.wait_ge(s.top_ready, UNITS * b + n + 1)
                wait_from(act, s.turned_p, UNITS * b + n - 3)
                if n == 0:
                    wait_from(act, s.o_ready, 2 * (b - 1))
                act.activation(prob[:, n % 4, :], pscore[:, n % 2, :], ACT.Exp, bias=top[:, n % 4, 1:2], scale=SCALE,
                               accum_out=total[:, p, i, h:h + 1]).then_inc(s.exp_ready, 1)

            def copy_turned(b, n):
                act.wait_ge(s.turned_p, UNITS * b + n + 1)
                wait_from(act, s.pv_ready, UNITS * b + n - 1)
                act.activation(probT[:, n % 2, :, :], pturn[:, n % 2, :, :], ACT.Copy).then_inc(s.copied, 1)

            def row(b, p, first=False, last=False, more=True, tail=False):
                for n in range(UNITS if not tail else SLOT_OF_ROUND[3] + 2):
                    if not tail:
                        exps(b, p, n)
                    if (n >= 3 or not first) and not (tail and n >= 3):
                        copy_turned(*((b, n - 3) if n >= 3 else (b - 1, n - 3 + UNITS)))
                    for r, kind, part, served, parity in rounds_in(n - 1, b, p, first, last, more, tail):
                        take_spare(kind, part, served, parity, round_number(b, r, first))

            for number, (kind, part, b) in enumerate(ROUNDS_AHEAD):
                take_spare(kind, part, b, b, number)
            rows_in_pairs(act, row)
            row(BATCH, 0, tail=True)

        @block.vector
        def _(dve):
            chain = Chain(dve, s.chain_dve)
            dve.wait_ge(s.loaded, LOADS)
            dve.wait_ge(s.consts, CONSTS)
            wide = lambda i: rows[:, i, :].unsqueeze(1).broadcast_to([P, 2, DIM])
            banked = spare[:, :].rearrange("p (j n) -> p j n", j=2)

            def take_spare(kind, part, b, p, number):
                if kind not in ("hash", "v", "y"):
                    return
                dve.wait_ge(s.spare_sent, number + 1)
                if kind == "hash":
                    pairs = spare[:, 0:TPB * 2 * HEADS].rearrange("p (j h two) -> p j h two", h=HEADS, two=2)
                    chain.link(dve.tensor_scalar(below[:, :, :], pairs[:, :, :, 1], 1e-4, None, ALU.add))
                    chain.link(dve.reciprocal(below[:, :, :], below[:, :, :]))
                    dve.tensor_tensor(angle[:, p, :, :], pairs[:, :, :, 0], below[:, :, :], ALU.mult).then_inc(s.spare_taken, 1)
                if kind == "v":
                    dve.tensor_tensor(v[:, p, 2 * part:2 * part + 2, :], banked, wide(0), ALU.add).then_inc(s.spare_taken, 1)
                if kind == "y":
                    dve.tensor_tensor(y[:, 2 * part:2 * part + 2, :], banked, wide(1), ALU.add).then_inc(s.spare_taken, 1)
                    dve.wait_ge(s.spare_taken, number + 1)


            def compare(b, p, n):
                h, j = n // TPB, n % TPB
                own, edge = angle[:, p, j, h:h + 1], (j + 1) * P
                if j == 0:
                    dve.wait_ge(others_ready[h], 16 * (b + 1))
                wait_from(dve, s.counted, UNITS * b + n - 1)
                dve.tensor_scalar(before[:, n % 2, 0:edge], others[:, h, 0:edge], own, None, ALU.is_gt)
                if edge < SEQ:
                    dve.tensor_scalar(before[:, n % 2, edge:], others[:, h, edge:], own, None, ALU.is_ge)
                dve.scalar_tensor_tensor(out=tied[:, n % 2, :], in0=others[:, h, j * P:edge], scalar=own, in1=later[:, :],
                                         op0=ALU.is_equal, op1=ALU.mult).then_inc(s.compared, 1)

            def heat(b, p):
                dve.wait_ge(s.counted, UNITS * (b + 1))
                chain.link(dve.tensor_scalar(least[:, :], ranks[:, :], limits[:, 0:1], None, ALU.is_ge))
                chain.link(dve.scalar_tensor_tensor(out=hot[:, p, :], in0=ranks[:, :], scalar=limits[:, 1:2], in1=least[:, :],
                                                    op0=ALU.is_lt, op1=ALU.mult))
                for side in range(2):
                    last = dve.tensor_scalar(cold[:, p, side, :], hot[:, p, :], 1.0, limits[:, 2 + side:3 + side], ALU.subtract, ALU.mult)
                last.then_inc(s.hot_ready, 1)

            def largest(b, n):
                dve.wait_ge(s.score_ready, UNITS * b + n + 1)
                chain.link(dve.reduce_max(top[:, n % 4, 0:1], pscore[:, n % 2, :], AX.X))
                dve.tensor_scalar(top[:, n % 4, 1:2], top[:, n % 4, 0:1], -SCALE, None, ALU.mult).then_inc(s.top_ready, 1)

            def divide(b, p):
                dve.wait_ge(s.pv_ready, UNITS * (b + 1))
                chain.link(dve.reciprocal(recip[:, :, :], total[:, p, :, :]))
                for bank in range(2):
                    tiles = slice(2 * bank, 2 * bank + 2)
                    by_head = lambda t: t[:, tiles, :].rearrange("p j (h e) -> p j h e", e=HD)
                    dve.tensor_tensor(by_head(o), by_head(pout), recip[:, tiles, :].unsqueeze(3).broadcast_to([P, 2, HEADS, HD]),
                                      ALU.mult).then_inc(s.o_ready, 1)

            def row(b, p, first=False, last=False, more=True, tail=False):
                for n in range(UNITS if not tail else AT_BACK + NORM_STAGES):
                    if not tail:
                        largest(b, n)
                    if n == 4 and not first:
                        divide(b - 1, 1 - p)
                    if not last and not tail:
                        for unit in range(compared_by(n), compared_by(n + 1)):
                            compare(b + 1, 1 - p, unit)
                    for r, kind, part, served, parity in rounds_in(n - 1, b, p, first, last, more, tail):
                        take_spare(kind, part, served, parity, round_number(b, r, first))
                    if AT_BACK <= n < AT_BACK + NORM_STAGES and not first:
                        back_stage(dve, chain, core, b - 1, y, n - AT_BACK)
                    if AT_FRONT <= n < AT_FRONT + NORM_STAGES and more and not tail:
                        front_stage(dve, chain, core, b + 2, xn, s.xn_ready, n - AT_FRONT)
                    if n == AT_HOT and not last and not tail:
                        heat(b + 1, 1 - p)
                chain.restart()

            front(dve, chain, core, 0, xn, s.xn_ready)
            for number, (kind, part, b) in enumerate(ROUNDS_AHEAD):
                take_spare(kind, part, b, b, number)
                if (kind, b) == ("hash", 0):
                    front(dve, chain, core, 1, xn, s.xn_ready)
            for n in range(UNITS):
                compare(0, 0, n)
            heat(0, 0)
            chain.restart()
            rows_in_pairs(dve, row)
            row(BATCH, 0, tail=True)


def decay_attention_layer(core, wqk_dram, wv_dram, wo_dram, decay_dram, log_dist_dram, pick_dram):
    nc = core.nc
    name = "causal"
    HEADS, HD, ROOM = 16, 16, 32
    GROUPS = HEADS * ROOM // P
    SIDES = ((0, 0, 1, 1, 0, 2, 1, 2), (0, 1, 0, 1, 2, 0, 2, 1))
    QKC = 2 * DIM // P
    BIG = 1e30
    UNITS = HEADS * TPB
    AT_Y, AT_TAKE, AT_FRONT, AT_TURN, AT_QK, AT_V = 6, 14, 24, 39, 40, 53
    scale_of = lambda chunk: 0.25 if chunk < DIM // P else 1.0
    with ExitStack() as ctx:
        sb = lambda n, shape, dt=F32: ctx.enter_context(nc.sbuf_tensor(f"{name}_{n}", shape, dt))
        ps = lambda n, shape: ctx.enter_context(nc.psum_tensor(f"{name}_{n}", shape, F32))
        wqk, wv, wo = sb("wqk", [P, KC, 2 * DIM]), sb("wv", [P, KC, DIM]), sb("wo", [P, GROUPS, DIM])
        log_dist = sb("log_dist", [P, SEQ])
        soft = sb("soft", [P, 5, HEADS])
        far = sb("far", [P, HEADS, SEQ])
        pick = sb("pick", [4, P])
        after = sb("after", [P, P])
        after_bf = sb("after_bf", [P, P], BF16)
        xn, xT = sb("xn", [P, TPB, DIM]), sb("xT", [P, KC, SEQ])
        rest = sb("rest", [P, 2, SEQ])
        parts = sb("parts", [P, 3, QKC, SEQ], BF16)
        stack = sb("stack", [P, 2, HEADS, SEQ], BF16)
        v = sb("v", [P, 2, TPB, HEADS, ROOM])
        top = sb("top", [P, 4])
        prob = sb("prob", [P, 4, SEQ])
        probT = sb("probT", [P, 2, TPB, SEQ])
        total = sb("total", [P, 2, TPB, HEADS])
        recipT = sb("recipT", [4, SEQ])
        recip = sb("recip", [P, SEQ])
        oT = sb("oT", [P, GROUPS, SEQ])
        y = sb("y", [P, TPB, DIM])
        pt, pscore = ps("pt", [P, 2, SEQ]), ps("pscore", [P, 2, SEQ])
        pturn, pout = ps("pturn", [P, 2, TPB, P]), ps("pout", [P, 2, SEQ])
        names = ("loaded consts far_ready xn_ready turned xT_ready qk_ready high_ready rest_ready parts_mid parts_ready parts_stored early_loaded "
                 "late_loaded score_ready top_ready exp_ready prob_ready turned_p copied pv_ready sums_ready recipT_sent recipT_ready "
                 "recip_sent recip_ready oT_ready y_ready y_taken v_sent v_ready chain_dve chain_act").split()
        sem = Signals(nc, ctx, name)
        s = type("Semaphores", (), {n: sem(n) for n in names})
        parts_dram = nc.dram_tensor("qk_parts", (3, 2 * HEADS, HD, SEQ), BF16, kind="Internal").ap()
        LOADS = 16 * (5 + HEADS)
        block = sem.block()

        @block.sync
        def _(sp):
            for dst, src in ((wqk, wqk_dram), (wv, wv_dram)):
                sp.dma_start(dst[:, :, :], src.rearrange("(k p) n -> p k n", p=P)).then_inc(s.loaded, 16)
            sp.dma_start(log_dist[:, :], log_dist_dram).then_inc(s.loaded, 16)
            sp.dma_start(soft[:, 0, :], row_of(decay_dram).broadcast_to([P, HEADS])).then_inc(s.loaded, 16)
            sp.dma_start(pick[:, :], pick_dram).then_inc(s.loaded, 16)
            sp.wait_ge(s.consts, 4)
            for h in range(HEADS):
                at = h % 4 * ROOM
                sp.dma_start(wo[at:at + HD, h // 4, :], wo_dram[h * HD:(h + 1) * HD, :]).then_inc(s.loaded, 16)

            for b in range(BATCH):
                sp.wait_ge(s.parts_ready, QKC * (b + 1))
                for part in range(3):
                    sp.dma_start(parts_dram[part].rearrange("(c h) d t -> (h d) c t", c=QKC), parts[:, part, :, :]
                                 ).then_inc(s.parts_stored, 16)
                sp.wait_ge(s.parts_stored, 48 * (b + 1))
                for half, done in enumerate((s.early_loaded, s.late_loaded)):
                    wait_from(sp, s.score_ready, UNITS * b - (UNITS // 2 if half == 0 else 0))
                    heads = slice(half * HEADS // 2, (half + 1) * HEADS // 2)
                    for side in range(2):
                        for row, part in enumerate(SIDES[side]):
                            src = parts_dram[part, side * HEADS:(side + 1) * HEADS][heads]
                            sp.dma_start(stack[row * HD:(row + 1) * HD, side, heads, :], src.rearrange("h d t -> d h t")).then_inc(done, 16)

        @block.gpsimd
        def _(pool):
            pool.memset(after[:, :], 0.0).then_inc(s.consts, 1)
            pool.memset(v[:, :, :, :, :], 0.0).then_inc(s.consts, 1)
            pool.wait_ge(s.consts, 2)
            pool.memset(v[:, :, :, :, HD:HD + 1], 1.0).then_inc(s.consts, 1)
            pool.memset(wo[:, :, :], 0.0).then_inc(s.consts, 1)
            pool.affine_select(out=after[:, :], in_=after[:, :], compare_op=ALU.is_ge, fill=-BIG, base=0,
                               pattern=[[-1, P]], channel_multiplier=1).then_inc(s.consts, 1)
            pool.wait_ge(s.consts, 5)
            pool.tensor_copy(after_bf[:, :], after[:, :]).then_inc(s.consts, 1)

            for b in range(BATCH):
                for c in range(QKC):
                    pool.wait_ge(s.rest_ready, QKC * b + c + 1)
                    wait_from(pool, s.parts_stored, 48 * b)
                    pool.tensor_copy(parts[:, 1, c, :], rest[:, c % 2, :]).then_inc(s.parts_mid, 1)
                    pool.wait_ge(s.parts_mid, QKC * b + c + 1)
                    pool.tensor_tensor(parts[:, 2, c, :], rest[:, c % 2, :], parts[:, 1, c, :], ALU.subtract).then_inc(s.parts_ready, 1)

        @block.tensor
        def _(pe):
            pe.wait_ge(s.loaded, LOADS)
            pe.wait_ge(s.consts, 6)

            def scores(b, n):
                h, i = n // TPB, n % TPB
                width = (i + 1) * P
                if n == 0:
                    pe.wait_ge(s.early_loaded, 16 * 16 * (b + 1))
                if n == UNITS // 2:
                    pe.wait_ge(s.late_loaded, 16 * 16 * (b + 1))
                wait_from(pe, s.exp_ready, UNITS * b + n - 1)
                pe.matmul(pscore[:, n % 2, 0:width], stack[:, 0, h, i * P:width], stack[:, 1, h, 0:width], start=True, stop=True)
                pe.matmul(pscore[:, n % 2, i * P:width], core.ident_bf[:, :], after_bf[:, :], start=False, stop=True,
                          skip_group_check=True).then_inc(s.score_ready, 1)

            def turn(b, n):
                pe.wait_ge(s.prob_ready, UNITS * b + n + 1)
                wait_from(pe, s.copied, UNITS * b + n - 1)
                for j in range(n % TPB + 1):
                    last = pe.transpose(pturn[:, n % 2, j, :], prob[:, n % 4, j * P:(j + 1) * P], core.ident[:, :])
                last.then_inc(s.turned_p, 1)

            def weigh(b, p, h):
                pe.wait_ge(s.copied, UNITS * b + TPB * (h + 1))
                if h == 0:
                    pe.wait_ge(s.v_ready, b + 1)
                g, at = h // 4, h % 4 * ROOM
                if h % 4 == 0:
                    wait_from(pe, s.oT_ready, GROUPS * b + g - 1)
                for j in range(TPB):
                    last = pe.matmul(pout[at:at + ROOM, g % 2, j * P:], v[:, p, j, h, :], probT[:, h % 2, j, j * P:],
                                     start=j == 0, stop=True, skip_group_check=True)
                last.then_inc(s.pv_ready, 1)

            def turn_sums(b, g):
                pe.wait_ge(s.sums_ready, GROUPS * b + g + 1)
                for i in range(TPB):
                    last = pe.transpose(pt[0:4, 0, i * P:(i + 1) * P], total[:, 1, i, 4 * g:4 * g + 4], core.ident[:, :])
                last.then_inc(s.recipT_sent, 1)

            def spread_sums(b, g):
                pe.wait_ge(s.recipT_ready, GROUPS * b + g + 1)
                pe.matmul(pt[:, 1, :], pick[:, :], recipT[:, :], start=True, stop=True).then_inc(s.recip_sent, 1)

            def project_out(b, j, half):
                pe.wait_ge(s.oT_ready, GROUPS * (b + 1))
                for g in range(GROUPS // 2 * half, GROUPS // 2 * (half + 1)):
                    last = pe.matmul(pt[:, j // 2, j % 2 * DIM:(j % 2 + 1) * DIM], oT[:, g, j * P:(j + 1) * P], wo[:, g, :],
                                     start=g == 0, stop=g == GROUPS - 1)
                if j == TPB - 1 and half == 1:
                    last.then_inc(s.y_ready, 1)

            def values(b, j):
                for k in range(KC):
                    last = pe.matmul(pt[:, j // 2, j % 2 * DIM:(j % 2 + 1) * DIM], xT[:, k, j * P:(j + 1) * P], wv[:, k, :],
                                     start=k == 0, stop=k == KC - 1)
                if j == TPB - 1:
                    last.then_inc(s.v_sent, 1)

            def turn_input(b):
                pe.wait_ge(s.xn_ready, b + 1)
                if not isinstance(b, int) or b > 0:
                    pe.wait_ge(s.oT_ready, GROUPS * (b - 1) + 2)
                transposes(pe, core, xn, pt, s.turned)

            def queries_keys(b, c):
                if c == 0:
                    pe.wait_ge(s.xT_ready, b + 1)
                if c >= 2:
                    pe.wait_ge(s.rest_ready, QKC * b + c - 1)
                for k in range(KC):
                    last = pe.matmul(pt[:, c % 2, :], wqk[:, k, c * P:(c + 1) * P], xT[:, k, :], start=k == 0, stop=k == KC - 1)
                last.then_inc(s.qk_ready, 1)

            def slot(b, p, n, first=False, last=False, tail=False):
                old = lambda lag: (b, n - lag) if n >= lag else (b - 1, n - lag + UNITS)
                if not tail:
                    scores(b, n)
                if n >= 3 and not tail or n < 3 and not first:
                    turn(*old(3))
                if n == 2 and not first:
                    turn_sums(b - 1, GROUPS - 1)
                if n == 3 and not first:
                    spread_sums(b - 1, GROUPS - 1)
                if n in (0, 4) and not first:
                    weigh(b - 1, 1 - p, HEADS - 2 + n // 4)
                if AT_Y <= n < AT_Y + 2 * TPB and not first:
                    project_out(b - 1, (n - AT_Y) // 2, (n - AT_Y) % 2)
                if tail:
                    return
                if n >= 8 and n % TPB == 0:
                    weigh(b, p, (n - 8) // TPB)
                if n >= 18 and (n - 18) % 16 == 0:
                    turn_sums(b, (n - 18) // 16)
                if n >= 19 and (n - 19) % 16 == 0:
                    spread_sums(b, (n - 19) // 16)
                if not last and n == AT_TURN:
                    turn_input(b + 1)
                if not last and AT_QK <= n < AT_QK + QKC:
                    queries_keys(b + 1, n - AT_QK)
                if not last and AT_V <= n < AT_V + TPB:
                    values(b + 1, n - AT_V)

            turn_input(0)
            for c in range(QKC):
                queries_keys(0, c)
            pe.wait_ge(s.rest_ready, QKC)
            for j in range(TPB):
                values(0, j)
            def row(b, p, first=False, last=False, more=True):
                for n in range(UNITS):
                    slot(b, p, n, first, last)

            rows_in_pairs(pe, row)
            for n in range(AT_TAKE):
                slot(BATCH, 0, n, tail=True)

        @block.scalar
        def _(act):
            chain = Chain(act, s.chain_act)
            act.wait_ge(s.loaded, LOADS)
            chain.link(act.activation(soft[:, 1, :], soft[:, 0, :], ACT.Abs))
            chain.link(act.activation(soft[:, 2, :], soft[:, 1, :], ACT.Exp, scale=-1.0))
            chain.link(act.activation(soft[:, 3, :], soft[:, 2, :], ACT.Identity, bias=1.0))
            act.activation(soft[:, 4, :], soft[:, 3, :], ACT.Ln).then_inc(s.far_ready, 1)

            def copy_input(b):
                act.wait_ge(s.turned, b + 1)
                wait_from(act, s.v_sent, b)
                act.activation(xT[:, :, :], pt[:, :, :], ACT.Copy).then_inc(s.xT_ready, 1)

            def high_parts(b, c):
                act.wait_ge(s.qk_ready, QKC * b + c + 1)
                wait_from(act, s.parts_stored, 48 * b)
                act.activation(parts[:, 0, c, :], pt[:, c % 2, :], ACT.Copy, scale=scale_of(c)).then_inc(s.high_ready, 1)

            def exps(b, n):
                width = (n % TPB + 1) * P
                act.wait_ge(s.top_ready, UNITS * b + n + 1)
                wait_from(act, s.turned_p, UNITS * b + n - 3)
                act.activation(prob[:, n % 4, 0:width], pscore[:, n % 2, 0:width], ACT.Exp,
                               bias=top[:, n % 4:n % 4 + 1]).then_inc(s.exp_ready, 1)

            def copy_turned(b, n):
                h, i = n // TPB, n % TPB
                act.wait_ge(s.turned_p, UNITS * b + n + 1)
                if i == 0:
                    wait_from(act, s.pv_ready, HEADS * b + h - 1)
                act.activation(probT[:, h % 2, 0:i + 1, i * P:(i + 1) * P], pturn[:, n % 2, 0:i + 1, :], ACT.Copy).then_inc(s.copied, 1)

            def copy_sums(b, g):
                act.wait_ge(s.recipT_sent, GROUPS * b + g + 1)
                act.activation(recipT[:, :], pt[0:4, 0, :], ACT.Copy).then_inc(s.recipT_ready, 1)

            def copy_spread(b, g):
                act.wait_ge(s.recip_sent, GROUPS * b + g + 1)
                wait_from(act, s.oT_ready, GROUPS * b + g)
                act.activation(recip[:, :], pt[:, 1, :], ACT.Copy).then_inc(s.recip_ready, 1)

            def copy_values(b, p):
                act.wait_ge(s.v_sent, b + 1)
                wait_from(act, s.pv_ready, HEADS * (b - 1))
                act.activation(v[:, p, :, :, 0:HD], pt[:, :, :].rearrange("p a (j h e) -> p (a j) h e", j=2, e=HD), ACT.Copy
                               ).then_inc(s.v_ready, 1)

            def slot(b, p, n, first=False, last=False, tail=False):
                old = lambda lag: (b, n - lag) if n >= lag else (b - 1, n - lag + UNITS)
                if not tail:
                    exps(b, n)
                if n >= 3 and not tail or n < 3 and not first:
                    copy_turned(*old(3))
                if n == 2 and not first:
                    copy_sums(b - 1, GROUPS - 1)
                if n == 4 and not first:
                    copy_spread(b - 1, GROUPS - 1)
                if tail:
                    return
                if n >= 18 and (n - 18) % 16 == 0:
                    copy_sums(b, (n - 18) // 16)
                if n >= 20 and (n - 20) % 16 == 0:
                    copy_spread(b, (n - 20) // 16)
                if not last and n == AT_TURN:
                    copy_input(b + 1)
                if not last and AT_QK <= n < AT_QK + QKC:
                    high_parts(b + 1, n - AT_QK)
                if not last and n == AT_V + TPB - 1:
                    copy_values(b + 1, 1 - p)

            copy_input(0)
            for c in range(QKC):
                high_parts(0, c)
            copy_values(0, 0)
            def row(b, p, first=False, last=False, more=True):
                for n in range(UNITS):
                    slot(b, p, n, first, last)

            rows_in_pairs(act, row)
            for n in range(AT_TAKE):
                slot(BATCH, 0, n, tail=True)

        @block.vector
        def _(dve):
            chain = Chain(dve, s.chain_dve)
            front(dve, chain, core, 0, xn, s.xn_ready)
            dve.wait_ge(s.loaded, LOADS)
            dve.wait_ge(s.far_ready, 1)
            chain.link(dve.scalar_tensor_tensor(out=soft[:, 3, :], in0=soft[:, 3, :], scalar=1.0, in1=soft[:, 2, :],
                                                op0=ALU.subtract, op1=ALU.subtract))
            chain.link(dve.tensor_tensor(soft[:, 4, :], soft[:, 4, :], soft[:, 3, :], ALU.subtract))
            chain.link(dve.scalar_tensor_tensor(out=soft[:, 0, :], in0=soft[:, 0, :], scalar=0.0, in1=soft[:, 4, :],
                                                op0=ALU.max, op1=ALU.add))
            for h in range(HEADS):
                chain.mark(dve.tensor_scalar(far[:, h, :], log_dist[:, :], soft[:, 0, h:h + 1], 1.0, ALU.mult, ALU.add))

            def rests(b, c):
                dve.wait_ge(s.high_ready, QKC * b + c + 1)
                wait_from(dve, s.parts_ready, QKC * b + c - 1)
                dve.scalar_tensor_tensor(out=rest[:, c % 2, :], in0=pt[:, c % 2, :], scalar=scale_of(c), in1=parts[:, 0, c, :],
                                         op0=ALU.mult, op1=ALU.subtract).then_inc(s.rest_ready, 1)

            def largest(b, n):
                width = (n % TPB + 1) * P
                dve.wait_ge(s.score_ready, UNITS * b + n + 1)
                dve.reduce_max(top[:, n % 4:n % 4 + 1], pscore[:, n % 2, 0:width], AX.X, negate=True).then_inc(s.top_ready, 1)

            def decayed(b, n):
                h, i = n // TPB, n % TPB
                dve.wait_ge(s.exp_ready, UNITS * b + n + 1)
                part = prob[:, n % 4, 0:(i + 1) * P]
                dve.scalar_tensor_tensor(out=part, in0=part, scalar=1.0, in1=far[:, h, (TPB - 1 - i) * P:],
                                         op0=ALU.mult, op1=ALU.mult, accum_out=total[:, 0, i, h:h + 1]).then_inc(s.prob_ready, 1)

            def invert_sums(b, g):
                dve.wait_ge(s.prob_ready, UNITS * b + 16 * (g + 1))
                dve.reciprocal(total[:, 1, :, 4 * g:4 * g + 4], total[:, 0, :, 4 * g:4 * g + 4]).then_inc(s.sums_ready, 1)

            def normalise(b, g):
                dve.wait_ge(s.recip_ready, GROUPS * b + g + 1)
                dve.wait_ge(s.pv_ready, HEADS * b + 4 * (g + 1))
                if g == 0:
                    wait_from(dve, s.y_ready, b)
                dve.tensor_tensor(oT[:, g, :], pout[:, g % 2, :], recip[:, :], ALU.mult).then_inc(s.oT_ready, 1)

            def take_y(b):
                dve.wait_ge(s.y_ready, b + 1)
                dve.tensor_copy(y[:, :, :], pt[:, :, :].rearrange("p a (j n) -> p (a j) n", j=2)).then_inc(s.y_taken, 1)
                dve.wait_ge(s.y_taken, b + 1)

            def slot(b, p, n, first=False, last=False, tail=False):
                old = lambda lag: (b, n - lag) if n >= lag else (b - 1, n - lag + UNITS)
                if not tail:
                    largest(b, n)
                if n >= 1 and not tail or n < 1 and not first:
                    decayed(*old(1))
                if n == 1 and not first:
                    invert_sums(b - 1, GROUPS - 1)
                if n == 5 and not first:
                    normalise(b - 1, GROUPS - 1)
                if n == AT_TAKE and not first:
                    take_y(b - 1)
                if AT_TAKE < n <= AT_TAKE + NORM_STAGES and not first:
                    back_stage(dve, chain, core, b - 1, y, n - AT_TAKE - 1)
                if tail:
                    return
                if n >= 17 and (n - 17) % 16 == 0:
                    invert_sums(b, (n - 17) // 16)
                if n >= 21 and (n - 21) % 16 == 0:
                    normalise(b, (n - 21) // 16)
                if not last and AT_FRONT <= n < AT_FRONT + NORM_STAGES:
                    front_stage(dve, chain, core, b + 1, xn, s.xn_ready, n - AT_FRONT)
                if not last and AT_QK <= n < AT_QK + QKC:
                    rests(b + 1, n - AT_QK)

            for c in range(QKC):
                rests(0, c)
            chain.wait()
            chain.link(dve.reciprocal(far[:, :, :], far[:, :, :]))
            def row(b, p, first=False, last=False, more=True):
                for n in range(UNITS):
                    slot(b, p, n, first, last)
                chain.restart()

            rows_in_pairs(dve, row)
            for n in range(AT_TAKE + NORM_STAGES + 1):
                slot(BATCH, 0, n, tail=True)
            chain.wait()
def linear_layer(core, name, w_dram, scale_dram, bias_dram, dft=None):
    nc = core.nc
    with ExitStack() as ctx:
        sb = lambda n, shape, dt=F32: ctx.enter_context(nc.sbuf_tensor(f"{name}_{n}", shape, dt))
        sem = Signals(nc, ctx, name)
        xn = sb("xn", [P, TPB, DIM])
        xT = sb("xT", [P, KC, SEQ])
        w = sb("w", [P, KC, DIM])
        bias = sb("bias", [P, DIM])
        scale = sb("scale", [P, DIM])
        y = sb("y", [P, TPB, DIM])
        if dft:
            wf = sb("wf", [P, 2, KC, DIM])
            cs = sb("cs", [P, 3, KC, DIM])
            fw = sb("fw", [P, 2, KC, DIM])
        pt = ctx.enter_context(nc.psum_tensor(f"{name}_pt", [P, KC, SEQ], F32))
        py = ctx.enter_context(nc.psum_tensor(f"{name}_py", [P, TPB, DIM], F32))
        loaded, w_ready, w_acc = sem("loaded"), sem("w_ready"), sem("w_acc")
        xn_ready, turned, xT_ready, y_ready, y_read = (sem(n) for n in ("xn_ready", "turned", "xT_ready", "y_ready", "y_read"))
        _, chain_dve = None, sem("chain_dve")
        loads = 16 * (5 if dft else 3)
        block = sem.block()

        @block.sync
        def _(sp):
            sp.dma_start(bias[:, :], row_of(bias_dram).broadcast_to([P, DIM])).then_inc(loaded, 16)
            if dft:
                for i in range(2):
                    sp.dma_start(wf[:, i, :, :], w_dram[i].rearrange("(k p) n -> p k n", p=P)).then_inc(loaded, 16)
                    sp.dma_start(cs[:, i, :, :], dft[i].rearrange("(k p) n -> p k n", p=P)).then_inc(loaded, 16)
            else:
                sp.dma_start(w[:, :, :], w_dram.rearrange("(k p) n -> p k n", p=P)).then_inc(loaded, 16)
                sp.dma_start(scale[:, :], row_of(scale_dram).broadcast_to([P, DIM])).then_inc(loaded, 16)

        @block.tensor
        def _(pe):
            pe.wait_ge(loaded, loads)
            if dft:
                pe.wait_ge(w_ready, 1)
                for part, terms in enumerate([((0, 0), (1, 1)), ((1, 0), (0, 2))]):
                    for m in range(KC):
                        n = 0
                        for wi, ci in terms:
                            for k in range(KC):
                                last = pe.matmul(pt[:, part, m * DIM:(m + 1) * DIM], wf[:, wi, k, m * P:(m + 1) * P],
                                                 cs[:, ci, k, :], start=n == 0, stop=n == 2 * KC - 1)
                                n += 1
                last.then_inc(w_acc, 1)
                pe.wait_ge(w_ready, 2)
                for m in range(KC):
                    n = 0
                    for part, ci in ((0, 0), (1, 2)):
                        for k in range(KC):
                            last = pe.matmul(py[:, m, :], fw[:, part, k, m * P:(m + 1) * P], cs[:, ci, k, :],
                                             start=n == 0, stop=n == 2 * KC - 1)
                            n += 1
                last.then_inc(w_acc, 1)
                pe.wait_ge(w_ready, 3)

            def row(b):
                pe.wait_ge(xn_ready, b + 1)
                transposes(pe, core, xn, pt, turned)
                pe.wait_ge(xT_ready, b + 1)
                if not (isinstance(b, int) and b == 0):
                    pe.wait_ge(y_read, b)
                for j in range(TPB):
                    for k in range(KC):
                        last = pe.matmul(py[:, j, :], xT[:, k, j * P:(j + 1) * P], w[:, k, :], start=k == 0, stop=k == KC - 1)
                last.then_inc(y_ready, 1)

            row(0)
            with pe.Fori(1, BATCH) as b:
                row(b)

        @block.scalar
        def _(act):
            def copy_xT(b):
                act.wait_ge(turned, b + 1)
                act.activation(xT[:, :, :], pt[:, :, :], ACT.Copy).then_inc(xT_ready, 1)
            copy_xT(0)
            with act.Fori(1, BATCH) as b:
                act.wait_ge(y_ready, b)
                copy_xT(b)

        @block.vector
        def _(dve):
            chain = Chain(dve, chain_dve)
            if dft:
                dve.wait_ge(loaded, loads)
                dve.tensor_scalar(cs[:, 2, :, :], cs[:, 1, :, :], -1.0, None, ALU.mult).then_inc(w_ready, 1)
                dve.wait_ge(w_acc, 1)
                dve.tensor_copy(fw[:, :, :, :], pt[:, :, :].rearrange("p a (m n) -> p a m n", m=KC)).then_inc(w_ready, 1)
                dve.wait_ge(w_acc, 2)
                dve.tensor_scalar(w[:, :, :], py[:, 0:KC, :], 1.0 / DIM, None, ALU.mult).then_inc(w_ready, 1)
            front(dve, chain, core, 0, xn, xn_ready)
            chain.restart()

            def row(b, last):
                if not last:
                    dve.wait_ge(turned, b + 1)
                    front(dve, chain, core, b + 1, xn, xn_ready)
                dve.wait_ge(y_ready, b + 1)
                if not dft:
                    chain.link(dve.scalar_tensor_tensor(out=y[:, :, :], in0=py[:, :, :], scalar=1.0 / 127.0,
                                                        in1=scale[:, :].unsqueeze(1).broadcast_to([P, TPB, DIM]),
                                                        op0=ALU.mult, op1=ALU.mult))
                src = py if dft else y
                dve.tensor_tensor(y[:, :, :], src[:, :, :], bias[:, :].unsqueeze(1).broadcast_to([P, TPB, DIM]),
                                  ALU.add).then_inc(y_read, 1)
                if last: dve.wait_ge(y_read, BATCH)
                else: dve.wait_ge(y_read, b + 1)
                back(dve, chain, core, b, y)
                chain.restart()

            with dve.Fori(0, BATCH - 1) as b:
                row(b, False)
            row(BATCH - 1, True)


def whole_network(nc, a, out):
    with ExitStack() as ctx:
        core = Core(nc, ctx)
        prologue(core, ctx, a["x"])
        delta_layer(core, a["l0a_conv_w"], a["l0a_conv_b"], a["l0a_norm1_w"], a["l0a_norm2_w"], a["l0a_wqkvba"], a["l0a_wo"],
                    a["l0a_wg"], a["l0a_wu"], a["l0a_wd"])
        fused_moe_layer(core, a["l0f_router"], a["l0f_wg"], a["l0f_wu"], a["l0f_wd"], a["l0f_spread"])
        side = lambda d: {n: a[f"{d}_{n}"] for n in MAMBA_WEIGHTS}
        mamba_layer(core, side("fw"), side("bw"), a["l1a_proj"], a["l1a_proj_b"], a["l1a_ln_w"], a["l1a_ln_b"])
        expert_mlp_layer(core, a["l1f_router"], a["l1f_w1"], a["l1f_w2"])
        bucket_attention_layer(core, a["l2a_hash"], a["l2a_wq"], a["l2a_bq"], a["l2a_wv"], a["l2a_bv"], a["l2a_wo"], a["l2a_bo"],
                               a["l2a_limits"])
        linear_layer(core, "l2f", a["l2f_w"], a["l2f_scale"], a["l2f_bias"])
        decay_attention_layer(core, a["l3a_wqk"], a["l3a_wv"], a["l3a_wo"], a["l3a_decay"], a["l3a_log_dist"],
                              a["l3a_pick"])
        linear_layer(core, "l3f", (a["l3f_real"], a["l3f_imag"]), None, a["l3f_bias"], (a["l3f_cos"], a["l3f_sin"]))
        epilogue(core, out)


MAMBA_WEIGHTS = ("in_w", "conv_w", "conv_b", "xproj_w", "dt_w", "dt_b", "Alog", "Dp", "out_w")


def side_by_side(routed, shared):
    flat = [np.moveaxis(w, 0, 1).reshape(w.shape[1], -1) for w in (routed, shared)]
    return np.concatenate(flat, axis=1)


def shape_constants():
    spread = np.zeros((32, 10, P), np.float32)
    for m in range(8):
        spread[2 * m, m, 0:64] = 1
        spread[2 * m + 1, m, 64:128] = 1
    spread[16, 8:] = 1
    limits = np.zeros((P, 4), np.float32)
    limits[:, 0:2] = 1e9
    for p in range(P):
        if p % 16 < 8:
            limits[p, 0:2] = 64 * (p % 16), 64 * (p % 16) + 64
        limits[p, 2 + p // 16 % 2] = 1e30
    distance = np.arange(P)[:, None] + (SEQ - P) - np.arange(SEQ)[None, :]
    n = np.arange(DIM)
    turn = 2 * np.pi * (np.outer(n, n) % DIM) / DIM
    return {"l0f_spread": spread, "l2a_limits": limits,
            "l3a_pick": np.kron(np.eye(4), np.ones((1, 32))).astype(np.float32),
            "l3a_log_dist": np.log1p(np.maximum(distance, 0)).astype(np.float32),
            "l3f_cos": np.cos(turn).astype(np.float32), "l3f_sin": np.sin(turn).astype(np.float32)}


def laid_out(v):
    a = {"x": v["L0_attn_x"]}
    for n in ("conv_w", "conv_b", "norm1_w", "norm2_w", "wo", "wg", "wu", "wd"):
        a["l0a_" + n] = v["L0_attn_" + n]
    a["l0a_wqkvba"] = np.concatenate([v["L0_attn_" + n] for n in ("wq", "wk", "wv", "wb", "wa")], axis=1)
    a["l0f_router"] = v["L0_ffn_router_w"]
    a["l0f_wg"] = side_by_side(v["L0_ffn_wg_r"], v["L0_ffn_wg_s"])
    a["l0f_wu"] = side_by_side(v["L0_ffn_wu_r"], v["L0_ffn_wu_s"])
    a["l0f_wd"] = np.concatenate([v["L0_ffn_wd_r"].reshape(-1, DIM), v["L0_ffn_wd_s"].reshape(-1, DIM)], axis=0)
    for d in ("fw", "bw"):
        w = {n: v[f"L1_attn_{d}_{n}"] for n in MAMBA_WEIGHTS}
        for n in ("in_w", "dt_w", "out_w"):
            w[n] = w[n].T
        w["conv_w"] = w["conv_w"][:, 0, :]
        xproj = np.zeros((w["xproj_w"].shape[1], 80), np.float32)
        for i in range(3):
            xproj[:, 32 * i:32 * i + 16] = w["xproj_w"].T[:, 16 * i:16 * i + 16]
        w["xproj_w"] = xproj
        for n in MAMBA_WEIGHTS:
            a[f"{d}_{n}"] = w[n]
    a["l1a_proj"], a["l1a_proj_b"] = v["L1_attn_proj_w"].T, v["L1_attn_proj_b"]
    a["l1a_ln_w"], a["l1a_ln_b"] = v["L1_attn_ln_w"], v["L1_attn_ln_b"]
    a["l1f_router"] = v["L1_ffn_router_w"].T
    a["l1f_w1"], a["l1f_w2"] = np.swapaxes(v["L1_ffn_w1"], 1, 2), np.swapaxes(v["L1_ffn_w2"], 1, 2)
    for to, n in (("hash", "W_hash"), ("wq", "W_q"), ("bq", "b_q"), ("wv", "W_v"), ("bv", "b_v"), ("wo", "W_o"), ("bo", "b_o")):
        a["l2a_" + to] = v["L2_attn_" + n]
    a["l2f_w"], a["l2f_scale"], a["l2f_bias"] = v["L2_ffn_CB"].T, v["L2_ffn_SCB"], v["L2_ffn_bias"]
    qkv = v["L3_attn_w_attn"]
    a["l3a_wqk"], a["l3a_wv"] = qkv[:, 0:2 * DIM], qkv[:, 2 * DIM:]
    a["l3a_wo"], a["l3a_decay"] = v["L3_attn_w_proj"], v["L3_attn_decay_raw"]
    a["l3f_real"], a["l3f_imag"], a["l3f_bias"] = v["L3_ffn_w_freq_real"], v["L3_ffn_w_freq_imag"], v["L3_ffn_bias"]
    a.update(shape_constants())
    return a


def kernel(**inputs):
    import concourse.bacc as bacc
    from concourse.bass_utils import run_bass_kernel_spmd

    nc = bacc.Bacc("TRN2", target_bir_lowering=False, num_devices=1)
    arrays, aps = {}, {}
    for name, value in laid_out({k: np.asarray(v) for k, v in inputs.items()}).items():
        arrays["in_" + name] = np.ascontiguousarray(value)
        aps[name] = nc.dram_tensor("in_" + name, value.shape, mybir.dt.from_np(value.dtype), kind="ExternalInput").ap()
    out = nc.dram_tensor("out", (BATCH, SEQ, DIM), F32, kind="ExternalOutput").ap()
    whole_network(nc, aps, out)
    return run_bass_kernel_spmd(nc, [arrays], core_ids=[0]).results[0]["out"]
```

```python
from contextlib import ExitStack

import numpy as np

import concourse.bass as bass
from concourse import mybir

F32 = mybir.dt.float32
BF16 = mybir.dt.bfloat16
I32 = mybir.dt.int32
U32 = mybir.dt.uint32
ALU = mybir.AluOpType
ACT = mybir.ActivationFunctionType
AX = mybir.AxisListType

P = 128
BATCH, SEQ, DIM = 8, 512, 256
TPB = SEQ // P
NT = BATCH * TPB
KC = DIM // P
LN_EPS = 1e-5
RSQRT_MAGIC = 0x5F3759DF


class Chain:

    def __init__(self, eng, sem):
        self.eng, self.sem, self.n = eng, sem, 0

    def mark(self, ins):
        self.n += 1
        return ins.then_inc(self.sem, 1)

    def wait(self):
        if self.n:
            self.eng.wait_ge(self.sem, self.n)

    def link(self, ins):
        self.mark(ins)
        self.wait()

    def restart(self):
        self.wait()
        self.eng.sem_clear(self.sem)
        self.n = 0


class Signals:

    def __init__(self, nc, ctx, layer):
        self.nc, self.ctx, self.layer, self.taken = nc, ctx, layer, []

    def __call__(self, name):
        self.taken.append(self.ctx.enter_context(self.nc.semaphore(f"{self.layer}_{name}")))
        return self.taken[-1]

    def block(self):
        self.ctx.callback(self.clear)
        return self.ctx.enter_context(self.nc.Block())

    def clear(self):
        with self.nc.Block() as block:
            @block.sync
            def _(sp):
                for sem in self.taken:
                    sp.sem_clear(sem)


class Core:

    def __init__(self, nc, ctx):
        self.nc = nc
        sb = lambda name, shape, dt=F32: ctx.enter_context(nc.sbuf_tensor(name, shape, dt))
        self.X = sb("X", [P, NT, DIM])
        self.ident = sb("ident", [P, P])
        self.ident_bf = sb("ident_bf", [P, P], BF16)
        self.stats = sb("stats", [P, TPB, 6])
        self.mv = sb("mv", [P, TPB, 2])
        self.rs = sb("rs", [P, 4, TPB])
        self.tmp = sb("tmp", [P, TPB, DIM])


def rsqrt_stage(dve, chain, y, v, half, t, stage):
    chain.wait()
    if stage == 0:
        chain.mark(dve.tensor_scalar(half, v, 0.5, None, ALU.mult))
        chain.mark(dve.tensor_scalar(y.bitcast(I32), v.bitcast(I32), -0.5, float(RSQRT_MAGIC), ALU.mult, ALU.add))
        return
    chain.link(dve.tensor_tensor(t, y, y, ALU.mult))
    chain.link(dve.tensor_tensor(t, t, half, ALU.mult))
    chain.mark(dve.scalar_tensor_tensor(out=y, in0=t, scalar=1.5, in1=y, op0=ALU.subtract, op1=ALU.mult))
    if stage == 3:
        chain.wait()
        chain.mark(dve.tensor_scalar(y, y, -1.0, None, ALU.mult))


def rsqrt(dve, chain, y, v, half, t):
    for stage in range(4):
        rsqrt_stage(dve, chain, y, v, half, t, stage)
    chain.wait()


NORM_STAGES = 7


def norm_stage(dve, chain, core, tiles, stage, eps=LN_EPS):
    if stage == 0:
        for j, tile in enumerate(tiles):
            chain.mark(dve.bn_stats(core.stats[:, j, :], tile))
    elif stage == 1:
        chain.wait()
        for j in range(TPB):
            chain.mark(dve.bn_aggr(core.mv[:, j, :], core.stats[:, j, :]))
        chain.wait()
        chain.mark(dve.tensor_scalar(core.rs[:, 1, :], core.mv[:, :, 1], eps, None, ALU.add))
    else:
        rsqrt_stage(dve, chain, core.rs[:, 0, :], core.rs[:, 1, :], core.rs[:, 2, :], core.rs[:, 3, :], stage - 2)


def norm_stats(dve, chain, core, tiles):
    for stage in range(NORM_STAGES - 1):
        norm_stage(dve, chain, core, tiles, stage)
    chain.wait()


def front_stage(dve, chain, core, b, xn, xn_ready, stage):
    tiles = [core.X[:, TPB * b + j, :] for j in range(TPB)]
    if stage < NORM_STAGES - 1:
        norm_stage(dve, chain, core, tiles, stage)
        return
    chain.wait()
    for j in range(TPB):
        last = dve.tensor_scalar(xn[:, j, :], tiles[j], core.mv[:, j, 0:1], core.rs[:, 0, j:j + 1], ALU.subtract, ALU.mult)
    last.then_inc(xn_ready, 1)


def front(dve, chain, core, b, xn, xn_ready):
    for stage in range(NORM_STAGES):
        front_stage(dve, chain, core, b, xn, xn_ready, stage)


def back_stage(dve, chain, core, b, y, stage, y_read=None):
    if stage < NORM_STAGES - 1:
        norm_stage(dve, chain, core, [y[:, j, :] for j in range(TPB)], stage)
        return
    chain.wait()
    for j in range(TPB):
        last = dve.tensor_scalar(core.tmp[:, j, :], y[:, j, :], core.mv[:, j, 0:1], core.rs[:, 0, j:j + 1],
                                 ALU.subtract, ALU.mult)
        if y_read is None or j < TPB - 1:
            chain.mark(last)
    chain.wait()
    if y_read is not None:
        last.then_inc(y_read, 1)
        dve.wait_ge(y_read, b + 1)
    xb = core.X[:, bass.ds(TPB * b, TPB), :]
    chain.mark(dve.tensor_tensor(xb, xb, core.tmp[:, :, :], ALU.add))


def back(dve, chain, core, b, y, y_read=None):
    for stage in range(NORM_STAGES):
        back_stage(dve, chain, core, b, y, stage, y_read)


def transposes(pe, core, xn, pt, sent):
    for j in range(TPB):
        for k in range(KC):
            last = pe.transpose(pt[:, k, j * P:(j + 1) * P], xn[:, j, k * P:(k + 1) * P], core.ident[:, :])
    last.then_inc(sent, 1)


def row_of(ap):
    return ap.rearrange("(a n) -> a n", a=1)


def prologue(core, ctx, x_dram):
    nc = core.nc
    core.first_loaded, core.x_loaded = (ctx.enter_context(nc.semaphore(n)) for n in ("first_loaded", "x_loaded"))
    blank = ctx.enter_context(nc.semaphore("ident_steps"))
    with nc.Block() as block:
        @block.sync
        def _(sp):
            for rows, tiles, done in ((slice(0, 1), slice(0, TPB), core.first_loaded), (slice(1, BATCH), slice(TPB, NT), core.x_loaded)):
                sp.dma_start(core.X[:, tiles, :], x_dram[rows].rearrange("b (j p) d -> p (b j) d", p=P)).then_inc(done, 16)

        @block.gpsimd
        def _(pool):
            pool.memset(core.ident[:, :], 0.0).then_inc(blank, 1)
            pool.wait_ge(blank, 1)
            pool.affine_select(out=core.ident[:, :], in_=core.ident[:, :], compare_op=ALU.not_equal, fill=1.0,
                               base=0, pattern=[[-1, P]], channel_multiplier=1).then_inc(blank, 1)
            pool.wait_ge(blank, 2)
            pool.tensor_copy(core.ident_bf[:, :], core.ident[:, :]).then_inc(blank, 1)
            pool.wait_ge(blank, 3)


def store_row(sp, core, out_dram, b, stored):
    sp.dma_start(out_dram[b].rearrange("(j p) d -> p j d", p=P), core.X[:, TPB * b:TPB * (b + 1), :]).then_inc(stored, 16)


def epilogue(core, out_dram, rows=range(BATCH)):
    nc = core.nc
    with nc.semaphore("x_stored") as x_stored, nc.Block() as block:
        @block.sync
        def _(sp):
            for b in rows:
                store_row(sp, core, out_dram, b, x_stored)
            sp.wait_ge(x_stored, 16 * len(rows))


def delta_project(core, qkv, gates, conv_w_dram, conv_b_dram, norm_w_dram, w_dram):
    nc = core.nc
    name = "proj"
    K = conv_w_dram.shape[1]
    HEADS, HD = 16, 16
    QK = 2 * DIM
    with ExitStack() as ctx:
        sb = lambda n, shape, dt=F32: ctx.enter_context(nc.sbuf_tensor(f"{name}_{n}", shape, dt))
        ps = lambda n, shape: ctx.enter_context(nc.psum_tensor(f"{name}_{n}", shape, F32))
        sem = Signals(nc, ctx, name)
        xn = sb("xn", [P, TPB, DIM])
        xs = sb("xs", [P, KC, K - 1 + SEQ])
        conv = sb("conv", [P, KC, SEQ])
        xc = sb("xc", [P, KC, SEQ])
        cw, cb, nw = sb("cw", [P, KC, K]), sb("cb", [P, KC]), sb("nw", [P, KC])
        w = sb("w", [P, KC, 3 * DIM + 2 * HEADS])
        sq = sb("sq", [P, TPB, 2 * HD, HEADS])
        norm = sb("norm", [P, 5, TPB * QK // HD])
        x_scale = sb("x_scale", [P, 2, TPB])
        gate_bias = sb("gate_bias", [P, 2])
        pt = ps("pt", [P, KC, SEQ])
        pq = ps("pq", [P, 2, 2, SEQ])
        loaded, consts = sem("loaded"), sem("consts")
        xn_ready, turned, xs_ready, conv_ready, xc_ready = (sem(n) for n in ("xn_ready", "turned", "xs_ready", "conv_ready", "xc_ready"))
        tile_ready, tile_read, qk_ready, sq_ready, qk_done = (sem(n) for n in ("tile_ready", "tile_read", "qk_ready", "sq_ready", "qk_done"))
        chain_dve = sem("chain_dve")
        block = sem.block()

        @block.sync
        def _(sp):
            sp.dma_start(cw[:, :, :], conv_w_dram.rearrange("(k p) n -> p k n", p=P)).then_inc(loaded, 16)
            with nc.allow_non_contiguous_dma(reason="two short vectors"):
                sp.dma_start(cb[:, :], conv_b_dram.rearrange("(k p) -> p k", p=P)).then_inc(loaded, 16)
                sp.dma_start(nw[:, :], norm_w_dram.rearrange("(k p) -> p k", p=P)).then_inc(loaded, 16)
            sp.dma_start(w[:, :, :], w_dram.rearrange("(k p) n -> p k n", p=P)).then_inc(loaded, 16)

        @block.tensor
        def _(pe):
            def turn_input(b):
                pe.wait_ge(xn_ready, b + 1)
                wait_from(pe, xs_ready, b)
                transposes(pe, core, xn, pt, turned)

            def row(b, last=False, more=True):
                pe.wait_ge(xc_ready, b + 1)
                for j in range(TPB):
                    wait_from(pe, tile_read, 3 * (TPB * b + j - 1))
                    for half, (lo, hi) in enumerate(((0, QK), (QK, 3 * DIM + 2 * HEADS))):
                        for k in range(KC):
                            done = pe.matmul(pq[:, j % 2, half, 0:hi - lo], xc[:, k, j * P:(j + 1) * P], w[:, k, lo:hi],
                                             start=k == 0, stop=k == KC - 1)
                    done.then_inc(tile_ready, 1)
                    if j == 1 and not last:
                        turn_input(b + 1)

            turn_input(0)
            pe.wait_ge(loaded, 16 * 4)
            rows_but_two(pe, row)

        @block.scalar
        def _(act):
            act.wait_ge(loaded, 16 * 4)
            act.wait_ge(consts, 2)

            def copy_input(b):
                act.wait_ge(turned, b + 1)
                wait_from(act, conv_ready, KC * b)
                for k in range(KC):
                    last = act.activation(xs[:, k, K - 1:], pt[:, k, :], ACT.Copy, scale=nw[:, k:k + 1])
                last.then_inc(xs_ready, 1)

            def row(b, last=False, more=True):
                wait_from(act, tile_ready, TPB * b)
                for k in range(KC):
                    act.wait_ge(conv_ready, KC * b + k + 1)
                    done = act.activation(xc[:, k, :], conv[:, k, :], ACT.Silu)
                done.then_inc(xc_ready, 1)
                for j in range(TPB):
                    act.wait_ge(tile_ready, TPB * b + j + 1)
                    heads = bass.ds(HEADS * b, HEADS)
                    for c in range(3):
                        src = pq[:, j % 2, c // 2, c % 2 * DIM:c % 2 * DIM + DIM].rearrange("p (h e) -> p e h", e=HD)
                        act.activation(qkv[:, j, c * HD:(c + 1) * HD, heads], src, ACT.Copy).then_inc(qk_ready if c == 1 else tile_read, 1)
                    for c in range(2):
                        at = DIM + c * HEADS
                        done = act.activation(gates[:, j, c, heads], pq[:, j % 2, 1, at:at + HEADS], ACT.Sigmoid,
                                              bias=gate_bias[:, c:c + 1])
                    done.then_inc(tile_read, 1)
                    if j == 1 and not last:
                        copy_input(b + 1)

            copy_input(0)
            rows_but_two(act, row)

        @block.gpsimd
        def _(pool):
            pool.memset(xs[:, :, 0:K - 1], 0.0).then_inc(consts, 1)
            pool.memset(gate_bias[:, 0:1], 0.0)
            pool.memset(gate_bias[:, 1:2], 4.0).then_inc(consts, 1)

            def row(b):
                pool.wait_ge(qk_ready, TPB * (b + 1))
                wait_from(pool, qk_done, b)
                own = qkv[:, :, 0:2 * HD, bass.ds(HEADS * b, HEADS)]
                pool.tensor_tensor(sq[:, :, :, :], own, own, ALU.mult).then_inc(sq_ready, 1)
            row(0)
            with pool.Fori(1, BATCH) as b:
                row(b)

        @block.vector
        def _(dve):
            chain = Chain(dve, chain_dve)

            def front_rms(b):
                tiles = [core.X[:, TPB * b + j, :] for j in range(TPB)]
                norm_stats(dve, chain, core, tiles)
                rs, var = core.rs, core.mv[:, :, 1]
                chain.link(dve.tensor_copy(x_scale[:, 0, :], rs[:, 0, :]))
                chain.link(dve.tensor_tensor(x_scale[:, 1, :], rs[:, 0, :], rs[:, 0, :], ALU.mult))
                chain.link(dve.tensor_tensor(x_scale[:, 1, :], x_scale[:, 1, :], var, ALU.mult))
                chain.link(dve.tensor_scalar(x_scale[:, 1, :], x_scale[:, 1, :], 1e-6, None, ALU.add))
                rsqrt(dve, chain, rs[:, 0, :], x_scale[:, 1, :], rs[:, 2, :], rs[:, 3, :])
                chain.link(dve.tensor_tensor(x_scale[:, 0, :], x_scale[:, 0, :], rs[:, 0, :], ALU.mult))
                for j in range(TPB):
                    last = dve.tensor_scalar(xn[:, j, :], tiles[j], core.mv[:, j, 0:1], x_scale[:, 0, j:j + 1],
                                             ALU.subtract, ALU.mult)
                last.then_inc(xn_ready, 1)

            def convolve(b):
                dve.wait_ge(xs_ready, b + 1)
                wait_from(dve, xc_ready, b)
                for k in range(KC):
                    chain.mark(dve.tensor_scalar(conv[:, k, :], xs[:, k, K - 1:], cw[:, k, K - 1:K], cb[:, k:k + 1], ALU.mult, ALU.add))
                chain.wait()
                for tap in range(K - 1):
                    for k in range(KC):
                        ins = dve.scalar_tensor_tensor(out=conv[:, k, :], in0=xs[:, k, tap:tap + SEQ], scalar=cw[:, k, tap:tap + 1],
                                                       in1=conv[:, k, :], op0=ALU.mult, op1=ALU.add)
                        if tap == K - 2:
                            ins.then_inc(conv_ready, 1)
                        else:
                            chain.mark(ins)
                    if tap < K - 2:
                        chain.wait()

            def lengths(b):
                dve.wait_ge(sq_ready, b + 1)
                chain.link(dve.tensor_reduce(norm[:, 1, :].rearrange("p (g h) -> p g h", h=HEADS), sq[:, :, :, :].rearrange("p j (c e) h -> p (j c) h e", e=HD), AX.X, ALU.add))
                chain.link(dve.tensor_scalar(norm[:, 2, :], norm[:, 1, :], 1e-6, None, ALU.add))
                rsqrt(dve, chain, norm[:, 0, :], norm[:, 2, :], norm[:, 3, :], norm[:, 4, :])
                for c in range(2):
                    part = qkv[:, :, c * HD:(c + 1) * HD, bass.ds(HEADS * b, HEADS)]
                    scale = norm[:, 0, :].rearrange("p (j c h) -> p j c h", j=TPB, c=2)[:, :, c, :]
                    last = dve.tensor_tensor(part, part, scale.unsqueeze(2).broadcast_to([P, TPB, HD, HEADS]), ALU.mult)
                last.then_inc(qk_done, 1)

            def row(b, last=False, more=True):
                if not last:
                    convolve(b + 1)
                lengths(b)
                if more:
                    dve.wait_ge(turned, b + 2)
                    front_rms(b + 2)
                chain.restart()

            dve.wait_ge(core.first_loaded, 16)
            front_rms(0)
            dve.wait_ge(loaded, 16 * 4)
            convolve(0)
            dve.wait_ge(turned, 1)
            dve.wait_ge(core.x_loaded, 16)
            front_rms(1)
            chain.restart()
            rows_but_two(dve, row)


def rows_but_two(eng, row):
    row(0)
    with eng.Fori(1, BATCH - 2) as b:
        row(b)
    row(BATCH - 2, more=False)
    row(BATCH - 1, last=True, more=False)


def delta_recurrence(core, qkv, gates):
    nc = core.nc
    name = "scan"
    HEADS, HD = 16, 16
    SPANS = SEQ // P
    GROUPS = 3 * HD // 4
    G = 4
    TURNS = P // G
    HALF = HD // 2
    with ExitStack() as ctx:
        sb = lambda n, shape, dt=F32: ctx.enter_context(nc.sbuf_tensor(f"{name}_{n}", shape, dt))
        ps = lambda n, shape: ctx.enter_context(nc.psum_tensor(f"{name}_{n}", shape, F32))
        sem = Signals(nc, ctx, name)
        kqv = sb("kqv", [P, P, 4, HD])
        ba = sb("ba", [P, 3, P])
        prod = sb("prod", [P, 2 * G, HD, HD + 1])
        d = sb("d", [P, 2, HD])
        outer = sb("outer", [P, HD, HD])
        states = sb("states", [P, 2 * G, HD, HD])
        times_q = sb("times_q", [P, G, HD, HD])
        o = sb("o", [P, P, HD])
        pk = ps("pk", [P, 4, 4, P])
        po = ps("po", [P, 4, 4, P])
        names = "sent taken scaled filled states_ready states_used o_sent o_taken chain_dve chain_pool".split()
        sent, taken, scaled, filled, states_ready, states_used, o_sent, o_taken, chain_dve, chain_pool = (sem(n) for n in names)
        block = sem.block()

        PER = GROUPS + 1

        @block.tensor
        def _(pe):
            for s in range(SPANS):
                for g in range(PER):
                    n = PER * s + g
                    wait_from(pe, taken, n - 3)
                    for i in range(4):
                        if g < GROUPS:
                            src = qkv[:, s, g * 4 + i, :]
                        elif i < 2:
                            src = gates[:, s, i, :]
                        else:
                            continue
                        last = pe.transpose(pk[:, n % 4, i, :], src, core.ident[:, :])
                    last.then_inc(sent, 1)
                for g in range(HD // 4):
                    pe.wait_ge(states_used, TURNS * (s + 1))
                    wait_from(pe, o_taken, 4 * (s - 1) + g + 1)
                    for i in range(4):
                        last = pe.transpose(po[:, g, i, :], o[:, :, 4 * g + i], core.ident[:, :])
                    last.then_inc(o_sent, 1)

        @block.scalar
        def _(act):
            for s in range(SPANS):
                wait_from(act, states_used, TURNS * s)
                for g in range(PER):
                    n = PER * s + g
                    act.wait_ge(sent, n + 1)
                    if g < GROUPS:
                        part, at = (1, 0, 2)[g // 4], g % 4 * 4
                        act.activation(kqv[:, :, part, at:at + 4].rearrange("p t i -> p i t"), pk[:, n % 4, :, :],
                                       ACT.Copy).then_inc(taken, 1)
                    else:
                        act.activation(ba[:, 0:2, :], pk[:, n % 4, 0:2, :], ACT.Copy).then_inc(taken, 1)
                act.wait_ge(scaled, s + 1)
                for g in range(TURNS):
                    wait_from(act, states_ready, TURNS * s + g - 1)
                    act.activation(prod[:, g % 2 * G:(g % 2 + 1) * G, :, HD], kqv[:, g * G:(g + 1) * G, 2, :], ACT.Copy).then_inc(filled, 1)
                for g in range(4):
                    act.wait_ge(o_sent, 4 * s + g + 1)
                    last = act.activation(qkv[:, s, 4 * g:4 * g + 4, :], po[:, g, :, :], ACT.Copy)
                    last.then_inc(o_taken, 1)

        @block.gpsimd
        def _(pool):
            chain = Chain(pool, chain_pool)

            def span(s):
                for g in range(TURNS):
                    pool.wait_ge(states_ready, TURNS * s + g + 1)
                    if g == 0:
                        wait_from(pool, o_sent, 4 * s)
                    tokens = slice(g * G, (g + 1) * G)
                    chain.link(pool.tensor_tensor(times_q[:, :, :, :], states[:, g % 2 * G:(g % 2 + 1) * G, :, :],
                                                  kqv[:, tokens, 1, :].unsqueeze(2).broadcast_to([P, G, HD, HD]), ALU.mult))
                    width = HD // 2
                    while width > 1:
                        chain.link(pool.tensor_tensor(times_q[:, :, :, 0:width], times_q[:, :, :, 0:width],
                                                      times_q[:, :, :, width:2 * width], ALU.add))
                        width //= 2
                    if g == TURNS - 1:
                        chain.restart()
                    pool.tensor_tensor(o[:, tokens, :], times_q[:, :, :, 0], times_q[:, :, :, 1], ALU.add).then_inc(states_used, 1)
                    pool.wait_ge(states_used, TURNS * s + g + 1)

            span(0)
            with pool.Fori(1, SPANS) as s:
                span(s)

        @block.vector
        def _(dve):
            chain = Chain(dve, chain_dve)
            chain.mark(dve.memset(states[:, 2 * G - 1, :, :], 0.0))

            def span(s):
                dve.wait_ge(taken, PER * (s + 1))
                beta, alpha = ba[:, 0, :], ba[:, 1, :]
                spread = lambda row: row.unsqueeze(2).broadcast_to([P, P, HD])
                chain.link(dve.scalar_tensor_tensor(out=ba[:, 2, :], in0=beta, scalar=-1.0, in1=alpha, op0=ALU.mult, op1=ALU.mult))
                chain.mark(dve.tensor_tensor(kqv[:, :, 3, :], kqv[:, :, 0, :], spread(ba[:, 2, :]), ALU.mult))
                dve.tensor_tensor(kqv[:, :, 2, :], kqv[:, :, 2, :], spread(beta), ALU.mult).then_inc(scaled, 1)
                chain.restart()
                for t in range(P):
                    g, now, old = t // G, t % (2 * G), (t - 1) % (2 * G)
                    if t % G == 0:
                        dve.wait_ge(filled, TURNS * s + g + 1)
                        wait_from(dve, states_used, TURNS * s + g - 1)
                    halves = [slice(i * HALF, (i + 1) * HALF) for i in range(2)]
                    key = lambda i: kqv[:, t, i, :].unsqueeze(1).broadcast_to([P, HALF, HD])
                    base = chain.n

                    def after(step):
                        dve.wait_ge(chain_dve, base + step)

                    for i, half in enumerate(halves):
                        if t % G > 0:
                            after(i - 1)
                        elif t > 0 and i == 0:
                            after(0)
                        elif t > 0:
                            dve.wait_ge(states_ready, TURNS * s + g)
                        chain.mark(dve.tensor_tensor(prod[:, now, half, 0:HD], states[:, old, half, :], key(3), ALU.mult))
                    for i, half in enumerate(halves):
                        after(1 + i)
                        chain.mark(dve.tensor_reduce(d[:, t % 2, half], prod[:, now, half, :], AX.X, ALU.add))
                    for i, half in enumerate(halves):
                        after(3 + i)
                        chain.mark(dve.tensor_tensor(outer[:, half, :], d[:, t % 2, half].unsqueeze(2).broadcast_to([P, HALF, HD]),
                                                     key(0), ALU.mult))
                    for i, half in enumerate(halves):
                        after(5 + i)
                        ins = dve.scalar_tensor_tensor(out=states[:, now, half, :], in0=states[:, old, half, :],
                                                       scalar=ba[:, 1, t:t + 1], in1=outer[:, half, :], op0=ALU.mult, op1=ALU.add)
                        if t % G == G - 1 and i == 1:
                            ins.then_inc(states_ready, 1)
                        else:
                            chain.mark(ins)
                chain.restart()

            span(0)
            with dve.Fori(1, SPANS) as s:
                span(s)


def delta_finish(core, o, wo_dram, norm_w_dram, wg_dram, wu_dram, wd_dram):
    nc = core.nc
    AT_OUTPUTS, AT_MIX, AT_NORMALISED = 0, 1, 4
    name = "fin"
    HEADS, HD = 16, 16
    I = wg_dram.shape[1]
    NB = -(-I // P)
    sizes = [min(P, I - P * m) for m in range(NB)]
    with ExitStack() as ctx:
        sb = lambda n, shape, dt=F32: ctx.enter_context(nc.sbuf_tensor(f"{name}_{n}", shape, dt))
        ps = lambda n, shape: ctx.enter_context(nc.psum_tensor(f"{name}_{n}", shape, F32))
        sem = Signals(nc, ctx, name)
        xn = sb("xn", [P, TPB, DIM])
        os = sb("os", [P, TPB, DIM])
        oT = sb("oT", [P, KC, SEQ])
        h, hn = sb("h", [P, 2, TPB, DIM]), sb("hn", [P, TPB, DIM])
        hnT = sb("hnT", [P, 2, KC, SEQ])
        y = sb("y", [P, TPB, DIM])
        act_g, mid = sb("act_g", [P, 2, SEQ]), sb("mid", [P, 2, SEQ])
        wo, wg, wu = sb("wo", [P, KC, DIM]), sb("wg", [P, KC, I]), sb("wu", [P, KC, I])
        wd, nw = sb("wd", [P, NB, DIM]), sb("nw", [P, KC])
        sq = sb("sq", [P, TPB])
        pt = ps("pt", [P, KC, SEQ])
        pgu = ps("pgu", [P, 2, 2, SEQ])
        py = ps("py", [P, TPB, DIM])
        loaded = sem("loaded")
        os_ready, o_sent, oT_ready, mix_ready, hn_ready, hn_sent, hnT_ready = (
            sem(n) for n in ("os_ready", "o_sent", "oT_ready", "mix_ready", "hn_ready", "hn_sent", "hnT_ready"))
        gu_ready, silu_ready, mid_ready, y_ready, y_read, chain_dve = (
            sem(n) for n in ("gu_ready", "silu_ready", "mid_ready", "y_ready", "y_read", "chain_dve"))
        block = sem.block()

        @block.sync
        def _(sp):
            sp.dma_start(wo[:, :, :], wo_dram.rearrange("(k p) n -> p k n", p=P)).then_inc(loaded, 16)
            sp.dma_start(wg[:, :, :], wg_dram.rearrange("(k p) n -> p k n", p=P)).then_inc(loaded, 16)
            sp.dma_start(wu[:, :, :], wu_dram.rearrange("(k p) n -> p k n", p=P)).then_inc(loaded, 16)
            for m in range(NB):
                sp.dma_start(wd[0:sizes[m], m, :], wd_dram[P * m:P * m + sizes[m], :]).then_inc(loaded, 16)
            with nc.allow_non_contiguous_dma(reason="a short vector"):
                sp.dma_start(nw[:, :], norm_w_dram.rearrange("(k p) -> p k", p=P)).then_inc(loaded, 16)

        LOADS = 16 * (4 + NB)

        @block.gpsimd
        def _(pool):
            def row(b):
                wait_from(pool, o_sent, b)
                pool.tensor_copy(os[:, :, :].rearrange("p j (h e) -> p j h e", e=HD),
                                 o[:, :, :, bass.ds(HEADS * b, HEADS)].rearrange("p j e h -> p j h e")).then_inc(os_ready, 1)
            row(0)
            with pool.Fori(1, BATCH) as b:
                row(b)

        @block.tensor
        def _(pe):
            def turn_outputs(b):
                pe.wait_ge(os_ready, b + 1)
                wait_from(pe, hnT_ready, b)
                transposes(pe, core, os, pt, o_sent)

            def mix(b):
                pe.wait_ge(oT_ready, b + 1)
                for j in range(TPB):
                    for k in range(KC):
                        last = pe.matmul(pt[:, j // 2, j % 2 * DIM:(j % 2 + 1) * DIM], oT[:, k, j * P:(j + 1) * P], wo[:, k, :],
                                         start=k == 0, stop=k == KC - 1)
                last.then_inc(mix_ready, 1)

            def turn_normalised(b):
                pe.wait_ge(hn_ready, b + 1)
                transposes(pe, core, hn, pt, hn_sent)

            def row(b, p, first=False, last=False, more=True):
                def up(m):
                    if m == 0:
                        pe.wait_ge(hnT_ready, b + 1)
                    wait_from(pe, mid_ready, NB * b + m - 1)
                    for i, w in enumerate((wg, wu)):
                        for k in range(KC):
                            done = pe.matmul(pgu[0:sizes[m], m % 2, i, :], w[:, k, m * P:m * P + sizes[m]], hnT[:, p, k, :],
                                             start=k == 0, stop=k == KC - 1)
                    done.then_inc(gu_ready, 1)

                def down(m):
                    pe.wait_ge(mid_ready, NB * b + m + 1)
                    if m == 0:
                        wait_from(pe, y_read, b)
                    for j in range(TPB):
                        done = pe.matmul(py[:, j, :], mid[0:sizes[m], m % 2, j * P:(j + 1) * P], wd[0:sizes[m], m, :],
                                         start=m == 0 and j % 2 == 0, stop=m == NB - 1, skip_group_check=True)
                    return done

                for m in range(NB):
                    up(m)
                    if m > 0:
                        down(m - 1)
                    if m == AT_OUTPUTS and not last:
                        turn_outputs(b + 1)
                    if m == AT_MIX and not last:
                        mix(b + 1)
                    if m == AT_NORMALISED and not last:
                        turn_normalised(b + 1)
                down(NB - 1).then_inc(y_ready, 1)

            turn_outputs(0)
            pe.wait_ge(loaded, LOADS)
            mix(0)
            turn_normalised(0)
            rows_in_pairs(pe, row)

        @block.scalar
        def _(act):
            def copy_outputs(b):
                act.wait_ge(o_sent, b + 1)
                wait_from(act, mix_ready, b)
                act.activation(oT[:, :, :], pt[:, :, :], ACT.Copy).then_inc(oT_ready, 1)

            def copy_normalised(b, p):
                act.wait_ge(hn_sent, b + 1)
                wait_from(act, y_ready, b - 1)
                for k in range(KC):
                    last = act.activation(hnT[:, p, k, :], pt[:, k, :], ACT.Copy, scale=nw[:, k:k + 1])
                last.then_inc(hnT_ready, 1)

            def row(b, p, first=False, last=False, more=True):
                for m in range(NB):
                    act.wait_ge(gu_ready, NB * b + m + 1)
                    wait_from(act, mid_ready, NB * b + m - 1)
                    act.activation(act_g[0:sizes[m], m % 2, :], pgu[0:sizes[m], m % 2, 0, :], ACT.Silu).then_inc(silu_ready, 1)
                    if m == AT_OUTPUTS and not last:
                        copy_outputs(b + 1)
                    if m == AT_NORMALISED and not last:
                        copy_normalised(b + 1, 1 - p)

            copy_outputs(0)
            act.wait_ge(loaded, LOADS)
            copy_normalised(0, 0)
            rows_in_pairs(act, row)

        @block.vector
        def _(dve):
            chain = Chain(dve, chain_dve)

            def residual(b):
                tiles = [core.X[:, TPB * b + j, :] for j in range(TPB)]
                norm_stats(dve, chain, core, tiles)
                for j in range(TPB):
                    chain.mark(dve.tensor_scalar(xn[:, j, :], tiles[j], core.mv[:, j, 0:1], core.rs[:, 0, j:j + 1],
                                                 ALU.subtract, ALU.mult))
                chain.wait()

            def normalise(b, p, part):
                own = h[:, p]
                rs = core.rs
                step = lambda stage: rsqrt_stage(dve, chain, rs[:, 0, :], rs[:, 1, :], rs[:, 2, :], rs[:, 3, :], stage)
                if part == 0:
                    dve.wait_ge(mix_ready, b + 1)
                    chain.link(dve.tensor_tensor(own[:, :, :], xn[:, :, :], pt[:, :, :].rearrange("p a (j n) -> p (a j) n", j=2), ALU.add))
                    for j in range(TPB):
                        chain.mark(dve.bn_stats(core.stats[:, j, :], own[:, j, :]))
                elif part == 1:
                    chain.wait()
                    for j in range(TPB):
                        chain.mark(dve.bn_aggr(core.mv[:, j, :], core.stats[:, j, :]))
                    chain.wait()
                    chain.link(dve.tensor_tensor(sq[:, :], core.mv[:, :, 0], core.mv[:, :, 0], ALU.mult))
                    chain.link(dve.scalar_tensor_tensor(out=rs[:, 1, :], in0=sq[:, :], scalar=1e-6, in1=core.mv[:, :, 1],
                                                        op0=ALU.add, op1=ALU.add))
                    step(0)
                    step(1)
                else:
                    step(2)
                    step(3)
                    chain.wait()
                    for j in range(TPB):
                        ins = dve.tensor_scalar(hn[:, j, :], own[:, j, :], rs[:, 0, j:j + 1], None, ALU.mult)
                    ins.then_inc(hn_ready, 1)

            def row(b, p, first=False, last=False, more=True):
                for m in range(NB):
                    dve.wait_ge(silu_ready, NB * b + m + 1)
                    if m < 2:
                        wait_from(dve, y_ready, b)
                    dve.tensor_tensor(mid[0:sizes[m], m % 2, :], act_g[0:sizes[m], m % 2, :], pgu[0:sizes[m], m % 2, 1, :],
                                      ALU.mult).then_inc(mid_ready, 1)
                    if m == 0 and not last:
                        residual(b + 1)
                    if 0 <= m - AT_MIX < 3 and not last:
                        normalise(b + 1, 1 - p, m - AT_MIX)
                dve.wait_ge(y_ready, b + 1)
                dve.tensor_tensor(y[:, :, :], h[:, p], py[:, :, :], ALU.add).then_inc(y_read, 1)
                dve.wait_ge(y_read, b + 1)
                back(dve, chain, core, b, y)
                chain.restart()

            residual(0)
            for part in range(3):
                normalise(0, 0, part)
            chain.restart()
            rows_in_pairs(dve, row)


def delta_layer(core, conv_w, conv_b, norm1_w, norm2_w, wqkvba, wo, wg, wu, wd):
    nc = core.nc
    with ExitStack() as ctx:
        qkv = ctx.enter_context(nc.sbuf_tensor("qkv", [P, TPB, 48, P], F32))
        gates = ctx.enter_context(nc.sbuf_tensor("gates", [P, TPB, 2, P], F32))
        delta_project(core, qkv, gates, conv_w, conv_b, norm1_w, wqkvba)
        delta_recurrence(core, qkv, gates)
        delta_finish(core, qkv[:, :, 0:16, :], wo, norm2_w, wg, wu, wd)


def wait_from(eng, sem, value):
    if not isinstance(value, int) or value > 0:
        eng.wait_ge(sem, value)


def fused_moe_layer(core, router_dram, wg_dram, wu_dram, wd_dram, spread_dram):
    nc = core.nc
    E = router_dram.shape[1]
    NB = wg_dram.shape[1] // P
    ROWS = spread_dram.shape[0]
    AT_TURN, AT_LOGITS, AT_WEIGHTS = 3, 5, 7
    name = "moe0"
    with ExitStack() as ctx:
        sb = lambda n, shape, dt=F32: ctx.enter_context(nc.sbuf_tensor(f"{name}_{n}", shape, dt))
        ps = lambda n, shape: ctx.enter_context(nc.psum_tensor(f"{name}_{n}", shape, F32))
        sem = Signals(nc, ctx, name)
        xn = sb("xn", [P, TPB, DIM])
        xT = sb("xT", [P, 2, KC, SEQ])
        wr = sb("wr", [P, KC, E])
        wg, wu = sb("wg", [P, KC, NB * P]), sb("wu", [P, KC, NB * P])
        wd = sb("wd", [P, NB, DIM])
        spread = sb("spread", [ROWS, NB, P])
        logit = sb("logit", [P, TPB, E])
        prob = sb("prob", [P, TPB, E])
        total = sb("total", [P, 4, TPB])
        best = sb("best", [P, TPB, 8])
        at = sb("at", [P, TPB, 8], U32)
        atf = sb("atf", [P, TPB, 8])
        share = sb("share", [P, 4, TPB])
        number = sb("number", [P, E])
        comb = sb("comb", [P, TPB, 2, ROWS])
        combT = sb("combT", [ROWS, 2, SEQ])
        act_g = sb("act_g", [P, 2, SEQ])
        hT = sb("hT", [P, 2, SEQ])
        pgu = ps("pgu", [P, 2, 2, SEQ])
        pr = ps("pr", [P, SEQ])
        spare = ps("spare", [P, SEQ])
        py = ps("py", [P, TPB, DIM])
        router_loaded, loaded, consts = sem("router_loaded"), sem("loaded"), sem("consts")
        xn_ready, turned, xT_ready = sem("xn_ready"), sem("turned"), sem("xT_ready")
        logits_ready, shifted, exps_ready, comb_ready = sem("logits_ready"), sem("shifted"), sem("exps_ready"), sem("comb_ready")
        combT_sent, combT_ready = sem("combT_sent"), sem("combT_ready")
        gu_ready, silu_ready, h_ready = sem("gu_ready"), sem("silu_ready"), sem("h_ready")
        y_ready, y_read, chain_dve = sem("y_ready"), sem("y_read"), sem("chain_dve")
        block = sem.block()

        @block.sync
        def _(sp):
            sp.dma_start(wr[:, :, :], router_dram.rearrange("(k p) n -> p k n", p=P)).then_inc(router_loaded, 16)
            sp.dma_start(spread[:, :, :], spread_dram).then_inc(loaded, 16)
            sp.dma_start(wg[:, :, :], wg_dram.rearrange("(k p) n -> p k n", p=P)).then_inc(loaded, 16)
            sp.dma_start(wu[:, :, :], wu_dram.rearrange("(k p) n -> p k n", p=P)).then_inc(loaded, 16)
            sp.dma_start(wd[:, :, :], wd_dram.rearrange("(m p) n -> p m n", p=P)).then_inc(loaded, 16)

        @block.gpsimd
        def _(pool):
            pool.iota(number[:, :], pattern=[[1, E]], base=0, channel_multiplier=0,
                      allow_small_or_imprecise_dtypes=True).then_inc(consts, 1)
            pool.memset(comb[:, :, :, :], 0.0).then_inc(consts, 1)
            pool.wait_ge(consts, 2)
            pool.memset(comb[:, :, 0, E:E + 1], 1.0).then_inc(consts, 1)

        @block.tensor
        def _(pe):
            def turn_input(b, k):
                pe.wait_ge(xn_ready, b + 1)
                if k == 0:
                    wait_from(pe, combT_ready, b)
                else:
                    pe.wait_ge(xT_ready, KC * b + 1)
                for j in range(TPB):
                    last = pe.transpose(spare[:, j * P:(j + 1) * P], xn[:, j, k * P:(k + 1) * P], core.ident[:, :])
                last.then_inc(turned, 1)

            def logits(b, p):
                pe.wait_ge(xT_ready, KC * (b + 1))
                for j in range(TPB):
                    for k in range(KC):
                        last = pe.matmul(spare[:, j * E:(j + 1) * E], xT[:, p, k, j * P:(j + 1) * P],
                                         wr[:, k, :], start=k == 0, stop=k == KC - 1)
                last.then_inc(logits_ready, 1)

            def turn_weights(b):
                pe.wait_ge(comb_ready, b + 1)
                for j in range(TPB):
                    last = pe.transpose(spare[0:ROWS, j * P:(j + 1) * P], comb[:, j, 0, :], core.ident[:, :])
                last.then_inc(combT_sent, 1)

            def row(b, p, first=False, last=False, more=True):
                def up(m):
                    wait_from(pe, h_ready, NB * b + m - 1)
                    if m == 0:
                        pe.wait_ge(xT_ready, KC * (b + 1))
                    for i, w in enumerate((wg, wu)):
                        for k in range(KC):
                            pe.matmul(pgu[:, m % 2, i, :], w[:, k, m * P:(m + 1) * P], xT[:, p, k, :], start=k == 0, stop=k == KC - 1)
                    if m == 0:
                        pe.wait_ge(combT_ready, b + 1)
                    wait_from(pe, h_ready, NB * b + m)
                    pe.matmul(pr[:, :], spread[:, m, :], combT[:, p, :], start=True, stop=True).then_inc(gu_ready, 1)

                def down(m):
                    pe.wait_ge(h_ready, NB * b + m + 1)
                    if m == 0:
                        wait_from(pe, y_read, b)
                    for j in range(TPB):
                        done = pe.matmul(py[:, j, :], hT[:, m % 2, j * P:(j + 1) * P], wd[:, m, :],
                                         start=m == 0 and j % 2 == 0, stop=m == NB - 1, skip_group_check=True)
                    return done

                for m in range(NB):
                    up(m)
                    if m > 0:
                        down(m - 1)
                    if last:
                        continue
                    if 0 <= m - AT_TURN < KC:
                        turn_input(b + 1, m - AT_TURN)
                    if m == AT_LOGITS:
                        logits(b + 1, 1 - p)
                    if m == AT_WEIGHTS:
                        turn_weights(b + 1)
                down(NB - 1).then_inc(y_ready, 1)

            for k in range(KC):
                turn_input(0, k)
            pe.wait_ge(router_loaded, 16)
            logits(0, 0)
            turn_weights(0)
            pe.wait_ge(loaded, 16 * 4)
            rows_in_pairs(pe, row)

        @block.scalar
        def _(act):
            def copy_input(b, p, k):
                act.wait_ge(turned, KC * b + k + 1)
                wait_from(act, y_ready, b - 1)
                act.activation(xT[:, p, k, :], spare[:, :], ACT.Copy).then_inc(xT_ready, 1)

            def exps(b):
                act.wait_ge(shifted, b + 1)
                act.activation(prob[:, :, :], logit[:, :, :], ACT.Exp).then_inc(exps_ready, 1)

            def copy_weights(b, p):
                act.wait_ge(combT_sent, b + 1)
                act.activation(combT[:, p, :], spare[0:ROWS, :], ACT.Copy).then_inc(combT_ready, 1)

            def row(b, p, first=False, last=False, more=True):
                for m in range(NB):
                    act.wait_ge(gu_ready, NB * b + m + 1)
                    wait_from(act, h_ready, NB * b + m - 1)
                    act.activation(act_g[:, m % 2, :], pgu[:, m % 2, 0, :], ACT.Silu).then_inc(silu_ready, 1)
                    if last:
                        continue
                    if 0 <= m - AT_TURN < KC:
                        copy_input(b + 1, 1 - p, m - AT_TURN)
                    if m == AT_LOGITS + 1:
                        exps(b + 1)
                    if m == AT_WEIGHTS:
                        copy_weights(b + 1, 1 - p)

            for k in range(KC):
                copy_input(0, 0, k)
            exps(0)
            copy_weights(0, 0)
            rows_in_pairs(act, row)

        @block.vector
        def _(dve):
            chain = Chain(dve, chain_dve)
            dve.wait_ge(consts, 3)
            front(dve, chain, core, 0, xn, xn_ready)
            chain.restart()

            def shift(b):
                dve.wait_ge(logits_ready, b + 1)
                pl = spare[:, 0:TPB * E].rearrange("p (j e) -> p j e", e=E)
                chain.link(dve.tensor_reduce(total[:, 0, :], pl, AX.X, ALU.max))
                dve.tensor_tensor(logit[:, :, :], pl, total[:, 0, :].unsqueeze(2).broadcast_to([P, TPB, E]),
                                  ALU.subtract).then_inc(shifted, 1)

            def weigh(b):
                dve.wait_ge(exps_ready, b + 1)
                chain.mark(dve.tensor_reduce(total[:, 1, :], prob[:, :, :], AX.X, ALU.add))
                for j in range(TPB):
                    chain.mark(dve.max(best[:, j, :], prob[:, j, :]))
                chain.wait()
                for j in range(TPB):
                    chain.mark(dve.max_index(at[:, j, :], best[:, j, :], prob[:, j, :]))
                chain.link(dve.reciprocal(total[:, 2, :], total[:, 1, :]))
                chain.mark(dve.tensor_copy(atf[:, :, 0:2], at[:, :, 0:2]))
                for i in range(2):
                    chain.mark(dve.tensor_tensor(share[:, i, :], best[:, :, i], total[:, 2, :], ALU.mult))
                chain.wait()
                chain.link(dve.scalar_tensor_tensor(out=share[:, 2, :], in0=share[:, 0, :], scalar=1e-9, in1=share[:, 1, :],
                                                    op0=ALU.add, op1=ALU.add))
                chain.link(dve.reciprocal(share[:, 3, :], share[:, 2, :]))
                for i in range(2):
                    chain.mark(dve.tensor_tensor(share[:, i, :], share[:, i, :], share[:, 3, :], ALU.mult))
                chain.wait()
                for j in range(TPB):
                    for i in range(2):
                        chain.mark(dve.tensor_scalar(comb[:, j, i, 0:E], number[:, :], atf[:, j, i:i + 1], share[:, i, j:j + 1],
                                                     ALU.is_equal, ALU.mult))
                chain.wait()
                dve.tensor_tensor(comb[:, :, 0, 0:E], comb[:, :, 0, 0:E], comb[:, :, 1, 0:E], ALU.add).then_inc(comb_ready, 1)

            def row(b, p, first=False, last=False, more=True):
                for m in range(NB):
                    dve.wait_ge(silu_ready, NB * b + m + 1)
                    if m < 2:
                        wait_from(dve, y_ready, b)
                    chain.link(dve.tensor_tensor(act_g[:, m % 2, :], act_g[:, m % 2, :], pgu[:, m % 2, 1, :], ALU.mult))
                    dve.tensor_tensor(hT[:, m % 2, :], act_g[:, m % 2, :], pr[:, :], ALU.mult).then_inc(h_ready, 1)
                    if last:
                        continue
                    if m == AT_TURN - 2:
                        front(dve, chain, core, b + 1, xn, xn_ready)
                    if m == AT_LOGITS:
                        shift(b + 1)
                    if m == AT_LOGITS + 1:
                        weigh(b + 1)
                dve.wait_ge(y_ready, b + 1)
                back(dve, chain, core, b, py, y_read)
                chain.restart()

            shift(0)
            weigh(0)
            rows_in_pairs(dve, row)


def mamba_direction(core, name, flipped, bc_dram, part_dram, w, proj_dram, post=None):
    nc = core.nc
    DVE_AT = {'y': 0, 'conv': (6, 8, 10, 12), 'cat': 15, 'end': 24, 'rest': 26, 'delta': 29, 'front': 31}
    PE_AT = {'turn': 0, 'xi': (2, 4, 6, 8, 10, 11, 21, 22), 'out': (3, 5, 7, 9), 'xproj': 13, 'dt': 17, 'proj': (15, 16, 19, 20)}
    ACT_AT = {'tap': (6, 8, 10, 12), 'cat': 3, 'xT': 4, 'silu': 14, 'z': (15, 16, 26, 27), 'silu_z': 30, 'xd': 19, 'dt': 22, 'abs': 23, 'exp': 24, 'w': 25, 'ln': 27}
    POOL_AT = {'yz': (1, 2, 4, 9), 'log': 26, 'du': 29}
    CI = w["Alog"].shape[0] // P
    N = w["Alog"].shape[1]
    R = w["dt_w"].shape[0]
    K = w["conv_w"].shape[1]
    XD = w["xproj_w"].shape[1]
    Q = 2
    STEPS = N // Q * CI
    REUSE = 8
    with ExitStack() as ctx:
        sb = lambda n, shape, dt=F32: ctx.enter_context(nc.sbuf_tensor(f"{name}_{n}", shape, dt))
        ps = lambda n, shape: ctx.enter_context(nc.psum_tensor(f"{name}_{n}", shape, F32))
        sem = Signals(nc, ctx, name)
        in_w, xproj_w, dt_w = sb("in_w", [P, KC, 2 * CI * P]), sb("xproj_w", [P, CI, XD]), sb("dt_w", [R, CI * P])
        out_w, proj = sb("out_w", [P, CI, DIM]), sb("proj", [P, KC, DIM])
        cw, vec = sb("cw", [P, CI, K]), sb("vec", [P, 3, CI])
        alog, A = sb("alog", [P, CI, N]), sb("A", [P, CI, N])
        xn, xT = sb("xn", [P, TPB, DIM]), sb("xT", [P, 2, KC, SEQ])
        u, sz = sb("u", [P, 2, CI, SEQ]), sb("sz", [P, 2, CI, SEQ])
        xd = sb("xd", [XD, SEQ])
        e = sb("e", [P, CI, SEQ])
        delta, du = sb("delta", [P, 2, CI, SEQ]), sb("du", [P, 2, CI, SEQ])
        Bs, Cs = sb("Bs", [P, 2, Q, SEQ]), sb("Cs", [P, 2, Q, SEQ])
        dA = sb("dA", [P, 2, Q, SEQ])
        G = sb("G", [P, REUSE, Q, SEQ])
        yz = sb("yz", [P, CI, SEQ])
        cat = xn.rearrange("p (k j) n -> p k (j n)", k=KC)
        y = core.tmp
        if post:
            rows = sb("rows", [P, 3, DIM])
        pt = ps("pt", [P, KC, SEQ])
        pw = ps("pw", [P, 2, SEQ])
        py = ps("py", [P, CI, SEQ])
        loaded, late_loaded, consts = sem("loaded"), sem("late_loaded"), sem("consts")
        names = ("xn_ready turned xT_ready x_ready xi_ready tap_ready conv_ready u_ready z_ready z_read sz_ready xd_ready xd_copied dt_ready dt_read "
                 "w_ready rest_ready ln_ready log_ready delta_ready du_ready bc_stored dA_ready g_ready scanned hc_ready summed y_ready yz_ready "
                 "out_ready cat_ready proj_ready proj_read stored chain_dve chain_act").split()
        (xn_ready, turned, xT_ready, x_ready, xi_ready, tap_ready, conv_ready, u_ready, z_ready, z_read, sz_ready, xd_ready, xd_copied, dt_ready, dt_read,
         w_ready, rest_ready, ln_ready, log_ready, delta_ready, du_ready, bc_stored, dA_ready, g_ready, scanned, hc_ready, summed, y_ready, yz_ready,
         out_ready, cat_ready, proj_ready, proj_read, stored, chain_dve, chain_act) = (sem(n) for n in names)
        b_loaded, c_loaded = ([sem(f"{n}_loaded{i}") for i in range(2)] for n in "bc")
        block = sem.block()
        LOADS, LATE_LOADS = 16 * 6, 16 * (4 + (3 if post else 0))

        def time(ap):
            return ap[:, ::-1] if flipped else ap

        @block.sync
        def _(sp):
            for dst, src in ((alog, w["Alog"]), (in_w, w["in_w"]), (cw, w["conv_w"])):
                sp.dma_start(dst[:, :, :], src.rearrange("(k p) n -> p k n", p=P)).then_inc(loaded, 16)
            with nc.allow_non_contiguous_dma(reason="short vectors"):
                for i, n in enumerate(("conv_b", "dt_b", "Dp")):
                    sp.dma_start(vec[:, i, :], w[n].rearrange("(k p) -> p k", p=P)).then_inc(loaded, 16)
            for dst, src in ((xproj_w, w["xproj_w"]), (out_w, w["out_w"]), (proj, proj_dram)):
                sp.dma_start(dst[:, :, :], src.rearrange("(k p) n -> p k n", p=P)).then_inc(late_loaded, 16)
            sp.dma_start(dt_w[:, :], w["dt_w"]).then_inc(late_loaded, 16)
            if post:
                for i, v in enumerate(post):
                    sp.dma_start(rows[:, i, :], row_of(v).broadcast_to([P, DIM])).then_inc(late_loaded, 16)

            def store_bc(b):
                sp.wait_ge(xd_copied, b + 1)
                for i in range(2):
                    sp.dma_start(bc_dram[b % 2, i], xd[32 * (i + 1):32 * (i + 1) + N, :]).then_inc(bc_stored, 16)

            def row(b):
                sp.wait_ge(bc_stored, 32 * b + 32)
                for q in range(N // Q):
                    wait_from(sp, g_ready, STEPS * b + CI * (q - 1))
                    if q == DVE_AT["end"] // CI and not post:
                        wait_from(sp, stored, 16 * (b - 1))
                    sp.dma_start(Bs[:, q % 2, :, :], bc_dram[b % 2, 0, Q * q:Q * q + Q, :].rearrange("(a n) t -> a (n t)", a=1)
                                 .broadcast_to([P, Q * SEQ])).then_inc(b_loaded[q % 2], 16)
                    wait_from(sp, hc_ready, STEPS * b + CI * (q - 1))
                    sp.dma_start(Cs[:, q % 2, :, :], bc_dram[b % 2, 1, Q * q:Q * q + Q, :].rearrange("(a n) t -> a (n t)", a=1)
                                 .broadcast_to([P, Q * SEQ])).then_inc(c_loaded[q % 2], 16)
                    if q == 5 and b + 1 < BATCH:
                        store_bc(b + 1)
                    if q == 2 and b > 0:
                        share(b - 1)

            def share(b):
                if post:
                    sp.dma_start(y[:, :, :], part_dram[:, TPB * b:TPB * (b + 1), :]).then_inc(stored, 16)
                elif b > 0:
                    store(b - 1)

            def store(b):
                sp.wait_ge(proj_read, b + 1)
                sp.dma_start(part_dram[:, TPB * b:TPB * (b + 1), :], y[:, :, :]).then_inc(stored, 16)

            store_bc(0)
            for b in range(BATCH):
                row(b)
            sp.wait_ge(scanned, STEPS * BATCH)
            share(BATCH - 1)
            if not post:
                store(BATCH - 1)
            sp.wait_ge(stored, 16 * BATCH)

        @block.tensor
        def _(pe):
            def turn_input(b):
                pe.wait_ge(xn_ready, b + 1)
                transposes(pe, core, xn, pt, turned)

            def inner(b, p, c):
                if c == 0:
                    pe.wait_ge(xT_ready, b + 1)
                    wait_from(pe, z_read, CI * b)
                elif 2 <= c < CI + 2:
                    pe.wait_ge(conv_ready, CI * b + c - 1)
                elif c >= CI + 2:
                    pe.wait_ge(dt_read, CI * b + CI)
                for k in range(KC):
                    last = pe.matmul(pw[:, c % 2, :], in_w[:, k, c * P:(c + 1) * P], xT[:, p, k, :], start=k == 0, stop=k == KC - 1)
                last.then_inc(xi_ready if c < CI else z_ready, 1)

            def xproj(b, p, c):
                pe.wait_ge(u_ready, b + 1)
                if c == 0:
                    pe.wait_ge(z_read, CI * b + 1)
                last = pe.matmul(pw[0:XD, 0, :], xproj_w[:, c, :], u[:, p, c, :], start=c == 0, stop=c == CI - 1)
                if c == CI - 1:
                    last.then_inc(xd_ready, 1)

            def dt(b, c):
                pe.wait_ge(xd_copied, b + 1)
                if c == 0:
                    pe.wait_ge(z_read, CI * b + 2)
                elif c >= 2:
                    pe.wait_ge(dt_read, CI * b + c - 1)
                pe.matmul(pw[:, (c + 1) % 2, :], dt_w[:, c * P:(c + 1) * P], xd[0:R, :], start=True, stop=True).then_inc(dt_ready, 1)

            def project_out(b, c, last):
                pe.wait_ge(yz_ready, CI * b + c + 1)
                if c == 0:
                    pe.wait_ge(xT_ready, b + 3 if not last else BATCH)
                for m in range(KC):
                    last = pe.matmul(pt[:, m, :], out_w[:, c, m * P:(m + 1) * P], yz[:, c, :], start=c == 0, stop=c == CI - 1)
                if c == CI - 1:
                    last.then_inc(out_ready, 1)

            def project(b, j):
                if j == 0:
                    pe.wait_ge(cat_ready, b + 1)
                for k in range(KC):
                    done = pe.matmul(pt[:, j // 2, j % 2 * DIM:(j % 2 + 1) * DIM], cat[:, k, j * P:(j + 1) * P], proj[:, k, :],
                                     start=k == 0, stop=k == KC - 1)
                if j == TPB - 1:
                    done.then_inc(proj_ready, 1)

            def head(b, p, s):
                if s == PE_AT["turn"]:
                    turn_input(b)
                if s in PE_AT["xi"]:
                    inner(b, p, PE_AT["xi"].index(s))
                at = s - PE_AT["xproj"]
                if 0 <= at < CI // 2:
                    xproj(b, p, 2 * at)
                    xproj(b, p, 2 * at + 1)
                at = s - PE_AT["dt"]
                if 0 <= at < CI // 2:
                    dt(b, 2 * at)
                    dt(b, 2 * at + 1)

            def tail(b, s, last=False):
                if s in PE_AT["out"]:
                    project_out(b, PE_AT["out"].index(s), last)
                if s in PE_AT["proj"]:
                    project(b, PE_AT["proj"].index(s))

            def row(b, p, first=False, last=False, more=True):
                for s in range(STEPS):
                    q, c = s // CI, s % CI
                    pe.wait_ge(hc_ready, STEPS * b + s + 1)
                    if q == 0:
                        wait_from(pe, y_ready, CI * (b - 1) + c + 1)
                    for i in range(Q):
                        done = pe.matmul(py[:, c, :], core.ident[:, :], G[:, s % REUSE, i, :],
                                         start=q == 0 and i == 0, stop=q == N // Q - 1 and i == Q - 1)
                    done.then_inc(summed, 1)
                    if not last:
                        head(b + 1, 1 - p, s)
                    if not first:
                        tail(b - 1, s, last)

            for s in range(STEPS):
                if s == PE_AT["xi"][0]:
                    pe.wait_ge(loaded, LOADS)
                if s == PE_AT["xproj"]:
                    pe.wait_ge(late_loaded, LATE_LOADS)
                head(0, 0, s)
            rows_in_pairs(pe, row)
            for s in range(STEPS):
                tail(BATCH - 1, s, True)

        @block.scalar
        def _(act):
            chain = Chain(act, chain_act)
            act.wait_ge(loaded, LOADS)
            chain.link(act.activation(A[:, :, :], alog[:, :, :], ACT.Exp))
            chain.link(act.activation(A[:, :, :], A[:, :, :], ACT.Copy, scale=-1.0))
            act.wait_ge(consts, 1)
            chain.restart()

            def head(b, p, s):
                if s == ACT_AT["xT"]:
                    act.wait_ge(turned, b + 1)
                    wait_from(act, x_ready, b - 1)
                    for k in range(KC):
                        last = act.activation(time(xT[:, p, k, :]), pt[:, k, :], ACT.Copy)
                    last.then_inc(xT_ready, 1)
                if s in ACT_AT["tap"]:
                    c = ACT_AT["tap"].index(s)
                    act.wait_ge(xi_ready, CI * b + c + 1)
                    wait_from(act, y_ready, CI * (b - 1))
                    act.activation(u[:, p, c, :], pw[:, c % 2, :], ACT.Identity, bias=vec[:, 0, c:c + 1], scale=cw[:, c, K - 1:K]
                                   ).then_inc(tap_ready, 1)
                if s == ACT_AT["silu"]:
                    act.wait_ge(conv_ready, CI * b + CI)
                    act.activation(u[:, p, :, :], u[:, p, :, :], ACT.Silu).then_inc(u_ready, 1)
                if s in ACT_AT["z"]:
                    c = ACT_AT["z"].index(s)
                    act.wait_ge(z_ready, CI * b + c + 1)
                    wait_from(act, yz_ready, CI * (b - 1))
                    act.activation(sz[:, p, c, :], pw[:, c % 2, :], ACT.Copy).then_inc(z_read, 1)
                if s == ACT_AT["silu_z"]:
                    act.wait_ge(z_read, CI * b + CI)
                    act.activation(sz[:, p, :, :], sz[:, p, :, :], ACT.Silu).then_inc(sz_ready, 1)
                if s == ACT_AT["xd"]:
                    act.wait_ge(xd_ready, b + 1)
                    wait_from(act, bc_stored, 32 * b)
                    act.activation(xd[:, :], pw[0:XD, 0, :], ACT.Copy).then_inc(xd_copied, 1)
                at = s - ACT_AT["dt"]
                if 0 <= at < CI // 2:
                    wait_from(act, g_ready, STEPS * (b - 1))
                    for c in (2 * at, 2 * at + 1):
                        act.wait_ge(dt_ready, CI * b + c + 1)
                        act.activation(du[:, p, c, :], pw[:, (c + 1) % 2, :], ACT.Identity, bias=vec[:, 1, c:c + 1]).then_inc(dt_read, 1)
                if s == ACT_AT["abs"]:
                    act.wait_ge(dt_read, CI * b + CI)
                    wait_from(act, delta_ready, b)
                    chain.mark(act.activation(e[:, :, :], du[:, p, :, :], ACT.Abs))
                if s == ACT_AT["exp"]:
                    chain.wait()
                    chain.mark(act.activation(e[:, :, :], e[:, :, :], ACT.Exp, scale=-1.0))
                if s == ACT_AT["w"]:
                    chain.wait()
                    act.activation(delta[:, p, :, :], e[:, :, :], ACT.Identity, bias=1.0).then_inc(w_ready, 1)
                if s == ACT_AT["ln"]:
                    act.wait_ge(rest_ready, b + 1)
                    act.activation(delta[:, p, :, :], delta[:, p, :, :], ACT.Ln).then_inc(ln_ready, 1)

            def tail(b, p, last_row=False):
                if not last_row:
                    act.wait_ge(turned, b + 3)
                else:
                    act.wait_ge(proj_ready, b)
                for k in range(KC):
                    last = act.activation(cat[:, k, :], time(xT[:, p, k, :]), ACT.Copy)
                last.then_inc(x_ready, 1)

            def row(b, p, first=False, last=False, more=True):
                for s in range(STEPS):
                    q, c = s // CI, s % CI
                    if s == 0:
                        act.wait_ge(delta_ready, b + 1)
                    wait_from(act, scanned, STEPS * b + s - 1)
                    for i in range(Q):
                        done = act.activation(dA[:, s % 2, i, 1:], delta[:, p, c, 1:], ACT.Exp, scale=A[:, c, Q * q + i:Q * q + i + 1])
                    done.then_inc(dA_ready, 1)
                    if s == ACT_AT["cat"] and not first:
                        tail(b - 1, 1 - p, last)
                    if not last:
                        head(b + 1, 1 - p, s)
                chain.restart()

            for s in range(STEPS):
                head(0, 0, s)
            chain.restart()
            rows_in_pairs(act, row)
            tail(BATCH - 1, (BATCH - 1) % 2, True)

        @block.gpsimd
        def _(pool):
            pool.memset(dA[:, :, :, 0:1], 0.0).then_inc(consts, 1)

            def log1p(b, p):
                pool.wait_ge(ln_ready, b + 1)
                pool.tensor_tensor(delta[:, p, :, :], delta[:, p, :, :], e[:, :, :], ALU.subtract).then_inc(log_ready, 1)

            def head(b, p, c):
                pool.wait_ge(delta_ready, b + 1)
                pool.wait_ge(u_ready, b + 1)
                pool.tensor_tensor(du[:, p, c, :], delta[:, p, c, :], u[:, p, c, :], ALU.mult).then_inc(du_ready, 1)

            def tail(b, p, c):
                pool.wait_ge(sz_ready, b + 1)
                pool.wait_ge(y_ready, CI * b + c + 1)
                pool.tensor_tensor(yz[:, c, :], yz[:, c, :], sz[:, p, c, :], ALU.mult).then_inc(yz_ready, 1)

            def row(b, p, first=False, last=False, more=True):
                for s in range(STEPS):
                    q, c = s // CI, s % CI
                    if s == POOL_AT["log"] and not last:
                        log1p(b + 1, 1 - p)
                    if s >= POOL_AT["du"] and not last:
                        head(b + 1, 1 - p, s - POOL_AT["du"])
                    pool.wait_ge(scanned, STEPS * b + s + 1)
                    if c == 0:
                        pool.wait_ge(c_loaded[q % 2], 16 * (N // Q // 2) * b + 16 * (q // 2 + 1))
                    pool.tensor_tensor(G[:, s % REUSE, :, :], G[:, s % REUSE, :, :], Cs[:, q % 2, :, :], ALU.mult).then_inc(hc_ready, 1)
                    if not first and s in POOL_AT["yz"]:
                        tail(b - 1, 1 - p, POOL_AT["yz"].index(s))
                for c in range(STEPS - POOL_AT["du"], CI):
                    if not last:
                        head(b + 1, 1 - p, c)

            log1p(0, 0)
            for c in range(CI):
                head(0, 0, c)
            rows_in_pairs(pool, row)
            for c in range(CI):
                tail(BATCH - 1, (BATCH - 1) % 2, c)

        @block.vector
        def _(dve):
            chain = Chain(dve, chain_dve)

            def convolve(b, p, c):
                dve.wait_ge(tap_ready, CI * b + c + 1)
                src, dst = pw[:, c % 2, :], u[:, p, c, :]
                for back_by in range(1, K):
                    ins = dve.scalar_tensor_tensor(out=dst[:, back_by:], in0=src[:, 0:SEQ - back_by],
                                                   scalar=cw[:, c, K - 1 - back_by:K - back_by], in1=dst[:, back_by:],
                                                   op0=ALU.mult, op1=ALU.add)
                    if back_by < K - 1:
                        chain.link(ins)
                    else:
                        ins.then_inc(conv_ready, 1)

            def head(b, p, s):
                if s in DVE_AT["conv"]:
                    convolve(b, p, DVE_AT["conv"].index(s))
                if s == DVE_AT["rest"]:
                    dve.wait_ge(w_ready, b + 1)
                    dve.scalar_tensor_tensor(out=e[:, :, :], in0=delta[:, p, :, :], scalar=1.0, in1=e[:, :, :],
                                             op0=ALU.subtract, op1=ALU.subtract).then_inc(rest_ready, 1)
                if s == DVE_AT["delta"]:
                    dve.wait_ge(log_ready, b + 1)
                    dve.scalar_tensor_tensor(out=delta[:, p, :, :], in0=du[:, p, :, :], scalar=0.0, in1=delta[:, p, :, :],
                                             op0=ALU.max, op1=ALU.add).then_inc(delta_ready, 1)

            def normalise(b):
                wait_from(dve, turned, b)
                wait_from(dve, proj_ready, b - 2)
                front(dve, chain, core, b, xn, xn_ready)

            def wide(i):
                return rows[:, i, :].unsqueeze(1).broadcast_to([P, TPB, DIM])

            def inner_norm(stage):
                chain.wait()
                if stage < NORM_STAGES - 1:
                    norm_stage(dve, chain, core, [y[:, j, :] for j in range(TPB)], stage)
                    return
                for j in range(TPB):
                    chain.mark(dve.tensor_scalar(y[:, j, :], y[:, j, :], core.mv[:, j, 0:1], core.rs[:, 0, j:j + 1],
                                                 ALU.subtract, ALU.mult))
                chain.wait()
                chain.link(dve.tensor_tensor(y[:, :, :], y[:, :, :], wide(1), ALU.mult))
                chain.link(dve.tensor_tensor(y[:, :, :], y[:, :, :], wide(2), ALU.add))

            def tail(b, p, s, final=False):
                c = s - DVE_AT["y"]
                if 0 <= c < CI:
                    dve.wait_ge(summed, STEPS * b + STEPS - CI + c + 1)
                    dve.scalar_tensor_tensor(out=yz[:, c, :], in0=u[:, p, c, :], scalar=vec[:, 2, c:c + 1], in1=py[:, c, :],
                                             op0=ALU.mult, op1=ALU.add).then_inc(y_ready, 1)
                if s == DVE_AT["cat"]:
                    dve.wait_ge(out_ready, b + 1)
                    dve.wait_ge(x_ready, b + 1)
                    for k in range(KC):
                        ins = dve.tensor_tensor(time(cat[:, k, :]), pt[:, k, :], time(cat[:, k, :]), ALU.add)
                        if k == KC - 1:
                            ins.then_inc(cat_ready, 1)
                if s == DVE_AT["end"]:
                    dve.wait_ge(proj_ready, b + 1)
                    pp = pt[:, :, :].rearrange("p a (j n) -> p (a j) n", n=DIM)
                    if not post:
                        if final:
                            dve.wait_ge(stored, 16 * (BATCH - 1))
                        dve.tensor_copy(y[:, :, :], pp).then_inc(proj_read, 1)
                        return
                    dve.wait_ge(stored, 16 * b + 16)
                    dve.tensor_tensor(y[:, :, :], pp, y[:, :, :], ALU.add).then_inc(proj_read, 1)
                    dve.wait_ge(proj_read, b + 1)
                    chain.mark(dve.tensor_tensor(y[:, :, :], y[:, :, :], wide(0), ALU.add))
                if post and DVE_AT["end"] < s <= DVE_AT["end"] + NORM_STAGES:
                    for stage in (2 * (s - DVE_AT["end"] - 1), 2 * (s - DVE_AT["end"] - 1) + 1):
                        if stage < NORM_STAGES:
                            inner_norm(stage)
                        else:
                            back_stage(dve, chain, core, b, y, stage - NORM_STAGES)

            def scan(b, s):
                dve.wait_ge(g_ready, STEPS * b + s + 1)
                dve.wait_ge(dA_ready, STEPS * b + s + 1)
                g = G[:, s % REUSE, :, :].rearrange("p n t -> p (n t)")
                dve.tensor_tensor_scan(g, dA[:, s % 2, :, :].rearrange("p n t -> p (n t)"), g, 0.0, ALU.mult, ALU.add
                                       ).then_inc(scanned, 1)

            def row(b, p, first=False, last=False, more=True):
                for s in range(STEPS):
                    q, c = s // CI, s % CI
                    if q == 0:
                        dve.wait_ge(du_ready, CI * b + c + 1)
                    if c == 0:
                        dve.wait_ge(b_loaded[q % 2], 16 * (N // Q // 2) * b + 16 * (q // 2 + 1))
                    wait_from(dve, summed, STEPS * b + s - REUSE + 1)
                    dve.tensor_tensor(G[:, s % REUSE, :, :], Bs[:, q % 2, :, :], du[:, p, c, :].unsqueeze(1).broadcast_to([P, Q, SEQ]),
                                      ALU.mult).then_inc(g_ready, 1)
                    if s > 0:
                        scan(b, s - 1)
                    elif not first:
                        scan(b - 1, STEPS - 1)
                    if not first:
                        tail(b - 1, 1 - p, s)
                    if not last:
                        head(b + 1, 1 - p, s)
                    if s == DVE_AT["front"] and more:
                        normalise(b + 2)
                chain.restart()

            normalise(0)
            dve.wait_ge(loaded, LOADS)
            for s in range(STEPS):
                head(0, 0, s)
            dve.wait_ge(late_loaded, LATE_LOADS)
            normalise(1)
            chain.restart()
            rows_in_pairs(dve, row)
            scan(BATCH - 1, STEPS - 1)
            for s in range(STEPS):
                tail(BATCH - 1, (BATCH - 1) % 2, s, final=True)
            chain.wait()


def rows_in_pairs(eng, row):
    row(0, 0, first=True)
    with eng.Fori(0, (BATCH - 4) // 2) as pair:
        row(pair * 2 + 1, 1)
        row(pair * 2 + 2, 0)
    row(BATCH - 3, 1)
    row(BATCH - 2, 0, more=False)
    row(BATCH - 1, 1, last=True, more=False)


def mamba_layer(core, fw, bw, proj_w, proj_b, ln_w, ln_b):
    nc = core.nc
    SCAN_N = fw["Alog"].shape[1]
    bc = nc.dram_tensor("b_and_c", (2, 2, 2, SCAN_N, SEQ), F32, kind="Internal").ap()
    part = nc.dram_tensor("part", (P, NT, DIM), F32, kind="Internal").ap()
    mamba_direction(core, "fw", False, bc[0], part, fw, proj_w[0:DIM, :])
    mamba_direction(core, "bw", True, bc[1], part, bw, proj_w[DIM:2 * DIM, :], (proj_b, ln_w, ln_b))


def expert_mlp_layer(core, router_dram, w1_dram, w2_dram):
    nc = core.nc
    E, _, H = w1_dram.shape
    HC = H // P
    UP = E * HC
    AT_TURN, AT_LOGITS = 3, 4
    name = "moe1"
    with ExitStack() as ctx:
        sb = lambda n, shape, dt=F32: ctx.enter_context(nc.sbuf_tensor(f"{name}_{n}", shape, dt))
        ps = lambda n, shape: ctx.enter_context(nc.psum_tensor(f"{name}_{n}", shape, F32))
        sem = Signals(nc, ctx, name)
        xn = sb("xn", [P, TPB, DIM])
        xT = sb("xT", [P, 2, KC, SEQ])
        wr = sb("wr", [P, KC, E])
        w1 = sb("w1", [P, E, KC, H])
        w2 = sb("w2", [P, E, HC, DIM])
        logit = sb("logit", [P, TPB, E])
        best = sb("best", [P, TPB, 8])
        at = sb("at", [P, TPB, 8], U32)
        atf = sb("atf", [P, TPB, 8])
        gap = sb("gap", [P, 4, TPB])
        share = sb("share", [P, 2, TPB])
        number = sb("number", [P, E])
        gate = sb("gate", [P, 2, TPB, E])
        second = sb("second", [P, TPB, E])
        hT = sb("hT", [P, 2, HC, SEQ])
        acc = sb("acc", [P, TPB, DIM])
        pt = ps("pt", [P, KC, SEQ])
        ph = ps("ph", [P, 2, SEQ])
        py = ps("py", [P, 2, TPB, DIM])
        loaded, consts = sem("loaded"), sem("consts")
        w_loaded = [sem(f"w_loaded{e}") for e in range(2)]
        xn_ready, turned, xT_ready = sem("xn_ready"), sem("turned"), sem("xT_ready")
        logits_ready, gap_ready, exps_ready = sem("logits_ready"), sem("gap_ready"), sem("exps_ready")
        up_ready, h_ready, y_ready, y_read, chain_dve = sem("up_ready"), sem("h_ready"), sem("y_ready"), sem("y_read"), sem("chain_dve")
        block = sem.block()

        @block.sync
        def _(sp):
            sp.dma_start(wr[:, :, :], router_dram.rearrange("(k p) n -> p k n", p=P)).then_inc(loaded, 16)
            for i in range(2):
                part = slice(i * E // 2, (i + 1) * E // 2)
                for k in range(KC):
                    sp.dma_start(w1[:, part, k, :], w1_dram[part, k * P:(k + 1) * P, :].rearrange("e p h -> p e h")).then_inc(w_loaded[i], 16)
                for c in range(HC):
                    sp.dma_start(w2[:, part, c, :], w2_dram[part, c * P:(c + 1) * P, :].rearrange("e p h -> p e h")).then_inc(w_loaded[i], 16)

        @block.gpsimd
        def _(pool):
            pool.iota(number[:, :], pattern=[[1, E]], base=0, channel_multiplier=0,
                      allow_small_or_imprecise_dtypes=True).then_inc(consts, 1)

        @block.tensor
        def _(pe):
            pe.wait_ge(loaded, 16)

            def turn_input(b):
                pe.wait_ge(xn_ready, b + 1)
                wait_from(pe, gap_ready, b)
                transposes(pe, core, xn, pt, turned)

            def logits(b, p):
                pe.wait_ge(xT_ready, b + 1)
                for j in range(TPB):
                    for k in range(KC):
                        last = pe.matmul(pt[:, 0, j * E:(j + 1) * E], xT[:, p, k, j * P:(j + 1) * P], wr[:, k, :],
                                         start=k == 0, stop=k == KC - 1)
                last.then_inc(logits_ready, 1)

            def row(b, p, first=False, last=False, more=True):
                def up(e):
                    for c in range(HC):
                        n = UP * b + HC * e + c
                        wait_from(pe, h_ready, n - 1)
                        for k in range(KC):
                            done = pe.matmul(ph[:, c % 2, :], w1[:, e, k, c * P:(c + 1) * P], xT[:, p, k, :],
                                             start=k == 0, stop=k == KC - 1)
                        done.then_inc(up_ready, 1)

                def down(e):
                    pe.wait_ge(h_ready, UP * b + HC * (e + 1))
                    wait_from(pe, y_read, E * b + e - 1)
                    for j in range(TPB):
                        for c in range(HC):
                            done = pe.matmul(py[:, e % 2, j, :], hT[:, e % 2, c, j * P:(j + 1) * P], w2[:, e, c, :],
                                             start=c == 0, stop=c == HC - 1)
                    done.then_inc(y_ready, 1)

                if first:
                    pe.wait_ge(w_loaded[0], 16 * (KC + HC))
                for e in range(E):
                    if first and e == E // 2:
                        pe.wait_ge(w_loaded[1], 16 * (KC + HC))
                    up(e)
                    if e > 0:
                        down(e - 1)
                    if e == AT_TURN and not last:
                        turn_input(b + 1)
                    if e == AT_LOGITS and not last:
                        logits(b + 1, 1 - p)
                down(E - 1)

            turn_input(0)
            logits(0, 0)
            rows_in_pairs(pe, row)

        @block.scalar
        def _(act):
            def copy_input(b, p):
                act.wait_ge(turned, b + 1)
                wait_from(act, y_ready, E * (b - 1))
                act.activation(xT[:, p, :, :], pt[:, :, :], ACT.Copy).then_inc(xT_ready, 1)

            def exp_gap(b):
                act.wait_ge(gap_ready, b + 1)
                act.activation(gap[:, 1, :], gap[:, 0, :], ACT.Exp).then_inc(exps_ready, 1)

            def row(b, p, first=False, last=False, more=True):
                for e in range(E):
                    wait_from(act, y_ready, E * b + e - 1)
                    for c in range(HC):
                        act.wait_ge(up_ready, UP * b + HC * e + c + 1)
                        act.activation(hT[:, e % 2, c, :], ph[:, c % 2, :], ACT.Gelu).then_inc(h_ready, 1)
                    if e == AT_TURN and not last:
                        copy_input(b + 1, 1 - p)
                    if e == AT_LOGITS + 1 and not last:
                        exp_gap(b + 1)

            copy_input(0, 0)
            exp_gap(0)
            rows_in_pairs(act, row)

        @block.vector
        def _(dve):
            chain = Chain(dve, chain_dve)
            dve.wait_ge(consts, 1)
            front(dve, chain, core, 0, xn, xn_ready)
            chain.restart()

            def gaps(b):
                dve.wait_ge(logits_ready, b + 1)
                chain.link(dve.tensor_copy(logit[:, :, :], pt[:, 0, 0:TPB * E].rearrange("p (j e) -> p j e", e=E)))
                for j in range(TPB):
                    chain.mark(dve.max(best[:, j, :], logit[:, j, :]))
                chain.wait()
                dve.tensor_tensor(gap[:, 0, :], best[:, :, 1], best[:, :, 0], ALU.subtract).then_inc(gap_ready, 1)
                for j in range(TPB):
                    chain.mark(dve.max_index(at[:, j, :], best[:, j, :], logit[:, j, :]))
                chain.wait()
                chain.mark(dve.tensor_copy(atf[:, :, 0:2], at[:, :, 0:2]))

            def weigh(b, p):
                dve.wait_ge(exps_ready, b + 1)
                chain.link(dve.tensor_scalar(gap[:, 2, :], gap[:, 1, :], 1.0, None, ALU.add))
                chain.link(dve.reciprocal(share[:, 0, :], gap[:, 2, :]))
                chain.link(dve.tensor_tensor(share[:, 1, :], gap[:, 1, :], share[:, 0, :], ALU.mult))
                for i, to in enumerate((gate[:, p], second)):
                    for j in range(TPB):
                        chain.mark(dve.tensor_scalar(to[:, j, :], number[:, :], atf[:, j, i:i + 1], share[:, i, j:j + 1],
                                                     ALU.is_equal, ALU.mult))
                chain.wait()
                chain.link(dve.tensor_tensor(gate[:, p, :, :], gate[:, p, :, :], second[:, :, :], ALU.add))

            def row(b, p, first=False, last=False, more=True):
                for e in range(E):
                    dve.wait_ge(y_ready, E * b + e + 1)
                    for j in range(TPB):
                        g = gate[:, p, j, e:e + 1]
                        if e == 0:
                            ins = dve.tensor_scalar(acc[:, j, :], py[:, 0, j, :], g, None, ALU.mult)
                        else:
                            ins = dve.scalar_tensor_tensor(out=acc[:, j, :], in0=py[:, e % 2, j, :], scalar=g, in1=acc[:, j, :],
                                                           op0=ALU.mult, op1=ALU.add)
                    ins.then_inc(y_read, 1)
                    dve.wait_ge(y_read, E * b + e + 1)
                    if e == AT_TURN - 2 and not last:
                        front(dve, chain, core, b + 1, xn, xn_ready)
                    if e == AT_LOGITS and not last:
                        gaps(b + 1)
                    if e == AT_LOGITS + 1 and not last:
                        weigh(b + 1, 1 - p)
                back(dve, chain, core, b, acc)
                chain.restart()

            gaps(0)
            weigh(0, 0)
            rows_in_pairs(dve, row)


def bucket_attention_layer(core, hash_dram, wq_dram, bq_dram, wv_dram, bv_dram, wo_dram, bo_dram, limits_dram):
    nc = core.nc
    name = "lsh"
    HEADS, HD = 8, 32
    SPAN = P // HEADS
    BIG = 1e30
    SCALE = float(np.float32(1.0) / np.sqrt(HD).astype(np.float32))
    UNITS = HEADS * TPB
    SIDES = (((0, 0, 1, 1), (0, 1, 0, 1)), ((0, 2, 1, 2), (2, 0, 2, 1)))
    ROUNDS = (("o", 0), ("o", 1), ("q", 0), ("q", 1), ("x", 0), ("x", 1), ("hash", 0), ("angle", 0),
              ("y", 0), ("y", 1), ("v", 0), ("v", 1))
    SLOT_OF_ROUND = (4, 6, 8, 11, 13, 15, 17, 19, 21, 24, 27, 30)
    SLOTS_IN_TAIL = 25
    AT_BACK, AT_FRONT, AT_HOT = 25, 5, UNITS - 1

    def compared_by(slot):
        return min(UNITS, slot + min(slot, 2))

    def rounds_of(first=False, last=False, more=True, tail=False):
        gone = ("o", "y") * first + ("q", "v") * (last or tail) + ("x", "hash", "angle") * (tail or not more)
        return [(kind, part) for kind, part in ROUNDS if kind not in gone]

    INPUT = [(kind, part) for kind, part in ROUNDS if kind in ("x", "hash", "angle")]
    OTHER = [(kind, part) for kind, part in ROUNDS if kind in ("q", "v")]
    ROUNDS_AHEAD = [(*r, 0) for r in INPUT] + [(*r, 0) for r in OTHER] + [(*r, 1) for r in INPUT]

    def flags(b):
        return {"first": b == 0, "last": b == BATCH - 1, "more": b < BATCH - 2, "tail": b == BATCH}

    def rounds_before(b):
        if isinstance(b, int):
            return len(ROUNDS_AHEAD) + sum(len(rounds_of(**flags(row))) for row in range(b))
        return len(ROUNDS_AHEAD) + len(rounds_of(first=True)) + len(ROUNDS) * (b - 1)

    def rounds_in(slot, b, p, first, last, more, tail):
        if slot not in SLOT_OF_ROUND:
            return []
        kind, part = ROUNDS[SLOT_OF_ROUND.index(slot)]
        present = rounds_of(first, last, more, tail)
        if (kind, part) not in present:
            return []
        number = rounds_before(b) + present.index((kind, part))
        ahead, parity = {"o": (-1, 1 - p), "y": (-1, 1 - p), "q": (1, 1 - p), "v": (1, 1 - p)}.get(kind, (2, p))
        return [(number, kind, part, b + ahead, parity)]

    def q_round(b, part):
        if b == 0:
            return ROUNDS_AHEAD.index(("q", part, 0))
        return rounds_before(b - 1) + rounds_of(**flags(b - 1)).index(("q", part))

    def angle_round(b):
        if b < 2:
            return ROUNDS_AHEAD.index(("angle", 0, b))
        return rounds_before(b - 2) + rounds_of(**flags(b - 2)).index(("angle", 0))

    with ExitStack() as ctx:
        sb = lambda n, shape, dt=F32: ctx.enter_context(nc.sbuf_tensor(f"{name}_{n}", shape, dt))
        ps = lambda n, shape: ctx.enter_context(nc.psum_tensor(f"{name}_{n}", shape, F32))
        wh, wq, wv, wo = sb("wh", [P, KC, 2 * HEADS]), sb("wq", [P, KC, DIM]), sb("wv", [P, KC, DIM]), sb("wo", [P, KC, DIM])
        bq = sb("bq", [P, KC])
        rows = sb("rows", [P, 2, DIM])
        limits = sb("limits", [P, 4])
        xn, xT = sb("xn", [P, TPB, DIM]), sb("xT", [P, 2, KC, SEQ])
        q = sb("q", [P, KC, SEQ])
        rest = sb("rest", [P, SEQ])
        parts = sb("parts", [P, 3, KC, SEQ], BF16)
        stack = sb("stack", [P, 2, 2, HEADS, SEQ], BF16)
        v = sb("v", [P, 2, TPB, DIM])
        below = sb("below", [P, TPB, HEADS])
        angle = sb("angle", [P, 2, TPB, HEADS])
        angleT = sb("angleT", [HEADS, SEQ])
        others = sb("others", [P, HEADS, SEQ])
        later = sb("later", [P, P])
        before = sb("before", [P, 2, SEQ], BF16)
        tied = sb("tied", [P, 2, P], BF16)
        mine = sb("mine", [P, HEADS, P], BF16)
        least = sb("least", [P, SEQ])
        hot = sb("hot", [P, 2, SEQ], BF16)
        cold = sb("cold", [P, 2, 2, SEQ], BF16)
        top = sb("top", [P, 4, 2])
        prob = sb("prob", [P, 4, SEQ])
        probT = sb("probT", [P, 2, TPB, P])
        total, recip = sb("total", [P, 2, TPB, HEADS]), sb("recip", [P, TPB, HEADS])
        o, oT = sb("o", [P, TPB, DIM]), sb("oT", [P, KC, SEQ])
        y = core.tmp
        ranks, spare = ps("ranks", [P, SEQ]), ps("spare", [P, SEQ])
        pscore = ps("pscore", [P, 2, SEQ])
        pturn, pout = ps("pturn", [P, 2, TPB, P]), ps("pout", [P, TPB, DIM])
        names = ("loaded consts xn_ready spare_sent spare_taken angles_stored compared counted hot_ready "
                 "high_ready rest_ready mid_ready parts_ready parts_stored early_loaded late_loaded "
                 "score_ready top_ready exp_ready turned_p copied pv_ready o_ready y_ready chain_dve").split()
        sem = Signals(nc, ctx, name)
        s = type("Semaphores", (), {n: sem(n) for n in names})
        others_ready = [sem(f"others_ready{h}") for h in range(HEADS)]
        angle_dram = nc.dram_tensor("lsh_angles", (2, HEADS, SEQ), F32, kind="Internal").ap()
        parts_dram = nc.dram_tensor("lsh_query_parts", (3, HEADS, HD, SEQ), BF16, kind="Internal").ap()
        LOADS = 16 * 8
        CONSTS = 3 + HEADS
        block = sem.block()

        @block.sync
        def _(sp):
            for dst, src in ((wh, hash_dram), (wq, wq_dram), (wv, wv_dram), (wo, wo_dram)):
                sp.dma_start(dst[:, :, :], src.rearrange("(k p) n -> p k n", p=P)).then_inc(s.loaded, 16)
            with nc.allow_non_contiguous_dma(reason="a short vector"):
                sp.dma_start(bq[:, :], bq_dram.rearrange("(k p) -> p k", p=P)).then_inc(s.loaded, 16)
            for i, vec in enumerate((bv_dram, bo_dram)):
                sp.dma_start(rows[:, i, :], row_of(vec).broadcast_to([P, DIM])).then_inc(s.loaded, 16)
            sp.dma_start(limits[:, :], limits_dram).then_inc(s.loaded, 16)

            def queries(b):
                sp.wait_ge(s.parts_ready, KC * (b + 1))
                wait_from(sp, s.late_loaded, 16 * 16 * b)
                for part in range(3):
                    sp.dma_start(parts_dram[part].rearrange("(c h) d t -> (h d) c t", c=KC), parts[:, part, :, :]).then_inc(s.parts_stored, 16)
                sp.wait_ge(s.parts_stored, 48 * (b + 1))

            def stacked(b, half):
                done = s.late_loaded if half else s.early_loaded
                wait_from(sp, s.score_ready, UNITS * b - (0 if half else UNITS // 2))
                heads = slice(half * HEADS // 2, (half + 1) * HEADS // 2)
                for turn in range(2):
                    for side in range(2):
                        for row, part in enumerate(SIDES[turn][side]):
                            sp.dma_start(stack[row * HD:(row + 1) * HD, turn, side, heads, :],
                                         parts_dram[part, heads].rearrange("h d t -> d h t")).then_inc(done, 16)

            def angles(b, heads):
                if 0 in heads:
                    sp.wait_ge(s.spare_taken, angle_round(b) + 1)
                    sp.dma_start(angle_dram[b % 2], angleT[:, :]).then_inc(s.angles_stored, 16)
                    sp.wait_ge(s.angles_stored, 16 * (b + 1))
                for h in heads:
                    wait_from(sp, s.compared, UNITS * (b - 1) + TPB * (h + 1))
                    sp.dma_start(others[:, h, :], angle_dram[b % 2, h:h + 1, :].broadcast_to([P, SEQ])).then_inc(others_ready[h], 16)

            angles(0, range(HEADS))
            queries(0)
            stacked(0, 0)
            stacked(0, 1)
            angles(1, range(HEADS))
            for b in range(BATCH):
                if b + 1 < BATCH:
                    queries(b + 1)
                    stacked(b + 1, 0)
                if b + 2 < BATCH:
                    angles(b + 2, range(HEADS))
                if b + 1 < BATCH:
                    stacked(b + 1, 1)

        @block.gpsimd
        def _(pool):
            pool.memset(later[:, :], 0.0).then_inc(s.consts, 1)
            pool.memset(mine[:, :, :], 0.0).then_inc(s.consts, 1)
            pool.wait_ge(s.consts, 2)
            pool.affine_select(out=later[:, :], in_=later[:, :], compare_op=ALU.is_ge, fill=1.0, base=0,
                               pattern=[[-1, P]], channel_multiplier=1).then_inc(s.consts, 1)
            for h in range(HEADS):
                pool.memset(mine[:, h, h * SPAN:h * SPAN + SEQ // 64], 1.0).then_inc(s.consts, 1)

            for b in range(BATCH):
                for m in range(KC):
                    n = KC * b + m + 1
                    pool.wait_ge(s.spare_taken, q_round(b, m) + 1)
                    wait_from(pool, s.parts_stored, 48 * b)
                    pool.tensor_copy(parts[:, 0, m, :], q[:, m, :]).then_inc(s.high_ready, 1)
                    pool.wait_ge(s.high_ready, n)
                    pool.tensor_tensor(rest[:, :], q[:, m, :], parts[:, 0, m, :], ALU.subtract).then_inc(s.rest_ready, 1)
                    pool.wait_ge(s.rest_ready, n)
                    pool.tensor_copy(parts[:, 1, m, :], rest[:, :]).then_inc(s.mid_ready, 1)
                    pool.wait_ge(s.mid_ready, n)
                    pool.tensor_tensor(parts[:, 2, m, :], rest[:, :], parts[:, 1, m, :], ALU.subtract).then_inc(s.parts_ready, 1)
                    pool.wait_ge(s.parts_ready, n)

        @block.tensor
        def _(pe):
            def long_step(kind, part, p, step):
                if kind == "q":
                    return pe.matmul(spare[:, :], wq[:, step, part * P:(part + 1) * P], xT[:, p, step, :], start=step == 0, stop=step == 1)
                at = (2 * part + step) * P
                for k in range(KC):
                    left = xT[:, p, k, at:at + P] if kind == "v" else oT[:, k, at:at + P]
                    last = pe.matmul(spare[:, step * DIM:(step + 1) * DIM], left, (wv if kind == "v" else wo)[:, k, :],
                                     start=k == 0, stop=k == KC - 1)
                return last

            def use_spare(number, kind, part, b, p, steps=(0, 1)):
                long = kind in ("q", "v", "y")
                if 0 in steps:
                    if long or 1 in steps:
                        wait_from(pe, s.spare_taken, number)
                    if long and 1 not in steps:
                        long_step(kind, part, p, 0)
                        return
                    if not long and 1 not in steps:
                        return
                elif not long:
                    wait_from(pe, s.spare_taken, number)
                if long:
                    for step in steps:
                        last = long_step(kind, part, p, step)
                if kind == "x":
                    pe.wait_ge(s.xn_ready, b + 1)
                    for j in range(TPB):
                        last = pe.transpose(spare[:, j * P:(j + 1) * P], xn[:, j, part * P:(part + 1) * P], core.ident[:, :])
                if kind == "hash":
                    for j in range(TPB):
                        for k in range(KC):
                            last = pe.matmul(spare[:, j * 2 * HEADS:(j + 1) * 2 * HEADS], xT[:, p, k, j * P:(j + 1) * P], wh[:, k, :],
                                             start=k == 0, stop=k == KC - 1)
                if kind == "angle":
                    for j in range(TPB):
                        last = pe.transpose(spare[0:HEADS, j * P:(j + 1) * P], angle[:, p, j, :], core.ident[:, :])
                if kind == "o":
                    pe.wait_ge(s.o_ready, 2 * (b + 1))
                    for j in range(TPB):
                        last = pe.transpose(spare[:, j * P:(j + 1) * P], o[:, j, part * P:(part + 1) * P], core.ident[:, :])
                last.then_inc(s.spare_sent, 1)

            def count(b, n):
                h, j = n // TPB, n % TPB
                pe.wait_ge(s.compared, UNITS * b + n + 1)
                if n == 0:
                    wait_from(pe, s.hot_ready, b)
                pe.matmul(ranks[:, :], mine[:, h, :], before[:, n % 2, :], start=n == 0, stop=False, skip_group_check=True)
                pe.matmul(ranks[:, j * P:(j + 1) * P], mine[:, h, :], tied[:, n % 2, :], start=False,
                          stop=n == UNITS - 1, skip_group_check=True).then_inc(s.counted, 1)

            def scores(b, p, n):
                h, i = n // TPB, n % TPB
                group = slice(h // 2 * 2 * SPAN, (h // 2 + 1) * 2 * SPAN)
                if n == 0:
                    pe.wait_ge(s.hot_ready, b + 1)
                    pe.wait_ge(s.early_loaded, 16 * 16 * (b + 1))
                if n == UNITS // 2:
                    pe.wait_ge(s.late_loaded, 16 * 16 * (b + 1))
                wait_from(pe, s.exp_ready, UNITS * b + n - 1)
                own = slice(i * P, (i + 1) * P)
                for turn in range(2):
                    pe.matmul(pscore[:, n % 2, :], stack[:, turn, 0, h, own], stack[:, turn, 1, h, :], start=turn == 0, stop=False)
                pe.matmul(pscore[:, n % 2, :], hot[group, p, own], cold[group, p, h % 2, :], start=False, stop=True).then_inc(s.score_ready, 1)

            def turn(b, n):
                pe.wait_ge(s.exp_ready, UNITS * b + n + 1)
                wait_from(pe, s.copied, UNITS * b + n - 1)
                for j in range(TPB):
                    last = pe.transpose(pturn[:, n % 2, j, :], prob[:, n % 4, j * P:(j + 1) * P], core.ident[:, :])
                last.then_inc(s.turned_p, 1)

            def weigh(b, p, n):
                h, i = n // TPB, n % TPB
                pe.wait_ge(s.copied, UNITS * b + n + 1)
                if n in (0, 2):
                    wait_from(pe, s.o_ready, 2 * (b - 1) + n // 2 + 1)
                for j in range(TPB):
                    last = pe.matmul(pout[:, i, h * HD:(h + 1) * HD], probT[:, n % 2, j, :], v[:, p, j, h * HD:(h + 1) * HD],
                                     start=j == 0, stop=j == TPB - 1)
                last.then_inc(s.pv_ready, 1)

            def row(b, p, first=False, last=False, more=True, tail=False):
                for n in range(UNITS if not tail else SLOTS_IN_TAIL):
                    old = lambda lag: (b, p, n - lag) if n >= lag else (b - 1, 1 - p, n - lag + UNITS)
                    if not tail:
                        scores(b, p, n)
                    if (n >= 3 or not first) and not (tail and n >= 3):
                        at, _, unit = old(3)
                        turn(at, unit)
                    if not last and not tail:
                        for unit in range(compared_by(n - 1) if n > 0 else 0, compared_by(n)):
                            count(b + 1, unit)
                    if (n >= 4 or not first) and not (tail and n >= 4):
                        weigh(*old(4))
                    for step in range(2):
                        for which in rounds_in(n + 1 - step, b, p, first, last, more, tail):
                            use_spare(*which, steps=(step,))

            def ahead():
                for number, (kind, part, b) in enumerate(ROUNDS_AHEAD):
                    if number == KC:
                        pe.wait_ge(s.loaded, LOADS)
                        pe.wait_ge(s.consts, CONSTS)
                    use_spare(number, kind, part, b, b)
                for n in range(UNITS):
                    count(0, n)

            ahead()
            rows_in_pairs(pe, row)
            row(BATCH, 0, tail=True)

        @block.scalar
        def _(act):
            def take_spare(number, kind, part, b, p):
                if kind not in ("x", "q", "angle", "o"):
                    return
                act.wait_ge(s.spare_sent, number + 1)
                if kind == "x":
                    act.activation(xT[:, p, part, :], spare[:, :], ACT.Copy).then_inc(s.spare_taken, 1)
                if kind == "q":
                    wait_from(act, s.parts_ready, KC * b)
                    act.activation(q[:, part, :], spare[:, :], ACT.Identity, bias=bq[:, part:part + 1]).then_inc(s.spare_taken, 1)
                if kind == "angle":
                    wait_from(act, s.angles_stored, 16 * b)
                    act.activation(angleT[:, :], spare[0:HEADS, :], ACT.Copy).then_inc(s.spare_taken, 1)
                if kind == "o":
                    act.activation(oT[:, part, :], spare[:, :], ACT.Copy).then_inc(s.spare_taken, 1)

            def exps(b, p, n):
                h, i = n // TPB, n % TPB
                act.wait_ge(s.top_ready, UNITS * b + n + 1)
                wait_from(act, s.turned_p, UNITS * b + n - 3)
                act.activation(prob[:, n % 4, :], pscore[:, n % 2, :], ACT.Exp, bias=top[:, n % 4, 1:2], scale=SCALE,
                               accum_out=total[:, p, i, h:h + 1]).then_inc(s.exp_ready, 1)

            def copy_turned(b, n):
                act.wait_ge(s.turned_p, UNITS * b + n + 1)
                wait_from(act, s.pv_ready, UNITS * b + n - 1)
                act.activation(probT[:, n % 2, :, :], pturn[:, n % 2, :, :], ACT.Copy).then_inc(s.copied, 1)

            def row(b, p, first=False, last=False, more=True, tail=False):
                for n in range(UNITS if not tail else SLOTS_IN_TAIL + 1):
                    if not tail:
                        exps(b, p, n)
                    if (n >= 3 or not first) and not (tail and n >= 3):
                        copy_turned(*((b, n - 3) if n >= 3 else (b - 1, n - 3 + UNITS)))
                    for which in rounds_in(n - 1, b, p, first, last, more, tail):
                        take_spare(*which)

            for number, (kind, part, b) in enumerate(ROUNDS_AHEAD):
                take_spare(number, kind, part, b, b)
            rows_in_pairs(act, row)
            row(BATCH, 0, tail=True)

        @block.vector
        def _(dve):
            chain = Chain(dve, s.chain_dve)
            wide = lambda i: rows[:, i, :].unsqueeze(1).broadcast_to([P, 2, DIM])
            banked = spare[:, :].rearrange("p (j n) -> p j n", j=2)

            def take_spare(number, kind, part, b, p):
                if kind not in ("hash", "v", "y"):
                    return
                dve.wait_ge(s.spare_sent, number + 1)
                if kind == "hash":
                    pairs = spare[:, 0:TPB * 2 * HEADS].rearrange("p (j h two) -> p j h two", h=HEADS, two=2)
                    chain.link(dve.tensor_scalar(below[:, :, :], pairs[:, :, :, 1], 1e-4, None, ALU.add))
                    chain.link(dve.reciprocal(below[:, :, :], below[:, :, :]))
                    dve.tensor_tensor(angle[:, p, :, :], pairs[:, :, :, 0], below[:, :, :], ALU.mult).then_inc(s.spare_taken, 1)
                if kind == "v":
                    dve.tensor_tensor(v[:, p, 2 * part:2 * part + 2, :], banked, wide(0), ALU.add).then_inc(s.spare_taken, 1)
                if kind == "y":
                    dve.tensor_tensor(y[:, 2 * part:2 * part + 2, :], banked, wide(1), ALU.add).then_inc(s.spare_taken, 1)
                    dve.wait_ge(s.spare_taken, number + 1)


            def compare(b, p, n):
                h, j = n // TPB, n % TPB
                own, edge = angle[:, p, j, h:h + 1], (j + 1) * P
                if j == 0:
                    dve.wait_ge(others_ready[h], 16 * (b + 1))
                wait_from(dve, s.counted, UNITS * b + n - 1)
                dve.tensor_scalar(before[:, n % 2, 0:edge], others[:, h, 0:edge], own, None, ALU.is_gt)
                if edge < SEQ:
                    dve.tensor_scalar(before[:, n % 2, edge:], others[:, h, edge:], own, None, ALU.is_ge)
                dve.scalar_tensor_tensor(out=tied[:, n % 2, :], in0=others[:, h, j * P:edge], scalar=own, in1=later[:, :],
                                         op0=ALU.is_equal, op1=ALU.mult).then_inc(s.compared, 1)

            def heat(b, p):
                dve.wait_ge(s.counted, UNITS * (b + 1))
                chain.link(dve.tensor_scalar(least[:, :], ranks[:, :], limits[:, 0:1], None, ALU.is_ge))
                chain.link(dve.scalar_tensor_tensor(out=hot[:, p, :], in0=ranks[:, :], scalar=limits[:, 1:2], in1=least[:, :],
                                                    op0=ALU.is_lt, op1=ALU.mult))
                for side in range(2):
                    last = dve.tensor_scalar(cold[:, p, side, :], hot[:, p, :], 1.0, limits[:, 2 + side:3 + side], ALU.subtract, ALU.mult)
                last.then_inc(s.hot_ready, 1)

            def largest(b, n):
                dve.wait_ge(s.score_ready, UNITS * b + n + 1)
                chain.link(dve.reduce_max(top[:, n % 4, 0:1], pscore[:, n % 2, :], AX.X))
                dve.tensor_scalar(top[:, n % 4, 1:2], top[:, n % 4, 0:1], -SCALE, None, ALU.mult).then_inc(s.top_ready, 1)

            def divide(b, p):
                dve.wait_ge(s.pv_ready, UNITS * (b + 1))
                chain.link(dve.reciprocal(recip[:, :, :], total[:, p, :, :]))
                for bank in range(2):
                    tiles = slice(2 * bank, 2 * bank + 2)
                    by_head = lambda t: t[:, tiles, :].rearrange("p j (h e) -> p j h e", e=HD)
                    dve.tensor_tensor(by_head(o), by_head(pout), recip[:, tiles, :].unsqueeze(3).broadcast_to([P, 2, HEADS, HD]),
                                      ALU.mult).then_inc(s.o_ready, 1)

            def row(b, p, first=False, last=False, more=True, tail=False):
                for n in range(UNITS if not tail else AT_BACK + NORM_STAGES):
                    if not tail:
                        largest(b, n)
                    if n == 4 and not first:
                        divide(b - 1, 1 - p)
                    if not last and not tail:
                        for unit in range(compared_by(n), compared_by(n + 1)):
                            compare(b + 1, 1 - p, unit)
                    for which in rounds_in(n - 1, b, p, first, last, more, tail):
                        take_spare(*which)
                    if AT_BACK <= n < AT_BACK + NORM_STAGES and not first:
                        back_stage(dve, chain, core, b - 1, y, n - AT_BACK)
                    if AT_FRONT <= n < AT_FRONT + NORM_STAGES and more and not tail:
                        front_stage(dve, chain, core, b + 2, xn, s.xn_ready, n - AT_FRONT)
                    if n == AT_HOT and not last and not tail:
                        heat(b + 1, 1 - p)
                chain.restart()

            front(dve, chain, core, 0, xn, s.xn_ready)
            dve.wait_ge(s.loaded, LOADS)
            dve.wait_ge(s.consts, CONSTS)
            for number, (kind, part, b) in enumerate(ROUNDS_AHEAD):
                take_spare(number, kind, part, b, b)
                if (kind, b) == ("hash", 0):
                    front(dve, chain, core, 1, xn, s.xn_ready)
            for n in range(UNITS):
                compare(0, 0, n)
            heat(0, 0)
            chain.restart()
            rows_in_pairs(dve, row)
            row(BATCH, 0, tail=True)


def decay_attention_layer(core, wqk_dram, wv_dram, wo_dram, decay_dram, log_dist_dram, pick_dram):
    nc = core.nc
    name = "causal"
    HEADS, HD, ROOM = 16, 16, 32
    GROUPS = HEADS * ROOM // P
    SIDES = ((0, 0, 1, 1, 0, 2, 1, 2), (0, 1, 0, 1, 2, 0, 2, 1))
    QKC = 2 * DIM // P
    BIG = 1e30
    UNITS = HEADS * TPB
    AT_Y, AT_TAKE, AT_FRONT, AT_TURN, AT_QK, AT_V = 9, 17, 25, 38, 40, 53
    scale_of = lambda chunk: 0.25 if chunk < DIM // P else 1.0
    with ExitStack() as ctx:
        sb = lambda n, shape, dt=F32: ctx.enter_context(nc.sbuf_tensor(f"{name}_{n}", shape, dt))
        ps = lambda n, shape: ctx.enter_context(nc.psum_tensor(f"{name}_{n}", shape, F32))
        wqk, wv, wo = sb("wqk", [P, KC, 2 * DIM]), sb("wv", [P, KC, DIM]), sb("wo", [P, GROUPS, DIM])
        log_dist = sb("log_dist", [P, SEQ])
        soft = sb("soft", [P, 5, HEADS])
        far = sb("far", [P, HEADS, SEQ])
        pick = sb("pick", [4, P])
        after = sb("after", [P, P])
        after_bf = sb("after_bf", [P, P], BF16)
        xn, xT = sb("xn", [P, TPB, DIM]), sb("xT", [P, KC, SEQ])
        rest = sb("rest", [P, 2, SEQ])
        parts = sb("parts", [P, 3, QKC, SEQ], BF16)
        stack = sb("stack", [P, 2, HEADS, SEQ], BF16)
        v = sb("v", [P, 2, TPB, HEADS, ROOM])
        top = sb("top", [P, 4])
        prob = sb("prob", [P, 4, SEQ])
        probT = sb("probT", [P, 4, TPB, SEQ])
        total = sb("total", [P, 2, TPB, HEADS])
        recipT = sb("recipT", [4, SEQ])
        recip = sb("recip", [P, SEQ])
        oT = sb("oT", [P, GROUPS, SEQ])
        y = core.tmp
        pt, pscore = ps("pt", [P, 2, SEQ]), ps("pscore", [P, 2, SEQ])
        pturn, pout = ps("pturn", [P, 2, TPB, P]), ps("pout", [P, 2, SEQ])
        names = ("loaded wo_loaded consts far_ready xn_ready turned xT_ready qk_ready high_ready rest_ready parts_mid parts_ready parts_stored early_loaded "
                 "late_loaded score_ready top_ready exp_ready prob_ready turned_p copied pv_ready sums_ready recipT_sent recipT_ready "
                 "recip_sent recip_ready oT_ready y_ready y_taken v_sent v_ready chain_dve chain_act").split()
        sem = Signals(nc, ctx, name)
        s = type("Semaphores", (), {n: sem(n) for n in names})
        parts_dram = nc.dram_tensor("qk_parts", (3, 2 * HEADS, HD, SEQ), BF16, kind="Internal").ap()
        LOADS = 16 * 5
        block = sem.block()

        @block.sync
        def _(sp):
            for dst, src in ((wqk, wqk_dram), (wv, wv_dram)):
                sp.dma_start(dst[:, :, :], src.rearrange("(k p) n -> p k n", p=P)).then_inc(s.loaded, 16)
            sp.dma_start(log_dist[:, :], log_dist_dram).then_inc(s.loaded, 16)
            sp.dma_start(soft[:, 0, :], row_of(decay_dram).broadcast_to([P, HEADS])).then_inc(s.loaded, 16)
            sp.dma_start(pick[:, :], pick_dram).then_inc(s.loaded, 16)
            sp.wait_ge(s.consts, 4)
            for h in range(HEADS):
                at = h % 4 * ROOM
                sp.dma_start(wo[at:at + HD, h // 4, :], wo_dram[h * HD:(h + 1) * HD, :]).then_inc(s.wo_loaded, 16)

            for b in range(BATCH):
                sp.wait_ge(s.parts_ready, QKC * (b + 1))
                for part in range(3):
                    sp.dma_start(parts_dram[part].rearrange("(c h) d t -> (h d) c t", c=QKC), parts[:, part, :, :]
                                 ).then_inc(s.parts_stored, 16)
                sp.wait_ge(s.parts_stored, 48 * (b + 1))
                for half, done in enumerate((s.early_loaded, s.late_loaded)):
                    wait_from(sp, s.score_ready, UNITS * b - (UNITS // 2 if half == 0 else 0))
                    heads = slice(half * HEADS // 2, (half + 1) * HEADS // 2)
                    for side in range(2):
                        for row, part in enumerate(SIDES[side]):
                            src = parts_dram[part, side * HEADS:(side + 1) * HEADS][heads]
                            sp.dma_start(stack[row * HD:(row + 1) * HD, side, heads, :], src.rearrange("h d t -> d h t")).then_inc(done, 16)

        @block.gpsimd
        def _(pool):
            pool.memset(after[:, :], 0.0).then_inc(s.consts, 1)
            pool.memset(v[:, :, :, :, :], 0.0).then_inc(s.consts, 1)
            pool.wait_ge(s.consts, 2)
            pool.memset(v[:, :, :, :, HD:HD + 1], 1.0).then_inc(s.consts, 1)
            pool.memset(wo[:, :, :], 0.0).then_inc(s.consts, 1)
            pool.affine_select(out=after[:, :], in_=after[:, :], compare_op=ALU.is_ge, fill=-BIG, base=0,
                               pattern=[[-1, P]], channel_multiplier=1).then_inc(s.consts, 1)
            pool.wait_ge(s.consts, 5)
            pool.tensor_copy(after_bf[:, :], after[:, :]).then_inc(s.consts, 1)

            for b in range(BATCH):
                for c in range(QKC):
                    pool.wait_ge(s.rest_ready, QKC * b + c + 1)
                    wait_from(pool, s.parts_stored, 48 * b)
                    pool.tensor_copy(parts[:, 1, c, :], rest[:, c % 2, :]).then_inc(s.parts_mid, 1)
                    pool.wait_ge(s.parts_mid, QKC * b + c + 1)
                    pool.tensor_tensor(parts[:, 2, c, :], rest[:, c % 2, :], parts[:, 1, c, :], ALU.subtract).then_inc(s.parts_ready, 1)

        @block.tensor
        def _(pe):
            def scores(b, n):
                h, i = n // TPB, n % TPB
                width = (i + 1) * P
                if n == 0:
                    pe.wait_ge(s.early_loaded, 16 * 16 * (b + 1))
                if n == UNITS // 2:
                    pe.wait_ge(s.late_loaded, 16 * 16 * (b + 1))
                wait_from(pe, s.exp_ready, UNITS * b + n - 1)
                pe.matmul(pscore[:, n % 2, 0:width], stack[:, 0, h, i * P:width], stack[:, 1, h, 0:width], start=True, stop=True)
                pe.matmul(pscore[:, n % 2, i * P:width], core.ident_bf[:, :], after_bf[:, :], start=False, stop=True,
                          skip_group_check=True).then_inc(s.score_ready, 1)

            def turn(b, n):
                pe.wait_ge(s.prob_ready, UNITS * b + n + 1)
                wait_from(pe, s.copied, UNITS * b + n - 1)
                for j in range(n % TPB + 1):
                    last = pe.transpose(pturn[:, n % 2, j, :], prob[:, n % 4, j * P:(j + 1) * P], core.ident[:, :])
                last.then_inc(s.turned_p, 1)

            def weigh(b, p, h, j):
                if j == 0:
                    pe.wait_ge(s.copied, UNITS * b + TPB * (h + 1))
                if h == 0 and j == 0:
                    pe.wait_ge(s.v_ready, b + 1)
                g, at = h // 4, h % 4 * ROOM
                if h % 4 == 0 and j == 0:
                    wait_from(pe, s.oT_ready, GROUPS * b + g - 1)
                last = pe.matmul(pout[at:at + ROOM, g % 2, j * P:], v[:, p, j, h, :], probT[:, h % 4, j, j * P:],
                                 start=j == 0, stop=True, skip_group_check=True)
                if j == TPB - 1:
                    last.then_inc(s.pv_ready, 1)

            def turn_sums(b, g):
                pe.wait_ge(s.sums_ready, GROUPS * b + g + 1)
                for i in range(TPB):
                    last = pe.transpose(pt[0:4, 0, i * P:(i + 1) * P], total[:, 1, i, 4 * g:4 * g + 4], core.ident[:, :])
                last.then_inc(s.recipT_sent, 1)

            def spread_sums(b, g):
                pe.wait_ge(s.recipT_ready, GROUPS * b + g + 1)
                pe.matmul(pt[:, 1, :], pick[:, :], recipT[:, :], start=True, stop=True).then_inc(s.recip_sent, 1)

            def project_out(b, j, half):
                pe.wait_ge(s.oT_ready, GROUPS * (b + 1))
                for g in range(GROUPS // 2 * half, GROUPS // 2 * (half + 1)):
                    last = pe.matmul(pt[:, j // 2, j % 2 * DIM:(j % 2 + 1) * DIM], oT[:, g, j * P:(j + 1) * P], wo[:, g, :],
                                     start=g == 0, stop=g == GROUPS - 1)
                if j == TPB - 1 and half == 1:
                    last.then_inc(s.y_ready, 1)

            def values(b, j):
                for k in range(KC):
                    last = pe.matmul(pt[:, j // 2, j % 2 * DIM:(j % 2 + 1) * DIM], xT[:, k, j * P:(j + 1) * P], wv[:, k, :],
                                     start=k == 0, stop=k == KC - 1)
                if j == TPB - 1:
                    last.then_inc(s.v_sent, 1)

            def turn_input(b):
                pe.wait_ge(s.xn_ready, b + 1)
                if not isinstance(b, int) or b > 0:
                    pe.wait_ge(s.recip_ready, GROUPS * (b - 1) + 2)
                transposes(pe, core, xn, pt, s.turned)

            def queries_keys(b, c, k):
                if c == 0 and k == 0:
                    pe.wait_ge(s.xT_ready, b + 1)
                if c >= 2 and k == 0:
                    pe.wait_ge(s.rest_ready, QKC * b + c - 1)
                last = pe.matmul(pt[:, c % 2, :], wqk[:, k, c * P:(c + 1) * P], xT[:, k, :], start=k == 0, stop=k == KC - 1)
                if k == KC - 1:
                    last.then_inc(s.qk_ready, 1)

            def slot(b, p, n, first=False, last=False, tail=False):
                old = lambda lag: (b, n - lag) if n >= lag else (b - 1, n - lag + UNITS)
                if not tail:
                    scores(b, n)
                if n >= 3 and not tail or n < 3 and not first:
                    turn(*old(3))
                if n == 2 and not first:
                    turn_sums(b - 1, GROUPS - 1)
                if n == 3 and not first:
                    spread_sums(b - 1, GROUPS - 1)
                if n < 8 and not first:
                    weigh(b - 1, 1 - p, HEADS - 2 + n // TPB, n % TPB)
                if AT_Y <= n < AT_Y + 2 * TPB and not first:
                    project_out(b - 1, (n - AT_Y) // 2, (n - AT_Y) % 2)
                if tail:
                    return
                if n >= 8:
                    weigh(b, p, (n - 8) // TPB, n % TPB)
                if n >= 18 and (n - 18) % 16 == 0:
                    turn_sums(b, (n - 18) // 16)
                if n >= 19 and (n - 19) % 16 == 0:
                    spread_sums(b, (n - 19) // 16)
                if not last and n == AT_TURN:
                    turn_input(b + 1)
                if not last and AT_QK <= n < AT_QK + KC * QKC:
                    queries_keys(b + 1, (n - AT_QK) // KC, (n - AT_QK) % KC)
                if not last and AT_V <= n < AT_V + TPB:
                    values(b + 1, n - AT_V)

            turn_input(0)
            pe.wait_ge(s.loaded, LOADS)
            for c in range(QKC):
                for k in range(KC):
                    queries_keys(0, c, k)
            pe.wait_ge(s.rest_ready, QKC)
            for j in range(TPB):
                values(0, j)
            pe.wait_ge(s.consts, 6)
            pe.wait_ge(s.wo_loaded, 16 * HEADS)

            def row(b, p, first=False, last=False, more=True):
                for n in range(UNITS):
                    slot(b, p, n, first, last)

            rows_in_pairs(pe, row)
            for n in range(AT_TAKE):
                slot(BATCH, 0, n, tail=True)

        @block.scalar
        def _(act):
            chain = Chain(act, s.chain_act)

            def copy_input(b):
                act.wait_ge(s.turned, b + 1)
                wait_from(act, s.v_sent, b)
                act.activation(xT[:, :, :], pt[:, :, :], ACT.Copy).then_inc(s.xT_ready, 1)

            def high_parts(b, c):
                act.wait_ge(s.qk_ready, QKC * b + c + 1)
                wait_from(act, s.parts_stored, 48 * b)
                act.activation(parts[:, 0, c, :], pt[:, c % 2, :], ACT.Copy, scale=scale_of(c)).then_inc(s.high_ready, 1)

            def exps(b, n):
                width = (n % TPB + 1) * P
                act.wait_ge(s.top_ready, UNITS * b + n + 1)
                wait_from(act, s.turned_p, UNITS * b + n - 3)
                act.activation(prob[:, n % 4, 0:width], pscore[:, n % 2, 0:width], ACT.Exp,
                               bias=top[:, n % 4:n % 4 + 1]).then_inc(s.exp_ready, 1)

            def copy_turned(b, n):
                h, i = n // TPB, n % TPB
                act.wait_ge(s.turned_p, UNITS * b + n + 1)
                if i == 0:
                    wait_from(act, s.pv_ready, HEADS * b + h - 3)
                act.activation(probT[:, h % 4, 0:i + 1, i * P:(i + 1) * P], pturn[:, n % 2, 0:i + 1, :], ACT.Copy).then_inc(s.copied, 1)

            def copy_sums(b, g):
                act.wait_ge(s.recipT_sent, GROUPS * b + g + 1)
                act.activation(recipT[:, :], pt[0:4, 0, :], ACT.Copy).then_inc(s.recipT_ready, 1)

            def copy_spread(b, g):
                act.wait_ge(s.recip_sent, GROUPS * b + g + 1)
                wait_from(act, s.oT_ready, GROUPS * b + g)
                act.activation(recip[:, :], pt[:, 1, :], ACT.Copy).then_inc(s.recip_ready, 1)

            def copy_values(b, p):
                act.wait_ge(s.v_sent, b + 1)
                wait_from(act, s.pv_ready, HEADS * (b - 1))
                act.activation(v[:, p, :, :, 0:HD], pt[:, :, :].rearrange("p a (j h e) -> p (a j) h e", j=2, e=HD), ACT.Copy
                               ).then_inc(s.v_ready, 1)

            def slot(b, p, n, first=False, last=False, tail=False):
                old = lambda lag: (b, n - lag) if n >= lag else (b - 1, n - lag + UNITS)
                if not tail:
                    exps(b, n)
                if n >= 3 and not tail or n < 3 and not first:
                    copy_turned(*old(3))
                if n == 2 and not first:
                    copy_sums(b - 1, GROUPS - 1)
                if n == 4 and not first:
                    copy_spread(b - 1, GROUPS - 1)
                if tail:
                    return
                if n >= 18 and (n - 18) % 16 == 0:
                    copy_sums(b, (n - 18) // 16)
                if n >= 20 and (n - 20) % 16 == 0:
                    copy_spread(b, (n - 20) // 16)
                if not last and n == AT_TURN:
                    copy_input(b + 1)
                if not last and AT_QK < n <= AT_QK + KC * QKC and (n - AT_QK) % KC == 0:
                    high_parts(b + 1, (n - AT_QK) // KC - 1)
                if not last and n == AT_V + TPB - 1:
                    copy_values(b + 1, 1 - p)

            copy_input(0)
            act.wait_ge(s.loaded, LOADS)
            chain.link(act.activation(soft[:, 1, :], soft[:, 0, :], ACT.Abs))
            chain.link(act.activation(soft[:, 2, :], soft[:, 1, :], ACT.Exp, scale=-1.0))
            chain.link(act.activation(soft[:, 3, :], soft[:, 2, :], ACT.Identity, bias=1.0))
            act.activation(soft[:, 4, :], soft[:, 3, :], ACT.Ln).then_inc(s.far_ready, 1)
            for c in range(QKC):
                high_parts(0, c)
            copy_values(0, 0)
            def row(b, p, first=False, last=False, more=True):
                for n in range(UNITS):
                    slot(b, p, n, first, last)

            rows_in_pairs(act, row)
            for n in range(AT_TAKE):
                slot(BATCH, 0, n, tail=True)

        @block.vector
        def _(dve):
            chain = Chain(dve, s.chain_dve)
            front(dve, chain, core, 0, xn, s.xn_ready)
            dve.wait_ge(s.loaded, LOADS)
            dve.wait_ge(s.far_ready, 1)
            chain.link(dve.scalar_tensor_tensor(out=soft[:, 3, :], in0=soft[:, 3, :], scalar=1.0, in1=soft[:, 2, :],
                                                op0=ALU.subtract, op1=ALU.subtract))
            chain.link(dve.tensor_tensor(soft[:, 4, :], soft[:, 4, :], soft[:, 3, :], ALU.subtract))
            chain.link(dve.scalar_tensor_tensor(out=soft[:, 0, :], in0=soft[:, 0, :], scalar=0.0, in1=soft[:, 4, :],
                                                op0=ALU.max, op1=ALU.add))
            for h in range(HEADS):
                chain.mark(dve.tensor_scalar(far[:, h, :], log_dist[:, :], soft[:, 0, h:h + 1], 1.0, ALU.mult, ALU.add))

            def rests(b, c):
                dve.wait_ge(s.high_ready, QKC * b + c + 1)
                wait_from(dve, s.parts_ready, QKC * b + c - 1)
                dve.scalar_tensor_tensor(out=rest[:, c % 2, :], in0=pt[:, c % 2, :], scalar=scale_of(c), in1=parts[:, 0, c, :],
                                         op0=ALU.mult, op1=ALU.subtract).then_inc(s.rest_ready, 1)

            def largest(b, n):
                width = (n % TPB + 1) * P
                dve.wait_ge(s.score_ready, UNITS * b + n + 1)
                dve.reduce_max(top[:, n % 4:n % 4 + 1], pscore[:, n % 2, 0:width], AX.X, negate=True).then_inc(s.top_ready, 1)

            def decayed(b, n):
                h, i = n // TPB, n % TPB
                dve.wait_ge(s.exp_ready, UNITS * b + n + 1)
                part = prob[:, n % 4, 0:(i + 1) * P]
                dve.scalar_tensor_tensor(out=part, in0=part, scalar=1.0, in1=far[:, h, (TPB - 1 - i) * P:],
                                         op0=ALU.mult, op1=ALU.mult, accum_out=total[:, 0, i, h:h + 1]).then_inc(s.prob_ready, 1)

            def invert_sums(b, g):
                dve.wait_ge(s.prob_ready, UNITS * b + 16 * (g + 1))
                dve.reciprocal(total[:, 1, :, 4 * g:4 * g + 4], total[:, 0, :, 4 * g:4 * g + 4]).then_inc(s.sums_ready, 1)

            def normalise(b, g):
                dve.wait_ge(s.recip_ready, GROUPS * b + g + 1)
                dve.wait_ge(s.pv_ready, HEADS * b + 4 * (g + 1))
                if g == 0:
                    wait_from(dve, s.y_ready, b)
                dve.tensor_tensor(oT[:, g, :], pout[:, g % 2, :], recip[:, :], ALU.mult).then_inc(s.oT_ready, 1)

            def take_y(b):
                dve.wait_ge(s.y_ready, b + 1)
                dve.tensor_copy(y[:, :, :], pt[:, :, :].rearrange("p a (j n) -> p (a j) n", j=2)).then_inc(s.y_taken, 1)
                dve.wait_ge(s.y_taken, b + 1)

            def slot(b, p, n, first=False, last=False, tail=False):
                old = lambda lag: (b, n - lag) if n >= lag else (b - 1, n - lag + UNITS)
                if not tail:
                    largest(b, n)
                if n >= 1 and not tail or n < 1 and not first:
                    decayed(*old(1))
                if n == AT_TAKE and not first:
                    take_y(b - 1)
                if n == 1 and not first:
                    invert_sums(b - 1, GROUPS - 1)
                if n == 8 and not first:
                    normalise(b - 1, GROUPS - 1)
                if AT_TAKE < n <= AT_TAKE + NORM_STAGES and not first:
                    back_stage(dve, chain, core, b - 1, y, n - AT_TAKE - 1)
                if tail:
                    return
                if n >= 17 and (n - 17) % 16 == 0:
                    invert_sums(b, (n - 17) // 16)
                if n >= 24 and (n - 24) % 16 == 0:
                    normalise(b, (n - 24) // 16)
                if not last and AT_FRONT <= n < AT_FRONT + NORM_STAGES:
                    front_stage(dve, chain, core, b + 1, xn, s.xn_ready, n - AT_FRONT)
                if not last and AT_QK < n <= AT_QK + KC * QKC and (n - AT_QK) % KC == 0:
                    rests(b + 1, (n - AT_QK) // KC - 1)

            for c in range(QKC):
                rests(0, c)
            chain.wait()
            chain.link(dve.reciprocal(far[:, :, :], far[:, :, :]))
            def row(b, p, first=False, last=False, more=True):
                for n in range(UNITS):
                    slot(b, p, n, first, last)
                chain.restart()

            rows_in_pairs(dve, row)
            for n in range(AT_TAKE + NORM_STAGES + 1):
                slot(BATCH, 0, n, tail=True)
            chain.wait()
def linear_layer(core, name, w_dram, scale_dram, bias_dram, dft=None, out_dram=None):
    nc = core.nc
    with ExitStack() as ctx:
        sb = lambda n, shape, dt=F32: ctx.enter_context(nc.sbuf_tensor(f"{name}_{n}", shape, dt))
        sem = Signals(nc, ctx, name)
        xn = sb("xn", [P, TPB, DIM])
        xT = sb("xT", [P, KC, SEQ])
        w = sb("w", [P, KC, DIM])
        bias = sb("bias", [P, DIM])
        scale = sb("scale", [P, DIM])
        y = sb("y", [P, TPB, DIM])
        if dft:
            wf = sb("wf", [P, 2, KC, DIM])
            cs = sb("cs", [P, 3, KC, DIM])
            fw = sb("fw", [P, 2, KC, DIM])
        pt = ctx.enter_context(nc.psum_tensor(f"{name}_pt", [P, KC, SEQ], F32))
        py = ctx.enter_context(nc.psum_tensor(f"{name}_py", [P, TPB, DIM], F32))
        loaded, w_ready, w_acc = sem("loaded"), sem("w_ready"), sem("w_acc")
        xn_ready, turned, xT_ready, y_ready, y_read = (sem(n) for n in ("xn_ready", "turned", "xT_ready", "y_ready", "y_read"))
        chain_dve = sem("chain_dve")
        stored = sem("stored")
        loads = 16 * (5 if dft else 3)
        block = sem.block()

        @block.sync
        def _(sp):
            sp.dma_start(bias[:, :], row_of(bias_dram).broadcast_to([P, DIM])).then_inc(loaded, 16)
            if dft:
                for i in range(2):
                    sp.dma_start(wf[:, i, :, :], w_dram[i].rearrange("(k p) n -> p k n", p=P)).then_inc(loaded, 16)
                    sp.dma_start(cs[:, i, :, :], dft[i].rearrange("(k p) n -> p k n", p=P)).then_inc(loaded, 16)
            else:
                sp.dma_start(w[:, :, :], w_dram.rearrange("(k p) n -> p k n", p=P)).then_inc(loaded, 16)
                sp.dma_start(scale[:, :], row_of(scale_dram).broadcast_to([P, DIM])).then_inc(loaded, 16)
            if out_dram is not None:
                for b in range(BATCH - 1):
                    sp.wait_ge(y_read, b + 2)
                    store_row(sp, core, out_dram, b, stored)
                sp.wait_ge(stored, 16 * (BATCH - 1))

        @block.tensor
        def _(pe):
            pe.wait_ge(loaded, loads)
            if dft:
                pe.wait_ge(w_ready, 1)
                for part, terms in enumerate([((0, 0), (1, 1)), ((1, 0), (0, 2))]):
                    for m in range(KC):
                        n = 0
                        for wi, ci in terms:
                            for k in range(KC):
                                last = pe.matmul(pt[:, part, m * DIM:(m + 1) * DIM], wf[:, wi, k, m * P:(m + 1) * P],
                                                 cs[:, ci, k, :], start=n == 0, stop=n == 2 * KC - 1)
                                n += 1
                last.then_inc(w_acc, 1)
                pe.wait_ge(w_ready, 2)
                for m in range(KC):
                    n = 0
                    for part, ci in ((0, 0), (1, 2)):
                        for k in range(KC):
                            last = pe.matmul(py[:, m, :], fw[:, part, k, m * P:(m + 1) * P], cs[:, ci, k, :],
                                             start=n == 0, stop=n == 2 * KC - 1)
                            n += 1
                last.then_inc(w_acc, 1)
                pe.wait_ge(w_ready, 3)

            def row(b):
                pe.wait_ge(xn_ready, b + 1)
                transposes(pe, core, xn, pt, turned)
                pe.wait_ge(xT_ready, b + 1)
                if not (isinstance(b, int) and b == 0):
                    pe.wait_ge(y_read, b)
                for j in range(TPB):
                    for k in range(KC):
                        last = pe.matmul(py[:, j, :], xT[:, k, j * P:(j + 1) * P], w[:, k, :], start=k == 0, stop=k == KC - 1)
                last.then_inc(y_ready, 1)

            row(0)
            with pe.Fori(1, BATCH) as b:
                row(b)

        @block.scalar
        def _(act):
            def copy_xT(b):
                act.wait_ge(turned, b + 1)
                act.activation(xT[:, :, :], pt[:, :, :], ACT.Copy).then_inc(xT_ready, 1)
            copy_xT(0)
            with act.Fori(1, BATCH) as b:
                act.wait_ge(y_ready, b)
                copy_xT(b)

        @block.vector
        def _(dve):
            chain = Chain(dve, chain_dve)
            if dft:
                dve.wait_ge(loaded, loads)
                dve.tensor_scalar(cs[:, 2, :, :], cs[:, 1, :, :], -1.0, None, ALU.mult).then_inc(w_ready, 1)
                dve.wait_ge(w_acc, 1)
                dve.tensor_copy(fw[:, :, :, :], pt[:, :, :].rearrange("p a (m n) -> p a m n", m=KC)).then_inc(w_ready, 1)
                dve.wait_ge(w_acc, 2)
                dve.tensor_scalar(w[:, :, :], py[:, 0:KC, :], 1.0 / DIM, None, ALU.mult).then_inc(w_ready, 1)
            front(dve, chain, core, 0, xn, xn_ready)
            chain.restart()

            def row(b, last):
                if not last:
                    dve.wait_ge(turned, b + 1)
                    front(dve, chain, core, b + 1, xn, xn_ready)
                dve.wait_ge(y_ready, b + 1)
                if not dft:
                    chain.link(dve.scalar_tensor_tensor(out=y[:, :, :], in0=py[:, :, :], scalar=1.0 / 127.0,
                                                        in1=scale[:, :].unsqueeze(1).broadcast_to([P, TPB, DIM]),
                                                        op0=ALU.mult, op1=ALU.mult))
                src = py if dft else y
                dve.tensor_tensor(y[:, :, :], src[:, :, :], bias[:, :].unsqueeze(1).broadcast_to([P, TPB, DIM]),
                                  ALU.add).then_inc(y_read, 1)
                dve.wait_ge(y_read, b + 1)
                back(dve, chain, core, b, y)
                chain.restart()

            with dve.Fori(0, BATCH - 1) as b:
                row(b, False)
            row(BATCH - 1, True)


def whole_network(nc, a, out):
    with ExitStack() as ctx:
        core = Core(nc, ctx)
        prologue(core, ctx, a["x"])
        delta_layer(core, a["l0a_conv_w"], a["l0a_conv_b"], a["l0a_norm1_w"], a["l0a_norm2_w"], a["l0a_wqkvba"], a["l0a_wo"],
                    a["l0a_wg"], a["l0a_wu"], a["l0a_wd"])
        fused_moe_layer(core, a["l0f_router"], a["l0f_wg"], a["l0f_wu"], a["l0f_wd"], a["l0f_spread"])
        side = lambda d: {n: a[f"{d}_{n}"] for n in MAMBA_WEIGHTS}
        mamba_layer(core, side("fw"), side("bw"), a["l1a_proj"], a["l1a_proj_b"], a["l1a_ln_w"], a["l1a_ln_b"])
        expert_mlp_layer(core, a["l1f_router"], a["l1f_w1"], a["l1f_w2"])
        bucket_attention_layer(core, a["l2a_hash"], a["l2a_wq"], a["l2a_bq"], a["l2a_wv"], a["l2a_bv"], a["l2a_wo"], a["l2a_bo"],
                               a["l2a_limits"])
        linear_layer(core, "l2f", a["l2f_w"], a["l2f_scale"], a["l2f_bias"])
        decay_attention_layer(core, a["l3a_wqk"], a["l3a_wv"], a["l3a_wo"], a["l3a_decay"], a["l3a_log_dist"],
                              a["l3a_pick"])
        linear_layer(core, "l3f", (a["l3f_real"], a["l3f_imag"]), None, a["l3f_bias"], (a["l3f_cos"], a["l3f_sin"]), out)
        epilogue(core, out, (BATCH - 1,))


MAMBA_WEIGHTS = ("in_w", "conv_w", "conv_b", "xproj_w", "dt_w", "dt_b", "Alog", "Dp", "out_w")


def side_by_side(routed, shared):
    flat = [np.moveaxis(w, 0, 1).reshape(w.shape[1], -1) for w in (routed, shared)]
    return np.concatenate(flat, axis=1)


def shape_constants():
    spread = np.zeros((32, 10, P), np.float32)
    for m in range(8):
        spread[2 * m, m, 0:64] = 1
        spread[2 * m + 1, m, 64:128] = 1
    spread[16, 8:] = 1
    limits = np.zeros((P, 4), np.float32)
    limits[:, 0:2] = 1e9
    for p in range(P):
        if p % 16 < 8:
            limits[p, 0:2] = 64 * (p % 16), 64 * (p % 16) + 64
        limits[p, 2 + p // 16 % 2] = 1e30
    distance = np.arange(P)[:, None] + (SEQ - P) - np.arange(SEQ)[None, :]
    n = np.arange(DIM)
    turn = 2 * np.pi * (np.outer(n, n) % DIM) / DIM
    return {"l0f_spread": spread, "l2a_limits": limits,
            "l3a_pick": np.kron(np.eye(4), np.ones((1, 32))).astype(np.float32),
            "l3a_log_dist": np.log1p(np.maximum(distance, 0)).astype(np.float32),
            "l3f_cos": np.cos(turn).astype(np.float32), "l3f_sin": np.sin(turn).astype(np.float32)}


def laid_out(v):
    a = {"x": v["L0_attn_x"]}
    for n in ("conv_w", "conv_b", "norm1_w", "norm2_w", "wo", "wg", "wu", "wd"):
        a["l0a_" + n] = v["L0_attn_" + n]
    a["l0a_wqkvba"] = np.concatenate([v["L0_attn_" + n] for n in ("wq", "wk", "wv", "wb", "wa")], axis=1)
    a["l0f_router"] = v["L0_ffn_router_w"]
    a["l0f_wg"] = side_by_side(v["L0_ffn_wg_r"], v["L0_ffn_wg_s"])
    a["l0f_wu"] = side_by_side(v["L0_ffn_wu_r"], v["L0_ffn_wu_s"])
    a["l0f_wd"] = np.concatenate([v["L0_ffn_wd_r"].reshape(-1, DIM), v["L0_ffn_wd_s"].reshape(-1, DIM)], axis=0)
    for d in ("fw", "bw"):
        w = {n: v[f"L1_attn_{d}_{n}"] for n in MAMBA_WEIGHTS}
        for n in ("in_w", "dt_w", "out_w"):
            w[n] = w[n].T
        w["conv_w"] = w["conv_w"][:, 0, :]
        xproj = np.zeros((w["xproj_w"].shape[1], 80), np.float32)
        for i in range(3):
            xproj[:, 32 * i:32 * i + 16] = w["xproj_w"].T[:, 16 * i:16 * i + 16]
        w["xproj_w"] = xproj
        for n in MAMBA_WEIGHTS:
            a[f"{d}_{n}"] = w[n]
    a["l1a_proj"], a["l1a_proj_b"] = v["L1_attn_proj_w"].T, v["L1_attn_proj_b"]
    a["l1a_ln_w"], a["l1a_ln_b"] = v["L1_attn_ln_w"], v["L1_attn_ln_b"]
    a["l1f_router"] = v["L1_ffn_router_w"].T
    a["l1f_w1"], a["l1f_w2"] = np.swapaxes(v["L1_ffn_w1"], 1, 2), np.swapaxes(v["L1_ffn_w2"], 1, 2)
    for to, n in (("hash", "W_hash"), ("wq", "W_q"), ("bq", "b_q"), ("wv", "W_v"), ("bv", "b_v"), ("wo", "W_o"), ("bo", "b_o")):
        a["l2a_" + to] = v["L2_attn_" + n]
    a["l2f_w"], a["l2f_scale"], a["l2f_bias"] = v["L2_ffn_CB"].T, v["L2_ffn_SCB"], v["L2_ffn_bias"]
    qkv = v["L3_attn_w_attn"]
    a["l3a_wqk"], a["l3a_wv"] = qkv[:, 0:2 * DIM], qkv[:, 2 * DIM:]
    a["l3a_wo"], a["l3a_decay"] = v["L3_attn_w_proj"], v["L3_attn_decay_raw"]
    a["l3f_real"], a["l3f_imag"], a["l3f_bias"] = v["L3_ffn_w_freq_real"], v["L3_ffn_w_freq_imag"], v["L3_ffn_bias"]
    a.update(shape_constants())
    return a


def kernel(**inputs):
    import concourse.bacc as bacc
    from concourse.bass_utils import run_bass_kernel_spmd

    nc = bacc.Bacc("TRN2", target_bir_lowering=False, num_devices=1)
    arrays, aps = {}, {}
    for name, value in laid_out({k: np.asarray(v) for k, v in inputs.items()}).items():
        arrays["in_" + name] = np.ascontiguousarray(value)
        aps[name] = nc.dram_tensor("in_" + name, value.shape, mybir.dt.from_np(value.dtype), kind="ExternalInput").ap()
    out = nc.dram_tensor("out", (BATCH, SEQ, DIM), F32, kind="ExternalOutput").ap()
    whole_network(nc, aps, out)
    return run_bass_kernel_spmd(nc, [arrays], core_ids=[0]).results[0]["out"]
```
